# Optimizing a Trainium2 kernel written in Bass

```python
import numpy as np
import jax
import jax.numpy as jnp

def _softmax(x, axis=-1):
    return jax.nn.softmax(x, axis=axis)

def _gelu(x):
    return jax.nn.gelu(x, approximate=True)

def _silu(x):
    return jax.nn.silu(x)

def _sigmoid(x):
    return jax.nn.sigmoid(x)

def _layernorm(x, axis=-1, eps=1e-05):
    m = jnp.mean(x, axis=axis, keepdims=True)
    v = jnp.var(x, axis=axis, keepdims=True)
    return (x - m) / jnp.sqrt(v + eps)

def _scatter_add(tgt, idx, src, axis=0):
    return tgt.at[idx].add(src)

def _segment_sum(src, seg, n):
    return jax.ops.segment_sum(src, seg, n)
kernel_name = 'mk_decoder_preln_d4_seqx_r4_a9b01e'

def setup_inputs(seed: int=0):
    np.random.seed(seed)
    _w = jnp.asarray

    def _rec_inputs():
        import jax
        import jax.numpy as jnp
        _rk = jax.random.key(seed)
        x = 7.22e-05 + 1 * jax.random.normal(jax.random.fold_in(_rk, 1), (16, 112, 256), jnp.float32)
        _lenS = 112 - jax.random.randint(jax.random.fold_in(_rk, 7), (16,), 0, max(1, 112 // 4) + 1, jnp.int32)
        _lenS2 = 375 - jax.random.randint(jax.random.fold_in(_rk, 8), (16,), 0, max(1, 375 // 4) + 1, jnp.int32)
        _ctx_768P = jax.random.normal(jax.random.fold_in(_rk, 11), (16, 16, 192), jnp.float32)
        _ctx_768c = jax.random.dirichlet(jax.random.fold_in(_rk, 511), 0.3 * jnp.ones((16,), jnp.float32), (16, 375))
        _ctx_768t = jnp.einsum('bsk,bkd->bsd', _ctx_768c, _ctx_768P)
        _ctx_768t = _ctx_768t * jax.lax.rsqrt(jnp.mean(jnp.square(_ctx_768t)) + 1e-12) * 0.953939
        ctx_768 = -0.000191848 + 0.999787 * (_ctx_768t + 0.3 * jax.random.normal(jax.random.fold_in(_rk, 611), (16, 375, 192), jnp.float32))
        _validS = jnp.arange(112)[None, :] < _lenS[:, None]
        _validS2 = jnp.arange(375)[None, :] < _lenS2[:, None]
        _causal = jnp.tril(jnp.ones((112, 112), dtype=bool))
        mask_BxS2_bf1 = jnp.ones((16, 375), dtype=bool)
        return (x, ctx_768, mask_BxS2_bf1)
    x, ctx_768, mask_BxS2_bf1 = _rec_inputs()

    def _L0_attn_setup():
        import jax, jax.numpy as jnp
        import numpy as np
        EPS = 1e-05
        key = jax.random.key(seed)
        ks = jax.random.split(key, 16)
        B, T, D = (8, 512, 256)
        Hh, KD, VD, LR, GLR = (4, 128, 256, 32, 64)
        s = 0.02
        w = lambda k, shape: jax.random.normal(k, shape, jnp.float32) * s
        return {'hidden_states': jax.random.normal(ks[0], (B, T, D), jnp.float32), 'mu_x': w(ks[1], (D,)), 'W_x1': w(ks[2], (5 * LR, D)), 'W_x2': w(ks[3], (D, 5 * LR)), 'x_bias': jnp.zeros((5, D), jnp.float32), 'W_r': w(ks[4], (KD, D)), 'W_k': w(ks[5], (KD, D)), 'W_v': w(ks[6], (VD, D)), 'W_g': w(ks[7], (VD, D)), 'A_w': w(ks[8], (GLR, D)), 'B_w': w(ks[9], (KD, GLR)), 'b_w': jnp.zeros((KD,), jnp.float32), 'bonus': w(ks[10], (Hh, KD // Hh)), 'gn_weight': jnp.ones((VD,), jnp.float32), 'gn_bias': jnp.zeros((VD,), jnp.float32), 'W_o': w(ks[11], (D, VD))}
    _L0_attn_all = _L0_attn_setup()
    _L0_attn_in = {k: v for k, v in _L0_attn_all.items() if k in ('mu_x', 'W_x1', 'W_x2', 'x_bias', 'W_r', 'W_k', 'W_v', 'W_g', 'A_w', 'B_w', 'b_w', 'bonus', 'gn_weight', 'gn_bias', 'W_o')}
    del _L0_attn_all

    def _L0_xattn_setup():
        import jax, jax.numpy as jnp
        import numpy as np
        NUM_HEADS = 16
        CLAMP = 10000.0
        key = jax.random.key(seed)
        ks = jax.random.split(key, 8)
        B, Nq, Nkv, Cq, Ckv = (4, 512, 512, 256, 192)
        s_q = 1.0 / np.sqrt(Cq)
        s_kv = 1.0 / np.sqrt(Ckv)
        return {'query': jax.random.normal(ks[0], (B, Nq, Cq), jnp.float32), 'key_value': jax.random.normal(ks[1], (B, Nkv, Ckv), jnp.float32), 'Wq': jax.random.normal(ks[2], (Cq, Cq), jnp.float32) * s_q, 'bq': jnp.zeros((Cq,), jnp.float32), 'Wk': jax.random.normal(ks[3], (Ckv, Cq), jnp.float32) * s_kv, 'bk': jnp.zeros((Cq,), jnp.float32), 'Wv': jax.random.normal(ks[4], (Ckv, Cq), jnp.float32) * s_kv, 'bv': jnp.zeros((Cq,), jnp.float32), 'Wo': jax.random.normal(ks[5], (Cq, Cq), jnp.float32) * s_q, 'bo': jnp.zeros((Cq,), jnp.float32)}
    _L0_xattn_all = _L0_xattn_setup()
    _L0_xattn_in = {k: v for k, v in _L0_xattn_all.items() if k in ('Wq', 'bq', 'Wk', 'bk', 'Wv', 'bv', 'Wo', 'bo')}
    del _L0_xattn_all

    def _L0_ffn_setup():
        import jax, jax.numpy as jnp
        import numpy as np
        NUM_EXPERTS = 8
        TOP_K = 2
        key = jax.random.key(seed)
        ks = jax.random.split(key, 4)
        B, S, H, F = (4, 1024, 256, 1024)
        x = jax.random.normal(ks[0], (B, S, H), dtype=jnp.float32)
        router_w = jax.random.normal(ks[1], (H, NUM_EXPERTS), dtype=jnp.float32) * 0.02
        w1 = jax.random.normal(ks[2], (H, F), dtype=jnp.float32) * 0.02
        b1 = jnp.zeros((F,), dtype=jnp.float32)
        w2 = jax.random.normal(ks[3], (F, H), dtype=jnp.float32) * 0.02
        b2 = jnp.zeros((H,), dtype=jnp.float32)
        return {'x': x, 'router_w': router_w, 'w1': w1, 'b1': b1, 'w2': w2, 'b2': b2}
    _L0_ffn_all = _L0_ffn_setup()
    _L0_ffn_in = {k: v for k, v in _L0_ffn_all.items() if k in ('router_w', 'w1', 'b1', 'w2', 'b2')}
    del _L0_ffn_all

    def _L1_attn_setup():
        import jax, jax.numpy as jnp
        import numpy as np
        B, L, D, S, K, FF = (2, 1024, 256, 16, 3, 672)
        EPS = 1e-06

        def rmsnorm(x, w):
            var = jnp.mean(x * x, axis=-1, keepdims=True)
            return x * jax.lax.rsqrt(var + EPS) * w
        key = jax.random.key(seed)
        ks = jax.random.split(key, 12)
        return {'u': jax.random.normal(ks[0], (B, L, D), jnp.float32), 'pre_norm_w': jnp.ones((D,), jnp.float32), 'in_proj_w': jax.random.normal(ks[1], (3 * D, D), jnp.float32) * D ** (-0.5), 'short_w': jax.random.normal(ks[2], (3 * D, 1, K), jnp.float32) * 0.3, 'short_b': jax.random.normal(ks[3], (3 * D,), jnp.float32) * 0.02, 'log_poles': -(jax.random.uniform(ks[4], (D, S, 1), jnp.float32) * 0.3 + 0.001), 'residues': jax.random.normal(ks[5], (D, S), jnp.float32) * S ** (-0.5), 'D_skip': jax.random.normal(ks[6], (D,), jnp.float32) * 0.02, 'out_proj_w': jax.random.normal(ks[7], (D, D), jnp.float32) * D ** (-0.5), 'post_norm_w': jnp.ones((D,), jnp.float32), 'l1_w': jax.random.normal(ks[8], (FF, D), jnp.float32) * D ** (-0.5), 'l2_w': jax.random.normal(ks[9], (FF, D), jnp.float32) * D ** (-0.5), 'l3_w': jax.random.normal(ks[10], (D, FF), jnp.float32) * FF ** (-0.5)}
    _L1_attn_all = _L1_attn_setup()
    _L1_attn_in = {k: v for k, v in _L1_attn_all.items() if k in ('pre_norm_w', 'in_proj_w', 'short_w', 'short_b', 'log_poles', 'residues', 'D_skip', 'out_proj_w', 'post_norm_w', 'l1_w', 'l2_w', 'l3_w')}
    del _L1_attn_all

    def _L1_xattn_setup():
        import jax, jax.numpy as jnp
        import numpy as np
        HEADS = 8
        DIM_HEAD = 64
        QUERY_DIM = 256
        CONTEXT_DIM = 192
        INNER = HEADS * DIM_HEAD
        key = jax.random.key(seed)
        ks = jax.random.split(key, 7)
        B, Sq, Skv = (4, 1024, 256)
        x = jax.random.normal(ks[0], (B, Sq, QUERY_DIM), dtype=jnp.float32)
        context = jax.random.normal(ks[1], (B, Skv, CONTEXT_DIM), dtype=jnp.float32)
        Wq = jax.random.normal(ks[2], (QUERY_DIM, INNER), dtype=jnp.float32) * QUERY_DIM ** (-0.5)
        Wk = jax.random.normal(ks[3], (CONTEXT_DIM, INNER), dtype=jnp.float32) * CONTEXT_DIM ** (-0.5)
        Wv = jax.random.normal(ks[4], (CONTEXT_DIM, INNER), dtype=jnp.float32) * CONTEXT_DIM ** (-0.5)
        Wo = jax.random.normal(ks[5], (INNER, QUERY_DIM), dtype=jnp.float32) * INNER ** (-0.5)
        bo = jax.random.normal(ks[6], (QUERY_DIM,), dtype=jnp.float32) * 0.01
        return {'x': x, 'context': context, 'Wq': Wq, 'Wk': Wk, 'Wv': Wv, 'Wo': Wo, 'bo': bo}
    _L1_xattn_all = _L1_xattn_setup()
    _L1_xattn_in = {k: v for k, v in _L1_xattn_all.items() if k in ('Wq', 'Wk', 'Wv', 'Wo', 'bo')}
    del _L1_xattn_all

    def _L1_ffn_setup():
        import jax, jax.numpy as jnp
        import numpy as np
        D = 256
        H = 512
        E = 8
        K = 2
        B, T = (4, 512)
        key = jax.random.key(seed)
        ks = jax.random.split(key, 7)
        s = 0.02
        return {'x': jax.random.normal(ks[0], (B, T, D), dtype=jnp.float32), 'W1': jax.random.normal(ks[1], (E, D, 2 * H), dtype=jnp.float32) * s, 'b1': jnp.zeros((E, 2 * H), dtype=jnp.float32), 'W2': jax.random.normal(ks[2], (E, H, D), dtype=jnp.float32) * s, 'b2': jnp.zeros((E, D), dtype=jnp.float32), 'Wr': jax.random.normal(ks[3], (D, E), dtype=jnp.float32) * s, 'br': jnp.zeros((E,), dtype=jnp.float32)}
    _L1_ffn_all = _L1_ffn_setup()
    _L1_ffn_in = {k: v for k, v in _L1_ffn_all.items() if k in ('W1', 'b1', 'W2', 'b2', 'Wr', 'br')}
    del _L1_ffn_all

    def _L2_attn_setup():
        import jax, jax.numpy as jnp
        import numpy as np
        EPS = 1e-05

        def _layernorm(x, gamma, beta):
            m = jnp.mean(x, axis=-1, keepdims=True)
            v = jnp.mean(jnp.square(x - m), axis=-1, keepdims=True)
            return (x - m) * jax.lax.rsqrt(v + EPS) * gamma + beta
        key = jax.random.key(seed)
        B, Q, C, H = (4, 1024, 256, 16)
        hd = C // H
        ks = jax.random.split(key, 8)
        s_in = 1.0 / np.sqrt(C)
        return {'x': jax.random.normal(ks[0], (B, Q, C), jnp.float32), 'qkv_w': jax.random.normal(ks[1], (3 * C, C), jnp.float32) * s_in, 'qkv_b': jnp.zeros((3 * C,), jnp.float32), 'kn_g': jnp.ones((hd,), jnp.float32), 'kn_b': jnp.zeros((hd,), jnp.float32), 'vn_g': jnp.ones((hd,), jnp.float32), 'vn_b': jnp.zeros((hd,), jnp.float32), 'temperature': jnp.ones((H, 1, 1), jnp.float32), 'attn_bias': jnp.zeros((H, hd, hd), jnp.float32), 'p1_w': jax.random.normal(ks[2], (C, C), jnp.float32) * s_in, 'p1_b': jnp.zeros((C,), jnp.float32), 'p2_w': jax.random.normal(ks[3], (C, C), jnp.float32) * s_in, 'p2_b': jnp.zeros((C,), jnp.float32)}
    _L2_attn_all = _L2_attn_setup()
    _L2_attn_in = {k: v for k, v in _L2_attn_all.items() if k in ('qkv_w', 'qkv_b', 'kn_g', 'kn_b', 'vn_g', 'vn_b', 'temperature', 'attn_bias', 'p1_w', 'p1_b', 'p2_w', 'p2_b')}
    del _L2_attn_all

    def _L2_xattn_setup():
        import jax, jax.numpy as jnp
        import numpy as np
        DIM = 256
        CTX_DIM = 192
        HEADS = 16
        key = jax.random.key(seed)
        ks = jax.random.split(key, 7)
        B, N, M = (4, 1024, 64)
        x = jax.random.normal(ks[0], (B, N, DIM), dtype=jnp.float32)
        context = jax.random.normal(ks[1], (B, M, CTX_DIM), dtype=jnp.float32)
        context_mask = jnp.ones((B, M), dtype=bool)
        s_d = 1.0 / np.sqrt(DIM)
        s_c = 1.0 / np.sqrt(CTX_DIM)
        Wq = jax.random.normal(ks[2], (DIM, DIM), dtype=jnp.float32) * s_d
        Wk = jax.random.normal(ks[3], (CTX_DIM, DIM), dtype=jnp.float32) * s_c
        Wv = jax.random.normal(ks[4], (CTX_DIM, DIM), dtype=jnp.float32) * s_c
        Wo = jax.random.normal(ks[5], (DIM, DIM), dtype=jnp.float32) * s_d
        return {'x': x, 'context': context, 'context_mask': context_mask, 'Wq': Wq, 'Wk': Wk, 'Wv': Wv, 'Wo': Wo}
    _L2_xattn_all = _L2_xattn_setup()
    _L2_xattn_in = {k: v for k, v in _L2_xattn_all.items() if k in ('Wq', 'Wk', 'Wv', 'Wo')}
    del _L2_xattn_all

    def _L2_ffn_setup():
        import jax, jax.numpy as jnp
        import numpy as np
        D_MODEL = 256
        N_EXPERTS = 8
        TOP_K = 2
        FFN_HIDDEN = 4 * D_MODEL
        key = jax.random.key(seed)
        ks = jax.random.split(key, 6)

        def xavier(k, shape):
            fan_in, fan_out = (shape[-2], shape[-1])
            lim = jnp.sqrt(6.0 / (fan_in + fan_out))
            return jax.random.uniform(k, shape, jnp.float32, -lim, lim)
        x = jax.random.normal(ks[0], (4, 512, D_MODEL), jnp.float32)
        w_gate = xavier(ks[1], (N_EXPERTS, D_MODEL))
        W1 = xavier(ks[2], (N_EXPERTS, D_MODEL, FFN_HIDDEN))
        b1 = jnp.zeros((N_EXPERTS, FFN_HIDDEN), jnp.float32)
        W2 = xavier(ks[3], (N_EXPERTS, FFN_HIDDEN, D_MODEL))
        b2 = jnp.zeros((N_EXPERTS, D_MODEL), jnp.float32)
        return {'x': x, 'w_gate': w_gate, 'W1': W1, 'b1': b1, 'W2': W2, 'b2': b2}
    _L2_ffn_all = _L2_ffn_setup()
    _L2_ffn_in = {k: v for k, v in _L2_ffn_all.items() if k in ('w_gate', 'W1', 'b1', 'W2', 'b2')}
    del _L2_ffn_all

    def _L3_attn_setup():
        import jax, jax.numpy as jnp
        import numpy as np
        HIDDEN = 256
        HEADS = 16
        HEAD_DIM = HIDDEN // HEADS
        B, S = (4, 512)
        key = jax.random.key(seed)
        ks = jax.random.split(key, 10)
        scale = 1.0 / np.sqrt(HIDDEN)

        def lin(k):
            return jax.random.uniform(k, (HIDDEN, HIDDEN), jnp.float32, -scale, scale)
        return {'x': jax.random.normal(ks[0], (B, S, HIDDEN), jnp.float32), 'Wq': lin(ks[1]), 'bq': jnp.zeros((HIDDEN,), jnp.float32), 'Wk': lin(ks[2]), 'bk': jnp.zeros((HIDDEN,), jnp.float32), 'Wv': lin(ks[3]), 'bv': jnp.zeros((HIDDEN,), jnp.float32), 'Wo': lin(ks[4]), 'bo': jnp.zeros((HIDDEN,), jnp.float32), 'head_mask': jnp.ones((HEADS,), jnp.float32)}
    _L3_attn_all = _L3_attn_setup()
    _L3_attn_in = {k: v for k, v in _L3_attn_all.items() if k in ('Wq', 'bq', 'Wk', 'bk', 'Wv', 'bv', 'Wo', 'bo', 'head_mask')}
    del _L3_attn_all

    def _L3_xattn_setup():
        import jax, jax.numpy as jnp
        import numpy as np
        Q_DIM, K_DIM, V_DIM, OUT_DIM = (256, 192, 192, 256)
        key = jax.random.key(seed)
        ks = jax.random.split(key, 9)
        s = lambda d: 1.0 / np.sqrt(d)
        return {'query': jax.random.normal(ks[0], (16, 512, Q_DIM), jnp.float32), 'key': jax.random.normal(ks[1], (16, 512, K_DIM), jnp.float32), 'value': jax.random.normal(ks[2], (16, 512, V_DIM), jnp.float32), 'Wq': jax.random.uniform(ks[3], (OUT_DIM, Q_DIM), jnp.float32, -s(Q_DIM), s(Q_DIM)), 'bq': jax.random.uniform(ks[4], (OUT_DIM,), jnp.float32, -s(Q_DIM), s(Q_DIM)), 'Wk': jax.random.uniform(ks[5], (OUT_DIM, K_DIM), jnp.float32, -s(K_DIM), s(K_DIM)), 'bk': jax.random.uniform(ks[6], (OUT_DIM,), jnp.float32, -s(K_DIM), s(K_DIM)), 'Wv': jax.random.uniform(ks[7], (OUT_DIM, V_DIM), jnp.float32, -s(V_DIM), s(V_DIM)), 'bv': jax.random.uniform(ks[8], (OUT_DIM,), jnp.float32, -s(V_DIM), s(V_DIM))}
    _L3_xattn_all = _L3_xattn_setup()
    _L3_xattn_in = {k: v for k, v in _L3_xattn_all.items() if k in ('Wq', 'bq', 'Wk', 'bk', 'Wv', 'bv')}
    del _L3_xattn_all

    def _L3_ffn_setup():
        import jax, jax.numpy as jnp
        import numpy as np
        B, S, D, O, H, E, K = (4, 256, 256, 256, 512, 16, 4)
        key = jax.random.key(seed)
        ks = jax.random.split(key, 8)
        x = jax.random.normal(ks[0], (B, S, D), dtype=jnp.float32)
        w_gate = jax.random.normal(ks[1], (D, E), dtype=jnp.float32) * 0.01
        w_noise = jnp.zeros((D, E), dtype=jnp.float32)
        W1 = jax.random.normal(ks[2], (E, D, H), dtype=jnp.float32) * (1.0 / np.sqrt(D))
        b1 = jnp.zeros((E, H), dtype=jnp.float32)
        W2 = jax.random.normal(ks[3], (E, H, O), dtype=jnp.float32) * (1.0 / np.sqrt(H))
        b2 = jnp.zeros((E, O), dtype=jnp.float32)
        return {'x': x, 'w_gate': w_gate, 'w_noise': w_noise, 'W1': W1, 'b1': b1, 'W2': W2, 'b2': b2}
    _L3_ffn_all = _L3_ffn_setup()
    _L3_ffn_in = {k: v for k, v in _L3_ffn_all.items() if k in ('w_gate', 'w_noise', 'W1', 'b1', 'W2', 'b2')}
    del _L3_ffn_all
    return {'x': x, 'ctx_768': ctx_768, 'mask_BxS2_bf1': mask_BxS2_bf1, 'L0_attn_mu_x': _L0_attn_in['mu_x'], 'L0_attn_W_x1': _L0_attn_in['W_x1'], 'L0_attn_W_x2': _L0_attn_in['W_x2'], 'L0_attn_x_bias': _L0_attn_in['x_bias'], 'L0_attn_W_r': _L0_attn_in['W_r'], 'L0_attn_W_k': _L0_attn_in['W_k'], 'L0_attn_W_v': _L0_attn_in['W_v'], 'L0_attn_W_g': _L0_attn_in['W_g'], 'L0_attn_A_w': _L0_attn_in['A_w'], 'L0_attn_B_w': _L0_attn_in['B_w'], 'L0_attn_b_w': _L0_attn_in['b_w'], 'L0_attn_bonus': _L0_attn_in['bonus'], 'L0_attn_gn_weight': _L0_attn_in['gn_weight'], 'L0_attn_gn_bias': _L0_attn_in['gn_bias'], 'L0_attn_W_o': _L0_attn_in['W_o'], 'L0_xattn_Wq': _L0_xattn_in['Wq'], 'L0_xattn_bq': _L0_xattn_in['bq'], 'L0_xattn_Wk': _L0_xattn_in['Wk'], 'L0_xattn_bk': _L0_xattn_in['bk'], 'L0_xattn_Wv': _L0_xattn_in['Wv'], 'L0_xattn_bv': _L0_xattn_in['bv'], 'L0_xattn_Wo': _L0_xattn_in['Wo'], 'L0_xattn_bo': _L0_xattn_in['bo'], 'L0_ffn_router_w': _L0_ffn_in['router_w'], 'L0_ffn_w1': _L0_ffn_in['w1'], 'L0_ffn_b1': _L0_ffn_in['b1'], 'L0_ffn_w2': _L0_ffn_in['w2'], 'L0_ffn_b2': _L0_ffn_in['b2'], 'L1_attn_pre_norm_w': _L1_attn_in['pre_norm_w'], 'L1_attn_in_proj_w': _L1_attn_in['in_proj_w'], 'L1_attn_short_w': _L1_attn_in['short_w'], 'L1_attn_short_b': _L1_attn_in['short_b'], 'L1_attn_log_poles': _L1_attn_in['log_poles'], 'L1_attn_residues': _L1_attn_in['residues'], 'L1_attn_D_skip': _L1_attn_in['D_skip'], 'L1_attn_out_proj_w': _L1_attn_in['out_proj_w'], 'L1_attn_post_norm_w': _L1_attn_in['post_norm_w'], 'L1_attn_l1_w': _L1_attn_in['l1_w'], 'L1_attn_l2_w': _L1_attn_in['l2_w'], 'L1_attn_l3_w': _L1_attn_in['l3_w'], 'L1_xattn_Wq': _L1_xattn_in['Wq'], 'L1_xattn_Wk': _L1_xattn_in['Wk'], 'L1_xattn_Wv': _L1_xattn_in['Wv'], 'L1_xattn_Wo': _L1_xattn_in['Wo'], 'L1_xattn_bo': _L1_xattn_in['bo'], 'L1_ffn_W1': _L1_ffn_in['W1'], 'L1_ffn_b1': _L1_ffn_in['b1'], 'L1_ffn_W2': _L1_ffn_in['W2'], 'L1_ffn_b2': _L1_ffn_in['b2'], 'L1_ffn_Wr': _L1_ffn_in['Wr'], 'L1_ffn_br': _L1_ffn_in['br'], 'L2_attn_qkv_w': _L2_attn_in['qkv_w'], 'L2_attn_qkv_b': _L2_attn_in['qkv_b'], 'L2_attn_kn_g': _L2_attn_in['kn_g'], 'L2_attn_kn_b': _L2_attn_in['kn_b'], 'L2_attn_vn_g': _L2_attn_in['vn_g'], 'L2_attn_vn_b': _L2_attn_in['vn_b'], 'L2_attn_temperature': _L2_attn_in['temperature'], 'L2_attn_attn_bias': _L2_attn_in['attn_bias'], 'L2_attn_p1_w': _L2_attn_in['p1_w'], 'L2_attn_p1_b': _L2_attn_in['p1_b'], 'L2_attn_p2_w': _L2_attn_in['p2_w'], 'L2_attn_p2_b': _L2_attn_in['p2_b'], 'L2_xattn_Wq': _L2_xattn_in['Wq'], 'L2_xattn_Wk': _L2_xattn_in['Wk'], 'L2_xattn_Wv': _L2_xattn_in['Wv'], 'L2_xattn_Wo': _L2_xattn_in['Wo'], 'L2_ffn_w_gate': _L2_ffn_in['w_gate'], 'L2_ffn_W1': _L2_ffn_in['W1'], 'L2_ffn_b1': _L2_ffn_in['b1'], 'L2_ffn_W2': _L2_ffn_in['W2'], 'L2_ffn_b2': _L2_ffn_in['b2'], 'L3_attn_Wq': _L3_attn_in['Wq'], 'L3_attn_bq': _L3_attn_in['bq'], 'L3_attn_Wk': _L3_attn_in['Wk'], 'L3_attn_bk': _L3_attn_in['bk'], 'L3_attn_Wv': _L3_attn_in['Wv'], 'L3_attn_bv': _L3_attn_in['bv'], 'L3_attn_Wo': _L3_attn_in['Wo'], 'L3_attn_bo': _L3_attn_in['bo'], 'L3_attn_head_mask': _L3_attn_in['head_mask'], 'L3_xattn_Wq': _L3_xattn_in['Wq'], 'L3_xattn_bq': _L3_xattn_in['bq'], 'L3_xattn_Wk': _L3_xattn_in['Wk'], 'L3_xattn_bk': _L3_xattn_in['bk'], 'L3_xattn_Wv': _L3_xattn_in['Wv'], 'L3_xattn_bv': _L3_xattn_in['bv'], 'L3_ffn_w_gate': _L3_ffn_in['w_gate'], 'L3_ffn_w_noise': _L3_ffn_in['w_noise'], 'L3_ffn_W1': _L3_ffn_in['W1'], 'L3_ffn_b1': _L3_ffn_in['b1'], 'L3_ffn_W2': _L3_ffn_in['W2'], 'L3_ffn_b2': _L3_ffn_in['b2']}

def reference(x, ctx_768, mask_BxS2_bf1, L0_attn_mu_x, L0_attn_W_x1, L0_attn_W_x2, L0_attn_x_bias, L0_attn_W_r, L0_attn_W_k, L0_attn_W_v, L0_attn_W_g, L0_attn_A_w, L0_attn_B_w, L0_attn_b_w, L0_attn_bonus, L0_attn_gn_weight, L0_attn_gn_bias, L0_attn_W_o, L0_xattn_Wq, L0_xattn_bq, L0_xattn_Wk, L0_xattn_bk, L0_xattn_Wv, L0_xattn_bv, L0_xattn_Wo, L0_xattn_bo, L0_ffn_router_w, L0_ffn_w1, L0_ffn_b1, L0_ffn_w2, L0_ffn_b2, L1_attn_pre_norm_w, L1_attn_in_proj_w, L1_attn_short_w, L1_attn_short_b, L1_attn_log_poles, L1_attn_residues, L1_attn_D_skip, L1_attn_out_proj_w, L1_attn_post_norm_w, L1_attn_l1_w, L1_attn_l2_w, L1_attn_l3_w, L1_xattn_Wq, L1_xattn_Wk, L1_xattn_Wv, L1_xattn_Wo, L1_xattn_bo, L1_ffn_W1, L1_ffn_b1, L1_ffn_W2, L1_ffn_b2, L1_ffn_Wr, L1_ffn_br, L2_attn_qkv_w, L2_attn_qkv_b, L2_attn_kn_g, L2_attn_kn_b, L2_attn_vn_g, L2_attn_vn_b, L2_attn_temperature, L2_attn_attn_bias, L2_attn_p1_w, L2_attn_p1_b, L2_attn_p2_w, L2_attn_p2_b, L2_xattn_Wq, L2_xattn_Wk, L2_xattn_Wv, L2_xattn_Wo, L2_ffn_w_gate, L2_ffn_W1, L2_ffn_b1, L2_ffn_W2, L2_ffn_b2, L3_attn_Wq, L3_attn_bq, L3_attn_Wk, L3_attn_bk, L3_attn_Wv, L3_attn_bv, L3_attn_Wo, L3_attn_bo, L3_attn_head_mask, L3_xattn_Wq, L3_xattn_bq, L3_xattn_Wk, L3_xattn_bk, L3_xattn_Wv, L3_xattn_bv, L3_ffn_w_gate, L3_ffn_w_noise, L3_ffn_W1, L3_ffn_b1, L3_ffn_W2, L3_ffn_b2):
    import jax
    import jax.numpy as jnp

    def _L0_attn_ref(hidden_states, mu_x, W_x1, W_x2, x_bias, W_r, W_k, W_v, W_g, A_w, B_w, b_w, bonus, gn_weight, gn_bias, W_o):
        import jax, jax.numpy as jnp
        import numpy as np
        EPS = 1e-05
        B, T, D = hidden_states.shape
        Hh = bonus.shape[0]
        x = hidden_states
        shifted = jnp.pad(x, ((0, 0), (1, 0), (0, 0)))[:, :T]
        delta = shifted - x
        lr = W_x1.shape[0] // 5
        z = jnp.tanh((x + delta * mu_x) @ W_x1.T).reshape(B, T, 5, lr)
        mus = jnp.einsum('blnr,dnr->blnd', z, W_x2.reshape(D, 5, lr)) + x_bias
        r_mu, w_mu, k_mu, v_mu, g_mu = (mus[:, :, i] for i in range(5))
        r = (x + delta * r_mu) @ W_r.T
        w = jnp.tanh((x + delta * w_mu) @ A_w.T) @ B_w.T + b_w
        k = (x + delta * k_mu) @ W_k.T
        v = (x + delta * v_mu) @ W_v.T
        g = (x + delta * g_mu) @ W_g.T
        K = W_r.shape[0] // Hh
        V = W_v.shape[0] // Hh
        r = r.reshape(B, T, Hh, K)
        k = k.reshape(B, T, Hh, K)
        w = -jnp.exp(w.reshape(B, T, Hh, K))
        v = v.reshape(B, T, Hh, V)
        u = bonus

        def step(S, inp):
            q_t, k_t, v_t, w_t = inp
            kv = k_t[..., :, None] * v_t[..., None, :]
            o_t = jnp.einsum('bhk,bhkv->bhv', q_t, S + u[None, :, :, None] * kv)
            S = jnp.exp(w_t)[..., None] * S + kv
            return (S, o_t)
        S0 = jnp.zeros((B, Hh, K, V), dtype=x.dtype)
        xs = (jnp.swapaxes(r, 0, 1), jnp.swapaxes(k, 0, 1), jnp.swapaxes(v, 0, 1), jnp.swapaxes(w, 0, 1))
        _, o = jax.lax.scan(step, S0, xs)
        o = jnp.swapaxes(o, 0, 1)
        mean = o.mean(-1, keepdims=True)
        var = o.var(-1, keepdims=True)
        o = (o - mean) / jnp.sqrt(var + EPS)
        o = o.reshape(B, T, Hh * V) * gn_weight + gn_bias
        o = o * jax.nn.silu(g)
        return o @ W_o.T

    def _L0_xattn_ref(query, key_value, Wq, bq, Wk, bk, Wv, bv, Wo, bo):
        import jax, jax.numpy as jnp
        import numpy as np
        NUM_HEADS = 16
        CLAMP = 10000.0
        B, Nq, Cq = query.shape
        Nkv = key_value.shape[1]
        H = NUM_HEADS
        D = Cq // H
        scale = D ** (-0.5)
        q = (query @ Wq + bq).reshape(B, Nq, H, D).transpose(0, 2, 1, 3)
        k = (key_value @ Wk + bk).reshape(B, Nkv, H, D).transpose(0, 2, 1, 3)
        v = (key_value @ Wv + bv).reshape(B, Nkv, H, D).transpose(0, 2, 1, 3)
        attn = jnp.einsum('bhqd,bhkd->bhqk', q, k) * scale
        attn = jnp.clip(attn, -CLAMP, CLAMP)
        attn = jax.nn.softmax(attn, axis=-1)
        attn = jnp.where(jnp.any(jnp.isnan(attn)), jnp.asarray(1.0 / Nkv, attn.dtype), attn)
        x = jnp.einsum('bhqk,bhkd->bqhd', attn, v).reshape(B, Nq, Cq)
        return x @ Wo + bo

    def _L0_ffn_ref(x, router_w, w1, b1, w2, b2):
        import jax, jax.numpy as jnp
        import numpy as np
        NUM_EXPERTS = 8
        TOP_K = 2
        B, S, H = x.shape
        xt = x.reshape(-1, H)
        router_logits = jnp.matmul(xt, router_w)
        router_probs = jax.nn.softmax(router_logits, axis=-1)
        top_k_probs, top_k_indices = jax.lax.top_k(router_probs, TOP_K)
        top_k_probs = top_k_probs / jnp.sum(top_k_probs, axis=-1, keepdims=True)
        one_hot = jax.nn.one_hot(top_k_indices, NUM_EXPERTS, dtype=xt.dtype)
        combine = jnp.einsum('tk,tke->te', top_k_probs, one_hot)
        expert_out = jnp.matmul(jax.nn.gelu(jnp.matmul(xt, w1) + b1), w2) + b2
        out = expert_out * jnp.sum(combine, axis=-1, keepdims=True)
        return out.reshape(B, S, H)

    def _L1_attn_ref(u, pre_norm_w, in_proj_w, short_w, short_b, log_poles, residues, D_skip, out_proj_w, post_norm_w, l1_w, l2_w, l3_w):
        import jax, jax.numpy as jnp
        import numpy as np
        B, L, D, S, K, FF = (2, 1024, 256, 16, 3, 672)
        EPS = 1e-06

        def rmsnorm(x, w):
            var = jnp.mean(x * x, axis=-1, keepdims=True)
            return x * jax.lax.rsqrt(var + EPS) * w
        Lc = u.shape[1]
        z = rmsnorm(u, pre_norm_w) @ in_proj_w.T
        zc = z.transpose(0, 2, 1)
        z_pre = jax.lax.conv_general_dilated(zc, short_w, window_strides=(1,), padding=[(K - 1, 0)], dimension_numbers=('NCH', 'OIH', 'NCH'), feature_group_count=3 * D)
        z_pre = z_pre + short_b[None, :, None]
        x2, x1, v = jnp.split(z_pre, 3, axis=1)
        t = jnp.arange(Lc, dtype=jnp.float32)
        h = jnp.sum(residues[:, :, None] * jnp.exp(log_poles * t[None, None, :]), axis=1)
        xv = x1 * v
        n = 2 * Lc
        Xf = jnp.fft.rfft(xv, n=n)
        Hf = jnp.fft.rfft(h, n=n)
        yconv = jnp.fft.irfft(Xf * Hf[None], n=n)[..., :Lc]
        y = (yconv + xv * D_skip[None, :, None]) * x2
        y = y.transpose(0, 2, 1)
        y = y @ out_proj_w.T + u
        zm = rmsnorm(y, post_norm_w)
        mlp = jax.nn.gelu(zm @ l1_w.T) * (zm @ l2_w.T) @ l3_w.T
        return y + mlp

    def _L1_xattn_ref(x, context, Wq, Wk, Wv, Wo, bo):
        import jax, jax.numpy as jnp
        import numpy as np
        HEADS = 8
        DIM_HEAD = 64
        QUERY_DIM = 256
        CONTEXT_DIM = 192
        INNER = HEADS * DIM_HEAD
        B, Sq, _ = x.shape
        h, d = (HEADS, DIM_HEAD)
        scale = d ** (-0.5)
        q = (x @ Wq).reshape(B, Sq, h, d).transpose(0, 2, 1, 3)
        k = (context @ Wk).reshape(B, -1, h, d).transpose(0, 2, 1, 3)
        v = (context @ Wv).reshape(B, -1, h, d).transpose(0, 2, 1, 3)
        scores = jnp.einsum('bhid,bhjd->bhij', q, k) * scale
        attn = jax.nn.softmax(scores, axis=-1)
        out = jnp.einsum('bhij,bhjd->bhid', attn, v)
        out = out.transpose(0, 2, 1, 3).reshape(B, Sq, h * d)
        return out @ Wo + bo

    def _L1_ffn_ref(x, W1, b1, W2, b2, Wr, br):
        import jax, jax.numpy as jnp
        import numpy as np
        D = 256
        H = 512
        E = 8
        K = 2
        B, T = (4, 512)
        Bb, Tt, Dd = x.shape
        xf = x.reshape(-1, Dd)
        logits = xf @ Wr + br
        topk_val, topk_idx = jax.lax.top_k(logits, K)
        scores = jax.nn.softmax(topk_val, axis=-1)
        h = jnp.einsum('nd,edh->enh', xf, W1) + b1[:, None, :]
        a, g = jnp.split(h, 2, axis=-1)
        act = jax.nn.silu(a) * g
        out_e = jnp.einsum('enh,ehd->end', act, W2) + b2[:, None, :]
        out_ne = out_e.transpose(1, 0, 2)
        gathered = jnp.take_along_axis(out_ne, topk_idx[:, :, None], axis=1)
        out = jnp.sum(gathered * scores[:, :, None], axis=1)
        return out.reshape(Bb, Tt, Dd)

    def _L2_attn_ref(x, qkv_w, qkv_b, kn_g, kn_b, vn_g, vn_b, temperature, attn_bias, p1_w, p1_b, p2_w, p2_b):
        import jax, jax.numpy as jnp
        import numpy as np
        EPS = 1e-05

        def _layernorm(x, gamma, beta):
            m = jnp.mean(x, axis=-1, keepdims=True)
            v = jnp.mean(jnp.square(x - m), axis=-1, keepdims=True)
            return (x - m) * jax.lax.rsqrt(v + EPS) * gamma + beta
        B, Q, C = x.shape
        H = temperature.shape[0]
        hd = C // H
        qkv = (x @ qkv_w.T + qkv_b).reshape(B, Q, 3, H, hd)
        qkv = jnp.transpose(qkv, (2, 0, 3, 1, 4))
        q, k, v = (qkv[0], qkv[1], qkv[2])
        k = _layernorm(k, kn_g, kn_b)
        v = _layernorm(v, vn_g, vn_b)
        kv = jnp.einsum('bhqd,bhqe->bhde', k, v) / Q * temperature + attn_bias
        att = jnp.einsum('bhqd,bhde->bhqe', q, kv)
        att = jnp.transpose(att, (0, 2, 1, 3)).reshape(B, Q, C) + x
        h = jax.nn.gelu(att @ p1_w.T + p1_b, approximate=False)
        return h @ p2_w.T + p2_b + x

    def _L2_xattn_ref(x, context, context_mask, Wq, Wk, Wv, Wo):
        import jax, jax.numpy as jnp
        import numpy as np
        DIM = 256
        CTX_DIM = 192
        HEADS = 16
        B, N, _ = x.shape
        M = context.shape[1]
        hd = DIM // HEADS
        scale = hd ** (-0.5)
        q = (x @ Wq).reshape(B, N, HEADS, hd).transpose(0, 2, 1, 3)
        k = (context @ Wk).reshape(B, M, HEADS, hd).transpose(0, 2, 1, 3)
        v = (context @ Wv).reshape(B, M, HEADS, hd).transpose(0, 2, 1, 3)
        scores = jnp.einsum('bhid,bhjd->bhij', q, k) * scale
        max_neg = -jnp.finfo(scores.dtype).max
        scores = jnp.where(context_mask[:, None, None, :], scores, max_neg)
        attn = jax.nn.softmax(scores, axis=-1)
        out = jnp.einsum('bhij,bhjd->bhid', attn, v)
        out = out.transpose(0, 2, 1, 3).reshape(B, N, DIM)
        return out @ Wo

    def _L2_ffn_ref(x, w_gate, W1, b1, W2, b2):
        import jax, jax.numpy as jnp
        import numpy as np
        D_MODEL = 256
        N_EXPERTS = 8
        TOP_K = 2
        FFN_HIDDEN = 4 * D_MODEL
        B, S, D = x.shape
        flat_x = x.reshape(-1, D)
        gate = jax.nn.softmax(flat_x @ w_gate.T, axis=-1)
        topk_scores, topk_idx = jax.lax.top_k(gate, TOP_K)
        cw = (jax.nn.one_hot(topk_idx, N_EXPERTS, dtype=flat_x.dtype) * topk_scores[..., None]).sum(axis=1)
        h = jax.nn.gelu(jnp.einsum('td,edh->teh', flat_x, W1) + b1, approximate=False)
        y = jnp.einsum('teh,ehd->ted', h, W2) + b2
        out = jnp.einsum('ted,te->td', y, cw)
        return out.reshape(B, S, D)

    def _L3_attn_ref(x, Wq, bq, Wk, bk, Wv, bv, Wo, bo, head_mask):
        import jax, jax.numpy as jnp
        import numpy as np
        HIDDEN = 256
        HEADS = 16
        HEAD_DIM = HIDDEN // HEADS
        B, S = (4, 512)
        b, s, _ = x.shape
        q = (x @ Wq.T + bq).reshape(b, s, HEADS, HEAD_DIM)
        k = (x @ Wk.T + bk).reshape(b, s, HEADS, HEAD_DIM)
        v = (x @ Wv.T + bv).reshape(b, s, HEADS, HEAD_DIM)
        attn = jnp.einsum('bqhd,bkhd->bhqk', q, k) / np.sqrt(HEAD_DIM).astype(np.float32)
        attn = jax.nn.softmax(attn, axis=-1)
        attn = attn * head_mask[None, :, None, None]
        out = jnp.einsum('bhqk,bkhd->bqhd', attn, v).reshape(b, s, HIDDEN)
        return out @ Wo.T + bo

    def _L3_xattn_ref(query, key, value, Wq, bq, Wk, bk, Wv, bv):
        import jax, jax.numpy as jnp
        import numpy as np
        Q_DIM, K_DIM, V_DIM, OUT_DIM = (256, 192, 192, 256)
        scale = OUT_DIM ** (-0.5)
        q = jnp.einsum('bsd,od->bso', query, Wq) + bq
        k = jnp.einsum('bsd,od->bso', key, Wk) + bk
        v = jnp.einsum('bsd,od->bso', value, Wv) + bv
        scores = jnp.einsum('bqo,bko->bqk', q, k) * scale
        probs = jax.nn.softmax(scores, axis=-1)
        return jnp.einsum('bqk,bko->bqo', probs, v)

    def _L3_ffn_ref(x, w_gate, w_noise, W1, b1, W2, b2):
        import jax, jax.numpy as jnp
        import numpy as np
        B, S, D, O, H, E, K = (4, 256, 256, 256, 512, 16, 4)
        logits = jnp.zeros((x.shape[0], x.shape[1], E), dtype=x.dtype).at[..., 1].set(100.0)
        top_vals, top_idx = jax.lax.top_k(logits, K)
        gates_k = jax.nn.softmax(top_vals, axis=-1)
        gates = jnp.einsum('bske,bsk->bse', jax.nn.one_hot(top_idx, E, dtype=x.dtype), gates_k)
        h = jax.nn.relu(jnp.einsum('bsd,edh->ebsh', x, W1) + b1[:, None, None, :])
        y = jnp.einsum('ebsh,eho->ebso', h, W2) + b2[:, None, None, :]
        out = jnp.einsum('ebso,bse->bso', y, gates)
        return out
    x = x + _L0_attn_ref(_layernorm(x, axis=-1), L0_attn_mu_x, L0_attn_W_x1, L0_attn_W_x2, L0_attn_x_bias, L0_attn_W_r, L0_attn_W_k, L0_attn_W_v, L0_attn_W_g, L0_attn_A_w, L0_attn_B_w, L0_attn_b_w, L0_attn_bonus, L0_attn_gn_weight, L0_attn_gn_bias, L0_attn_W_o)
    x = x + _L0_xattn_ref(_layernorm(x, axis=-1), ctx_768, L0_xattn_Wq, L0_xattn_bq, L0_xattn_Wk, L0_xattn_bk, L0_xattn_Wv, L0_xattn_bv, L0_xattn_Wo, L0_xattn_bo)
    x = x + _L0_ffn_ref(_layernorm(x, axis=-1), L0_ffn_router_w, L0_ffn_w1, L0_ffn_b1, L0_ffn_w2, L0_ffn_b2)
    x = x + _L1_attn_ref(_layernorm(x, axis=-1), L1_attn_pre_norm_w, L1_attn_in_proj_w, L1_attn_short_w, L1_attn_short_b, L1_attn_log_poles, L1_attn_residues, L1_attn_D_skip, L1_attn_out_proj_w, L1_attn_post_norm_w, L1_attn_l1_w, L1_attn_l2_w, L1_attn_l3_w)
    x = x + _L1_xattn_ref(_layernorm(x, axis=-1), ctx_768, L1_xattn_Wq, L1_xattn_Wk, L1_xattn_Wv, L1_xattn_Wo, L1_xattn_bo)
    x = x + _L1_ffn_ref(_layernorm(x, axis=-1), L1_ffn_W1, L1_ffn_b1, L1_ffn_W2, L1_ffn_b2, L1_ffn_Wr, L1_ffn_br)
    x = x + _L2_attn_ref(_layernorm(x, axis=-1), L2_attn_qkv_w, L2_attn_qkv_b, L2_attn_kn_g, L2_attn_kn_b, L2_attn_vn_g, L2_attn_vn_b, L2_attn_temperature, L2_attn_attn_bias, L2_attn_p1_w, L2_attn_p1_b, L2_attn_p2_w, L2_attn_p2_b)
    x = x + _L2_xattn_ref(_layernorm(x, axis=-1), ctx_768, mask_BxS2_bf1, L2_xattn_Wq, L2_xattn_Wk, L2_xattn_Wv, L2_xattn_Wo)
    x = x + _L2_ffn_ref(_layernorm(x, axis=-1), L2_ffn_w_gate, L2_ffn_W1, L2_ffn_b1, L2_ffn_W2, L2_ffn_b2)
    x = x + _L3_attn_ref(_layernorm(x, axis=-1), L3_attn_Wq, L3_attn_bq, L3_attn_Wk, L3_attn_bk, L3_attn_Wv, L3_attn_bv, L3_attn_Wo, L3_attn_bo, L3_attn_head_mask)
    x = x + _L3_xattn_ref(_layernorm(x, axis=-1), ctx_768, ctx_768, L3_xattn_Wq, L3_xattn_bq, L3_xattn_Wk, L3_xattn_bk, L3_xattn_Wv, L3_xattn_bv)
    x = x + _L3_ffn_ref(_layernorm(x, axis=-1), L3_ffn_w_gate, L3_ffn_w_noise, L3_ffn_W1, L3_ffn_b1, L3_ffn_W2, L3_ffn_b2)
    return x

_drawn_inputs = setup_inputs


def setup_inputs(seed=0):
    import zlib

    import numpy as np

    out = dict(_drawn_inputs(seed))
    spreads = {'L0_attn_x_bias': (0.0, 0.414),
     'L0_attn_b_w': (0.0, 0.8),
     'L0_attn_gn_weight': (1.0, 0.6),
     'L0_attn_gn_bias': (0.0, 0.8),
     'L0_xattn_bq': (0.0, 0.325),
     'L0_xattn_bk': (0.0, 2.0),
     'L0_xattn_bv': (0.0, 0.1),
     'L0_xattn_bo': (0.0, 0.1),
     'L0_ffn_b1': (0.0, 0.1),
     'L0_ffn_b2': (0.0, 0.1),
     'L1_attn_pre_norm_w': (1.0, 0.2),
     'L1_attn_post_norm_w': (1.0, 0.2),
     'L1_ffn_b1': (0.0, 0.8),
     'L1_ffn_b2': (0.0, 1.07),
     'L1_ffn_br': (0.0, 0.519),
     'L2_attn_qkv_b': (0.0, 0.487),
     'L2_attn_kn_g': (1.0, 0.6),
     'L2_attn_kn_b': (0.0, 0.673),
     'L2_attn_vn_g': (1.0, 0.6),
     'L2_attn_vn_b': (0.0, 0.564),
     'L2_attn_temperature': (1.0, 0.6),
     'L2_attn_attn_bias': (0.0, 0.293),
     'L2_attn_p1_b': (0.0, 1.106),
     'L2_attn_p2_b': (0.0, 0.807),
     'L2_ffn_b1': (0.0, 1.924),
     'L2_ffn_b2': (0.0, 1.507),
     'L3_attn_bq': (0.0, 2.0),
     'L3_attn_bk': (0.0, 2.0),
     'L3_attn_bv': (0.0, 1.622),
     'L3_attn_bo': (0.0, 0.887),
     'L3_ffn_w_noise': (0.0, 0.1),
     'L3_ffn_b1': (0.0, 1.335),
     'L3_ffn_b2': (0.0, 0.868)}
    factors = {'L0_attn_mu_x': 8.0,
     'L0_attn_W_x1': 7.877,
     'L0_attn_W_x2': 8.0,
     'L0_attn_A_w': 8.0,
     'L0_attn_B_w': 8.0,
     'L0_attn_bonus': 8.0,
     'L0_ffn_router_w': 64.0,
     'L1_attn_D_skip': 8.0,
     'L1_xattn_bo': 8.0,
     'L1_ffn_W1': 7.12,
     'L1_ffn_W2': 7.184,
     'L3_attn_Wq': 8.0,
     'L3_attn_Wk': 8.0,
     'L3_xattn_Wq': 6.031,
     'L3_xattn_bq': 37.132,
     'L3_xattn_Wk': 6.107,
     'L3_xattn_bk': 64.0,
     'L3_xattn_bv': 14.823,
     'L2_xattn_Wq': 2.813,
     'L2_xattn_Wk': 2.809}
    for name, (base, spread) in spreads.items():
        noise = np.random.default_rng([zlib.crc32(name.encode()), seed]).standard_normal(out[name].shape)
        drawn = base * np.exp(spread * noise) if base else spread * noise
        out[name] = jnp.asarray(drawn.astype(out[name].dtype))
    for name, factor in factors.items():
        out[name] = (out[name] * factor).astype(out[name].dtype)
    return out
```

```python
from contextlib import ExitStack

import numpy as np
import concourse.bass as bass
from concourse import mybir

F32 = mybir.dt.float32
U8 = mybir.dt.uint8
ACT = mybir.ActivationFunctionType
ALU = mybir.AluOpType
AX = mybir.AxisListType

T, B, D = 112, 16, 256
N = T * B
S2, CD = 375, 192
GB = 4
G = B // GB
GT = GB * T
KP = 128
KW, KN = 125, 3
CR = CD // 2
LN_EPS = 1e-5
RMS_EPS = 1e-6
HEAD = 64
CLAMP = 10000.0
FMAX = float(np.finfo(np.float32).max)


class Signal:

    def __init__(self, sem):
        self.sem, self.base = sem, HEAD

    def at(self, n):
        return self.sem, self.base + n

    def advance(self, n):
        self.base += n


class Chain:

    def __init__(self, eng, signal):
        self.eng, self.counter, self.n, self.start = eng, signal, 0, 0

    def link(self, ins):
        ins.then_inc(self.counter.sem, 1)
        self.n += 1
        self.eng.wait_ge(*self.counter.at(self.start + self.n))

    def mark(self, ins):
        ins.then_inc(self.counter.sem, 1)
        self.n += 1

    def turn(self, i, per):
        self.per, self.done = per, self.start + self.n
        self.start = self.done + i * per
        self.n = 0

    def end(self, trips):
        assert self.n == self.per, f"links a turn: {self.n}, stated: {self.per}"
        self.start, self.n = self.done + trips * self.per, 0

    def close(self):
        self.counter.advance(self.start + self.n)


class Core:

    def __init__(self, nc, ctx):
        self.nc, self.signals, self.tiles = nc, {}, 0
        self.X = ctx.enter_context(nc.sbuf_tensor("X", [T, B * D], F32))
        self.XT = ctx.enter_context(nc.sbuf_tensor("XT", [KP, 2, N], F32))
        self.ident = ctx.enter_context(nc.sbuf_tensor("ident", [KP, KP], F32))
        self.ps = ctx.enter_context(nc.psum_tensor("ps", [KP, 8, 512], F32))
        for name in SIGNALS:
            self.signals[name] = Signal(ctx.enter_context(nc.semaphore(name)))

    def tile(self, ctx, name, shape, dtype=F32):
        self.tiles += 1
        return ctx.enter_context(self.nc.sbuf_tensor(f"{name}_{self.tiles}", shape, dtype))

    def __getitem__(self, name):
        return self.signals[name]

    def advance(self, **events):
        for name, n in events.items():
            self.signals[name].advance(n)

    def x(self, b):
        return self.X[:, bass.ds(b * D, D)]


SIGNALS = ["vec_step", "act_step", "pool_step",
           "pack_in", "const_in", "ctx_in0", "ctx_in1", "exp_in0", "exp_in1", "toep_in0", "toep_in1",
           "x_in", "x_out", "stats_done", "rstd_done", "norm_done", "norm_tr", "norm_ev",
           "up_mm", "up_act", "up_used", "down_mm", "down_added",
           "lin_mm", "lin_act", "lin_vec",
           "rt_mm", "rt_ev", "rt_tr", "rt_lg", "gate_v", "gate_a", "gs_copied", "gt_tr", "gt_ev", "gb_mm", "gb_added",
           "kt_mm", "kt_ev", "v_mm", "v_ev", "qm_done", "ctx_used", "xs_copied",
           "sc_mm", "sc_read", "max_done", "exp_done", "prob_done", "pt_mm", "pt_ev_a", "pt_ev_v",
           "pv_mm", "ot_ev", "wo_mm", "res_done", "mask_done",
           "p_a", "p_b", "p_c", "p_d", "p_e", "p_f", "p_g", "p_h", "p_i", "p_j", "p_k", "p_l"]


def pack_tile(k, ctx, name, layout):
    total = layout["_total"]
    tile = k.tile(ctx, name, [KP, total], F32)

    def view(field, parts=None):
        off, p, cols = layout[field]
        return tile[0:(parts or p), off:off + cols]

    return tile, view


def chunks(ap, n):
    return ap.rearrange("p (k n) -> p k n", k=n)


def layer_norm(k, pack=None, keep=None, rms_w=None, source=None, plain=True):
    nc = k.nc
    src = source if source is not None else k.X
    with ExitStack() as ctx:
        sb = lambda n, s: k.tile(ctx, n, s, F32)
        st = sb("ln_st", [T, B * 6])
        mv = sb("ln_mv", [T, B * 2])
        rstd = sb("ln_rstd", [T, B])
        both = sb("ln_both", [T, B])
        tmp = sb("ln_tmp", [T, B])
        half = sb("ln_half", [T, B])
        xn = sb("ln_xn", [T, 2, D])
        mv3 = mv[:, :].rearrange("p (b s) -> p b s", s=2)
        two_pows = plain and rms_w is not None
        stats, rdone, ndone, ntr, nev = (k[s] for s in ("stats_done", "rstd_done", "norm_done", "norm_tr",
                                                        "norm_ev"))
        with nc.Block(no_gpsimd_drain=True) as block:
            @block.sync
            def _(sp):
                if pack is not None:
                    tile, dram, total = pack
                    h = total // 2
                    sp.dma_start(tile[:, 0:h], dram[:, 0:h]).then_inc(k["pack_in"].sem, 16)
                    sp.dma_start(tile[:, h:total], dram[:, h:total]).then_inc(k["pack_in"].sem, 16)
                    sp.wait_ge(*k["pack_in"].at(32))

            @block.vector
            def _(v):
                ch = Chain(v, k["vec_step"])
                with v.Fori(0, B // 4) as i:
                    ch.turn(0, 0)
                    for j in range(4):
                        last = v.bn_stats(st[:, bass.ds((4 * i + j) * 6, 6)], src[:, bass.ds((4 * i + j) * D, D)])
                    ch.end(4)
                ch.link(v.memset(half[:, :], -0.5))
                for b in range(B):
                    last = v.bn_aggr(mv[:, 2 * b:2 * b + 2], st[:, 6 * b:6 * b + 6])
                ch.link(last)
                if plain:
                    v.tensor_scalar(tmp[:, :], mv3[:, :, 1], LN_EPS, None, ALU.add).then_inc(stats.sem, 1)
                    if two_pows:
                        v.wait_ge(*rdone.at(1))
                        ch.link(v.tensor_tensor(both[:, :], rstd[:, :], rstd[:, :], ALU.mult))
                        ch.link(v.tensor_tensor(both[:, :], both[:, :], mv3[:, :, 1], ALU.mult))
                        v.tensor_scalar(tmp[:, :], both[:, :], RMS_EPS, None, ALU.add).then_inc(stats.sem, 1)
                        v.wait_ge(*rdone.at(2))
                        ch.link(v.tensor_tensor(both[:, :], both[:, :], rstd[:, :], ALU.mult))
                    else:
                        v.wait_ge(*rdone.at(1))
                else:
                    ch.link(v.tensor_tensor(both[:, :], mv3[:, :, 0], mv3[:, :, 0], ALU.mult))
                    ch.link(v.tensor_tensor(both[:, :], both[:, :], mv3[:, :, 1], ALU.add))
                    v.tensor_scalar(tmp[:, :], both[:, :], RMS_EPS, None, ALU.add).then_inc(stats.sem, 1)
                    v.wait_ge(*rdone.at(1))
                scale = both if two_pows else rstd
                with v.Fori(0, B // 2) as i:
                    for u in range(2):
                        v.wait_ge(*ntr.at(2 * i + u - 1))
                        xin = src[:, bass.ds((2 * i + u) * D, D)]
                        if plain:
                            v.tensor_scalar(xn[:, u, :], xin, mv[:, bass.ds(2 * (2 * i + u), 1)],
                                            scale[:, bass.ds(2 * i + u, 1)], ALU.subtract,
                                            ALU.mult).then_inc(ndone.sem, 1)
                            if keep is not None:
                                v.tensor_scalar(keep[:, bass.ds((2 * i + u) * D, D)], xin,
                                                mv[:, bass.ds(2 * (2 * i + u), 1)],
                                                rstd[:, bass.ds(2 * i + u, 1)], ALU.subtract, ALU.mult)
                        else:
                            v.tensor_scalar(xn[:, u, :], xin, scale[:, bass.ds(2 * i + u, 1)], None,
                                            ALU.mult).then_inc(ndone.sem, 1)
                ch.close()

            @block.gpsimd
            def _(g):
                g.wait_ge(*stats.at(1))
                g.tensor_tensor(rstd[:, :], tmp[:, :], half[:, :], ALU.pow).then_inc(rdone.sem, 1)
                if two_pows:
                    g.wait_ge(*stats.at(2))
                    g.tensor_tensor(both[:, :], tmp[:, :], half[:, :], ALU.pow).then_inc(rdone.sem, 1)

            @block.tensor
            def _(pe):
                with pe.Fori(0, B // 2) as i:
                    for u in range(2):
                        pe.wait_ge(*ndone.at(2 * i + u + 1))
                        pe.wait_ge(*nev.at(2 * i + u - 1))
                        for c in range(2):
                            last = pe.transpose(k.ps[0:KP, u, c * T:(c + 1) * T], xn[:, u, c * KP:(c + 1) * KP],
                                                k.ident[0:T, 0:T])
                        last.then_inc(ntr.sem, 1)

            @block.scalar
            def _(act):
                if rms_w is not None and pack is not None:
                    act.wait_ge(*k["pack_in"].at(32))
                with act.Fori(0, B // 2) as i:
                    for u in range(2):
                        act.wait_ge(*ntr.at(2 * i + u + 1))
                        if rms_w is None:
                            last = act.activation(k.XT[:, :, bass.ds((2 * i + u) * T, T)],
                                                  chunks(k.ps[0:KP, u, 0:2 * T], 2), ACT.Copy)
                        else:
                            for c in range(2):
                                last = act.activation(k.XT[:, c, bass.ds((2 * i + u) * T, T)],
                                                      k.ps[0:KP, u, c * T:(c + 1) * T], ACT.Copy,
                                                      scale=rms_w[:, c:c + 1])
                        last.then_inc(nev.sem, 1)
        k.advance(pack_in=32 if pack is not None else 0, stats_done=2 if two_pows else 1,
                  rstd_done=2 if two_pows else 1, norm_done=B, norm_tr=B, norm_ev=B)


def feed_forward(k, name, dram, layout, experts, rows, hidden, gated, act_fn, gates=None, src=None):
    nc = k.nc
    src = k.XT if src is None else src
    ring = min(hidden, 4)
    up, used, down, added = k["up_mm"], k["up_used"], k["down_mm"], k["down_added"]
    acted = k["up_act"]
    w_in = [k["exp_in0"], k["exp_in1"]]
    pairs = max(experts // 2, 1)
    per_pair = min(experts, 2)
    with ExitStack() as ctx:
        total = layout["_total"]
        slots = [k.tile(ctx, f"{name}_w{e}", [KP, total], F32) for e in range(per_pair)]
        hT = k.tile(ctx, f"{name}_h", [rows, 2, hidden, GT], F32)
        if gated:
            first = k.tile(ctx, f"{name}_a", [rows, 2, GT], F32)

        def part(slot, field):
            off, p, cols = layout[field]
            return slots[slot][0:p, off:off + cols]

        w1 = [chunks(part(s, "w1"), 2) for s in range(per_pair)]
        w2 = [chunks(part(s, "w2"), hidden) for s in range(per_pair)]
        b1 = [part(s, "b1") for s in range(per_pair)] if "b1" in layout else None

        def steps(eng):
            if pairs == 1:
                for ep in range(per_pair):
                    with eng.Fori(0, G // 2) as g0:
                        for gu in range(2):
                            yield 2 * g0 + gu + ep * G, ep, gu, ep, 2 * g0 + gu
            else:
                with eng.Fori(0, pairs) as ei:
                    for ep in range(per_pair):
                        with eng.Fori(0, G // 2) as g0:
                            for gu in range(2):
                                yield (ei * 2 + ep) * G + 2 * g0 + gu, ep, gu, ei * 2 + ep, 2 * g0 + gu

        with nc.Block(no_gpsimd_drain=True) as block:
            @block.sync
            def _(sp):
                if pairs == 1:
                    for ep in range(per_pair):
                        sp.dma_start(slots[ep][:, :], dram[ep, :, :]).then_inc(w_in[ep].sem, 16)
                else:
                    with sp.Fori(0, pairs) as ei:
                        for ep in range(2):
                            sp.wait_ge(*down.at((ei * 2 + ep - 1) * G))
                            sp.dma_start(slots[ep][:, :], dram[bass.ds(ei * 2 + ep, 1), :, :].rearrange(
                                "e p n -> (e p) n")).then_inc(w_in[ep].sem, 16)

            @block.tensor
            def _(pe):
                for t, s, h, e, g in steps(pe):
                    turn = e // 2 if isinstance(e, int) else None
                    pe.wait_ge(*w_in[s].at(16 * (e // 2 + 1) if turn is not None else 8 * (e - s) + 16))
                    for m in range(hidden):
                        if gated:
                            pe.wait_ge(*used.at(t * hidden + m - 1))
                        else:
                            pe.wait_ge(*acted.at(t * hidden + m - ring + 1))
                        for half in range(2 if gated else 1):
                            bank = 2 * (m % 2) + half if gated else m % ring
                            col = (half * hidden + m) * rows
                            for c in range(2):
                                last = pe.matmul(k.ps[0:rows, bank, 0:GT], w1[s][:, c, col:col + rows],
                                                 src[:, c, bass.ds(g * GT, GT)], start=(c == 0), stop=(c == 1))
                        last.then_inc(up.sem, 1)
                    for m in range(hidden):
                        if gated:
                            pe.wait_ge(*used.at(t * hidden + m + 1))
                        else:
                            pe.wait_ge(*acted.at(t * hidden + m + 1))
                        for j in range(GB):
                            if m == 0:
                                pe.wait_ge(*added.at((t - 1) * GB + j + 1))
                            last = pe.matmul(k.ps[0:T, 4 + j, 0:D], hT[:, h, m, j * T:(j + 1) * T], w2[s][:, m, :],
                                             start=(m == 0), stop=(m == hidden - 1))
                    last.then_inc(down.sem, 1)

            @block.scalar
            def _(act):
                for t, s, h, e, g in steps(act):
                    if gated:
                        for m in range(hidden):
                            act.wait_ge(*up.at(t * hidden + m + 1))
                            act.wait_ge(*used.at(t * hidden + m - 1))
                            act.activation(first[:, m % 2, :], k.ps[0:rows, 2 * (m % 2), 0:GT], act_fn,
                                           bias=b1[s][:, m:m + 1] if b1 else 0.0).then_inc(acted.sem, 1)
                    else:
                        act.wait_ge(*down.at(t - 1))
                        for m in range(hidden):
                            act.wait_ge(*up.at(t * hidden + m + 1))
                            act.activation(hT[:, h, m, :], k.ps[0:rows, m % ring, 0:GT], act_fn,
                                           bias=b1[s][:, m:m + 1] if b1 else 0.0).then_inc(acted.sem, 1)

            @block.vector
            def _(v):
                for t, s, h, e, g in steps(v):
                    if gated:
                        v.wait_ge(*down.at(t - 1))
                        for m in range(hidden):
                            v.wait_ge(*acted.at(t * hidden + m + 1))
                            second = k.ps[0:rows, 2 * (m % 2) + 1, 0:GT]
                            if b1:
                                v.scalar_tensor_tensor(hT[:, h, m, :], second, b1[s][:, hidden + m:hidden + m + 1],
                                                       first[:, m % 2, :], ALU.add, ALU.mult).then_inc(used.sem, 1)
                            else:
                                v.tensor_tensor(hT[:, h, m, :], second, first[:, m % 2, :],
                                                ALU.mult).then_inc(used.sem, 1)
                    v.wait_ge(*down.at(t + 1))
                    for j in range(GB):
                        b = g * GB + j
                        if gates is None:
                            v.tensor_tensor(k.x(b), k.ps[0:T, 4 + j, 0:D], k.x(b), ALU.add).then_inc(added.sem, 1)
                        else:
                            v.scalar_tensor_tensor(k.x(b), k.ps[0:T, 4 + j, 0:D],
                                                   gates[:, bass.ds(e * B + b, 1)], k.x(b), ALU.mult,
                                                   ALU.add).then_inc(added.sem, 1)
        n = experts * G
        k.advance(up_mm=n * hidden, up_act=n * hidden, up_used=n * hidden if gated else 0, down_mm=n,
                  down_added=n * GB, exp_in0=16 * ((experts + 1) // 2), exp_in1=16 * (experts // 2))


def router(k, E, w, bias, gates, mode, b2):
    nc = k.nc
    with ExitStack() as ctx:
        sb = lambda n, s: k.tile(ctx, n, s, F32)
        lt = sb("rt_lt", [E, 2, GT])
        lg = sb("rt_lg_t", [T, B, E])
        ahead = sb("rt_ahead", [T, B, E])
        cmp = sb("rt_cmp", [T, B, E])
        ex = sb("rt_ex", [T, B, E])
        one = sb("rt_one", [T, B])
        inv = sb("rt_inv", [T, B])
        mm, ev, tr, lgd = k["rt_mm"], k["rt_ev"], k["rt_tr"], k["rt_lg"]
        gv, ga = k["gate_v"], k["gate_a"]
        n_g = 1 if mode == "topk_sum" else E
        g3 = gates[:, :].rearrange("p (e b) -> p b e", b=B)
        gs = sb("rt_gs", [T, 2, n_g])
        gT = sb("rt_gT", [n_g, 2, T])
        with nc.Block(no_gpsimd_drain=True) as block:
            @block.tensor
            def _(pe):
                for g in range(G):
                    u = g % 2
                    pe.wait_ge(*ev.at(g - 1))
                    for c in range(2):
                        last = pe.matmul(k.ps[0:E, u, 0:GT], w[:, c, :], k.XT[:, c, g * GT:(g + 1) * GT],
                                         start=(c == 0), stop=(c == 1))
                    last.then_inc(mm.sem, 1)
                    pe.wait_ge(*ev.at(g + 1))
                    pe.wait_ge(*lgd.at(g - 1))
                    for j in range(GB):
                        last = pe.transpose(k.ps[0:T, 2 + u, j * E:(j + 1) * E], lt[:, u, j * T:(j + 1) * T],
                                            k.ident[0:E, 0:E])
                    last.then_inc(tr.sem, 1)
                with pe.Fori(0, B // 2) as i:
                    for u in range(2):
                        pe.wait_ge(*k["gs_copied"].at(2 * i + u + 1))
                        pe.wait_ge(*k["gt_ev"].at(2 * i + u - 1))
                        pe.transpose(k.ps[0:n_g, 4 + u, 0:T], gs[:, u, :], k.ident[0:T, 0:T]).then_inc(
                            k["gt_tr"].sem, 1)
                        pe.wait_ge(*k["gt_ev"].at(2 * i + u + 1))
                        pe.wait_ge(*k["gb_added"].at(2 * i + u - 1))
                        pe.matmul(k.ps[0:T, 6 + u, 0:D], gT[:, u, :], b2, start=True, stop=True).then_inc(
                            k["gb_mm"].sem, 1)

            @block.scalar
            def _(act):
                with act.Fori(0, G // 2) as i:
                    for u in range(2):
                        act.wait_ge(*mm.at(2 * i + u + 1))
                        act.wait_ge(*tr.at(2 * i + u - 1))
                        act.activation(lt[:, u, :], k.ps[0:E, u, 0:GT], ACT.Identity,
                                       bias=bias if bias is not None else 0.0).then_inc(ev.sem, 1)
                act.wait_ge(*gv.at(1))
                act.activation(ex[:, :, :], ex[:, :, :], ACT.Exp).then_inc(ga.sem, 1)
                with act.Fori(0, B // 2) as i:
                    for u in range(2):
                        act.wait_ge(*k["gt_tr"].at(2 * i + u + 1))
                        act.wait_ge(*k["gb_mm"].at(2 * i + u - 1))
                        act.activation(gT[:, u, :], k.ps[0:n_g, 4 + u, 0:T], ACT.Copy).then_inc(k["gt_ev"].sem, 1)

            @block.vector
            def _(v):
                ch = Chain(v, k["vec_step"])
                with v.Fori(0, G // 2) as i:
                    for u in range(2):
                        v.wait_ge(*tr.at(2 * i + u + 1))
                        v.tensor_copy(lg[:, bass.ds((2 * i + u) * GB, GB), :],
                                      chunks(k.ps[0:T, 2 + u, 0:GB * E], GB)).then_inc(lgd.sem, 1)
                v.wait_ge(*lgd.at(G))
                ch.link(v.memset(ahead[:, :, :], 0.0))
                for e in range(E):
                    other = lg[:, :, e:e + 1]
                    if e + 1 < E:
                        v.tensor_tensor(cmp[:, :, e + 1:E], other.broadcast_to([T, B, E - e - 1]),
                                        lg[:, :, e + 1:E], ALU.is_ge)
                    ch.link(v.tensor_tensor(cmp[:, :, 0:e + 1], other.broadcast_to([T, B, e + 1]),
                                            lg[:, :, 0:e + 1], ALU.is_gt))
                    ch.link(v.tensor_tensor(ahead[:, :, :], ahead[:, :, :], cmp[:, :, :], ALU.add))
                ch.link(v.tensor_scalar(ahead[:, :, :], ahead[:, :, :], 2.0, None, ALU.is_lt))
                ch.link(v.tensor_reduce(one[:, :], lg[:, :, :], AX.X, ALU.max))
                v.tensor_tensor(ex[:, :, :], lg[:, :, :], one[:, :].unsqueeze(2).broadcast_to([T, B, E]),
                                ALU.subtract).then_inc(gv.sem, 1)
                v.wait_ge(*ga.at(1))
                if mode in ("topk_sum", "topk_softmax"):
                    ch.link(v.tensor_reduce(one[:, :], ex[:, :, :], AX.X, ALU.add))
                    ch.link(v.reciprocal(inv[:, :], one[:, :]))
                    ch.link(v.tensor_tensor(ex[:, :, :], ex[:, :, :],
                                            inv[:, :].unsqueeze(2).broadcast_to([T, B, E]), ALU.mult))
                if mode == "topk_softmax":
                    ch.link(v.tensor_tensor(g3, ex[:, :, :], ahead[:, :, :], ALU.mult))
                else:
                    ch.link(v.tensor_tensor(ex[:, :, :], ex[:, :, :], ahead[:, :, :], ALU.mult))
                    ch.link(v.tensor_reduce(one[:, :], ex[:, :, :], AX.X, ALU.add))
                    ch.link(v.reciprocal(inv[:, :], one[:, :]))
                    if mode == "softmax_topk":
                        ch.link(v.tensor_tensor(g3, ex[:, :, :], inv[:, :].unsqueeze(2).broadcast_to([T, B, E]),
                                                ALU.mult))
                    else:
                        ch.link(v.tensor_tensor(ex[:, :, :], ex[:, :, :],
                                                inv[:, :].unsqueeze(2).broadcast_to([T, B, E]), ALU.mult))
                        ch.link(v.tensor_reduce(gates[:, :], ex[:, :, :], AX.X, ALU.add))
                with v.Fori(0, B // 2) as i:
                    for u in range(2):
                        v.wait_ge(*k["gt_tr"].at(2 * i + u - 1))
                        v.tensor_copy(gs[:, u, :], g3[:, bass.ds(2 * i + u, 1), :]).then_inc(k["gs_copied"].sem, 1)
                        v.wait_ge(*k["gb_mm"].at(2 * i + u + 1))
                        v.tensor_tensor(k.x(2 * i + u), k.ps[0:T, 6 + u, 0:D], k.x(2 * i + u), ALU.add).then_inc(
                            k["gb_added"].sem, 1)
                ch.close()
        k.advance(rt_mm=G, rt_ev=G, rt_tr=G, rt_lg=G, gate_v=1, gate_a=1, gs_copied=B, gt_tr=B, gt_ev=B, gb_mm=B,
                  gb_added=B)




def sub_ffn(k, ctx, name, packs, spec):
    lay, dram = packs[name]
    tile, p = pack_tile(k, ctx, name + "_pack", lay)
    gates = k.tile(ctx, name + "_gates", [T, spec["experts"] * B], F32)
    layer_norm(k, pack=(tile, dram, lay["_total"]))
    if spec["mode"] == "fixed":
        fixed_gates(k, gates, p("b2"))
    else:
        E = lay["router"][2] // 2
        router(k, E, chunks(p("router"), 2), p("router_b") if "router_b" in lay else None, gates, spec["mode"],
               p("b2"))
    elay, edram = packs[name + "_experts"]
    feed_forward(k, name, edram, elay, spec["experts"], KP, spec["hidden"], spec["gated"], spec["act"], gates)


def fixed_gates(k, gates, b2):
    nc = k.nc
    logits = [0.0, 100.0, 0.0, 0.0]
    E = len(logits)
    with ExitStack() as ctx:
        sb = lambda n, s: k.tile(ctx, n, s, F32)
        ex = sb("fg_ex", [T, E])
        sm = sb("fg_sum", [T, 1])
        gT = sb("fg_gT", [E, T])
        br = sb("fg_b", [T, D])
        with nc.Block(no_gpsimd_drain=True) as block:
            @block.vector
            def _(v):
                ch = Chain(v, k["vec_step"])
                for e, x in enumerate(logits):
                    last = v.memset(ex[:, e:e + 1], x - max(logits))
                last.then_inc(k["gate_v"].sem, 1)
                v.wait_ge(*k["gate_a"].at(1))
                ch.link(v.tensor_reduce(sm[:, :], ex[:, :], AX.X, ALU.add))
                ch.link(v.reciprocal(sm[:, :], sm[:, :]))
                ch.link(v.tensor_scalar(ex[:, :], ex[:, :], sm[:, :], None, ALU.mult))
                for e in range(E):
                    last = v.tensor_copy(gates[:, e * B:(e + 1) * B], ex[:, e:e + 1].broadcast_to([T, B]))
                last.then_inc(k["gate_v"].sem, 1)
                v.wait_ge(*k["gb_mm"].at(1))
                ch.link(v.tensor_copy(br[:, :], k.ps[0:T, 6, 0:D]))
                v.tensor_tensor(k.X[:, :].rearrange("p (b d) -> p b d", b=B),
                                k.X[:, :].rearrange("p (b d) -> p b d", b=B),
                                br[:, :].unsqueeze(1).broadcast_to([T, B, D]), ALU.add)
                ch.close()

            @block.scalar
            def _(act):
                act.wait_ge(*k["gate_v"].at(1))
                act.activation(ex[:, :], ex[:, :], ACT.Exp).then_inc(k["gate_a"].sem, 1)
                act.wait_ge(*k["gt_tr"].at(1))
                act.activation(gT[:, :], k.ps[0:E, 4, 0:T], ACT.Copy).then_inc(k["gt_ev"].sem, 1)

            @block.tensor
            def _(pe):
                pe.wait_ge(*k["gate_v"].at(2))
                pe.transpose(k.ps[0:E, 4, 0:T], ex[:, :], k.ident[0:T, 0:T]).then_inc(k["gt_tr"].sem, 1)
                pe.wait_ge(*k["gt_ev"].at(1))
                pe.matmul(k.ps[0:T, 6, 0:D], gT[:, :], b2, start=True, stop=True).then_inc(k["gb_mm"].sem, 1)
        k.advance(gate_v=2, gate_a=1, gt_tr=1, gt_ev=1, gb_mm=1)


FFN = {
    "L0_ffn": dict(mode="topk_sum", experts=1, hidden=8, gated=False, act=ACT.Gelu_apprx_tanh),
    "L1_ffn": dict(mode="softmax_topk", experts=8, hidden=4, gated=True, act=ACT.Silu),
    "L2_ffn": dict(mode="topk_softmax", experts=8, hidden=8, gated=False, act=ACT.Gelu),
    "L3_ffn": dict(mode="fixed", experts=4, hidden=4, gated=False, act=ACT.Relu),
}



def attention(k, name, pack, H, dh, self_attn=False, mask=False, clamp=False, head_mask=False):
    nc = k.nc
    HD = H * dh
    C = HD // KP
    HC = KP // dh
    OW = max(dh, 32)
    OH = KP // OW
    OC = H // OH
    kn, kw = (1, T) if self_attn else (KN, KW)
    keys = kn * kw
    kr = KP if self_attn else CR
    scale = float(dh) ** -0.5
    UB = H // 2
    U = 2 * UB
    TURNS = B // 2
    first_pass = mask or clamp
    wq, wk, wv, wo = (pack[n] for n in ("wq", "wk", "wv", "wo"))
    with ExitStack() as ctx:
        sb = lambda n, s, d=F32: k.tile(ctx, name + "_" + n, s, d)
        QT = sb("qT", [KP, C, N])
        src = sb("src", [KP, 2, 2, keys])
        KT = sb("kT", [KP, 2, C, keys])
        V = sb("v", [kw, 2, kn, H, OW])
        qm = sb("qm", [KP, 2, H, T])
        sa = sb("sa", [T, 2, 2, keys]) if first_pass else None
        P = sb("p", [T, 4, 2, keys])
        PT = sb("pT", [kw, 2, kn, 2, T])
        oT = sb("oT", [KP, 2, OC, T])
        mx = sb("mx", [T, 4, 2])
        ng = sb("ng", [T, 4, 2])
        rs = sb("rs", [T, 4, 2])
        ri = sb("ri", [T, 4, 2])
        mu8 = sb("mu8", [T, B * S2], U8) if mask else None
        mb = sb("mb", [T, 2, S2]) if mask else None
        s = k.signals
        ctx_in = [s["ctx_in0"], s["ctx_in1"]]
        sc_read = s["sc_read"] if first_pass else s["exp_done"]

        with nc.Block(no_gpsimd_drain=True) as block:
            @block.sync
            def _(sp):
                if mask:
                    sp.dma_start(mu8[:, :], k.aps["in_mask"].rearrange("(a b) n -> a (b n)", a=1)
                                 .broadcast_to([T, B * S2])).then_inc(s["x_in"].sem, 16)
                    sp.wait_ge(*s["x_in"].at(16))

            @block.tensor
            def _(pe):
                with pe.Fori(0, G) as g:
                    for c in range(C):
                        pe.wait_ge(*s["lin_act"].at(g * C + c - C + 1))
                        for kc in range(2):
                            last = pe.matmul(k.ps[:, c, 0:GT], wq[:, kc, c * KP:(c + 1) * KP],
                                             k.XT[:, kc, bass.ds(g * GT, GT)], start=(kc == 0), stop=(kc == 1))
                        last.then_inc(s["lin_mm"].sem, 1)

            @block.scalar
            def _(act):
                with act.Fori(0, G) as g:
                    for c in range(C):
                        act.wait_ge(*s["lin_mm"].at(g * C + c + 1))
                        act.activation(QT[:, c, bass.ds(g * GT, GT)], k.ps[:, c, 0:GT], ACT.Identity,
                                       bias=pack["bq"][:, c:c + 1] if "bq" in pack else 0.0).then_inc(
                                           s["lin_act"].sem, 1)

            @block.gpsimd
            def _(g):
                if OW > dh:
                    g.memset(V[:, :, :, :, dh:OW], 0.0)
                g.drain()

            @block.vector
            def _(v):
                if not self_attn:
                    v.memset(src[CR:CR + 1, :, :, :], 1.0)
        k.advance(lin_mm=G * C, lin_act=G * C, x_in=16 if mask else 0)

        with nc.Block(no_gpsimd_drain=True) as block:
            @block.sync
            def _(sp):
                if not self_attn:
                    with sp.Fori(0, TURNS) as i:
                        for u in range(2):
                            sp.wait_ge(*s["v_mm"].at((i * 2 + u - 1) * kn))
                            sp.dma_start(src[0:CR, u, :, :], k.aps["in_ctx"][bass.ds(i * 2 + u, 1), :, :, :]
                                         .rearrange("b p c n -> (b p) c n")).then_inc(ctx_in[u].sem, 16)

            @block.tensor
            def _(pe):
                with pe.Fori(0, TURNS) as i:
                    for u in range(2):
                        b = i * 2 + u
                        if self_attn:
                            pe.wait_ge(*s["xs_copied"].at(b + 1))
                        else:
                            pe.wait_ge(*ctx_in[u].at((i + 1) * 16))
                        for c in range(C):
                            pe.wait_ge(*s["kt_ev"].at(b * C + c))
                            if c == 0:
                                pe.wait_ge(*s["res_done"].at(b if u == 0 else b - 1))
                            for kc in range(2):
                                last = pe.matmul(k.ps[:, 6, 0:keys], wk[0:kr, kc, c * KP:(c + 1) * KP],
                                                 src[0:kr, u, kc, :], start=(kc == 0), stop=(kc == 1))
                            last.then_inc(s["kt_mm"].sem, 1)
                        for j in range(kn):
                            pe.wait_ge(*s["v_ev"].at(b * kn + j))
                            if j == 0:
                                pe.wait_ge(*s["ot_ev"].at(b if u == 0 else b - 1))
                            for kc in range(2):
                                rows = kr if kc == 0 or self_attn else kr + 1
                                last = pe.matmul(k.ps[0:kw, 7, 0:HD], src[0:rows, u, kc, j * kw:(j + 1) * kw],
                                                 wv[0:rows, kc, :], start=(kc == 0), stop=(kc == 1))
                            last.then_inc(s["v_mm"].sem, 1)

                    for n in range(U + 4):
                        if n < U:
                            u, p = n // UB, n % UB
                            if p == 0:
                                pe.wait_ge(*s["kt_ev"].at((i * 2 + u + 1) * C))
                                pe.wait_ge(*s["qm_done"].at(i * 2 + u + 1))
                            pe.wait_ge(*sc_read.at(i * U + n - 1))
                            for j in range(2):
                                h = 2 * p + j
                                last = pe.matmul(k.ps[0:T, 2 * (n % 2) + j, 0:keys], qm[:, u, h, :],
                                                 KT[:, u, h // HC, :], start=True, stop=True)
                            last.then_inc(s["sc_mm"].sem, 1)
                        m = n - 2
                        if 0 <= m < U:
                            pe.wait_ge(*s["prob_done"].at(i * U + m + 1))
                            pe.wait_ge(*s["pt_ev_a"].at(i * U + m))
                            if kn > 1:
                                pe.wait_ge(*s["pt_ev_v"].at(i * U + m))
                            for kc in range(kn):
                                for j in range(2):
                                    at = (kc % 2) * 2 * T + j * T
                                    last = pe.transpose(k.ps[0:kw, 4 + kc // 2, at:at + T],
                                                        P[:, m % 4, j, kc * kw:(kc + 1) * kw], k.ident[0:T, 0:T])
                            last.then_inc(s["pt_mm"].sem, 1)
                        m = n - 3
                        if 0 <= m < U:
                            u, p = m // UB, m % UB
                            pe.wait_ge(*s["pt_ev_a"].at(i * U + m + 1))
                            if kn > 1:
                                pe.wait_ge(*s["pt_ev_v"].at(i * U + m + 1))
                            if p == 0:
                                pe.wait_ge(*s["v_ev"].at((i * 2 + u + 1) * kn))
                                if u == 1:
                                    pe.wait_ge(*s["ot_ev"].at(i * 2 + 1))
                            for kc in range(kn):
                                for j in range(2):
                                    h = 2 * p + j
                                    row = (h % OH) * OW
                                    last = pe.matmul(k.ps[row:row + OW, 7, (h // OH) * T:(h // OH + 1) * T],
                                                     V[:, u, kc, h, :], PT[:, m % 2, kc, j, :],
                                                     start=(kc == 0), stop=(kc == kn - 1))
                            last.then_inc(s["pv_mm"].sem, 1)
                        if n in (UB + 3, 2 * UB + 3):
                            u = 0 if n == UB + 3 else 1
                            pe.wait_ge(*s["ot_ev"].at(i * 2 + u + 1))
                            pe.wait_ge(*s["res_done"].at(i * 2 + u))
                            for c in range(OC):
                                last = pe.matmul(k.ps[0:T, 6, 0:D], oT[:, u, c, :], wo[:, c, :],
                                                 start=(c == 0), stop=(c == OC - 1))
                            last.then_inc(s["wo_mm"].sem, 1)

            @block.scalar
            def _(act):
                with act.Fori(0, TURNS) as i:
                    for u in range(2):
                        b = i * 2 + u
                        for c in range(C):
                            act.wait_ge(*s["kt_mm"].at(b * C + c + 1))
                            act.wait_ge(*s["sc_mm"].at((b - 1) * UB))
                            act.activation(KT[:, u, c, :], k.ps[:, 6, 0:keys], ACT.Identity,
                                           bias=pack["bk"][:, c:c + 1] if "bk" in pack else 0.0).then_inc(
                                               s["kt_ev"].sem, 1)
                    for n in range(U + 4):
                        if n < U:
                            act.wait_ge(*s["max_done"].at(i * U + n + 1))
                            act.wait_ge(*s["pt_mm"].at(i * U + n - 3))
                            for j in range(2):
                                at = sa[:, n % 2, j, :] if first_pass else k.ps[0:T, 2 * (n % 2) + j, 0:keys]
                                last = act.activation(P[:, n % 4, j, :], at, ACT.Exp, bias=ng[:, n % 4, j:j + 1],
                                                      scale=1.0 if first_pass else scale,
                                                      accum_out=rs[:, n % 4, j:j + 1])
                            last.then_inc(s["exp_done"].sem, 1)
                        m = n - 2
                        if 0 <= m < U:
                            act.wait_ge(*s["pt_mm"].at(i * U + m + 1))
                            act.wait_ge(*s["pv_mm"].at(i * U + m - 1))
                            na = min(kn, 2)
                            act.activation(PT[:, m % 2, 0:na, :, :],
                                           k.ps[0:kw, 4, 0:na * 2 * T].rearrange("p (c h t) -> p c h t", c=na, h=2),
                                           ACT.Copy).then_inc(s["pt_ev_a"].sem, 1)
                        if n in (UB + 2, 2 * UB + 2):
                            u = 0 if n == UB + 2 else 1
                            act.wait_ge(*s["pv_mm"].at(i * U + (u + 1) * UB))
                            act.wait_ge(*s["wo_mm"].at(i * 2 + u - 1))
                            act.activation(oT[:, u, :, :], chunks(k.ps[:, 7, 0:OC * T], OC), ACT.Copy).then_inc(
                                s["ot_ev"].sem, 1)

            @block.vector
            def _(v):
                ch = Chain(v, s["vec_step"])
                per = U * (2 + clamp + head_mask) + (2 if "bo" in pack else 0)
                with v.Fori(0, TURNS) as i:
                    ch.turn(i, per)
                    for u in range(2):
                        b = i * 2 + u
                        if self_attn:
                            v.wait_ge(*s["v_mm"].at((b - 1) * kn))
                            v.tensor_copy(src[:, u, :, :], k.XT[:, :, bass.ds(b * T, T)]).then_inc(
                                s["xs_copied"].sem, 1)
                        v.wait_ge(*s["sc_mm"].at((b - 1) * UB))
                        for c in range(C):
                            last = v.tensor_tensor(
                                qm[:, u, c * HC:(c + 1) * HC, :],
                                QT[:, c, bass.ds(b * T, T)].unsqueeze(1).broadcast_to([KP, HC, T]),
                                pack["hmask"][:, 0:HC].unsqueeze(2).broadcast_to([KP, HC, T]), ALU.mult)
                        last.then_inc(s["qm_done"].sem, 1)
                        if mask:
                            v.tensor_scalar(mb[:, u, :], mu8[:, bass.ds(b * S2, S2)], -1.0, FMAX, ALU.add, ALU.mult).then_inc(
                                s["mask_done"].sem, 1)
                        for j in range(kn):
                            v.wait_ge(*s["v_mm"].at(b * kn + j + 1))
                            v.wait_ge(*s["pv_mm"].at((b - 1) * UB))
                            at = k.ps[0:kw, 7, 0:HD].rearrange("p (h d) -> p h d", h=H)
                            if self_attn:
                                v.tensor_tensor(V[:, u, j, :, 0:dh], at,
                                                pack["bv"][0:kw, :].rearrange("p (h d) -> p h d", h=H),
                                                ALU.add).then_inc(s["v_ev"].sem, 1)
                            else:
                                v.tensor_copy(V[:, u, j, :, 0:dh], at).then_inc(s["v_ev"].sem, 1)
                    for n in range(U + 4):
                        if n < U:
                            u = n // UB
                            v.wait_ge(*s["sc_mm"].at(i * U + n + 1))
                            at = k.ps[0:T, 2 * (n % 2):2 * (n % 2) + 2, 0:keys]
                            r = n % 4
                            if first_pass:
                                v.wait_ge(*s["exp_done"].at(i * U + n - 1))
                                if clamp:
                                    v.tensor_scalar(sa[:, n % 2, :, :], at, scale, CLAMP, ALU.mult,
                                                    ALU.min).then_inc(s["sc_read"].sem, 1)
                                    v.wait_ge(*s["sc_read"].at(i * U + n + 1))
                                    ch.link(v.tensor_scalar(sa[:, n % 2, :, :], sa[:, n % 2, :, :], -CLAMP, None,
                                                            ALU.max))
                                else:
                                    if n % UB == 0:
                                        v.wait_ge(*s["mask_done"].at(i * 2 + u + 1))
                                    v.scalar_tensor_tensor(
                                        sa[:, n % 2, :, :], at, scale,
                                        mb[:, u, :].unsqueeze(1).broadcast_to([T, 2, keys]), ALU.mult,
                                        ALU.add).then_inc(s["sc_read"].sem, 1)
                                    v.wait_ge(*s["sc_read"].at(i * U + n + 1))
                                ch.link(v.tensor_reduce(mx[:, r, :], sa[:, n % 2, :, :], AX.X, ALU.max))
                                v.tensor_scalar(ng[:, r, :], mx[:, r, :], -1.0, None, ALU.mult).then_inc(
                                    s["max_done"].sem, 1)
                            else:
                                ch.link(v.tensor_reduce(mx[:, r, :], at, AX.X, ALU.max))
                                v.tensor_scalar(ng[:, r, :], mx[:, r, :], -scale, None, ALU.mult).then_inc(
                                    s["max_done"].sem, 1)
                        m = n - 1
                        if 0 <= m < U:
                            v.wait_ge(*s["exp_done"].at(i * U + m + 1))
                            ch.link(v.reciprocal(ri[:, m % 4, :], rs[:, m % 4, :]))
                            if head_mask:
                                p = m % UB
                                ch.link(v.tensor_tensor(ri[:, m % 4, :], ri[:, m % 4, :],
                                                        pack["hm"][0:T, 2 * p:2 * p + 2], ALU.mult))
                            for j in range(2):
                                last = v.tensor_scalar(P[:, m % 4, j, :], P[:, m % 4, j, :], ri[:, m % 4, j:j + 1],
                                                       None, ALU.mult)
                            last.then_inc(s["prob_done"].sem, 1)
                        m = n - 2
                        if 0 <= m < U and kn > 1:
                            v.wait_ge(*s["pt_mm"].at(i * U + m + 1))
                            v.wait_ge(*s["pv_mm"].at(i * U + m - 1))
                            v.tensor_copy(PT[:, m % 2, 2, :, :],
                                          chunks(k.ps[0:kw, 5, 0:2 * T], 2)).then_inc(s["pt_ev_v"].sem, 1)
                        if n in (UB + 3, 2 * UB + 3):
                            u = 0 if n == UB + 3 else 1
                            v.wait_ge(*s["wo_mm"].at(i * 2 + u + 1))
                            v.tensor_tensor(k.x(i * 2 + u), k.ps[0:T, 6, 0:D], k.x(i * 2 + u), ALU.add).then_inc(
                                s["res_done"].sem, 1)
                            v.wait_ge(*s["res_done"].at(i * 2 + u + 1))
                            if "bo" in pack:
                                ch.link(v.tensor_tensor(k.x(i * 2 + u), pack["bo"][0:T, :], k.x(i * 2 + u),
                                                        ALU.add))
                    ch.end(TURNS)
                ch.close()

        units = TURNS * U
        k.advance(xs_copied=B if self_attn else 0, kt_mm=B * C, kt_ev=B * C, v_mm=B * kn, v_ev=B * kn, qm_done=B,
                  sc_mm=units, sc_read=units if first_pass else 0, max_done=units, exp_done=units, prob_done=units,
                  pt_mm=units, pt_ev_a=units, pt_ev_v=units if kn > 1 else 0, pv_mm=units, ot_ev=B, wo_mm=B,
                  res_done=B, mask_done=B if mask else 0)
        if not self_attn:
            k.advance(ctx_in0=TURNS * 16, ctx_in1=TURNS * 16)


def sub_attention(k, ctx, name, packs, spec):
    lay, dram = packs[name]
    tile, p = pack_tile(k, ctx, name + "_pack", lay)
    pack = {f: p(f) for f in lay if f != "_total"}
    for f in ("wq", "wk", "wv"):
        pack[f] = chunks(pack[f], 2)
    heads_out = KP // max(spec["dh"], 32)
    pack["wo"] = chunks(pack["wo"], spec["H"] // heads_out)
    layer_norm(k, pack=(tile, dram, lay["_total"]))
    attention(k, name, pack, **spec)


ATTENTION = {
    "L0_xattn": dict(H=16, dh=16, clamp=True),
    "L1_xattn": dict(H=8, dh=64),
    "L2_xattn": dict(H=16, dh=16, mask=True),
    "L3_attn": dict(H=16, dh=16, self_attn=True, head_mask=True),
}


def head_rows(dh):
    return np.repeat(np.eye(KP // dh, dtype=np.float32), dh, axis=0)


def spread_heads(wo, H, dh):
    wide = np.zeros((H, max(dh, 32), wo.shape[1]), np.float32)
    wide[:, :dh] = wo.reshape(H, dh, -1)
    return wide.reshape(-1, wo.shape[1])


def with_bias_row(w, bias):
    out = np.zeros((CR + 1, 2, w.shape[1]), np.float32)
    out[:CR] = w.reshape(2, CR, -1).transpose(1, 0, 2)
    if bias is not None:
        out[CR, 1] = bias
    return out.reshape(CR + 1, -1)


def host_attention(name, a):
    w = {key[len(name) + 1:]: v for key, v in a.items() if key.startswith(name + "_")}
    spec = ATTENTION[name]
    H, dh = spec["H"], spec["dh"]
    turned = spec.get("self_attn")
    m = {n: (w[n].T if turned else w[n]) for n in ("Wq", "Wk", "Wv", "Wo")}
    f = dict(wq=by_rows(m["Wq"]), wo=by_rows(spread_heads(m["Wo"], H, dh)), hmask=head_rows(dh))
    if turned:
        f.update(wk=by_rows(m["Wk"]), wv=by_rows(m["Wv"]), bv=on_rows(w["bv"]), hm=on_rows(w["head_mask"]))
    else:
        f.update(wk=by_rows(m["Wk"], CR), wv=with_bias_row(m["Wv"], w.get("bv")))
    for n in ("bq", "bk"):
        if n in w:
            f[n] = columns(w[n])
    if "bo" in w:
        f["bo"] = on_rows(w["bo"])
    return {name: packed(f)}



def sub_l3_xattn(k, ctx, name, packs):
    nc = k.nc
    lay, dram = packs[name]
    tile, p = pack_tile(k, ctx, name + "_pack", lay)
    layer_norm(k, pack=(tile, dram, lay["_total"]))
    wq, wk, wv = (chunks(p(n), 2) for n in ("wq", "wk", "wv"))
    scale = float(D) ** -0.5
    s = k.signals
    sb = lambda n, sh: k.tile(ctx, name + "_" + n, sh, F32)
    src = sb("src", [CR + 1, 2, 2, S2])
    qT = sb("qT", [KP, 2, 2, T])
    KT = sb("kT", [KP, 2, 2, S2])
    V = sb("v", [KW, 2, KN, D])
    P = sb("p", [T, 2, S2])
    PT = sb("pT", [KW, 2, KN, T])
    mx, ng, rs, ri = (sb(n, [T, 2]) for n in ("mx", "ng", "rs", "ri"))
    ctx_in = [s["ctx_in0"], s["ctx_in1"]]
    TURNS = B // 2
    with nc.Block(no_gpsimd_drain=True) as block:
        @block.vector
        def _(v):
            v.memset(src[CR:CR + 1, :, :, :], 1.0)

    with nc.Block(no_gpsimd_drain=True) as block:
        @block.sync
        def _(sp):
            with sp.Fori(0, TURNS) as i:
                for u in range(2):
                    sp.wait_ge(*s["v_mm"].at((i * 2 + u - 1) * KN))
                    sp.dma_start(src[0:CR, u, :, :], k.aps["in_ctx"][bass.ds(i * 2 + u, 1), :, :, :]
                                 .rearrange("b p c n -> (b p) c n")).then_inc(ctx_in[u].sem, 16)

        @block.tensor
        def _(pe):
            with pe.Fori(0, TURNS) as i:
                for u in range(2):
                    b = i * 2 + u
                    pe.wait_ge(*ctx_in[u].at((i + 1) * 16))
                    pe.wait_ge(*s["qm_done"].at(b))
                    for c in range(2):
                        for kc in range(2):
                            last = pe.matmul(k.ps[:, 0, c * T:(c + 1) * T], wq[:, kc, c * KP:(c + 1) * KP],
                                             k.XT[:, kc, bass.ds(b * T, T)], start=(kc == 0), stop=(kc == 1))
                    last.then_inc(s["lin_mm"].sem, 1)
                    for c in range(2):
                        pe.wait_ge(*s["kt_ev"].at(b * 2 + c - 1))
                        for kc in range(2):
                            rows = CR + kc
                            last = pe.matmul(k.ps[:, 1 + c, 0:S2], wk[0:rows, kc, c * KP:(c + 1) * KP],
                                             src[0:rows, u, kc, :], start=(kc == 0), stop=(kc == 1))
                        last.then_inc(s["kt_mm"].sem, 1)
                    for j in range(KN):
                        pe.wait_ge(*s["v_ev"].at(b * KN + j - 1))
                        bank = 3 + (u * KN + j) % 2
                        for kc in range(2):
                            rows = CR + kc
                            last = pe.matmul(k.ps[0:KW, bank, 0:D], src[0:rows, u, kc, j * KW:(j + 1) * KW],
                                             wv[0:rows, kc, :], start=(kc == 0), stop=(kc == 1))
                        last.then_inc(s["v_mm"].sem, 1)
                for u in range(2):
                    b = i * 2 + u
                    pe.wait_ge(*s["qm_done"].at(b + 1))
                    pe.wait_ge(*s["kt_ev"].at((b + 1) * 2))
                    pe.wait_ge(*s["exp_done"].at(b - 1))
                    for c in range(2):
                        last = pe.matmul(k.ps[0:T, 5 + u, 0:S2], qT[:, u, c, :], KT[:, u, c, :], start=(c == 0),
                                         stop=(c == 1))
                    last.then_inc(s["sc_mm"].sem, 1)
                for u in range(2):
                    b = i * 2 + u
                    pe.wait_ge(*s["exp_done"].at(b + 1))
                    pe.wait_ge(*s["res_done"].at(b))
                    pe.wait_ge(*s["pt_ev_a"].at(b))
                    for kc in range(KN):
                        last = pe.transpose(k.ps[0:KW, 7, kc * T:(kc + 1) * T], P[:, u, kc * KW:(kc + 1) * KW],
                                            k.ident[0:T, 0:T])
                    last.then_inc(s["pt_mm"].sem, 1)
                    pe.wait_ge(*s["pt_ev_a"].at(b + 1))
                    pe.wait_ge(*s["v_ev"].at((b + 1) * KN))
                    for kc in range(KN):
                        last = pe.matmul(k.ps[0:T, 7, 0:D], PT[:, u, kc, :], V[:, u, kc, :], start=(kc == 0),
                                         stop=(kc == KN - 1))
                    last.then_inc(s["pv_mm"].sem, 1)

        @block.scalar
        def _(act):
            with act.Fori(0, TURNS) as i:
                for u in range(2):
                    b = i * 2 + u
                    act.wait_ge(*s["lin_mm"].at(b + 1))
                    act.wait_ge(*s["sc_mm"].at(b - 1))
                    for c in range(2):
                        last = act.activation(qT[:, u, c, :], k.ps[:, 0, c * T:(c + 1) * T], ACT.Identity,
                                              bias=p("bq")[:, c:c + 1])
                    last.then_inc(s["qm_done"].sem, 1)
                    for c in range(2):
                        act.wait_ge(*s["kt_mm"].at(b * 2 + c + 1))
                        act.activation(KT[:, u, c, :], k.ps[:, 1 + c, 0:S2], ACT.Copy).then_inc(s["kt_ev"].sem, 1)
                for u in range(2):
                    b = i * 2 + u
                    act.wait_ge(*s["max_done"].at(b + 1))
                    act.wait_ge(*s["pt_mm"].at(b - 1))
                    act.activation(P[:, u, :], k.ps[0:T, 5 + u, 0:S2], ACT.Exp, bias=ng[:, u:u + 1], scale=scale,
                                   accum_out=rs[:, u:u + 1]).then_inc(s["exp_done"].sem, 1)
                for u in range(2):
                    b = i * 2 + u
                    act.wait_ge(*s["pt_mm"].at(b + 1))
                    act.wait_ge(*s["pv_mm"].at(b - 1))
                    act.activation(PT[:, u, :, :], chunks(k.ps[0:KW, 7, 0:KN * T], KN), ACT.Copy).then_inc(
                        s["pt_ev_a"].sem, 1)

        @block.vector
        def _(v):
            ch = Chain(v, s["vec_step"])
            with v.Fori(0, TURNS) as i:
                ch.turn(i, 4)
                for u in range(2):
                    b = i * 2 + u
                    v.wait_ge(*s["pv_mm"].at(b - 1))
                    for j in range(KN):
                        v.wait_ge(*s["v_mm"].at(b * KN + j + 1))
                        v.tensor_copy(V[:, u, j, :], k.ps[0:KW, 3 + (u * KN + j) % 2, 0:D]).then_inc(
                            s["v_ev"].sem, 1)
                for u in range(2):
                    b = i * 2 + u
                    v.wait_ge(*s["sc_mm"].at(b + 1))
                    ch.link(v.tensor_reduce(mx[:, u:u + 1], k.ps[0:T, 5 + u, 0:S2], AX.X, ALU.max))
                    v.tensor_scalar(ng[:, u:u + 1], mx[:, u:u + 1], -scale, None, ALU.mult).then_inc(
                        s["max_done"].sem, 1)
                for u in range(2):
                    b = i * 2 + u
                    v.wait_ge(*s["exp_done"].at(b + 1))
                    ch.link(v.reciprocal(ri[:, u:u + 1], rs[:, u:u + 1]))
                    v.wait_ge(*s["pv_mm"].at(b + 1))
                    v.scalar_tensor_tensor(k.x(b), k.ps[0:T, 7, 0:D], ri[:, u:u + 1], k.x(b), ALU.mult,
                                           ALU.add).then_inc(s["res_done"].sem, 1)
                ch.end(TURNS)
            ch.close()
    k.advance(lin_mm=B, qm_done=B, kt_mm=2 * B, kt_ev=2 * B, v_mm=B * KN, v_ev=B * KN, sc_mm=B, max_done=B,
              exp_done=B, pt_mm=B, pt_ev_a=B, pv_mm=B, res_done=B, ctx_in0=TURNS * 16, ctx_in1=TURNS * 16)


def host_l3_xattn(name, a):
    w = {key[len(name) + 1:]: v for key, v in a.items() if key.startswith(name + "_")}
    return {name: packed(dict(wq=by_rows(w["Wq"].T), wk=with_bias_row(w["Wk"].T, w["bk"]),
                              wv=with_bias_row(w["Wv"].T, w["bv"]), bq=columns(w["bq"])))}



CH = 8
NCH = T // CH
GCH = GB * NCH


def project_out(k, make, wo, residual="X", out=None, per=1):
    nc = k.nc
    s = k.signals
    with ExitStack() as ctx:
        sb = lambda n, sh: k.tile(ctx, "po_" + n, sh, F32)
        xo = sb("x", [T, 2, D])
        oT = sb("oT", [KP, 2, 2, T])
        with nc.Block(no_gpsimd_drain=True) as block:
            @block.vector
            def _(v):
                ch = Chain(v, s["vec_step"])
                with v.Fori(0, B // 2) as i:
                    ch.turn(i, 2 * (per - 1))
                    for u in range(2):
                        b = 2 * i + u
                        v.wait_ge(*s["norm_tr"].at(b - 1))
                        make(v, ch, b, xo[:, u, :]).then_inc(s["norm_done"].sem, 1)
                    for u in range(2):
                        b = 2 * i + u
                        v.wait_ge(*s["wo_mm"].at(b + 1))
                        if out is None:
                            v.tensor_tensor(k.x(b), k.ps[0:T, 2 + u, 0:D], k.x(b), ALU.add).then_inc(
                                s["res_done"].sem, 1)
                        else:
                            v.tensor_tensor(out[:, bass.ds(b * D, D)], k.ps[0:T, 2 + u, 0:D],
                                            residual[:, bass.ds(b * D, D)], ALU.add).then_inc(s["res_done"].sem, 1)
                    ch.end(B // 2)
                ch.close()

            @block.tensor
            def _(pe):
                with pe.Fori(0, B // 2) as i:
                    for u in range(2):
                        b = 2 * i + u
                        pe.wait_ge(*s["norm_done"].at(b + 1))
                        pe.wait_ge(*s["norm_ev"].at(b - 1))
                        for c in range(2):
                            last = pe.transpose(k.ps[:, u, c * T:(c + 1) * T], xo[:, u, c * KP:(c + 1) * KP],
                                                k.ident[0:T, 0:T])
                        last.then_inc(s["norm_tr"].sem, 1)
                    for u in range(2):
                        b = 2 * i + u
                        pe.wait_ge(*s["norm_ev"].at(b + 1))
                        pe.wait_ge(*s["res_done"].at(b - 1))
                        for c in range(2):
                            last = pe.matmul(k.ps[0:T, 2 + u, 0:D], oT[:, u, c, :], wo[:, c, :], start=(c == 0),
                                             stop=(c == 1))
                        last.then_inc(s["wo_mm"].sem, 1)

            @block.scalar
            def _(act):
                with act.Fori(0, B // 2) as i:
                    for u in range(2):
                        b = 2 * i + u
                        act.wait_ge(*s["norm_tr"].at(b + 1))
                        act.wait_ge(*s["wo_mm"].at(b - 1))
                        act.activation(oT[:, u, :, :], chunks(k.ps[:, u, 0:2 * T], 2), ACT.Copy).then_inc(
                            s["norm_ev"].sem, 1)
        k.advance(norm_done=B, norm_tr=B, norm_ev=B, wo_mm=B, res_done=B)


def sub_l0_attn(k, ctx, name, packs):
    nc = k.nc
    lay, dram = packs[name]
    tile, p = pack_tile(k, ctx, name + "_pack", lay)
    layer_norm(k, pack=(tile, dram, lay["_total"]))
    s = k.signals
    outer = lambda n, sh: k.tile(ctx, name + "_" + n, sh, F32)
    V = outer("V", [T, B * D])
    GV = outer("G", [T, B * D])
    R, K, E = (outer(n, [KP, N]) for n in ("R", "K", "E"))

    with ExitStack() as mid:
        sb = lambda n, sh: k.tile(mid, name + "_" + n, sh, F32)
        dT = sb("dT", [KP, 2, N])
        z0 = sb("z0", [KP, N])
        z1 = sb("z1", [KP, N])
        wx1, wx2 = chunks(p("wx1"), 2), p("wx2").rearrange("p (i n) -> p i n", i=5)
        with ExitStack() as inner:
            xm = k.tile(inner, name + "_xm", [KP, 2, N], F32)
            with nc.Block(no_gpsimd_drain=True) as block:
                @block.vector
                def _(v):
                    for c in range(2):
                        x3 = k.XT[:, c, :].rearrange("p (b t) -> p b t", b=B)
                        d3 = dT[:, c, :].rearrange("p (b t) -> p b t", b=B)
                        v.tensor_tensor(d3[:, :, 1:T], x3[:, :, 0:T - 1], x3[:, :, 1:T], ALU.subtract)
                        v.tensor_scalar(d3[:, :, 0:1], x3[:, :, 0:1], -1.0, None, ALU.mult).then_inc(
                            s["p_a"].sem, 1)
                        v.wait_ge(*s["p_a"].at(c + 1))
                        v.scalar_tensor_tensor(xm[:, c, :], dT[:, c, :], p("mu_x")[:, c:c + 1], k.XT[:, c, :],
                                               ALU.mult, ALU.add).then_inc(s["p_b"].sem, 1)

                @block.tensor
                def _(pe):
                    pe.wait_ge(*s["p_b"].at(2))
                    with pe.Fori(0, G) as g:
                        for m in range(2):
                            pe.wait_ge(*s["lin_act"].at(2 * g + m - 1))
                            for c in range(2):
                                last = pe.matmul(k.ps[:, m, 0:GT], wx1[:, c, m * KP:(m + 1) * KP],
                                                 xm[:, c, bass.ds(g * GT, GT)], start=(c == 0), stop=(c == 1))
                            last.then_inc(s["lin_mm"].sem, 1)

                @block.scalar
                def _(act):
                    with act.Fori(0, G) as g:
                        for m in range(2):
                            z = (z0, z1)[m]
                            act.wait_ge(*s["lin_mm"].at(2 * g + m + 1))
                            act.activation(z[:, bass.ds(g * GT, GT)], k.ps[:, m, 0:GT], ACT.Tanh).then_inc(
                                s["lin_act"].sem, 1)
            k.advance(p_a=2, p_b=2, lin_mm=2 * G, lin_act=2 * G)

        inp = sb("inp", [KP, 2, 5, 2, GT])
        tmp = sb("tmp", [KP, 2, GT])
        ta = sb("ta", [64, 2, GT])
        wr, wk, wa, wv, wg = (chunks(p(n), 2) for n in ("wr", "wk", "wa", "wv", "wg"))
        R_, W_, K_, V_, G_ = range(5)
        mixed, mus, prod, done = s["p_a"], s["p_b"], s["p_c"], s["p_d"]
        with nc.Block(no_gpsimd_drain=True) as block:
            @block.tensor
            def _(pe):
                with pe.Fori(0, G // 2) as i:
                    for u in range(2):
                        g = 2 * i + u
                        tok = bass.ds(g * GT, GT)
                        for r in range(10):
                            j, c = r // 2, r % 2
                            pe.wait_ge(*mixed.at(g * 10 + r - 3))
                            pe.matmul(k.ps[:, (u * 10 + r) % 4, 0:GT], wx2[:, j, c * KP:(c + 1) * KP],
                                      (z0 if j < 4 else z1)[:, tok], start=True, stop=True).then_inc(mus.sem, 1)
                    for u in range(2):
                        g = 2 * i + u

                        def product(q, rows, w, j):
                            pe.wait_ge(*done.at(g * 8 + q - 3))
                            pe.wait_ge(*mixed.at(g * 10 + 2 * j + 2))
                            for c in range(2):
                                last = pe.matmul(k.ps[0:rows, 4 + q % 4, 0:GT], w[:, c, :], inp[:, u, j, c, :],
                                                 start=(c == 0), stop=(c == 1))
                            last.then_inc(prod.sem, 1)

                        product(0, KP, wr, R_)
                        product(1, 64, wa, W_)
                        product(2, KP, wk, K_)
                        pe.wait_ge(*done.at(g * 8 + 2))
                        pe.matmul(k.ps[:, 7, 0:GT], p("wb"), ta[:, u, :], start=True, stop=True).then_inc(
                            prod.sem, 1)
                        for q, (w, j) in enumerate([(wv, V_), (wv, V_), (wg, G_), (wg, G_)]):
                            pe.wait_ge(*done.at(g * 8 + 4 + q - 3))
                            pe.wait_ge(*mixed.at(g * 10 + 2 * j + 2))
                            for b in range(2):
                                at = (2 * (q % 2) + b) * T
                                for c in range(2):
                                    last = pe.matmul(k.ps[0:T, 4 + q, b * D:(b + 1) * D], inp[:, u, j, c, at:at + T],
                                                     w[:, c, :], start=(c == 0), stop=(c == 1))
                            last.then_inc(prod.sem, 1)

            @block.vector
            def _(v):
                ch = Chain(v, s["vec_step"])
                with v.Fori(0, G // 2) as i:
                    ch.turn(i, 20)
                    for u in range(2):
                        g = 2 * i + u
                        tok = bass.ds(g * GT, GT)
                        for r in range(10):
                            j, c = r // 2, r % 2
                            v.wait_ge(*mus.at(g * 10 + r + 1))
                            ch.link(v.scalar_tensor_tensor(tmp[:, r % 2, :], k.ps[:, (u * 10 + r) % 4, 0:GT],
                                                           p("x_bias")[:, r:r + 1], dT[:, c, tok], ALU.add,
                                                           ALU.mult))
                            if r == 0:
                                v.wait_ge(*prod.at((g - 1) * 8))
                            v.tensor_tensor(inp[:, u, j, c, :], tmp[:, r % 2, :], k.XT[:, c, tok],
                                            ALU.add).then_inc(mixed.sem, 1)
                    ch.end(G // 2)
                ch.close()

            @block.scalar
            def _(act):
                with act.Fori(0, G // 2) as i:
                    for u in range(2):
                        g = 2 * i + u
                        tok = bass.ds(g * GT, GT)
                        for q, (dst, rows, fn) in enumerate([(R[:, tok], KP, ACT.Copy), (ta[:, u, :], 64, ACT.Tanh),
                                                             (K[:, tok], KP, ACT.Copy)]):
                            act.wait_ge(*prod.at(g * 8 + q + 1))
                            act.activation(dst, k.ps[0:rows, 4 + q, 0:GT], fn).then_inc(done.sem, 1)
                        act.wait_ge(*prod.at(g * 8 + 4))
                        act.activation(E[:, tok], k.ps[:, 7, 0:GT], ACT.Exp, bias=p("b_w")).then_inc(done.sem, 1)
                        for q in range(4):
                            dst = V if q < 2 else GV
                            act.wait_ge(*prod.at(g * 8 + 5 + q))
                            act.activation(dst[:, bass.ds((g * GB + 2 * (q % 2)) * D, 2 * D)],
                                           k.ps[0:T, 4 + q, 0:2 * D], ACT.Copy).then_inc(done.sem, 1)
        k.advance(p_a=10 * G, p_b=10 * G, p_c=8 * G, p_d=8 * G)

    O = outer("O", [T, B * D])
    rwkv_matrix(k, name, p, R, K, E, V, O)

    with ExitStack() as mid:
        sb = lambda n, sh: k.tile(mid, name + "_" + n, sh, F32)
        BH, HV = B * 4, D // 4
        gw, sq = sb("gw", [T, B * D]), sb("sq", [T, B * D])
        mean, var, rstd, half = (sb(n, [T, BH]) for n in ("mean", "var", "rstd", "half"))
        heads = lambda t: t[:, :].rearrange("p (h v) -> p h v", v=HV)
        batches = lambda t: t[:, :].rearrange("p (b d) -> p b d", b=B)
        wide = lambda t: t[:, :].unsqueeze(2).broadcast_to([T, BH, HV])
        row = lambda f: p(f)[0:T, :].unsqueeze(1).broadcast_to([T, B, D])
        with nc.Block(no_gpsimd_drain=True) as block:
            @block.vector
            def _(v):
                ch = Chain(v, s["vec_step"])
                v.memset(half[:, :], -0.5)
                ch.link(v.tensor_reduce(mean[:, :], heads(O), AX.X, ALU.add))
                ch.link(v.tensor_scalar(mean[:, :], mean[:, :], 1.0 / HV, None, ALU.mult))
                v.tensor_tensor(heads(O), heads(O), wide(mean), ALU.subtract).then_inc(s["p_a"].sem, 1)
                v.wait_ge(*s["p_b"].at(1))
                ch.link(v.tensor_reduce(var[:, :], heads(sq), AX.X, ALU.add))
                v.tensor_scalar(var[:, :], var[:, :], 1.0 / HV, LN_EPS, ALU.mult, ALU.add).then_inc(s["p_a"].sem, 1)
                v.wait_ge(*s["p_b"].at(2))
                v.tensor_tensor(batches(gw), batches(GV), row("gn_w"), ALU.mult)
                ch.link(v.tensor_tensor(batches(GV), batches(GV), row("gn_b"), ALU.mult))
                v.wait_ge(*s["p_c"].at(1))
                ch.link(v.tensor_tensor(heads(O), heads(O), wide(rstd), ALU.mult))
                ch.link(v.tensor_tensor(O[:, :], O[:, :], gw[:, :], ALU.mult))
                ch.close()

            @block.scalar
            def _(act):
                act.wait_ge(*s["p_a"].at(1))
                act.activation(sq[:, :], O[:, :], ACT.Square).then_inc(s["p_b"].sem, 1)
                act.activation(GV[:, :], GV[:, :], ACT.Silu).then_inc(s["p_b"].sem, 1)

            @block.gpsimd
            def _(g):
                g.wait_ge(*s["p_a"].at(2))
                g.tensor_tensor(rstd[:, :], var[:, :], half[:, :], ALU.pow).then_inc(s["p_c"].sem, 1)
        k.advance(p_a=2, p_b=2, p_c=1)

    def gated(v, ch, b, dst):
        return v.tensor_tensor(dst, O[:, bass.ds(b * D, D)], GV[:, bass.ds(b * D, D)], ALU.add)

    project_out(k, gated, chunks(p("wo"), 2))


def rwkv_matrix(k, name, p, R, K, E, V, O):
    nc, s = k.nc, k.signals
    with ExitStack() as ctx:
        sb = lambda n, sh: k.tile(ctx, name + "_" + n, sh, F32)
        ci, cx, eq, ek, qd, kd = (sb(n, [KP, GT]) for n in ("ci", "cx", "eq", "ek", "qd", "kd"))
        gd = sb("gd", [KP, GCH])
        PW = CH * (CH - 1) // 2
        dd = sb("dd", [KP, PW, GCH])
        PP = sb("P", [KP, CH, GT])
        KA = sb("KA", [KP, NCH, GB, T])
        QB = sb("QB", [KP, GB, 4, T])
        ad = sb("ad", [T, GB, CH, 4])
        tm = sb("tm", [T, 4, NCH, CH])
        A = sb("A", [T, GB, 4, T])
        by_chunk = lambda t: t.rearrange("p (n s) -> p s n", s=CH)


        def pairs(d):
            return bass.AP(tensor=PP[:, :, :].tensor, offset=d * GT,
                           ap=[[CH * GT, KP], [GT + 1, CH - d], [CH, GCH]])

        offs = [0]
        for d in range(1, CH):
            offs.append(offs[-1] + CH - d)
        sums, exps, made, part, whole, outs, copied = (s[n] for n in ("p_a", "p_b", "p_c", "p_d", "p_e",
                                                                      "p_f", "p_g"))
        with nc.Block(no_gpsimd_drain=True) as block:
            @block.vector
            def _(v):
                v.memset(PP[:, :, :], 0.0)

            @block.gpsimd
            def _(g):
                g.memset(KA[:, :, :, :], 0.0)
                g.drain()

        with nc.Block(no_gpsimd_drain=True) as block:
            @block.vector
            def _(v):
                ch = Chain(v, s["vec_step"])
                with v.Fori(0, G) as g:
                    tok = bass.ds(g * GT, GT)
                    ch.turn(g, 23)
                    r, kk, e = by_chunk(R[:, tok]), by_chunk(K[:, tok]), E[:, tok]
                    ch.link(v.tensor_tensor_scan(ci[:, :], p("reset"), e, 0.0, ALU.mult, ALU.add))
                    ch.link(v.tensor_tensor(cx[:, :], ci[:, :], e, ALU.subtract))
                    c3, x3 = by_chunk(ci[:, :]), by_chunk(cx[:, :])
                    ends = c3[:, CH - 1:CH, :].broadcast_to([KP, CH, GCH])
                    v.tensor_tensor(by_chunk(ek[:, :]), c3, ends, ALU.subtract)
                    for d in range(1, CH):
                        last = v.tensor_tensor(dd[:, offs[d - 1]:offs[d], :], c3[:, 0:CH - d, :], x3[:, d:CH, :],
                                               ALU.subtract)
                    last.then_inc(sums.sem, 1)
                    v.wait_ge(*exps.at(g + 1))
                    v.wait_ge(*part.at(g))
                    ch.link(v.tensor_tensor(qd[:, :], R[:, tok], eq[:, :], ALU.mult))
                    v.tensor_tensor(QB[:, :, :, :],
                                    qd[:, :].rearrange("p (b t) -> p b t", b=GB).unsqueeze(2)
                                    .broadcast_to([KP, GB, 4, T]),
                                    p("hmask").unsqueeze(1).unsqueeze(3).broadcast_to([KP, GB, 4, T]), ALU.mult)
                    ch.link(v.tensor_tensor(kd[:, :], K[:, tok], ek[:, :], ALU.mult))
                    flat = KA[:, :, :, :].rearrange("p i b (c s) -> p (i b c) s", s=CH)
                    for b in range(GB):
                        first = GCH + b * NCH
                        last = v.tensor_copy(flat[:, first:first + (GCH + 1) * (NCH - 2) + 1:GCH + 1, :],
                                             kd[:, b * T:(b + 1) * T - CH].rearrange("p (c s) -> p c s", s=CH))
                    ch.link(last)
                    g4 = gd[:, :].rearrange("p (b n) -> p b n", b=GB)
                    for i in range(2, NCH):
                        ch.link(v.tensor_tensor(KA[:, i, :, 0:CH * (i - 1)], KA[:, i - 1, :, 0:CH * (i - 1)],
                                                g4[:, :, i - 1:i].broadcast_to([KP, GB, CH * (i - 1)]), ALU.mult))
                    for d in range(1, CH):
                        at = dd[:, offs[d - 1]:offs[d], :]
                        last = v.tensor_tensor(at, at, kk[:, 0:CH - d, :], ALU.mult)
                    ch.link(last)
                    for d in range(1, CH):
                        last = v.tensor_tensor(pairs(d), dd[:, offs[d - 1]:offs[d], :], r[:, d:CH, :], ALU.mult)
                    v.scalar_tensor_tensor(pairs(0), r, p("bonus"), kk, ALU.mult,
                                           ALU.mult).then_inc(made.sem, 1)
                    v.wait_ge(*part.at(g + 1))
                    ch.link(v.tensor_copy(ad[:, :, :, :], k.ps[0:T, 4, 0:GB * CH * 4].rearrange(
                        "p (b j h) -> p b j h", b=GB, j=CH)))
                    v.wait_ge(*outs.at(g * GB))
                    for b in range(GB):
                        v.wait_ge(*whole.at(g * GB + b))
                        ch.link(v.tensor_tensor(
                            tm[:, :, :, :],
                            ad[:, b, :, :].rearrange("p j h -> p h j").unsqueeze(2).broadcast_to([T, 4, NCH, CH]),
                            p("same")[0:T, :].rearrange("p (n j) -> p n j", j=CH).unsqueeze(1)
                            .broadcast_to([T, 4, NCH, CH]), ALU.mult))
                        v.tensor_tensor(A[:, b, :, :], tm[:, :, :, :].rearrange("p h n j -> p h (n j)"),
                                        chunks(k.ps[0:T, b, 0:GT], 4), ALU.add).then_inc(whole.sem, 1)
                    ch.end(G)
                ch.close()

            @block.scalar
            def _(act):
                with act.Fori(0, G) as g:
                    act.wait_ge(*sums.at(g + 1))
                    act.activation(eq[:, :], cx[:, :], ACT.Exp, scale=-1.0)
                    act.activation(ek[:, :], ek[:, :], ACT.Exp)
                    act.activation(gd[:, :], by_chunk(ci[:, :])[:, CH - 1, :], ACT.Exp, scale=-1.0)
                    act.activation(dd[:, :, :], dd[:, :, :], ACT.Exp).then_inc(exps.sem, 1)
                    for b in range(GB):
                        act.wait_ge(*outs.at(g * GB + b + 1))
                        act.activation(O[:, bass.ds((g * GB + b) * D, D)], k.ps[0:T, 5 + b % 2, 0:D],
                                       ACT.Copy).then_inc(copied.sem, 1)

            @block.tensor
            def _(pe):
                with pe.Fori(0, G) as g:
                    pe.wait_ge(*made.at(g + 1))
                    pe.wait_ge(*whole.at(g * GB))
                    for b in range(GB):
                        for j in range(CH):
                            at = (b * CH + j) * 4
                            last = pe.matmul(k.ps[0:T, 4, at:at + 4],
                                             PP[:, j, b * T:(b + 1) * T], p("hmask"), start=True, stop=True)
                    for b in range(GB):
                        out = chunks(k.ps[0:T, b, 0:GT], 4)
                        for i in range(NCH):
                            last = pe.matmul(out[:, :, i * CH:(i + 1) * CH], KA[:, i, b, :],
                                             QB[:, b, :, i * CH:(i + 1) * CH], start=True, stop=True)
                    last.then_inc(part.sem, 1)
                    for b in range(GB):
                        pe.wait_ge(*whole.at(g * GB + b + 1))
                        pe.wait_ge(*copied.at(g * GB + b - 1))
                        for h in range(4):
                            last = pe.matmul(k.ps[0:T, 5 + b % 2, h * 64:(h + 1) * 64], A[:, b, h, :],
                                             V[:, bass.ds((g * GB + b) * D + h * 64, 64)], start=True, stop=True)
                        last.then_inc(outs.sem, 1)
        k.advance(p_a=G, p_b=G, p_c=G, p_d=G, p_e=B, p_f=B, p_g=B)


def host_l0_attn(name, a):
    w = {key[len(name) + 1:]: v for key, v in a.items() if key.startswith(name + "_")}
    wx2 = np.zeros((KP, 5, D), np.float32)
    per_mix = w["W_x2"].reshape(D, 5, 32)
    for j in range(4):
        wx2[32 * j:32 * j + 32, j] = per_mix[:, j].T
    wx2[0:32, 4] = per_mix[:, 4].T
    wx1 = np.zeros((D, 2 * KP), np.float32)
    wx1[:, :160] = w["W_x1"].T
    reset = np.ones((1, GT), np.float32)
    reset[:, ::CH] = 0.0
    f = dict(mu_x=columns(w["mu_x"]), wx1=by_rows(wx1), wx2=wx2.reshape(KP, -1),
             x_bias=w["x_bias"].reshape(5, 2, KP).transpose(2, 0, 1).reshape(KP, 10),
             wr=by_rows(w["W_r"].T), wk=by_rows(w["W_k"].T), wv=by_rows(w["W_v"].T), wg=by_rows(w["W_g"].T),
             wa=by_rows(w["A_w"].T), wb=w["B_w"].T, b_w=w["b_w"][:, None], bonus=w["bonus"].reshape(KP, 1),
             gn_w=on_rows(w["gn_weight"]), gn_b=on_rows(w["gn_bias"]), wo=by_rows(w["W_o"].T),
             hmask=head_rows(32), reset=on_rows(reset),
             same=np.repeat(np.repeat(np.eye(NCH, dtype=np.float32), CH, axis=0), CH, axis=1))
    return {name: packed(f)}



def project_features(k, w, C, dst, bias=None, fn=ACT.Identity):
    s = k.signals
    with k.nc.Block(no_gpsimd_drain=True) as block:
        @block.tensor
        def _(pe):
            with pe.Fori(0, G) as g:
                for c in range(C):
                    pe.wait_ge(*s["lin_act"].at(g * C + c - C + 1))
                    for kc in range(2):
                        last = pe.matmul(k.ps[:, c, 0:GT], w[:, kc, c * KP:(c + 1) * KP],
                                         k.XT[:, kc, bass.ds(g * GT, GT)], start=(kc == 0), stop=(kc == 1))
                    last.then_inc(s["lin_mm"].sem, 1)

        @block.scalar
        def _(act):
            with act.Fori(0, G) as g:
                for c in range(C):
                    act.wait_ge(*s["lin_mm"].at(g * C + c + 1))
                    act.activation(dst[:, c, bass.ds(g * GT, GT)], k.ps[:, c, 0:GT], fn,
                                   bias=bias[:, c:c + 1] if bias is not None else 0.0).then_inc(
                                       s["lin_act"].sem, 1)
    k.advance(lin_mm=G * C, lin_act=G * C)


def backwards(ap):
    step, n = ap.ap[-1]
    return bass.AP(tensor=ap.tensor, offset=ap.offset + (n - 1) * step, ap=[*ap.ap[:-1], [-step, n]])


TQ = 64
NQ = D // TQ


def sub_l1_attn(k, ctx, name, packs):
    nc, s = k.nc, k.signals
    lay, dram = packs[name]
    tile, p = pack_tile(k, ctx, name + "_pack", lay)
    outer = lambda n, sh: k.tile(ctx, name + "_" + n, sh, F32)
    U = outer("u", [T, B * D])
    layer_norm(k, pack=(tile, dram, lay["_total"]), keep=U, rms_w=p("pre_w"))
    YR = outer("yr", [T, B * D])
    rows_dram = nc.dram_tensor(name + "_h", [2 * T - 1, D], F32).ap()
    with ExitStack() as mid:
        sb = lambda n, sh: k.tile(mid, name + "_" + n, sh, F32)
        XV, X2 = sb("xv", [T, B, D]), sb("x2", [T, B, D])
        poles = 16
        with ExitStack() as inner:
            ib = lambda n, sh: k.tile(inner, name + "_" + n, sh, F32)
            h, ex = ib("filter", [KP, 2, T]), ib("ex", [KP, 4, T])
            hT, zero = ib("hT", [T, D]), ib("zero", [T, D])
            with nc.Block(no_gpsimd_drain=True) as block:
                @block.vector
                def _(v):
                    ch = Chain(v, s["vec_step"])
                    v.memset(zero[:, :], 0.0).then_inc(s["p_d"].sem, 1)
                    ch.link(v.memset(h[:, :, :], 0.0))
                    with v.Fori(0, poles // 2) as i:
                        for r in range(4):
                            c, at = r % 2, r // 2 + 2 * i
                            v.wait_ge(*s["p_a"].at(4 * i + r + 1))
                            v.scalar_tensor_tensor(h[:, c, :], ex[:, r, :],
                                                   p("residues")[:, bass.ds(c * poles + at, 1)],
                                                   h[:, c, :], ALU.mult, ALU.add).then_inc(s["p_f"].sem, 1)
                            v.wait_ge(*s["p_f"].at(4 * i + r + 1))
                    v.tensor_tensor(h[:, :, T - 1:T], h[:, :, T - 1:T], p("skip").unsqueeze(2), ALU.add).then_inc(
                        s["p_b"].sem, 1)
                    ch.close()

                @block.scalar
                def _(act):
                    with act.Fori(0, poles // 2) as i:
                        for r in range(4):
                            c, at = r % 2, r // 2 + 2 * i
                            act.wait_ge(*s["p_f"].at(4 * i + r - 3))
                            act.activation(ex[:, r, :], p("times"), ACT.Exp,
                                           scale=p("poles")[:, bass.ds(c * poles + at, 1)]).then_inc(
                                               s["p_a"].sem, 1)
                    act.wait_ge(*s["p_c"].at(1))
                    act.activation(hT[:, :], k.ps[0:T, 0, 0:D], ACT.Copy).then_inc(s["p_d"].sem, 1)

                @block.tensor
                def _(pe):
                    pe.wait_ge(*s["p_b"].at(1))
                    for c in range(2):
                        last = pe.transpose(k.ps[0:T, 0, c * KP:(c + 1) * KP], h[:, c, :], k.ident[:, :])
                    last.then_inc(s["p_c"].sem, 1)

                @block.sync
                def _(sp):
                    sp.wait_ge(*s["p_d"].at(2))
                    sp.dma_start(rows_dram[T:2 * T - 1, :], zero[0:T - 1, :]).then_inc(s["p_e"].sem, 16)
                    sp.dma_start(rows_dram[0:T, :], hT[:, :]).then_inc(s["p_e"].sem, 16)
                    sp.wait_ge(*s["p_e"].at(32))
            k.advance(p_a=2 * poles, p_b=1, p_c=1, p_d=2, p_e=32, p_f=2 * poles)

        with ExitStack() as inner:
            ib = lambda n, sh: k.tile(inner, name + "_" + n, sh, F32)
            z = ib("z", [KP, 2, 6, GT])
            xv = ib("xvT", [KP, 2, 2, GT])
            w = chunks(p("in_proj"), 2)
            sw = p("short_w").rearrange("p (m j) -> p m j", j=3)
            prod, based, conv, ready, turned, moved = (s[n] for n in ("p_a", "p_b", "p_c", "p_d", "p_e", "p_f"))
            with nc.Block(no_gpsimd_drain=True) as block:
                @block.tensor
                def _(pe):
                    with pe.Fori(0, G // 2) as i:
                        for u in range(2):
                            g = 2 * i + u
                            for m in range(6):
                                pe.wait_ge(*conv.at(g * 6 + m - 5))
                                for kc in range(2):
                                    last = pe.matmul(k.ps[:, m, 0:GT], w[:, kc, m * KP:(m + 1) * KP],
                                                     k.XT[:, kc, bass.ds(g * GT, GT)], start=(kc == 0),
                                                     stop=(kc == 1))
                                last.then_inc(prod.sem, 1)
                        for u in range(2):
                            g = 2 * i + u
                            pe.wait_ge(*ready.at(g + 1))
                            for b in range(GB):
                                pe.wait_ge(*moved.at(2 * (g * GB + b - 1)))
                                for c in range(2):
                                    pe.transpose(k.ps[0:T, 6 + b % 2, c * KP:(c + 1) * KP],
                                                 xv[:, u, c, b * T:(b + 1) * T], k.ident[:, :])
                                for c in range(2):
                                    last = pe.transpose(k.ps[0:T, 6 + b % 2, D + c * KP:D + (c + 1) * KP],
                                                        z[:, u, c, b * T:(b + 1) * T], k.ident[:, :])
                                last.then_inc(turned.sem, 1)

                @block.scalar
                def _(act):
                    with act.Fori(0, G // 2) as i:
                        for u in range(2):
                            g = 2 * i + u
                            act.wait_ge(*turned.at((g - 1) * GB))
                            for m in range(6):
                                act.wait_ge(*prod.at(g * 6 + m + 1))
                                act.activation(z[:, u, m, :], k.ps[:, m, 0:GT], ACT.Identity,
                                               scale=sw[:, m, 2:3], bias=p("short_b")[:, m:m + 1]).then_inc(
                                                   based.sem, 1)
                        for u in range(2):
                            g = 2 * i + u
                            for b in range(GB):
                                act.wait_ge(*turned.at(g * GB + b + 1))
                                act.activation(XV[:, bass.ds(g * GB + b, 1), :],
                                               k.ps[0:T, 6 + b % 2, 0:D].unsqueeze(1), ACT.Copy)
                                act.activation(X2[:, bass.ds(g * GB + b, 1), :],
                                               k.ps[0:T, 6 + b % 2, D:2 * D].unsqueeze(1), ACT.Copy).then_inc(
                                                   moved.sem, 2)

                @block.vector
                def _(v):
                    ch = Chain(v, s["vec_step"])
                    with v.Fori(0, G // 2) as i:
                        ch.turn(i, 14)
                        for u in range(2):
                            g = 2 * i + u
                            for m in range(6):
                                v.wait_ge(*based.at(g * 6 + m + 1))
                                z3 = z[:, u, m, :].rearrange("p (b t) -> p b t", b=GB)
                                p3 = chunks(k.ps[:, m, 0:GT], GB)
                                ch.link(v.scalar_tensor_tensor(z3[:, :, 1:T], p3[:, :, 0:T - 1], sw[:, m, 1:2],
                                                               z3[:, :, 1:T], ALU.mult, ALU.add))
                                v.scalar_tensor_tensor(z3[:, :, 2:T], p3[:, :, 0:T - 2], sw[:, m, 0:1],
                                                       z3[:, :, 2:T], ALU.mult, ALU.add).then_inc(conv.sem, 1)
                            v.wait_ge(*conv.at(g * 6 + 6))
                            v.wait_ge(*turned.at((g - 1) * GB))
                            ch.link(v.tensor_tensor(xv[:, u, :, :], z[:, u, 2:4, :], z[:, u, 4:6, :], ALU.mult))
                            v.sem_inc(ready.sem, 1)
                        ch.end(G // 2)
                    ch.close()
            k.advance(p_a=6 * G, p_b=6 * G, p_c=6 * G, p_d=G, p_e=B, p_f=2 * B)

        with ExitStack() as inner:
            ib = lambda n, sh: k.tile(inner, name + "_" + n, sh, F32)
            TP = ib("toeplitz", [T, 2, T, TQ])
            xq = ib("xq", [T, 2, 32, TQ])
            ys = ib("ys", [KP, 2, GT])
            cut, prod, out, turned, done = (s[n] for n in ("p_a", "p_b", "p_c", "p_d", "p_e"))
            t_in = [s["toep_in0"], s["toep_in1"]]
            per = TQ // 16
            with nc.Block(no_gpsimd_drain=True) as block:
                @block.vector
                def _(v):
                    v.memset(xq[:, :, :, :], 0.0)

            with nc.Block(no_gpsimd_drain=True) as block:
                @block.sync
                def _(sp):
                    for q in range(NQ):
                        if q >= 2:
                            sp.wait_ge(*prod.at((q - 1) * per))
                        sp.dma_start(TP[:, q % 2, :, :],
                                     bass.AP(tensor=rows_dram.tensor, offset=q * TQ, ap=[[D, T], [D, T], [1, TQ]])).then_inc(t_in[q % 2].sem, 16)

                @block.tensor
                def _(pe):
                    def back(q, r):
                        n = q * per + r
                        pe.wait_ge(*out.at(n + 1))
                        pe.wait_ge(*done.at(n - 1))
                        for f in range(4):
                            last = pe.transpose(k.ps[0:T, 4 + r % 2, f * KP:(f + 1) * KP],
                                                ys[:, r % 2, f * T:(f + 1) * T], k.ident[:, :])
                        last.then_inc(turned.sem, 1)

                    with pe.Fori(0, NQ // 2) as i:
                        for u in range(2):
                            q = 2 * i + u
                            pe.wait_ge(*cut.at(q + 1))
                            pe.wait_ge(*t_in[u].at((i + 1) * 16))
                            for r in range(per):
                                pe.wait_ge(*out.at(q * per + r - 3))
                                for f in range(4):
                                    for j in range(4):
                                        d = r * 16 + f * 4 + j
                                        last = pe.matmul(k.ps[32 * j:32 * j + 32, r % 4, f * T:(f + 1) * T],
                                                         xq[:, u, :, d], TP[:, u, :, d], start=True, stop=True)
                                last.then_inc(prod.sem, 1)
                                if r >= 1:
                                    back(q, r - 1)
                            back(q, per - 1)

                @block.scalar
                def _(act):
                    with act.Fori(0, NQ // 2) as i:
                        for r in range(2 * per):
                            n = i * 2 * per + r
                            act.wait_ge(*prod.at(n + 1))
                            act.wait_ge(*turned.at(n - 1))
                            act.activation(ys[:, r % 2, :].rearrange("p (f t) -> p f t", f=4),
                                           backwards(chunks(k.ps[:, r % 4, 0:GT], 4)), ACT.Copy).then_inc(
                                               out.sem, 1)

                @block.vector
                def _(v):
                    with v.Fori(0, NQ // 2) as i:
                        for u in range(2):
                            q = 2 * i + u
                            v.wait_ge(*prod.at((q - 1) * per))
                            v.tensor_copy(xq[:, u, 0:B, :], XV[:, :, bass.ds(q * TQ, TQ)]).then_inc(cut.sem, 1)
                            for r in range(per):
                                n = q * per + r
                                v.wait_ge(*turned.at(n + 1))
                                y = X2[:, :, bass.ds(q * TQ + r * 16, 16)].rearrange("p b d -> p d b")
                                v.tensor_tensor(y, k.ps[0:T, 4 + r % 2, 0:512].rearrange("p (d b) -> p d b", b=32)
                                                [:, :, 0:B], y, ALU.mult).then_inc(done.sem, 1)
            nb = NQ * per
            k.advance(p_a=NQ, p_b=nb, p_c=nb, p_d=nb, p_e=nb, toep_in0=32, toep_in1=32)

        def gated(v, ch, b, dst):
            return v.tensor_copy(dst, X2[:, bass.ds(b, 1), :].rearrange("p b d -> p (b d)"))

        project_out(k, gated, chunks(p("out_proj"), 2), residual=U, out=YR)
    layer_norm(k, rms_w=p("post_w"), source=YR, plain=False)
    with nc.Block(no_gpsimd_drain=True) as block:
        @block.vector
        def _(v):
            v.tensor_tensor(k.X[:, :], k.X[:, :], YR[:, :], ALU.add)
    lay2, dram2 = packs[name + "_mlp"]
    feed_forward(k, name + "_mlp", dram2, lay2, 1, T, 6, True, ACT.Gelu_apprx_tanh)


def host_l1_attn(name, a):
    w = {key[len(name) + 1:]: v for key, v in a.items() if key.startswith(name + "_")}
    by_channel = lambda v: v.reshape(2, KP, -1).transpose(1, 0, 2).reshape(KP, -1)
    f = dict(pre_w=columns(w["pre_norm_w"]), post_w=columns(w["post_norm_w"]), in_proj=by_rows(w["in_proj_w"].T),
             short_w=w["short_w"].reshape(6, KP, 3).transpose(1, 0, 2).reshape(KP, 18),
             short_b=columns(w["short_b"]), poles=by_channel(w["log_poles"]), residues=by_channel(w["residues"]),
             skip=columns(w["D_skip"]), out_proj=by_rows(w["out_proj_w"].T),
             times=on_rows(np.arange(T, dtype=np.float32)[::-1]))
    both = np.concatenate([w["l1_w"], w["l2_w"]], axis=0).T
    done, lay = packed(dict(w1=by_rows(both), w2=by_rows(w["l3_w"].T, T)))
    return {name: packed(f), name + "_mlp": (done[None], lay)}


def sub_l2_attn(k, ctx, name, packs):
    nc, s = k.nc, k.signals
    lay, dram = packs[name]
    tile, p = pack_tile(k, ctx, name + "_pack", lay)
    sb = lambda n, sh: k.tile(ctx, name + "_" + n, sh, F32)
    U = sb("u", [T, B * D])
    layer_norm(k, pack=(tile, dram, lay["_total"]), keep=U)
    QT = sb("qT", [KP, 2, N])
    project_features(k, chunks(p("wq"), 2), 2, QT, bias=p("bq"))
    AT = sb("aT", [KP, 2, N])
    hd, HV = 16, 32
    xs = sb("xs", [KP, 2, 2, T])
    kv, sq, kn = (sb(n, [T, 2, 2 * D]) for n in ("kv", "sq", "kn"))
    mean, var, rstd = (sb(n, [T, 2, HV]) for n in ("mean", "var", "rstd"))
    km = sb("km", [KP, 2, 2, KP])
    wkv = chunks(p("wkv"), 2)
    copied, prod, cent, sqd, vard, roots, normed, mats, mixed, atts, added = (
        s[n] for n in ("p_a", "p_b", "p_c", "p_d", "p_e", "p_f", "p_g", "p_h", "p_i", "p_j", "p_k"))
    heads = lambda t: t.rearrange("p (h d) -> p h d", d=hd)
    with nc.Block(no_gpsimd_drain=True) as block:
        @block.gpsimd
        def _(g):
            x3 = k.X[:, :].rearrange("p (b d) -> p b d", b=B)
            g.tensor_tensor(k.X[:, :], k.X[:, :], U[:, :], ALU.add).then_inc(s["pool_step"].sem, 1)
            g.wait_ge(*s["pool_step"].at(1))
            g.tensor_tensor(x3, x3, p("p2_b")[0:T, :].unsqueeze(1).broadcast_to([T, B, D]), ALU.add)
            g.drain()

        @block.tensor
        def _(pe):
            with pe.Fori(0, B // 2) as i:
                for u in range(2):
                    b = 2 * i + u
                    pe.wait_ge(*copied.at(b + 1))
                    pe.wait_ge(*cent.at(b - 1))
                    for c in range(2):
                        last = pe.matmul(k.ps[0:T, u, 0:2 * D], xs[:, u, c, :], wkv[:, c, :], start=(c == 0),
                                         stop=(c == 1))
                    last.then_inc(prod.sem, 1)
                for u in range(2):
                    b = 2 * i + u
                    pe.wait_ge(*normed.at(b + 1))
                    pe.wait_ge(*mixed.at(b - 1))
                    for c in range(2):
                        last = pe.matmul(k.ps[:, 2 + u, c * KP:(c + 1) * KP], kn[:, u, c * KP:(c + 1) * KP],
                                         kn[:, u, D + c * KP:D + (c + 1) * KP], start=True, stop=True)
                    last.then_inc(mats.sem, 1)
                for u in range(2):
                    b = 2 * i + u
                    pe.wait_ge(*mixed.at(b + 1))
                    pe.wait_ge(*added.at(b - 1))
                    for c in range(2):
                        last = pe.matmul(k.ps[:, 4 + u, c * T:(c + 1) * T], km[:, u, c, :],
                                         QT[:, c, bass.ds(b * T, T)], start=True, stop=True)
                    last.then_inc(atts.sem, 1)

        @block.scalar
        def _(act):
            with act.Fori(0, B // 2) as i:
                for u in range(2):
                    b = 2 * i + u
                    act.wait_ge(*cent.at(b + 1))
                    act.activation(sq[:, u, :], kv[:, u, :], ACT.Square).then_inc(sqd.sem, 1)
                for u in range(2):
                    b = 2 * i + u
                    act.wait_ge(*vard.at(b + 1))
                    act.activation(rstd[:, u, :], var[:, u, :], ACT.Sqrt).then_inc(roots.sem, 1)

        @block.vector
        def _(v):
            ch = Chain(v, s["vec_step"])
            with v.Fori(0, B // 2) as i:
                ch.turn(i, 18)
                for u in range(2):
                    b = 2 * i + u
                    v.wait_ge(*prod.at(b - 1))
                    v.tensor_copy(xs[:, u, :, :], k.XT[:, :, bass.ds(b * T, T)]).then_inc(copied.sem, 1)
                for u in range(2):
                    b = 2 * i + u
                    v.wait_ge(*prod.at(b + 1))
                    ch.link(v.tensor_tensor(kv[:, u, :], k.ps[0:T, u, 0:2 * D], p("bkv")[0:T, :], ALU.add))
                    ch.link(v.tensor_reduce(mean[:, u, :], heads(kv[:, u, :]), AX.X, ALU.add))
                    ch.link(v.tensor_scalar(mean[:, u, :], mean[:, u, :], 1.0 / hd, None, ALU.mult))
                    v.tensor_tensor(heads(kv[:, u, :]), heads(kv[:, u, :]),
                                    mean[:, u, :].unsqueeze(2).broadcast_to([T, HV, hd]),
                                    ALU.subtract).then_inc(cent.sem, 1)
                for u in range(2):
                    b = 2 * i + u
                    v.wait_ge(*sqd.at(b + 1))
                    ch.link(v.tensor_reduce(var[:, u, :], heads(sq[:, u, :]), AX.X, ALU.add))
                    v.tensor_scalar(var[:, u, :], var[:, u, :], 1.0 / hd, LN_EPS, ALU.mult, ALU.add).then_inc(
                        vard.sem, 1)
                for u in range(2):
                    b = 2 * i + u
                    v.wait_ge(*roots.at(b + 1))
                    ch.link(v.reciprocal(rstd[:, u, :], rstd[:, u, :]))
                    v.wait_ge(*mats.at(b - 1))
                    ch.link(v.tensor_tensor(heads(kv[:, u, :]), heads(kv[:, u, :]),
                                            rstd[:, u, :].unsqueeze(2).broadcast_to([T, HV, hd]), ALU.mult))
                    ch.link(v.tensor_tensor(kv[:, u, :], kv[:, u, :], p("gamma")[0:T, :], ALU.mult))
                    v.tensor_tensor(kn[:, u, :], kv[:, u, :], p("beta")[0:T, :], ALU.add).then_inc(normed.sem, 1)
                for u in range(2):
                    b = 2 * i + u
                    v.wait_ge(*mats.at(b + 1))
                    v.wait_ge(*atts.at(b - 1))
                    ch.link(v.scalar_tensor_tensor(km[:, u, :, :], chunks(k.ps[:, 2 + u, 0:2 * KP], 2), 1.0 / T,
                                                   chunks(p("temp"), 2), ALU.mult, ALU.mult))
                    v.tensor_tensor(km[:, u, :, :], km[:, u, :, :], chunks(p("bias"), 2), ALU.add).then_inc(
                        mixed.sem, 1)
                for u in range(2):
                    b = 2 * i + u
                    v.wait_ge(*atts.at(b + 1))
                    ch.link(v.tensor_tensor(AT[:, :, bass.ds(b * T, T)], chunks(k.ps[:, 4 + u, 0:2 * T], 2),
                                            k.XT[:, :, bass.ds(b * T, T)], ALU.add))
                    v.sem_inc(added.sem, 1)
                ch.end(B // 2)
            ch.close()
    k.advance(pool_step=1, p_a=B, p_b=B, p_c=B, p_d=B, p_e=B, p_f=B, p_g=B, p_h=B, p_i=B, p_j=B, p_k=B)
    lay2, dram2 = packs[name + "_mlp"]
    feed_forward(k, name + "_mlp", dram2, lay2, 1, KP, 2, False, ACT.Gelu, src=AT)


def on_diagonal(blocks, rows=16):
    out = np.zeros((KP, 2, KP), np.float32)
    for h in range(16):
        c, at = h // 8, (h % 8) * rows
        out[at:at + rows, c, at:at + rows] = blocks[h]
    return out.reshape(KP, -1)


def host_l2_attn(name, a):
    w = {key[len(name) + 1:]: v for key, v in a.items() if key.startswith(name + "_")}
    wt = w["qkv_w"].T
    each = lambda kk, vv: on_rows(np.concatenate([np.tile(kk, 16), np.tile(vv, 16)]))
    f = dict(wq=by_rows(wt[:, :D]), wkv=by_rows(wt[:, D:]), bq=columns(w["qkv_b"][:D]),
             bkv=on_rows(w["qkv_b"][D:]), gamma=each(w["kn_g"], w["vn_g"]), beta=each(w["kn_b"], w["vn_b"]),
             temp=on_diagonal(np.broadcast_to(w["temperature"], (16, 16, 16))), bias=on_diagonal(w["attn_bias"]),
             p2_b=on_rows(w["p2_b"]))
    done, lay = packed(dict(w1=by_rows(w["p1_w"].T), w2=by_rows(w["p2_w"].T), b1=columns(w["p1_b"])))
    return {name: packed(f), name + "_mlp": (done[None], lay)}



def build_program(nc, aps, layouts, layers):
    with ExitStack() as ctx:
        k = Core(nc, ctx)
        packs = {name: (lay, aps["in_" + name]) for name, lay in layouts.items()}
        k.aps = aps
        with nc.Block(no_gpsimd_drain=True) as block:
            names = list(SIGNALS)

            def raise_all(eng, part):
                for name in names[part::4]:
                    eng.sem_inc(k[name].sem, HEAD)

            @block.vector
            def _(v):
                raise_all(v, 0)

            @block.scalar
            def _(act):
                raise_all(act, 1)

            @block.tensor
            def _(pe):
                raise_all(pe, 2)

            @block.sync
            def _(sp):
                raise_all(sp, 3)

        with nc.Block(no_gpsimd_drain=True) as block:
            @block.sync
            def _(sp):
                sp.dma_start(k.X[:, :].rearrange("t (b d) -> t b d", b=B),
                             aps["in_x"].rearrange("b t d -> t b d")).then_inc(k["x_in"].sem, 16)
                sp.wait_ge(*k["x_in"].at(16))

            @block.gpsimd
            def _(g):
                g.memset(k.ident[:, :], 0.0).then_inc(k["pool_step"].sem, 1)
                g.wait_ge(*k["pool_step"].at(1))
                g.affine_select(out=k.ident[:, :], in_=k.ident[:, :], compare_op=ALU.not_equal, fill=1.0, base=0,
                                pattern=[[-1, KP]], channel_multiplier=1).then_inc(k["pool_step"].sem, 1)
                g.wait_ge(*k["pool_step"].at(2))
        k.advance(pool_step=2, x_in=16)

        for name in layers:
            with ExitStack() as layer:
                if name in FFN:
                    sub_ffn(k, layer, name, packs, FFN[name])
                elif name in ATTENTION:
                    sub_attention(k, layer, name, packs, ATTENTION[name])
                else:
                    SUB[name](k, layer, name, packs)

        with nc.Block(no_gpsimd_drain=True) as block:
            @block.sync
            def _(sp):
                sp.dma_start(aps["out"].rearrange("b t d -> t b d"),
                             k.X[:, :].rearrange("t (b d) -> t b d", b=B)).then_inc(k["x_out"].sem, 16)
                sp.wait_ge(*k["x_out"].at(16))



def by_rows(w, rows=KP):
    return w.reshape(-1, rows, w.shape[1]).transpose(1, 0, 2).reshape(rows, -1)


def columns(v, rows=KP):
    return v.reshape(-1, rows).T


def on_rows(v, parts=KP):
    return np.broadcast_to(v.reshape(1, -1), (parts, v.size))


def packed(fields):
    total = sum(a.shape[1] for a in fields.values())
    out, lay, off = np.zeros((KP, total), np.float32), {}, 0
    for name, a in fields.items():
        out[:a.shape[0], off:off + a.shape[1]] = a
        lay[name] = (off, a.shape[0], a.shape[1])
        off += a.shape[1]
    lay["_total"] = total
    return out, lay


def host_ffn(name, a):
    w = {key[len(name) + 1:]: v for key, v in a.items() if key.startswith(name + "_")}
    if name == "L0_ffn":
        small = dict(router=by_rows(w["router_w"]), b2=w["b2"][None])
        experts = [dict(w1=by_rows(w["w1"]), w2=by_rows(w["w2"]), b1=columns(w["b1"]))]
    elif name == "L1_ffn":
        small = dict(router=by_rows(w["Wr"]), router_b=w["br"][:, None], b2=w["b2"])
        experts = [dict(w1=by_rows(w["W1"][e]), w2=by_rows(w["W2"][e]), b1=columns(w["b1"][e])) for e in range(8)]
    elif name == "L2_ffn":
        small = dict(router=by_rows(w["w_gate"].T), b2=w["b2"])
        experts = [dict(w1=by_rows(w["W1"][e]), w2=by_rows(w["W2"][e]), b1=columns(w["b1"][e])) for e in range(8)]
    else:
        small = dict(b2=w["b2"][:4])
        experts = [dict(w1=by_rows(w["W1"][e]), w2=by_rows(w["W2"][e]), b1=columns(w["b1"][e])) for e in range(4)]
    done = [packed(e) for e in experts]
    return {name: packed(small), name + "_experts": (np.stack([d[0] for d in done]), done[0][1])}


def lay_out(inputs, layers):
    a = {n: np.asarray(v) for n, v in inputs.items()}
    out = {}
    for name in layers:
        host = host_ffn if name in FFN else host_attention if name in ATTENTION else HOST[name]
        out.update(host(name, a))
    return out


def kernel(**inputs):
    import concourse.bacc as bacc
    from concourse.bass_utils import run_bass_kernel_spmd

    laid = lay_out(inputs, LAYERS)
    arrays = {"in_" + n: np.ascontiguousarray(v[0]) for n, v in laid.items()}
    arrays["in_x"] = np.ascontiguousarray(inputs["x"])
    if "ctx_768" in inputs:
        arrays.update(host_context(inputs))
    nc = bacc.Bacc("TRN2", target_bir_lowering=False, num_devices=1)
    aps = {n: nc.dram_tensor(n, v.shape, mybir.dt.from_np(v.dtype), kind="ExternalInput").ap()
           for n, v in arrays.items()}
    aps["out"] = nc.dram_tensor("out", (B, T, D), F32, kind="ExternalOutput").ap()
    build_program(nc, aps, {n: v[1] for n, v in laid.items()}, LAYERS)
    r = run_bass_kernel_spmd(nc, [arrays], core_ids=[0])
    return r.results[0]["out"]


def host_context(inputs):
    c = np.asarray(inputs["ctx_768"]).transpose(0, 2, 1).reshape(B, 2, CR, S2).transpose(0, 2, 1, 3)
    m = np.asarray(inputs["mask_BxS2_bf1"]).view(np.uint8)
    return {"in_ctx": np.ascontiguousarray(c), "in_mask": np.ascontiguousarray(m)}

SUB = {"L3_xattn": sub_l3_xattn, "L0_attn": sub_l0_attn, "L1_attn": sub_l1_attn, "L2_attn": sub_l2_attn}
HOST = {"L3_xattn": host_l3_xattn, "L0_attn": host_l0_attn, "L1_attn": host_l1_attn, "L2_attn": host_l2_attn}
LAYERS = ["L0_attn", "L0_xattn", "L0_ffn", "L1_attn", "L1_xattn", "L1_ffn", "L2_attn", "L2_xattn", "L2_ffn",
          "L3_attn", "L3_xattn", "L3_ffn"]
```

```python
from contextlib import ExitStack

import numpy as np
import concourse.bass as bass
from concourse import mybir

F32 = mybir.dt.float32
U8 = mybir.dt.uint8
ACT = mybir.ActivationFunctionType
ALU = mybir.AluOpType
AX = mybir.AxisListType

T, B, D = 112, 16, 256
N = T * B
S2, CD = 375, 192
GB = 4
G = B // GB
GT = GB * T
KP = 128
KW, KN = 125, 3
CR = CD // 2
LN_EPS = 1e-5
RMS_EPS = 1e-6
HEAD = 64
CLAMP = 10000.0
FMAX = float(np.finfo(np.float32).max)


class Signal:

    def __init__(self, sem, base=HEAD):
        self.sem, self.base = sem, base

    def at(self, n):
        return self.sem, self.base + n

    def advance(self, n):
        self.base += n


class Chain:

    def __init__(self, eng, signal):
        self.eng, self.counter, self.n, self.start = eng, signal, 0, 0

    def link(self, ins):
        ins.then_inc(self.counter.sem, 1)
        self.n += 1
        self.eng.wait_ge(*self.counter.at(self.start + self.n))

    def mark(self, ins):
        ins.then_inc(self.counter.sem, 1)
        self.n += 1

    def turn(self, i, per):
        self.per, self.done = per, self.start + self.n
        self.start = self.done + i * per
        self.n = 0

    def end(self, trips):
        assert self.n == self.per, f"links a turn: {self.n}, stated: {self.per}"
        self.start, self.n = self.done + trips * self.per, 0

    def close(self):
        self.counter.advance(self.start + self.n)


class Core:

    def __init__(self, nc, ctx):
        self.nc, self.signals, self.tiles = nc, {}, 0
        self.X = ctx.enter_context(nc.sbuf_tensor("X", [T, B * D], F32))
        self.XT = ctx.enter_context(nc.sbuf_tensor("XT", [KP, 2, N], F32))
        self.ident = ctx.enter_context(nc.sbuf_tensor("ident", [KP, KP], F32))
        self.ps = ctx.enter_context(nc.psum_tensor("ps", [KP, 8, 512], F32))
        self.spark, self.sparks = ctx.enter_context(nc.sbuf_tensor("spark", [1, 64], F32)), 0
        for name in SIGNALS:
            self.signals[name] = Signal(ctx.enter_context(nc.semaphore(name)))
        for name in FROM_ZERO:
            self.signals[name] = Signal(ctx.enter_context(nc.semaphore(name)), 0)

    def tile(self, ctx, name, shape, dtype=F32):
        self.tiles += 1
        return ctx.enter_context(self.nc.sbuf_tensor(f"{name}_{self.tiles}", shape, dtype))

    def __getitem__(self, name):
        return self.signals[name]

    def advance(self, **events):
        for name, n in events.items():
            self.signals[name].advance(n)

    def table(self, act, fn):
        self.sparks += 1
        act.activation(self.spark[0:1, self.sparks:self.sparks + 1], self.spark[0:1, 0:1], fn)

    def x(self, b):
        return self.X[:, bass.ds(b * D, D)]


SIGNALS = ["vec_step", "act_step", "pool_step",
           "pack_in", "const_in", "ctx_in0", "ctx_in1", "exp_in0", "exp_in1", "toep_in0", "toep_in1",
           "x_in", "x_out", "stats_done", "rstd_done", "norm_done", "norm_tr", "norm_ev",
           "up_mm", "up_act", "up_used", "down_mm", "down_added",
           "lin_mm", "lin_act", "lin_vec",
           "rt_mm", "rt_ev", "rt_tr", "rt_lg", "gate_v", "gate_a", "gs_copied", "gt_tr", "gt_ev", "gb_mm", "gb_added",
           "rows_zeroed", "rg_const", "rg_chosen", "rg_counted", "rg_placed", "rg_in0", "rg_in1", "rg_out0",
           "rg_out1", "rg_turned", "rg_xT", "rg_up", "rg_hs", "rg_ut", "rg_first", "rg_hT", "rg_down", "rg_y",
           "rg_added",
           "v_padded", "ones_row", "kt_mm", "kt_ev", "v_mm", "v_ev", "qm_done", "ctx_used", "xs_copied",
           "sc_mm", "sc_read", "max_done", "exp_done", "prob_done", "pt_mm", "pt_ev_a", "pt_ev_v",
           "pv_mm", "ot_ev", "wo_mm", "res_done", "mask_done",
           "p_a", "p_b", "p_c", "p_d", "p_e", "p_f", "p_g", "p_h", "p_i", "p_j", "p_k", "p_l"]


FROM_ZERO = ["rg_put", "rg_got0", "rg_got1", "rg_got2", "rg_got3"]


def pack_tile(k, ctx, name, layout):
    total = layout["_total"]
    tile = k.tile(ctx, name, [KP, total], F32)

    def view(field, parts=None):
        off, p, cols = layout[field]
        return tile[0:(parts or p), off:off + cols]

    return tile, view


def chunks(ap, n):
    return ap.rearrange("p (k n) -> p k n", k=n)


def layer_norm(k, pack=None, keep=None, rms_w=None, source=None, plain=True, ahead=None):
    nc = k.nc
    src = source if source is not None else k.X
    with ExitStack() as ctx:
        sb = lambda n, s: k.tile(ctx, n, s, F32)
        st = sb("ln_st", [T, B * 6])
        mv = sb("ln_mv", [T, B * 2])
        rstd = sb("ln_rstd", [T, B])
        both = sb("ln_both", [T, B])
        tmp = sb("ln_tmp", [T, B])
        half = sb("ln_half", [T, B])
        xn = sb("ln_xn", [T, 2, D])
        mv3 = mv[:, :].rearrange("p (b s) -> p b s", s=2)
        two_pows = plain and rms_w is not None
        stats, rdone, ndone, ntr, nev = (k[s] for s in ("stats_done", "rstd_done", "norm_done", "norm_tr",
                                                        "norm_ev"))
        with nc.Block(no_gpsimd_drain=True) as block:
            @block.sync
            def _(sp):
                if pack is not None:
                    tile, dram, total = pack
                    h = total // 2
                    sp.dma_start(tile[:, 0:h], dram[:, 0:h]).then_inc(k["pack_in"].sem, 16)
                    sp.dma_start(tile[:, h:total], dram[:, h:total]).then_inc(k["pack_in"].sem, 16)
                    if ahead is not None:
                        ahead(sp)
                    sp.wait_ge(*k["pack_in"].at(32))

            @block.vector
            def _(v):
                ch = Chain(v, k["vec_step"])
                with v.Fori(0, B // 4) as i:
                    ch.turn(0, 0)
                    for j in range(4):
                        last = v.bn_stats(st[:, bass.ds((4 * i + j) * 6, 6)], src[:, bass.ds((4 * i + j) * D, D)])
                    ch.end(4)
                ch.link(v.memset(half[:, :], -0.5))
                for b in range(B):
                    last = v.bn_aggr(mv[:, 2 * b:2 * b + 2], st[:, 6 * b:6 * b + 6])
                ch.link(last)
                if plain:
                    v.tensor_scalar(tmp[:, :], mv3[:, :, 1], LN_EPS, None, ALU.add).then_inc(stats.sem, 1)
                    if two_pows:
                        v.wait_ge(*rdone.at(1))
                        ch.link(v.tensor_tensor(both[:, :], rstd[:, :], rstd[:, :], ALU.mult))
                        ch.link(v.tensor_tensor(both[:, :], both[:, :], mv3[:, :, 1], ALU.mult))
                        v.tensor_scalar(tmp[:, :], both[:, :], RMS_EPS, None, ALU.add).then_inc(stats.sem, 1)
                        v.wait_ge(*rdone.at(2))
                        ch.link(v.tensor_tensor(both[:, :], both[:, :], rstd[:, :], ALU.mult))
                    else:
                        v.wait_ge(*rdone.at(1))
                else:
                    ch.link(v.tensor_tensor(both[:, :], mv3[:, :, 0], mv3[:, :, 0], ALU.mult))
                    ch.link(v.tensor_tensor(both[:, :], both[:, :], mv3[:, :, 1], ALU.add))
                    v.tensor_scalar(tmp[:, :], both[:, :], RMS_EPS, None, ALU.add).then_inc(stats.sem, 1)
                    v.wait_ge(*rdone.at(1))
                scale = both if two_pows else rstd
                with v.Fori(0, B // 2) as i:
                    for u in range(2):
                        v.wait_ge(*ntr.at(2 * i + u - 1))
                        xin = src[:, bass.ds((2 * i + u) * D, D)]
                        if plain:
                            v.tensor_scalar(xn[:, u, :], xin, mv[:, bass.ds(2 * (2 * i + u), 1)],
                                            scale[:, bass.ds(2 * i + u, 1)], ALU.subtract,
                                            ALU.mult).then_inc(ndone.sem, 1)
                            if keep is not None:
                                v.tensor_scalar(keep[:, bass.ds((2 * i + u) * D, D)], xin,
                                                mv[:, bass.ds(2 * (2 * i + u), 1)],
                                                rstd[:, bass.ds(2 * i + u, 1)], ALU.subtract, ALU.mult)
                        else:
                            v.tensor_scalar(xn[:, u, :], xin, scale[:, bass.ds(2 * i + u, 1)], None,
                                            ALU.mult).then_inc(ndone.sem, 1)
                ch.close()

            @block.gpsimd
            def _(g):
                g.wait_ge(*stats.at(1))
                g.tensor_tensor(rstd[:, :], tmp[:, :], half[:, :], ALU.pow).then_inc(rdone.sem, 1)
                if two_pows:
                    g.wait_ge(*stats.at(2))
                    g.tensor_tensor(both[:, :], tmp[:, :], half[:, :], ALU.pow).then_inc(rdone.sem, 1)

            @block.tensor
            def _(pe):
                with pe.Fori(0, B // 2) as i:
                    for u in range(2):
                        pe.wait_ge(*ndone.at(2 * i + u + 1))
                        pe.wait_ge(*nev.at(2 * i + u - 1))
                        for c in range(2):
                            last = pe.transpose(k.ps[0:KP, u, c * T:(c + 1) * T], xn[:, u, c * KP:(c + 1) * KP],
                                                k.ident[0:T, 0:T])
                        last.then_inc(ntr.sem, 1)

            @block.scalar
            def _(act):
                if rms_w is not None and pack is not None:
                    act.wait_ge(*k["pack_in"].at(32))
                k.table(act, ACT.Copy)
                with act.Fori(0, B // 2) as i:
                    for u in range(2):
                        act.wait_ge(*ntr.at(2 * i + u + 1))
                        if rms_w is None:
                            last = act.activation(k.XT[:, :, bass.ds((2 * i + u) * T, T)],
                                                  chunks(k.ps[0:KP, u, 0:2 * T], 2), ACT.Copy)
                        else:
                            for c in range(2):
                                last = act.activation(k.XT[:, c, bass.ds((2 * i + u) * T, T)],
                                                      k.ps[0:KP, u, c * T:(c + 1) * T], ACT.Copy,
                                                      scale=rms_w[:, c:c + 1])
                        last.then_inc(nev.sem, 1)
        k.advance(pack_in=32 if pack is not None else 0, stats_done=2 if two_pows else 1,
                  rstd_done=2 if two_pows else 1, norm_done=B, norm_tr=B, norm_ev=B)


def feed_forward(k, name, dram, layout, experts, rows, hidden, gated, act_fn, gates=None, src=None):
    nc = k.nc
    src = k.XT if src is None else src
    ring = min(hidden, 4)
    up, used, down, added = k["up_mm"], k["up_used"], k["down_mm"], k["down_added"]
    acted = k["up_act"]
    w_in = [k["exp_in0"], k["exp_in1"]]
    pairs = max(experts // 2, 1)
    per_pair = min(experts, 2)
    with ExitStack() as ctx:
        total = layout["_total"]
        slots = [k.tile(ctx, f"{name}_w{e}", [KP, total], F32) for e in range(per_pair)]
        hT = k.tile(ctx, f"{name}_h", [rows, 2, hidden, GT], F32)
        if gated:
            first = k.tile(ctx, f"{name}_a", [rows, 2, GT], F32)

        def part(slot, field):
            off, p, cols = layout[field]
            return slots[slot][0:p, off:off + cols]

        w1 = [chunks(part(s, "w1"), 2) for s in range(per_pair)]
        w2 = [chunks(part(s, "w2"), hidden) for s in range(per_pair)]
        b1 = [part(s, "b1") for s in range(per_pair)] if "b1" in layout else None

        def steps(eng):
            if pairs == 1:
                for ep in range(per_pair):
                    with eng.Fori(0, G // 2) as g0:
                        for gu in range(2):
                            yield 2 * g0 + gu + ep * G, ep, gu, ep, 2 * g0 + gu
            else:
                with eng.Fori(0, pairs) as ei:
                    for ep in range(per_pair):
                        with eng.Fori(0, G // 2) as g0:
                            for gu in range(2):
                                yield (ei * 2 + ep) * G + 2 * g0 + gu, ep, gu, ei * 2 + ep, 2 * g0 + gu

        with nc.Block(no_gpsimd_drain=True) as block:
            @block.sync
            def _(sp):
                if pairs == 1:
                    for ep in range(per_pair):
                        sp.dma_start(slots[ep][:, :], dram[ep, :, :]).then_inc(w_in[ep].sem, 16)
                else:
                    with sp.Fori(0, pairs) as ei:
                        for ep in range(2):
                            sp.wait_ge(*down.at((ei * 2 + ep - 1) * G))
                            sp.dma_start(slots[ep][:, :], dram[bass.ds(ei * 2 + ep, 1), :, :].rearrange(
                                "e p n -> (e p) n")).then_inc(w_in[ep].sem, 16)

            @block.tensor
            def _(pe):
                for t, s, h, e, g in steps(pe):
                    turn = e // 2 if isinstance(e, int) else None
                    pe.wait_ge(*w_in[s].at(16 * (e // 2 + 1) if turn is not None else 8 * (e - s) + 16))
                    for m in range(hidden):
                        if gated:
                            pe.wait_ge(*used.at(t * hidden + m - 1))
                        else:
                            pe.wait_ge(*acted.at(t * hidden + m - ring + 1))
                        for half in range(2 if gated else 1):
                            bank = 2 * (m % 2) + half if gated else m % ring
                            col = (half * hidden + m) * rows
                            for c in range(2):
                                last = pe.matmul(k.ps[0:rows, bank, 0:GT], w1[s][:, c, col:col + rows],
                                                 src[:, c, bass.ds(g * GT, GT)], start=(c == 0), stop=(c == 1))
                        last.then_inc(up.sem, 1)
                    for m in range(hidden):
                        if gated:
                            pe.wait_ge(*used.at(t * hidden + m + 1))
                        else:
                            pe.wait_ge(*acted.at(t * hidden + m + 1))
                        for j in range(GB):
                            if m == 0:
                                pe.wait_ge(*added.at((t - 1) * GB + j + 1))
                            last = pe.matmul(k.ps[0:T, 4 + j, 0:D], hT[:, h, m, j * T:(j + 1) * T], w2[s][:, m, :],
                                             start=(m == 0), stop=(m == hidden - 1))
                    last.then_inc(down.sem, 1)

            @block.scalar
            def _(act):
                for t, s, h, e, g in steps(act):
                    if gated:
                        for m in range(hidden):
                            act.wait_ge(*up.at(t * hidden + m + 1))
                            act.wait_ge(*used.at(t * hidden + m - 1))
                            act.activation(first[:, m % 2, :], k.ps[0:rows, 2 * (m % 2), 0:GT], act_fn,
                                           bias=b1[s][:, m:m + 1] if b1 else 0.0).then_inc(acted.sem, 1)
                    else:
                        act.wait_ge(*down.at(t - 1))
                        for m in range(hidden):
                            act.wait_ge(*up.at(t * hidden + m + 1))
                            act.activation(hT[:, h, m, :], k.ps[0:rows, m % ring, 0:GT], act_fn,
                                           bias=b1[s][:, m:m + 1] if b1 else 0.0).then_inc(acted.sem, 1)

            @block.vector
            def _(v):
                for t, s, h, e, g in steps(v):
                    if gated:
                        v.wait_ge(*down.at(t - 1))
                        for m in range(hidden):
                            v.wait_ge(*acted.at(t * hidden + m + 1))
                            second = k.ps[0:rows, 2 * (m % 2) + 1, 0:GT]
                            if b1:
                                v.scalar_tensor_tensor(hT[:, h, m, :], second, b1[s][:, hidden + m:hidden + m + 1],
                                                       first[:, m % 2, :], ALU.add, ALU.mult).then_inc(used.sem, 1)
                            else:
                                v.tensor_tensor(hT[:, h, m, :], second, first[:, m % 2, :],
                                                ALU.mult).then_inc(used.sem, 1)
                    v.wait_ge(*down.at(t + 1))
                    for j in range(GB):
                        b = g * GB + j
                        if gates is None:
                            v.tensor_tensor(k.x(b), k.ps[0:T, 4 + j, 0:D], k.x(b), ALU.add).then_inc(added.sem, 1)
                        else:
                            v.scalar_tensor_tensor(k.x(b), k.ps[0:T, 4 + j, 0:D],
                                                   gates[:, bass.ds(e * B + b, 1)], k.x(b), ALU.mult,
                                                   ALU.add).then_inc(added.sem, 1)
        n = experts * G
        k.advance(up_mm=n * hidden, up_act=n * hidden, up_used=n * hidden if gated else 0, down_mm=n,
                  down_added=n * GB, exp_in0=16 * ((experts + 1) // 2), exp_in1=16 * (experts // 2))


def router(k, E, w, bias, gates, mode):
    nc = k.nc
    with ExitStack() as ctx:
        sb = lambda n, s: k.tile(ctx, n, s, F32)
        lt = sb("rt_lt", [E, 2, GT])
        lg = sb("rt_lg_t", [T, B, E])
        ahead = sb("rt_ahead", [T, B, E])
        cmp = sb("rt_cmp", [T, B, E])
        ex = sb("rt_ex", [T, B, E])
        one = sb("rt_one", [T, B])
        inv = sb("rt_inv", [T, B])
        mm, ev, tr, lgd = k["rt_mm"], k["rt_ev"], k["rt_tr"], k["rt_lg"]
        gv, ga = k["gate_v"], k["gate_a"]
        n_g = 1 if mode == "topk_sum" else E
        g3 = gates[:, :].rearrange("p (e b) -> p b e", b=B)
        with nc.Block(no_gpsimd_drain=True) as block:
            @block.tensor
            def _(pe):
                for g in range(G):
                    u = g % 2
                    pe.wait_ge(*ev.at(g - 1))
                    for c in range(2):
                        last = pe.matmul(k.ps[0:E, u, 0:GT], w[:, c, :], k.XT[:, c, g * GT:(g + 1) * GT],
                                         start=(c == 0), stop=(c == 1))
                    last.then_inc(mm.sem, 1)
                    pe.wait_ge(*ev.at(g + 1))
                    pe.wait_ge(*lgd.at(g - 1))
                    for j in range(GB):
                        last = pe.transpose(k.ps[0:T, 2 + u, j * E:(j + 1) * E], lt[:, u, j * T:(j + 1) * T],
                                            k.ident[0:E, 0:E])
                    last.then_inc(tr.sem, 1)

            @block.scalar
            def _(act):
                k.table(act, ACT.Identity)
                with act.Fori(0, G // 2) as i:
                    for u in range(2):
                        act.wait_ge(*mm.at(2 * i + u + 1))
                        act.wait_ge(*tr.at(2 * i + u - 1))
                        act.activation(lt[:, u, :], k.ps[0:E, u, 0:GT], ACT.Identity,
                                       bias=bias if bias is not None else 0.0).then_inc(ev.sem, 1)
                act.wait_ge(*gv.at(1))
                act.activation(ex[:, :, :], ex[:, :, :], ACT.Exp).then_inc(ga.sem, 1)

            @block.vector
            def _(v):
                ch = Chain(v, k["vec_step"])
                with v.Fori(0, G // 2) as i:
                    for u in range(2):
                        v.wait_ge(*tr.at(2 * i + u + 1))
                        v.tensor_copy(lg[:, bass.ds((2 * i + u) * GB, GB), :],
                                      chunks(k.ps[0:T, 2 + u, 0:GB * E], GB)).then_inc(lgd.sem, 1)
                v.wait_ge(*lgd.at(G))
                ch.link(v.memset(ahead[:, :, :], 0.0))
                for e in range(E):
                    other = lg[:, :, e:e + 1]
                    if e + 1 < E:
                        v.tensor_tensor(cmp[:, :, e + 1:E], other.broadcast_to([T, B, E - e - 1]),
                                        lg[:, :, e + 1:E], ALU.is_ge)
                    ch.link(v.tensor_tensor(cmp[:, :, 0:e + 1], other.broadcast_to([T, B, e + 1]),
                                            lg[:, :, 0:e + 1], ALU.is_gt))
                    ch.link(v.tensor_tensor(ahead[:, :, :], ahead[:, :, :], cmp[:, :, :], ALU.add))
                ch.link(v.tensor_scalar(ahead[:, :, :], ahead[:, :, :], 2.0, None, ALU.is_lt))
                ch.link(v.tensor_reduce(one[:, :], lg[:, :, :], AX.X, ALU.max))
                v.tensor_tensor(ex[:, :, :], lg[:, :, :], one[:, :].unsqueeze(2).broadcast_to([T, B, E]),
                                ALU.subtract).then_inc(gv.sem, 1)
                v.wait_ge(*ga.at(1))
                if mode in ("topk_sum", "topk_softmax"):
                    ch.link(v.tensor_reduce(one[:, :], ex[:, :, :], AX.X, ALU.add))
                    ch.link(v.reciprocal(inv[:, :], one[:, :]))
                    ch.link(v.tensor_tensor(ex[:, :, :], ex[:, :, :],
                                            inv[:, :].unsqueeze(2).broadcast_to([T, B, E]), ALU.mult))
                if mode == "topk_softmax":
                    ch.link(v.tensor_tensor(g3, ex[:, :, :], ahead[:, :, :], ALU.mult))
                else:
                    ch.link(v.tensor_tensor(ex[:, :, :], ex[:, :, :], ahead[:, :, :], ALU.mult))
                    ch.link(v.tensor_reduce(one[:, :], ex[:, :, :], AX.X, ALU.add))
                    ch.link(v.reciprocal(inv[:, :], one[:, :]))
                    if mode == "softmax_topk":
                        ch.link(v.tensor_tensor(g3, ex[:, :, :], inv[:, :].unsqueeze(2).broadcast_to([T, B, E]),
                                                ALU.mult))
                    else:
                        ch.link(v.tensor_tensor(ex[:, :, :], ex[:, :, :],
                                                inv[:, :].unsqueeze(2).broadcast_to([T, B, E]), ALU.mult))
                        ch.link(v.tensor_reduce(gates[:, :], ex[:, :, :], AX.X, ALU.add))
                ch.close()
        k.advance(rt_mm=G, rt_ev=G, rt_tr=G, rt_lg=G, gate_v=1, gate_a=1)


def add_second_biases(k, gates, n_g, b2, meanwhile=None):
    g3 = gates[:, :].rearrange("p (e b) -> p b e", b=B)
    with ExitStack() as ctx:
        gs = k.tile(ctx, "gates_in_order", [T, B, n_g], F32)
        gT = k.tile(ctx, "gates_turned", [n_g, B, T], F32)
        with k.nc.Block(no_gpsimd_drain=True) as block:
            if meanwhile is not None:
                block.gpsimd(meanwhile)

            @block.tensor
            def _(pe):
                pe.wait_ge(*k["gs_copied"].at(1))
                for q in range(B // 4):
                    for j in range(4):
                        last = pe.transpose(k.ps[0:n_g, q, j * T:(j + 1) * T], gs[:, 4 * q + j, :],
                                            k.ident[0:T, 0:T])
                    last.then_inc(k["gt_tr"].sem, 1)
                for b in range(0, B, 2):
                    pe.wait_ge(*k["gt_ev"].at(b // 4 + 1))
                    pe.wait_ge(*k["gb_added"].at(b // 2 - 1))
                    for j in range(2):
                        last = pe.matmul(k.ps[0:T, 4 + b // 2 % 2, j * D:(j + 1) * D], gT[:, b + j, :], b2,
                                         start=True, stop=True)
                    last.then_inc(k["gb_mm"].sem, 1)

            @block.scalar
            def _(act):
                for q in range(B // 4):
                    act.wait_ge(*k["gt_tr"].at(q + 1))
                    act.activation(gT[:, 4 * q:4 * q + 4, :], chunks(k.ps[0:n_g, q, 0:4 * T], 4),
                                   ACT.Copy).then_inc(k["gt_ev"].sem, 1)

            @block.vector
            def _(v):
                v.tensor_copy(gs[:, :, :], g3).then_inc(k["gs_copied"].sem, 1)
                for b in range(0, B, 2):
                    v.wait_ge(*k["gb_mm"].at(b // 2 + 1))
                    v.tensor_tensor(k.X[:, b * D:(b + 2) * D], k.ps[0:T, 4 + b // 2 % 2, 0:2 * D],
                                    k.X[:, b * D:(b + 2) * D], ALU.add).then_inc(k["gb_added"].sem, 1)
        k.advance(gs_copied=1, gt_tr=B // 4, gt_ev=B // 4, gb_mm=B // 2, gb_added=B // 2)




def sub_ffn(k, ctx, name, packs, spec):
    lay, dram = packs[name]
    tile, p = pack_tile(k, ctx, name + "_pack", lay)
    gates = k.tile(ctx, name + "_gates", [T, spec["experts"] * B], F32)
    layer_norm(k, pack=(tile, dram, lay["_total"]))
    if spec["mode"] == "fixed":
        fixed_gates(k, gates, p("b2"))
    else:
        E = lay["router"][2] // 2
        gates_n = 1 if spec["mode"] == "topk_sum" else E
        router(k, E, chunks(p("router"), 2), p("router_b") if "router_b" in lay else None, gates, spec["mode"])
        add_second_biases(k, gates, gates_n, p("b2"))
    elay, edram = packs[name + "_experts"]
    feed_forward(k, name, edram, elay, spec["experts"], KP, spec["hidden"], spec["gated"], spec["act"], gates)


def fixed_gates(k, gates, b2):
    nc = k.nc
    logits = [0.0, 100.0, 0.0, 0.0]
    E = len(logits)
    with ExitStack() as ctx:
        sb = lambda n, s: k.tile(ctx, n, s, F32)
        ex = sb("fg_ex", [T, E])
        sm = sb("fg_sum", [T, 1])
        gT = sb("fg_gT", [E, T])
        br = sb("fg_b", [T, D])
        with nc.Block(no_gpsimd_drain=True) as block:
            @block.vector
            def _(v):
                ch = Chain(v, k["vec_step"])
                for e, x in enumerate(logits):
                    last = v.memset(ex[:, e:e + 1], x - max(logits))
                last.then_inc(k["gate_v"].sem, 1)
                v.wait_ge(*k["gate_a"].at(1))
                ch.link(v.tensor_reduce(sm[:, :], ex[:, :], AX.X, ALU.add))
                ch.link(v.reciprocal(sm[:, :], sm[:, :]))
                ch.link(v.tensor_scalar(ex[:, :], ex[:, :], sm[:, :], None, ALU.mult))
                for e in range(E):
                    last = v.tensor_copy(gates[:, e * B:(e + 1) * B], ex[:, e:e + 1].broadcast_to([T, B]))
                last.then_inc(k["gate_v"].sem, 1)
                v.wait_ge(*k["gb_mm"].at(1))
                ch.link(v.tensor_copy(br[:, :], k.ps[0:T, 6, 0:D]))
                v.tensor_tensor(k.X[:, :].rearrange("p (b d) -> p b d", b=B),
                                k.X[:, :].rearrange("p (b d) -> p b d", b=B),
                                br[:, :].unsqueeze(1).broadcast_to([T, B, D]), ALU.add)
                ch.close()

            @block.scalar
            def _(act):
                act.wait_ge(*k["gate_v"].at(1))
                act.activation(ex[:, :], ex[:, :], ACT.Exp).then_inc(k["gate_a"].sem, 1)
                act.wait_ge(*k["gt_tr"].at(1))
                act.activation(gT[:, :], k.ps[0:E, 4, 0:T], ACT.Copy).then_inc(k["gt_ev"].sem, 1)

            @block.tensor
            def _(pe):
                pe.wait_ge(*k["gate_v"].at(2))
                pe.transpose(k.ps[0:E, 4, 0:T], ex[:, :], k.ident[0:T, 0:T]).then_inc(k["gt_tr"].sem, 1)
                pe.wait_ge(*k["gt_ev"].at(1))
                pe.matmul(k.ps[0:T, 6, 0:D], gT[:, :], b2, start=True, stop=True).then_inc(k["gb_mm"].sem, 1)
        k.advance(gate_v=2, gate_a=1, gt_tr=1, gt_ev=1, gb_mm=1)


FFN = {
    "L0_ffn": dict(mode="topk_sum", experts=1, hidden=8, gated=False, act=ACT.Gelu_apprx_tanh),
    "L1_ffn": dict(mode="softmax_topk", experts=8, hidden=4, gated=True, act=ACT.Silu),
    "L2_ffn": dict(mode="topk_softmax", experts=8, hidden=8, gated=False, act=ACT.Gelu),
    "L3_ffn": dict(mode="fixed", experts=4, hidden=4, gated=False, act=ACT.Relu),
}




KT = 128
PICKS = 2


def token_tiles(E):
    return (PICKS * N + E * (KT - 1)) // KT


class Routing:

    def __init__(self, k, ctx, E):
        self.tiles = token_tiles(E)
        self.slot = k.tile(ctx, "slot", [T, PICKS, B], mybir.dt.int32)
        self.weight = k.tile(ctx, "weight", [T, PICKS, B], F32)
        self.expert = k.tile(ctx, "expert", [1, self.tiles], mybir.dt.int32)


def place_tokens(k, route, gates, E):
    nc, s = k.nc, k.signals
    most = N // KT
    none = float((route.tiles + 1) * KT)
    with ExitStack() as ctx:
        sb = lambda n, sh: k.tile(ctx, n, sh, F32)
        earlier, ones = sb("earlier", [T, T]), sb("ones", [T, T])
        steps, turns = sb("steps", [T, E, most]), sb("turns", [1, route.tiles, E])
        chosen, slot, hit = sb("chosen", [T, E, B]), sb("slot_f", [T, E, B]), sb("hit", [T, E, B])
        total, sums = sb("total", [T, E, B]), sb("sums", [T, 2, E, B])
        over, used = sb("over", [T, E, most]), sb("used", [T, E])
        ends, start = sb("ends", [T, 2, E]), sb("start", [T, E])
        passed, owner = sb("passed", [1, route.tiles, E]), sb("owner", [1, route.tiles])
        pick = sb("pick", [T, PICKS, B])
        two = sb("two", [T, B])
        flat = lambda ap: ap[:, :, :].rearrange("p e b -> p (e b)")
        by_token = lambda ap: ap[:, :, :].rearrange("p e b -> p b e")
        g3 = gates[:, :].rearrange("p (e b) -> p e b", e=E)
        with nc.Block(no_gpsimd_drain=True) as block:
            @block.gpsimd
            def _(g):
                g.memset(ones[:, :], 1.0).then_inc(s["rg_const"].sem, 1)
                g.wait_ge(*s["rg_const"].at(1))
                g.affine_select(out=earlier[:, :], in_=ones[:, :], compare_op=ALU.is_gt, fill=0.0, base=0,
                                pattern=[[1, T]], channel_multiplier=-1).then_inc(s["rg_const"].sem, 1)

            @block.tensor
            def _(pe):
                pe.wait_ge(*s["rg_const"].at(2))
                pe.wait_ge(*s["rg_chosen"].at(1))
                pe.matmul(k.ps[0:T, 0, 0:E * B], earlier[:, :], flat(chosen), start=True, stop=True)
                pe.matmul(k.ps[0:T, 1, 0:E * B], ones[:, :], flat(chosen), start=True, stop=True).then_inc(
                    s["rg_counted"].sem, 1)

            @block.vector
            def _(v):
                ch = Chain(v, s["vec_step"])
                v.tensor_scalar(flat(chosen), gates[:, :], 0.0, None, ALU.is_gt).then_inc(s["rg_chosen"].sem, 1)
                for j in range(most):
                    v.memset(steps[:, :, j:j + 1], float(j * KT))
                for t in range(route.tiles):
                    last = v.memset(turns[:, t:t + 1, :], float(t))
                ch.link(last)
                v.wait_ge(*s["rg_chosen"].at(1))
                v.wait_ge(*s["rg_counted"].at(1))
                v.tensor_copy(flat(total), k.ps[0:T, 1, 0:E * B])
                ch.link(v.tensor_copy(sums[:, 0, :, :].rearrange("p e b -> p (e b)"), k.ps[0:T, 1, 0:E * B]))
                at = 0
                reach = 1
                while reach < B:
                    v.tensor_copy(sums[:, 1 - at, :, 0:reach], sums[:, at, :, 0:reach])
                    ch.link(v.tensor_tensor(sums[:, 1 - at, :, reach:B], sums[:, at, :, reach:B],
                                            sums[:, at, :, 0:B - reach], ALU.add))
                    at, reach = 1 - at, 2 * reach
                count = sums[:, at, :, B - 1:B]
                ch.link(v.tensor_tensor(over[:, :, :], count.broadcast_to([T, E, most]), steps[:, :, :],
                                        ALU.is_gt))
                ch.link(v.tensor_reduce(used[:, :], over[:, :, :], AX.X, ALU.add))
                ch.link(v.tensor_copy(ends[:, 0, :], used[:, :]))
                ea, reach = 0, 1
                while reach < E:
                    v.tensor_copy(ends[:, 1 - ea, 0:reach], ends[:, ea, 0:reach])
                    ch.link(v.tensor_tensor(ends[:, 1 - ea, reach:E], ends[:, ea, reach:E],
                                            ends[:, ea, 0:E - reach], ALU.add))
                    ea, reach = 1 - ea, 2 * reach
                ch.link(v.tensor_tensor(start[:, :], ends[:, ea, :], used[:, :], ALU.subtract))
                ch.link(v.tensor_scalar(start[:, :], start[:, :], float(KT), None, ALU.mult))
                ch.link(v.tensor_tensor(slot[:, :, :], sums[:, at, :, :], total[:, :, :], ALU.subtract))
                ch.link(v.tensor_tensor(flat(slot), flat(slot), k.ps[0:T, 0, 0:E * B], ALU.add))
                ch.link(v.tensor_tensor(slot[:, :, :], slot[:, :, :],
                                        start[:, :].unsqueeze(2).broadcast_to([T, E, B]), ALU.add))
                ch.link(v.scalar_tensor_tensor(hit[:, :, :], slot[:, :, :], none, chosen[:, :, :], ALU.subtract,
                                               ALU.mult))
                ch.link(v.tensor_reduce(pick[:, 0, :], by_token(hit), AX.X, ALU.min))
                ch.link(v.tensor_scalar(pick[:, 0, :], pick[:, 0, :], none, None, ALU.add))
                ch.link(v.scalar_tensor_tensor(hit[:, :, :], slot[:, :, :], 1.0, chosen[:, :, :], ALU.add,
                                               ALU.mult))
                ch.link(v.tensor_reduce(pick[:, 1, :], by_token(hit), AX.X, ALU.max))
                ch.link(v.tensor_scalar(pick[:, 1, :], pick[:, 1, :], 1.0, None, ALU.subtract))
                ch.link(v.tensor_tensor(pick[:, 1, :], pick[:, 1, :], pick[:, 0, :], ALU.max))
                v.tensor_copy(route.slot[:, :, :], pick[:, :, :]).then_inc(s["rg_placed"].sem, 1)
                for n in range(PICKS):
                    ch.link(v.tensor_tensor(hit[:, :, :], slot[:, :, :],
                                            pick[:, n:n + 1, :].broadcast_to([T, E, B]), ALU.is_equal))
                    ch.link(v.tensor_tensor(hit[:, :, :], hit[:, :, :], g3, ALU.mult))
                    ch.link(v.tensor_reduce(route.weight[:, n, :], by_token(hit), AX.X, ALU.add))
                ch.link(v.tensor_tensor(two[:, :], pick[:, 1, :], pick[:, 0, :], ALU.is_gt))
                v.tensor_tensor(route.weight[:, 1, :], route.weight[:, 1, :], two[:, :], ALU.mult)
                ch.link(v.tensor_tensor(passed[:, :, :], turns[:, :, :],
                                        ends[0:1, ea:ea + 1, :].broadcast_to([1, route.tiles, E]), ALU.is_ge))
                ch.link(v.tensor_reduce(owner[:, :], passed[:, :, :], AX.X, ALU.add))
                ch.link(v.tensor_scalar(owner[:, :], owner[:, :], float(E - 1), None, ALU.min))
                v.tensor_copy(route.expert[:, :], owner[:, :])
                ch.close()
        k.advance(rg_const=2, rg_chosen=1, rg_counted=1, rg_placed=1)


def scatter_tokens(k, route, xn, rows):
    s = k.signals

    def scatter(g):
        g.wait_ge(*s["rows_zeroed"].at(16))
        for b in range(B):
            for n in range(PICKS):
                g.indirect_dma_start(rows[:, :],
                                     bass.IndirectOffsetOnAxis(ap=route.slot[:, n, b:b + 1], axis=0),
                                     xn[:, b * D:(b + 1) * D], None).then_inc(s["rg_put"].sem, 16)
        g.wait_ge(*s["rg_put"].at(16 * PICKS * B))
    return scatter


def expert_tiles(k, route, name, weights, layout, rows_in, rows_out, hidden, gated, act_fn):
    nc, s = k.nc, k.signals
    NT, total = route.tiles, layout["_total"]
    o1, o2, ob = (layout[f][0] for f in ("w1", "w2", "b1"))
    turned = (2 if gated else 1) * hidden
    wide = turned * KP
    halves = wide // 512
    assert halves == 2 and NT % 2 == 1
    with ExitStack() as ctx:
        sb = lambda n, sh: k.tile(ctx, name + "_" + n, sh, F32)
        xs, xT = sb("xs", [KT, 2, D]), sb("xsT", [KP, 2, 2, KT])
        hs = sb("hs", [KT, wide])
        hT = sb("hT", [KP, 2, hidden, KT])
        if gated:
            first = sb("first", [KP, hidden, KT])
        y = sb("y", [KT, 2, D])
        x_in, y_out = [s["rg_in0"], s["rg_in1"]], [s["rg_out0"], s["rg_out1"]]

        def expert(eng, t):
            return nc.values_load(route.expert[0:1, bass.ds(t, 1)], engines=[eng], min_val=0,
                                  max_val=layout["_experts"] - 1,
                                  skip_runtime_bounds_check_because="place_tokens clamps it to the experts")

        def in_turn(eng, step):
            step(0, 0)
            with eng.Fori(0, NT // 2) as i:
                for u in range(2):
                    step(2 * i + u + 1, 1 - u)

        with nc.Block(no_gpsimd_drain=True) as block:
            @block.sync
            def _(sp):
                def load(t, u):
                    sp.dma_start(xs[:, u, :], rows_in[bass.ds(t * KT, KT), :]).then_inc(x_in[u].sem, 16)

                def store(t, u):
                    sp.wait_ge(*s["rg_y"].at(t + 1))
                    sp.dma_start(rows_out[bass.ds(t * KT, KT), :], y[:, u, :]).then_inc(y_out[u].sem, 16)

                load(0, 0)
                load(1, 1)
                sp.wait_ge(*s["rg_turned"].at(1))
                load(2, 0)
                with sp.Fori(0, NT // 2) as i:
                    for u in range(2):
                        t = 2 * i + u + 1
                        sp.wait_ge(*s["rg_turned"].at(t + 1))
                        load(t + 2, 1 - u)
                        store(t - 1, u)
                store(NT - 1, 0)
                sp.wait_ge(*x_in[0].at(16 * ((NT + 3) // 2)))
                sp.wait_ge(*x_in[1].at(16 * ((NT + 2) // 2)))
                sp.wait_ge(*y_out[0].at(16 * ((NT + 1) // 2)))
                sp.wait_ge(*y_out[1].at(16 * (NT // 2)))

            @block.tensor
            def _(pe):
                def turn_tokens(t, u):
                    pe.wait_ge(*x_in[u].at(8 * (t - u) + 16))
                    pe.wait_ge(*s["rg_xT"].at(t - 1))
                    for c in range(2):
                        last = pe.transpose(k.ps[:, 4 + u, c * KT:(c + 1) * KT], xs[:, u, c * KP:(c + 1) * KP],
                                            k.ident[:, :])
                    last.then_inc(s["rg_turned"].sem, 1)

                def first_product(t, u):
                    e = expert(mybir.EngineType.PE, t)
                    pe.wait_ge(*s["rg_xT"].at(t + 1))
                    for half in range(2):
                        pe.wait_ge(*s["rg_hs"].at(2 * t + half - 1))
                        for c in range(2):
                            last = pe.matmul(k.ps[:, half, 0:512], xT[:, u, c, :],
                                             weights[:, bass.ds(e * total + (o1 + c * wide + half * 512), 512)],
                                             start=(c == 0), stop=(c == 1))
                        last.then_inc(s["rg_up"].sem, 1)

                def second_product(t, u):
                    e = expert(mybir.EngineType.PE, t)
                    pe.wait_ge(*s["rg_hT"].at(t + 1))
                    pe.wait_ge(*s["rg_y"].at(t - 1))
                    for m in range(hidden):
                        last = pe.matmul(k.ps[:, 6 + u, 0:D], hT[:, u, m, :],
                                         weights[:, bass.ds(e * total + (o2 + m * D), D)],
                                         start=(m == 0), stop=(m == hidden - 1))
                    last.then_inc(s["rg_down"].sem, 1)

                def turn_hidden(t, u):
                    for half in range(2):
                        pe.wait_ge(*s["rg_hs"].at(2 * t + half + 1))
                        pe.wait_ge(*s["rg_first" if gated and half == 0 else "rg_hT"].at(t))
                        for j in range(4):
                            last = pe.transpose(k.ps[:, 2 + half, j * KT:(j + 1) * KT],
                                                hs[:, (half * 4 + j) * KP:(half * 4 + j + 1) * KP], k.ident[:, :])
                        last.then_inc(s["rg_ut"].sem, 1)

                turn_tokens(0, 0)
                first_product(0, 0)
                turn_tokens(1, 1)
                turn_hidden(0, 0)
                with pe.Fori(0, NT // 2) as i:
                    for u in range(2):
                        t = 2 * i + u + 1
                        first_product(t, 1 - u)
                        turn_tokens(t + 1, u)
                        second_product(t - 1, u)
                        turn_hidden(t, 1 - u)
                second_product(NT - 1, 0)

            @block.scalar
            def _(act):
                def copy_tokens(t, u):
                    act.wait_ge(*s["rg_turned"].at(t + 1))
                    act.wait_ge(*s["rg_up"].at(2 * (t - 1)))
                    act.activation(xT[:, u, :, :], chunks(k.ps[:, 4 + u, 0:2 * KT], 2), ACT.Copy).then_inc(
                        s["rg_xT"].sem, 1)

                def step(t, u):
                    copy_tokens(t + 1, 1 - u)
                    e = expert(mybir.EngineType.Activation, t)
                    act.wait_ge(*s["rg_ut"].at(2 * t + 1))
                    if gated:
                        act.wait_ge(*s["rg_hT"].at(t))
                    else:
                        act.wait_ge(*s["rg_down"].at(t - 1))
                    for m in range(hidden):
                        if m == 4:
                            act.wait_ge(*s["rg_ut"].at(2 * t + 2))
                        last = act.activation(first[:, m, :] if gated else hT[:, u, m, :],
                                              k.ps[:, 2 + m // 4, (m % 4) * KT:(m % 4 + 1) * KT], act_fn,
                                              bias=weights[:, bass.ds(e * total + (ob + m), 1)])
                    last.then_inc(s["rg_first" if gated else "rg_hT"].sem, 1)

                copy_tokens(0, 0)
                in_turn(act, step)

            @block.vector
            def _(v):
                def copy_y(t, u):
                    v.wait_ge(*s["rg_down"].at(t + 1))
                    v.wait_ge(*y_out[u].at(8 * (t - u)))
                    v.tensor_copy(y[:, u, :], k.ps[:, 6 + u, 0:D]).then_inc(s["rg_y"].sem, 1)

                def step(t, u):
                    v.wait_ge(*s["rg_ut"].at(2 * t))
                    for half in range(2):
                        v.wait_ge(*s["rg_up"].at(2 * t + half + 1))
                        v.tensor_copy(hs[:, half * 512:(half + 1) * 512], k.ps[:, half, 0:512]).then_inc(
                            s["rg_hs"].sem, 1)
                    if not (isinstance(t, int) and t == 0):
                        copy_y(t - 1, 1 - u)
                    if gated:
                        e = expert(mybir.EngineType.DVE, t)
                        v.wait_ge(*s["rg_first"].at(t + 1))
                        v.wait_ge(*s["rg_ut"].at(2 * t + 2))
                        v.wait_ge(*s["rg_down"].at(t - 1))
                        for m in range(hidden):
                            last = v.scalar_tensor_tensor(hT[:, u, m, :], k.ps[:, 3, m * KT:(m + 1) * KT],
                                                          weights[:, bass.ds(e * total + (ob + 4 + m), 1)],
                                                          first[:, m, :], ALU.add, ALU.mult)
                        last.then_inc(s["rg_hT"].sem, 1)

                in_turn(v, step)
                copy_y(NT - 1, 0)
        k.advance(rg_in0=16 * ((NT + 3) // 2), rg_in1=16 * ((NT + 2) // 2), rg_out0=16 * ((NT + 1) // 2),
                  rg_out1=16 * (NT // 2), rg_turned=NT + 1, rg_xT=NT + 1, rg_up=2 * NT, rg_hs=2 * NT,
                  rg_ut=2 * NT, rg_hT=NT, rg_first=NT if gated else 0, rg_down=NT, rg_y=NT)


def gather_results(k, route, name, rows):
    s = k.signals
    ring = 4
    with ExitStack() as ctx:
        got = k.tile(ctx, name + "_got", [T, ring, PICKS * D], F32)
        into = [s[f"rg_got{r}"] for r in range(ring)]
        with k.nc.Block(no_gpsimd_drain=True) as block:
            @block.gpsimd
            def _(g):
                for b in range(B):
                    if b >= ring:
                        g.wait_ge(*s["rg_added"].at(b - ring + 1))
                    for n in range(PICKS):
                        g.indirect_dma_start(got[:, b % ring, n * D:(n + 1) * D], None, rows[:, :],
                                             bass.IndirectOffsetOnAxis(ap=route.slot[:, n, b:b + 1], axis=0)
                                             ).then_inc(into[b % ring].sem, 16)

            @block.vector
            def _(v):
                ch = Chain(v, s["vec_step"])
                for b in range(B):
                    v.wait_ge(*into[b % ring].at(16 * PICKS * (b // ring + 1)))
                    ch.link(v.scalar_tensor_tensor(k.x(b), got[:, b % ring, 0:D], route.weight[:, 0, b:b + 1],
                                                   k.x(b), ALU.mult, ALU.add))
                    v.scalar_tensor_tensor(k.x(b), got[:, b % ring, D:2 * D], route.weight[:, 1, b:b + 1],
                                           k.x(b), ALU.mult, ALU.add).then_inc(s["rg_added"].sem, 1)
                ch.close()
        k.advance(rg_added=B, **{f"rg_got{r}": 16 * PICKS * (B // ring) for r in range(ring)})


def sub_routed_ffn(k, ctx, name, packs, spec):
    E = spec["experts"]
    lay, dram = packs[name]
    tile, p = pack_tile(k, ctx, name + "_pack", lay)
    elay, edram = packs[name + "_experts"]
    elay = dict(elay, _experts=E)
    total = elay["_total"]
    weights = k.tile(ctx, name + "_weights", [KP, E * total])
    gates = k.tile(ctx, name + "_gates", [T, E * B])
    xn = k.tile(ctx, name + "_xn", [T, B * D])
    route = Routing(k, ctx, E)

    def load_experts(sp):
        for e in range(E):
            sp.dma_start(weights[:, e * total:(e + 1) * total], edram[e, :, :]).then_inc(k["exp_in0"].sem, 16)

    layer_norm(k, pack=(tile, dram, lay["_total"]), keep=xn, ahead=load_experts)
    router(k, E, chunks(p("router"), 2), p("router_b") if "router_b" in lay else None, gates, spec["mode"])
    place_tokens(k, route, gates, E)
    add_second_biases(k, gates, E, p("b2"), meanwhile=scatter_tokens(k, route, xn, k.rows_in))
    k.advance(rg_put=16 * PICKS * B)
    with k.nc.Block(no_gpsimd_drain=True) as block:
        @block.tensor
        def _(pe):
            pe.wait_ge(*k["exp_in0"].at(16 * E))
    k.advance(exp_in0=16 * E)
    expert_tiles(k, route, name, weights, elay, k.rows_in, k.rows_out, spec["hidden"], spec["gated"], spec["act"])
    gather_results(k, route, name, k.rows_out)



def attention(k, name, pack, H, dh, self_attn=False, mask=False, clamp=False, head_mask=False):
    nc = k.nc
    HD = H * dh
    C = HD // KP
    HC = KP // dh
    OW = max(dh, 32)
    OH = KP // OW
    OC = H // OH
    kn, kw = (1, T) if self_attn else (KN, KW)
    keys = kn * kw
    kr = KP if self_attn else CR
    scale = float(dh) ** -0.5
    UB = H // 2
    U = 2 * UB
    TURNS = B // 2
    first_pass = mask or clamp
    wq, wk, wv, wo = (pack[n] for n in ("wq", "wk", "wv", "wo"))
    with ExitStack() as ctx:
        sb = lambda n, s, d=F32: k.tile(ctx, name + "_" + n, s, d)
        QT = sb("qT", [KP, C, N])
        src = sb("src", [KP, 2, 2, keys])
        KT = sb("kT", [KP, 2, C, keys])
        V = sb("v", [kw, 2, kn, H, OW])
        qm = sb("qm", [KP, 2, H, T])
        sa = sb("sa", [T, 2, 2, keys]) if first_pass else None
        P = sb("p", [T, 4, 2, keys])
        PT = sb("pT", [kw, 2, kn, 2, T])
        oT = sb("oT", [KP, 2, OC, T])
        mx = sb("mx", [T, 4, 2])
        ng = sb("ng", [T, 4, 2])
        rs = sb("rs", [T, 4, 2])
        ri = sb("ri", [T, 4, 2])
        mu8 = sb("mu8", [T, B * S2], U8) if mask else None
        mb = sb("mb", [T, 2, S2]) if mask else None
        s = k.signals
        ctx_in = [s["ctx_in0"], s["ctx_in1"]]
        sc_read = s["sc_read"] if first_pass else s["exp_done"]

        def project_queries(pe):
            with pe.Fori(0, G) as g:
                for c in range(C):
                    pe.wait_ge(*s["lin_act"].at(g * C + c - C + 1))
                    for kc in range(2):
                        last = pe.matmul(k.ps[:, c, 0:GT], wq[:, kc, c * KP:(c + 1) * KP],
                                         k.XT[:, kc, bass.ds(g * GT, GT)], start=(kc == 0), stop=(kc == 1))
                    last.then_inc(s["lin_mm"].sem, 1)

        def store_queries(act):
            k.table(act, ACT.Identity)
            with act.Fori(0, G) as g:
                for c in range(C):
                    act.wait_ge(*s["lin_mm"].at(g * C + c + 1))
                    act.activation(QT[:, c, bass.ds(g * GT, GT)], k.ps[:, c, 0:GT], ACT.Identity,
                                   bias=pack["bq"][:, c:c + 1] if "bq" in pack else 0.0).then_inc(
                                       s["lin_act"].sem, 1)

        if UB == 8:
            places = {(c, "early"): ("K", c) for c in range(C)}
            places[4, "late"] = ("O", 0)
            places.update({(5 + j, "early"): ("V", j) for j in range(kn)})
        else:
            assert UB == 4 and C == 4 and kn == 3
            places = {(0, "early"): ("K", 0), (0, "late"): ("K", 1), (1, "early"): ("K", 2),
                      (1, "late"): ("K", 3), (2, "early"): ("V", 0), (2, "late"): ("V", 1),
                      (3, "early"): ("O", 0), (3, "late"): ("V", 2)}
        order = list(places.values())
        SHARE, TURN, OUT = (2, 3, 4) if UB == 8 else (1, 2, 3)
        END = OUT + 1

        def stream(eng, step, before_loop=lambda i: None, after_loop=lambda: None):
            for n in range(U):
                step(0, n, True, False)
            with eng.Fori(1, TURNS - 1) as i:
                before_loop(i)
                for n in range(U):
                    step(i, n, False, False)
                after_loop()
            for n in range(U + END):
                step(TURNS - 1, n, False, True)

        RING = 4 if 2 * keys <= 512 else 2

        def scores(n):
            if RING == 4:
                return k.ps[0:T, n % 4, 0:512].rearrange("p (j n) -> p j n", j=2)[:, :, 0:keys]
            return k.ps[0:T, 2 * (n % 2):2 * (n % 2) + 2, 0:keys]

        def batch_of(i, n):
            return 2 * i + n // UB, (n // UB) % 2, n % UB

        with nc.Block(no_gpsimd_drain=True) as block:
            @block.sync
            def _(sp):
                if mask:
                    sp.dma_start(mu8[:, :], k.aps["in_mask"].rearrange("(a b) n -> a (b n)", a=1)
                                 .broadcast_to([T, B * S2])).then_inc(s["x_in"].sem, 16)
                if not self_attn:
                    with sp.Fori(0, TURNS) as i:
                        for u in range(2):
                            sp.wait_ge(*s["v_mm"].at((i * 2 + u - 1) * kn))
                            sp.dma_start(src[0:CR, u, :, :], k.aps["in_ctx"][bass.ds(i * 2 + u, 1), :, :, :]
                                         .rearrange("b p c n -> (b p) c n")).then_inc(ctx_in[u].sem, 16)

            @block.gpsimd
            def _(g):
                if OW > dh:
                    g.memset(V[:, :, :, :, dh:OW], 0.0).then_inc(s["v_padded"].sem, 1)

            @block.tensor
            def _(pe):
                def bank_free(b, what, first):
                    j = order.index(what)
                    kind, c = order[j - 1]
                    at = b if j == 0 else b + 1
                    if kind == "O":
                        if not first:
                            pe.wait_ge(*s["res_done"].at(b))
                            return
                        kind, c = order[j - 2]
                    if kind == "K":
                        pe.wait_ge(*s["kt_ev"].at(at * C + c + 1))
                    else:
                        pe.wait_ge(*s["v_ev"].at(at * kn + c + 1))

                def project(b, u, kind, c):
                    if kind == "K":
                        if c == 0 and self_attn:
                            pe.wait_ge(*s["xs_copied"].at(b + 1))
                        elif c == 0:
                            pe.wait_ge(*ctx_in[u].at(8 * (b - u) + 16))
                        for kc in range(2):
                            last = pe.matmul(k.ps[:, 6, 0:keys], wk[0:kr, kc, c * KP:(c + 1) * KP],
                                             src[0:kr, u, kc, :], start=(kc == 0), stop=(kc == 1))
                        last.then_inc(s["kt_mm"].sem, 1)
                    else:
                        for kc in range(2):
                            rows = kr if kc == 0 or self_attn else kr + 1
                            last = pe.matmul(k.ps[0:kw, 6, 0:HD], src[0:rows, u, kc, c * kw:(c + 1) * kw],
                                             wv[0:rows, kc, :], start=(kc == 0), stop=(kc == 1))
                        last.then_inc(s["v_mm"].sem, 1)

                def in_bank6(i, n, place, first, last_turn):
                    b, u, p = batch_of(i, n)
                    kind, c = places.get((p, place), (None, 0))
                    opening = first and n < UB
                    closing = last_turn and n >= UB
                    if kind == "O" and not opening:
                        if closing:
                            pe.wait_ge(*s["v_ev"].at(B * kn))
                            pe.wait_ge(*s["res_done"].at(b - 1))
                        else:
                            bank_free(b, (kind, c), opening)
                        pe.wait_ge(*s["ot_ev"].at(b))
                        for c in range(OC):
                            last = pe.matmul(k.ps[0:T, 6, 0:D], oT[:, 1 - u, c, :], wo[:, c, :],
                                             start=(c == 0), stop=(c == OC - 1))
                        last.then_inc(s["wo_mm"].sem, 1)
                    elif kind in ("K", "V") and not closing:
                        bank_free(b, (kind, c), opening)
                        project(b + 1, 1 - u, kind, c)

                def step(i, n, first, last_turn):
                    if n < U:
                        b, u, p = batch_of(i, n)
                        if p == 0:
                            pe.wait_ge(*s["kt_ev"].at((b + 1) * C))
                            pe.wait_ge(*s["qm_done"].at(b + 1))
                        pe.wait_ge(*sc_read.at(i * U + n - RING + 1))
                        for j in range(2):
                            h = 2 * p + j
                            last = pe.matmul(scores(n)[:, j, :], qm[:, u, h, :],
                                             KT[:, u, h // HC, :], start=True, stop=True)
                        last.then_inc(s["sc_mm"].sem, 1)
                    in_bank6(i, n, "early", first, last_turn)
                    m = n - TURN
                    if m < U and not (first and m < 0):
                        pe.wait_ge(*s["prob_done"].at(i * U + m + 1))
                        pe.wait_ge(*s["pt_ev_a"].at(i * U + m))
                        if kn > 1:
                            pe.wait_ge(*s["pt_ev_v"].at(i * U + m))
                        for kc in range(kn):
                            for j in range(2):
                                at = (kc % 2) * 2 * T + j * T
                                last = pe.transpose(k.ps[0:kw, 4 + kc // 2, at:at + T],
                                                    P[:, m % 4, j, kc * kw:(kc + 1) * kw], k.ident[0:T, 0:T])
                        last.then_inc(s["pt_mm"].sem, 1)
                    m = n - OUT
                    if m < U and not (first and m < 0):
                        b, u, p = batch_of(i, m)
                        pe.wait_ge(*s["pt_ev_a"].at(i * U + m + 1))
                        if kn > 1:
                            pe.wait_ge(*s["pt_ev_v"].at(i * U + m + 1))
                        if p == 0:
                            pe.wait_ge(*s["v_ev"].at((b + 1) * kn))
                            pe.wait_ge(*s["ot_ev"].at(b))
                        for kc in range(kn):
                            for j in range(2):
                                h = 2 * p + j
                                row = (h % OH) * OW
                                last = pe.matmul(k.ps[row:row + OW, 7, (h // OH) * T:(h // OH + 1) * T],
                                                 V[:, u, kc, h, :], PT[:, m % 2, kc, j, :],
                                                 start=(kc == 0), stop=(kc == kn - 1))
                        last.then_inc(s["pv_mm"].sem, 1)
                    in_bank6(i, n, "late", first, last_turn)

                project_queries(pe)
                if not self_attn:
                    pe.wait_ge(*s["ones_row"].at(1))
                for kind, c in [what for what in order if what[0] != "O"]:
                    if kind == "K":
                        pe.wait_ge(*s["kt_ev"].at(c))
                    else:
                        pe.wait_ge(*s["kt_ev"].at(C))
                        pe.wait_ge(*s["v_ev"].at(c))
                    project(0, 0, kind, c)
                pe.wait_ge(*s["lin_act"].at(G * C))
                if OW > dh:
                    pe.wait_ge(*s["v_padded"].at(1))
                stream(pe, step)

            @block.scalar
            def _(act):
                def evacuate(b, u, c):
                    act.wait_ge(*s["kt_mm"].at(b * C + c + 1))
                    if c == 0:
                        act.wait_ge(*s["sc_mm"].at((b - 1) * UB))
                    act.activation(KT[:, u, c, :], k.ps[:, 6, 0:keys], ACT.Identity,
                                   bias=pack["bk"][:, c:c + 1] if "bk" in pack else 0.0).then_inc(
                                       s["kt_ev"].sem, 1)

                def in_bank6(i, n, place, last_turn):
                    b, u, p = batch_of(i, n)
                    kind, c = places.get((p, place), (None, 0))
                    if kind == "K" and not (last_turn and n >= UB):
                        evacuate(b + 1, 1 - u, c)

                def step(i, n, first, last_turn):
                    if n > 0 or not first:
                        in_bank6(i, n - 1, "late", last_turn)
                    in_bank6(i, n, "early", last_turn)
                    if n < U:
                        act.wait_ge(*s["max_done"].at(i * U + n + 1))
                        act.wait_ge(*s["pt_mm"].at(i * U + n - 3))
                        for j in range(2):
                            at = sa[:, n % 2, j, :] if first_pass else scores(n)[:, j, :]
                            last = act.activation(P[:, n % 4, j, :], at, ACT.Exp, bias=ng[:, n % 4, j:j + 1],
                                                  scale=1.0 if mask else scale,
                                                  accum_out=rs[:, n % 4, j:j + 1])
                        last.then_inc(s["exp_done"].sem, 1)
                    m = n - TURN
                    if m < U and not (first and m < 0):
                        act.wait_ge(*s["pt_mm"].at(i * U + m + 1))
                        act.wait_ge(*s["pv_mm"].at(i * U + m - 1))
                        na = min(kn, 2)
                        act.activation(PT[:, m % 2, 0:na, :, :],
                                       k.ps[0:kw, 4, 0:na * 2 * T].rearrange("p (c h t) -> p c h t", c=na, h=2),
                                       ACT.Copy).then_inc(s["pt_ev_a"].sem, 1)
                    b, u, p = batch_of(i, n)
                    if p == OUT - 1 and not (first and n < UB):
                        act.wait_ge(*s["pv_mm"].at(b * UB))
                        act.wait_ge(*s["wo_mm"].at(b - 2))
                        act.activation(oT[:, 1 - u, :, :], chunks(k.ps[:, 7, 0:OC * T], OC), ACT.Copy).then_inc(
                            s["ot_ev"].sem, 1)

                store_queries(act)
                for c in range(C):
                    evacuate(0, 0, c)
                stream(act, step)

            @block.vector
            def _(v):
                ch = Chain(v, s["vec_step"])
                per = U * (2 + head_mask) + (2 if "bo" in pack else 0)

                def copy_tokens(b, u):
                    v.wait_ge(*s["v_mm"].at((b - 1) * kn))
                    v.tensor_copy(src[:, u, :, :], k.XT[:, :, bass.ds(b * T, T)]).then_inc(
                        s["xs_copied"].sem, 1)

                def mask_queries(b, u):
                    if isinstance(b, int) and b == 1:
                        v.wait_ge(*s["lin_act"].at(G * C))
                    v.wait_ge(*s["sc_mm"].at((b - 1) * UB))
                    for c in range(C):
                        last = v.tensor_tensor(
                            qm[:, u, c * HC:(c + 1) * HC, :],
                            QT[:, c, bass.ds(b * T, T)].unsqueeze(1).broadcast_to([KP, HC, T]),
                            pack["hmask"][:, 0:HC].unsqueeze(2).broadcast_to([KP, HC, T]), ALU.mult)
                    last.then_inc(s["qm_done"].sem, 1)
                    if mask:
                        v.tensor_scalar(mb[:, u, :], mu8[:, bass.ds(b * S2, S2)], -1.0, FMAX, ALU.add,
                                        ALU.mult).then_inc(s["mask_done"].sem, 1)

                def store_v(b, u, j):
                    v.wait_ge(*s["v_mm"].at(b * kn + j + 1))
                    if j == 0:
                        v.wait_ge(*s["pv_mm"].at((b - 1) * UB))
                    at = k.ps[0:kw, 6, 0:HD].rearrange("p (h d) -> p h d", h=H)
                    if self_attn:
                        v.tensor_tensor(V[:, u, j, :, 0:dh], at,
                                        pack["bv"][0:kw, :].rearrange("p (h d) -> p h d", h=H),
                                        ALU.add).then_inc(s["v_ev"].sem, 1)
                    else:
                        v.tensor_copy(V[:, u, j, :, 0:dh], at).then_inc(s["v_ev"].sem, 1)

                def in_bank6(i, n, place, first, last_turn):
                    b, u, p = batch_of(i, n)
                    kind, c = places.get((p, place), (None, 0))
                    if kind == "V" and not (last_turn and n >= UB):
                        store_v(b + 1, 1 - u, c)
                    if kind == "O" and not (first and n < UB):
                        v.wait_ge(*s["wo_mm"].at(b))
                        v.tensor_tensor(k.x(b - 1), k.ps[0:T, 6, 0:D], k.x(b - 1), ALU.add).then_inc(
                            s["res_done"].sem, 1)
                        if "bo" in pack:
                            v.wait_ge(*s["res_done"].at(b))
                            ch.link(v.tensor_tensor(k.x(b - 1), pack["bo"][0:T, :], k.x(b - 1), ALU.add))

                def step(i, n, first, last_turn):
                    if n > 0 or not first:
                        in_bank6(i, n - 1, "late", first, last_turn)
                    b, u, p = batch_of(i, n)
                    more = not (last_turn and n >= UB)
                    if n < U:
                        v.wait_ge(*s["sc_mm"].at(i * U + n + 1))
                        at = scores(n)
                        r = n % 4
                        if first_pass:
                            v.wait_ge(*s["exp_done"].at(i * U + n - 1))
                            if clamp:
                                v.tensor_scalar(sa[:, n % 2, :, :], at, CLAMP / scale, -CLAMP / scale, ALU.min,
                                                ALU.max).then_inc(s["sc_read"].sem, 1)
                            else:
                                if p == 0:
                                    v.wait_ge(*s["mask_done"].at(b + 1))
                                v.scalar_tensor_tensor(
                                    sa[:, n % 2, :, :], at, scale,
                                    mb[:, u, :].unsqueeze(1).broadcast_to([T, 2, keys]), ALU.mult,
                                    ALU.add).then_inc(s["sc_read"].sem, 1)
                            v.wait_ge(*s["sc_read"].at(i * U + n + 1))
                            at = sa[:, n % 2, :, :]
                        ch.link(v.tensor_reduce(mx[:, r, :], at, AX.X, ALU.max))
                        v.tensor_scalar(ng[:, r, :], mx[:, r, :], -1.0 if mask else -scale, None,
                                        ALU.mult).then_inc(s["max_done"].sem, 1)
                    m = n - SHARE
                    if m < U and not (first and m < 0):
                        v.wait_ge(*s["exp_done"].at(i * U + m + 1))
                        ch.link(v.reciprocal(ri[:, m % 4, :], rs[:, m % 4, :]))
                        if head_mask:
                            h = 2 * (m % UB)
                            ch.link(v.tensor_tensor(ri[:, m % 4, :], ri[:, m % 4, :], pack["hm"][0:T, h:h + 2],
                                                    ALU.mult))
                        for j in range(2):
                            last = v.tensor_scalar(P[:, m % 4, j, :], P[:, m % 4, j, :], ri[:, m % 4, j:j + 1],
                                                   None, ALU.mult)
                        last.then_inc(s["prob_done"].sem, 1)
                    m = n - TURN
                    if kn > 1 and m < U and not (first and m < 0):
                        v.wait_ge(*s["pt_mm"].at(i * U + m + 1))
                        v.wait_ge(*s["pv_mm"].at(i * U + m - 1))
                        v.tensor_copy(PT[:, m % 2, 2, :, :],
                                      chunks(k.ps[0:kw, 5, 0:2 * T], 2)).then_inc(s["pt_ev_v"].sem, 1)
                    in_bank6(i, n, "early", first, last_turn)
                    if more and n < U:
                        if self_attn and p == UB - 2:
                            if not (last_turn and n >= 0 and n // UB == 0):
                                copy_tokens(b + 2, u)
                        if p == UB // 2:
                            mask_queries(b + 1, 1 - u)

                if self_attn:
                    copy_tokens(0, 0)
                    copy_tokens(1, 1)
                else:
                    v.memset(src[CR:CR + 1, :, :, :], 1.0).then_inc(s["ones_row"].sem, 1)
                if mask:
                    v.wait_ge(*s["x_in"].at(16))
                v.wait_ge(*s["lin_act"].at(C))
                mask_queries(0, 0)
                for j in range(kn):
                    store_v(0, 0, j)
                stream(v, step, lambda i: ch.turn(i - 1, per), lambda: ch.end(TURNS - 2))
                in_bank6(TURNS - 1, U + END - 1, "late", False, True)
                ch.close()

        units = TURNS * U
        k.advance(lin_mm=G * C, lin_act=G * C, x_in=16 if mask else 0, v_padded=1 if OW > dh else 0,
                  ones_row=0 if self_attn else 1)
        k.advance(xs_copied=B if self_attn else 0, kt_mm=B * C, kt_ev=B * C, v_mm=B * kn, v_ev=B * kn, qm_done=B,
                  sc_mm=units, sc_read=units if first_pass else 0, max_done=units, exp_done=units, prob_done=units,
                  pt_mm=units, pt_ev_a=units, pt_ev_v=units if kn > 1 else 0, pv_mm=units, ot_ev=B, wo_mm=B,
                  res_done=B, mask_done=B if mask else 0)
        if not self_attn:
            k.advance(ctx_in0=TURNS * 16, ctx_in1=TURNS * 16)


def sub_attention(k, ctx, name, packs, spec):
    lay, dram = packs[name]
    tile, p = pack_tile(k, ctx, name + "_pack", lay)
    pack = {f: p(f) for f in lay if f != "_total"}
    for f in ("wq", "wk", "wv"):
        pack[f] = chunks(pack[f], 2)
    heads_out = KP // max(spec["dh"], 32)
    pack["wo"] = chunks(pack["wo"], spec["H"] // heads_out)
    layer_norm(k, pack=(tile, dram, lay["_total"]))
    attention(k, name, pack, **spec)


ATTENTION = {
    "L0_xattn": dict(H=16, dh=16, clamp=True),
    "L1_xattn": dict(H=8, dh=64),
    "L2_xattn": dict(H=16, dh=16, mask=True),
    "L3_attn": dict(H=16, dh=16, self_attn=True, head_mask=True),
}


def head_rows(dh):
    return np.repeat(np.eye(KP // dh, dtype=np.float32), dh, axis=0)


def spread_heads(wo, H, dh):
    wide = np.zeros((H, max(dh, 32), wo.shape[1]), np.float32)
    wide[:, :dh] = wo.reshape(H, dh, -1)
    return wide.reshape(-1, wo.shape[1])


def with_bias_row(w, bias):
    out = np.zeros((CR + 1, 2, w.shape[1]), np.float32)
    out[:CR] = w.reshape(2, CR, -1).transpose(1, 0, 2)
    if bias is not None:
        out[CR, 1] = bias
    return out.reshape(CR + 1, -1)


def host_attention(name, a):
    w = {key[len(name) + 1:]: v for key, v in a.items() if key.startswith(name + "_")}
    spec = ATTENTION[name]
    H, dh = spec["H"], spec["dh"]
    turned = spec.get("self_attn")
    m = {n: (w[n].T if turned else w[n]) for n in ("Wq", "Wk", "Wv", "Wo")}
    f = dict(wq=by_rows(m["Wq"]), wo=by_rows(spread_heads(m["Wo"], H, dh)), hmask=head_rows(dh))
    if turned:
        f.update(wk=by_rows(m["Wk"]), wv=by_rows(m["Wv"]), bv=on_rows(w["bv"]), hm=on_rows(w["head_mask"]))
    else:
        f.update(wk=by_rows(m["Wk"], CR), wv=with_bias_row(m["Wv"], w.get("bv")))
    for n in ("bq", "bk"):
        if n in w:
            f[n] = columns(w[n])
    if "bo" in w:
        f["bo"] = on_rows(w["bo"])
    return {name: packed(f)}



def sub_l3_xattn(k, ctx, name, packs):
    nc = k.nc
    lay, dram = packs[name]
    tile, p = pack_tile(k, ctx, name + "_pack", lay)
    layer_norm(k, pack=(tile, dram, lay["_total"]))
    wq, wk, wv = (chunks(p(n), 2) for n in ("wq", "wk", "wv"))
    scale = float(D) ** -0.5
    s = k.signals
    sb = lambda n, sh: k.tile(ctx, name + "_" + n, sh, F32)
    src = sb("src", [CR + 1, 2, 2, S2])
    qT = sb("qT", [KP, 2, 2, T])
    KT = sb("kT", [KP, 2, 2, S2])
    V = sb("v", [KW, 2, KN, D])
    P = sb("p", [T, 2, S2])
    PT = sb("pT", [KW, 2, KN, T])
    mx, ng, rs, ri = (sb(n, [T, 2]) for n in ("mx", "ng", "rs", "ri"))
    ctx_in = [s["ctx_in0"], s["ctx_in1"]]
    TURNS = B // 2
    with nc.Block(no_gpsimd_drain=True) as block:
        @block.vector
        def _(v):
            v.memset(src[CR:CR + 1, :, :, :], 1.0)

    with nc.Block(no_gpsimd_drain=True) as block:
        @block.sync
        def _(sp):
            with sp.Fori(0, TURNS) as i:
                for u in range(2):
                    sp.wait_ge(*s["v_mm"].at((i * 2 + u - 1) * KN))
                    sp.dma_start(src[0:CR, u, :, :], k.aps["in_ctx"][bass.ds(i * 2 + u, 1), :, :, :]
                                 .rearrange("b p c n -> (b p) c n")).then_inc(ctx_in[u].sem, 16)

        @block.tensor
        def _(pe):
            with pe.Fori(0, TURNS) as i:
                for u in range(2):
                    b = i * 2 + u
                    pe.wait_ge(*ctx_in[u].at((i + 1) * 16))
                    pe.wait_ge(*s["qm_done"].at(b))
                    for c in range(2):
                        for kc in range(2):
                            last = pe.matmul(k.ps[:, 0, c * T:(c + 1) * T], wq[:, kc, c * KP:(c + 1) * KP],
                                             k.XT[:, kc, bass.ds(b * T, T)], start=(kc == 0), stop=(kc == 1))
                    last.then_inc(s["lin_mm"].sem, 1)
                    for c in range(2):
                        pe.wait_ge(*s["kt_ev"].at(b * 2 + c - 1))
                        for kc in range(2):
                            rows = CR + kc
                            last = pe.matmul(k.ps[:, 1 + c, 0:S2], wk[0:rows, kc, c * KP:(c + 1) * KP],
                                             src[0:rows, u, kc, :], start=(kc == 0), stop=(kc == 1))
                        last.then_inc(s["kt_mm"].sem, 1)
                    for j in range(KN):
                        pe.wait_ge(*s["v_ev"].at(b * KN + j - 1))
                        bank = 3 + (u * KN + j) % 2
                        for kc in range(2):
                            rows = CR + kc
                            last = pe.matmul(k.ps[0:KW, bank, 0:D], src[0:rows, u, kc, j * KW:(j + 1) * KW],
                                             wv[0:rows, kc, :], start=(kc == 0), stop=(kc == 1))
                        last.then_inc(s["v_mm"].sem, 1)
                for u in range(2):
                    b = i * 2 + u
                    pe.wait_ge(*s["qm_done"].at(b + 1))
                    pe.wait_ge(*s["kt_ev"].at((b + 1) * 2))
                    pe.wait_ge(*s["exp_done"].at(b - 1))
                    for c in range(2):
                        last = pe.matmul(k.ps[0:T, 5 + u, 0:S2], qT[:, u, c, :], KT[:, u, c, :], start=(c == 0),
                                         stop=(c == 1))
                    last.then_inc(s["sc_mm"].sem, 1)
                for u in range(2):
                    b = i * 2 + u
                    pe.wait_ge(*s["exp_done"].at(b + 1))
                    pe.wait_ge(*s["res_done"].at(b))
                    pe.wait_ge(*s["pt_ev_a"].at(b))
                    for kc in range(KN):
                        last = pe.transpose(k.ps[0:KW, 7, kc * T:(kc + 1) * T], P[:, u, kc * KW:(kc + 1) * KW],
                                            k.ident[0:T, 0:T])
                    last.then_inc(s["pt_mm"].sem, 1)
                    pe.wait_ge(*s["pt_ev_a"].at(b + 1))
                    pe.wait_ge(*s["v_ev"].at((b + 1) * KN))
                    for kc in range(KN):
                        last = pe.matmul(k.ps[0:T, 7, 0:D], PT[:, u, kc, :], V[:, u, kc, :], start=(kc == 0),
                                         stop=(kc == KN - 1))
                    last.then_inc(s["pv_mm"].sem, 1)

        @block.scalar
        def _(act):
            k.table(act, ACT.Exp)
            with act.Fori(0, TURNS) as i:
                for u in range(2):
                    b = i * 2 + u
                    act.wait_ge(*s["lin_mm"].at(b + 1))
                    act.wait_ge(*s["sc_mm"].at(b - 1))
                    for c in range(2):
                        last = act.activation(qT[:, u, c, :], k.ps[:, 0, c * T:(c + 1) * T], ACT.Identity,
                                              bias=p("bq")[:, c:c + 1])
                    last.then_inc(s["qm_done"].sem, 1)
                    for c in range(2):
                        act.wait_ge(*s["kt_mm"].at(b * 2 + c + 1))
                        act.activation(KT[:, u, c, :], k.ps[:, 1 + c, 0:S2], ACT.Copy).then_inc(s["kt_ev"].sem, 1)
                for u in range(2):
                    b = i * 2 + u
                    act.wait_ge(*s["max_done"].at(b + 1))
                    act.wait_ge(*s["pt_mm"].at(b - 1))
                    act.activation(P[:, u, :], k.ps[0:T, 5 + u, 0:S2], ACT.Exp, bias=ng[:, u:u + 1], scale=scale,
                                   accum_out=rs[:, u:u + 1]).then_inc(s["exp_done"].sem, 1)
                for u in range(2):
                    b = i * 2 + u
                    act.wait_ge(*s["pt_mm"].at(b + 1))
                    act.wait_ge(*s["pv_mm"].at(b - 1))
                    act.activation(PT[:, u, :, :], chunks(k.ps[0:KW, 7, 0:KN * T], KN), ACT.Copy).then_inc(
                        s["pt_ev_a"].sem, 1)

        @block.vector
        def _(v):
            ch = Chain(v, s["vec_step"])
            with v.Fori(0, TURNS) as i:
                ch.turn(i, 4)
                for u in range(2):
                    b = i * 2 + u
                    v.wait_ge(*s["pv_mm"].at(b - 1))
                    for j in range(KN):
                        v.wait_ge(*s["v_mm"].at(b * KN + j + 1))
                        v.tensor_copy(V[:, u, j, :], k.ps[0:KW, 3 + (u * KN + j) % 2, 0:D]).then_inc(
                            s["v_ev"].sem, 1)
                for u in range(2):
                    b = i * 2 + u
                    v.wait_ge(*s["sc_mm"].at(b + 1))
                    ch.link(v.tensor_reduce(mx[:, u:u + 1], k.ps[0:T, 5 + u, 0:S2], AX.X, ALU.max))
                    v.tensor_scalar(ng[:, u:u + 1], mx[:, u:u + 1], -scale, None, ALU.mult).then_inc(
                        s["max_done"].sem, 1)
                for u in range(2):
                    b = i * 2 + u
                    v.wait_ge(*s["exp_done"].at(b + 1))
                    ch.link(v.reciprocal(ri[:, u:u + 1], rs[:, u:u + 1]))
                    v.wait_ge(*s["pv_mm"].at(b + 1))
                    v.scalar_tensor_tensor(k.x(b), k.ps[0:T, 7, 0:D], ri[:, u:u + 1], k.x(b), ALU.mult,
                                           ALU.add).then_inc(s["res_done"].sem, 1)
                ch.end(TURNS)
            ch.close()
    k.advance(lin_mm=B, qm_done=B, kt_mm=2 * B, kt_ev=2 * B, v_mm=B * KN, v_ev=B * KN, sc_mm=B, max_done=B,
              exp_done=B, pt_mm=B, pt_ev_a=B, pv_mm=B, res_done=B, ctx_in0=TURNS * 16, ctx_in1=TURNS * 16)


def host_l3_xattn(name, a):
    w = {key[len(name) + 1:]: v for key, v in a.items() if key.startswith(name + "_")}
    return {name: packed(dict(wq=by_rows(w["Wq"].T), wk=with_bias_row(w["Wk"].T, w["bk"]),
                              wv=with_bias_row(w["Wv"].T, w["bv"]), bq=columns(w["bq"])))}



CH = 8
NCH = T // CH
GCH = GB * NCH


def project_out(k, make, wo, residual="X", out=None, per=1):
    nc = k.nc
    s = k.signals
    with ExitStack() as ctx:
        sb = lambda n, sh: k.tile(ctx, "po_" + n, sh, F32)
        xo = sb("x", [T, 2, D])
        oT = sb("oT", [KP, 2, 2, T])
        with nc.Block(no_gpsimd_drain=True) as block:
            @block.vector
            def _(v):
                ch = Chain(v, s["vec_step"])
                with v.Fori(0, B // 2) as i:
                    ch.turn(i, 2 * (per - 1))
                    for u in range(2):
                        b = 2 * i + u
                        v.wait_ge(*s["norm_tr"].at(b - 1))
                        make(v, ch, b, xo[:, u, :]).then_inc(s["norm_done"].sem, 1)
                    for u in range(2):
                        b = 2 * i + u
                        v.wait_ge(*s["wo_mm"].at(b + 1))
                        if out is None:
                            v.tensor_tensor(k.x(b), k.ps[0:T, 2 + u, 0:D], k.x(b), ALU.add).then_inc(
                                s["res_done"].sem, 1)
                        else:
                            v.tensor_tensor(out[:, bass.ds(b * D, D)], k.ps[0:T, 2 + u, 0:D],
                                            residual[:, bass.ds(b * D, D)], ALU.add).then_inc(s["res_done"].sem, 1)
                    ch.end(B // 2)
                ch.close()

            @block.tensor
            def _(pe):
                with pe.Fori(0, B // 2) as i:
                    for u in range(2):
                        b = 2 * i + u
                        pe.wait_ge(*s["norm_done"].at(b + 1))
                        pe.wait_ge(*s["norm_ev"].at(b - 1))
                        for c in range(2):
                            last = pe.transpose(k.ps[:, u, c * T:(c + 1) * T], xo[:, u, c * KP:(c + 1) * KP],
                                                k.ident[0:T, 0:T])
                        last.then_inc(s["norm_tr"].sem, 1)
                    for u in range(2):
                        b = 2 * i + u
                        pe.wait_ge(*s["norm_ev"].at(b + 1))
                        pe.wait_ge(*s["res_done"].at(b - 1))
                        for c in range(2):
                            last = pe.matmul(k.ps[0:T, 2 + u, 0:D], oT[:, u, c, :], wo[:, c, :], start=(c == 0),
                                             stop=(c == 1))
                        last.then_inc(s["wo_mm"].sem, 1)

            @block.scalar
            def _(act):
                k.table(act, ACT.Copy)
                with act.Fori(0, B // 2) as i:
                    for u in range(2):
                        b = 2 * i + u
                        act.wait_ge(*s["norm_tr"].at(b + 1))
                        act.wait_ge(*s["wo_mm"].at(b - 1))
                        act.activation(oT[:, u, :, :], chunks(k.ps[:, u, 0:2 * T], 2), ACT.Copy).then_inc(
                            s["norm_ev"].sem, 1)
        k.advance(norm_done=B, norm_tr=B, norm_ev=B, wo_mm=B, res_done=B)


def sub_l0_attn(k, ctx, name, packs):
    nc = k.nc
    lay, dram = packs[name]
    tile, p = pack_tile(k, ctx, name + "_pack", lay)
    layer_norm(k, pack=(tile, dram, lay["_total"]))
    s = k.signals
    outer = lambda n, sh: k.tile(ctx, name + "_" + n, sh, F32)
    V = outer("V", [T, B * D])
    GV = outer("G", [T, B * D])
    R, K, E = (outer(n, [KP, N]) for n in ("R", "K", "E"))

    with ExitStack() as mid:
        sb = lambda n, sh: k.tile(mid, name + "_" + n, sh, F32)
        dT = sb("dT", [KP, 2, N])
        z0 = sb("z0", [KP, N])
        z1 = sb("z1", [KP, N])
        wx1, wx2 = chunks(p("wx1"), 2), p("wx2").rearrange("p (i n) -> p i n", i=5)
        with ExitStack() as inner:
            xm = k.tile(inner, name + "_xm", [KP, 2, N], F32)
            with nc.Block(no_gpsimd_drain=True) as block:
                @block.vector
                def _(v):
                    for c in range(2):
                        x3 = k.XT[:, c, :].rearrange("p (b t) -> p b t", b=B)
                        d3 = dT[:, c, :].rearrange("p (b t) -> p b t", b=B)
                        v.tensor_tensor(d3[:, :, 1:T], x3[:, :, 0:T - 1], x3[:, :, 1:T], ALU.subtract)
                        v.tensor_scalar(d3[:, :, 0:1], x3[:, :, 0:1], -1.0, None, ALU.mult).then_inc(
                            s["p_a"].sem, 1)
                        v.wait_ge(*s["p_a"].at(c + 1))
                        v.scalar_tensor_tensor(xm[:, c, :], dT[:, c, :], p("mu_x")[:, c:c + 1], k.XT[:, c, :],
                                               ALU.mult, ALU.add).then_inc(s["p_b"].sem, 1)

                @block.tensor
                def _(pe):
                    pe.wait_ge(*s["p_b"].at(2))
                    with pe.Fori(0, G) as g:
                        for m in range(2):
                            pe.wait_ge(*s["lin_act"].at(2 * g + m - 1))
                            for c in range(2):
                                last = pe.matmul(k.ps[:, m, 0:GT], wx1[:, c, m * KP:(m + 1) * KP],
                                                 xm[:, c, bass.ds(g * GT, GT)], start=(c == 0), stop=(c == 1))
                            last.then_inc(s["lin_mm"].sem, 1)

                @block.scalar
                def _(act):
                    k.table(act, ACT.Tanh)
                    with act.Fori(0, G) as g:
                        for m in range(2):
                            z = (z0, z1)[m]
                            act.wait_ge(*s["lin_mm"].at(2 * g + m + 1))
                            act.activation(z[:, bass.ds(g * GT, GT)], k.ps[:, m, 0:GT], ACT.Tanh).then_inc(
                                s["lin_act"].sem, 1)
            k.advance(p_a=2, p_b=2, lin_mm=2 * G, lin_act=2 * G)

        inp = sb("inp", [KP, 2, 5, 2, GT])
        tmp = sb("tmp", [KP, 2, GT])
        ta = sb("ta", [64, 2, GT])
        wr, wk, wa, wv, wg = (chunks(p(n), 2) for n in ("wr", "wk", "wa", "wv", "wg"))
        R_, W_, K_, V_, G_ = range(5)
        mixed, mus, prod, done = s["p_a"], s["p_b"], s["p_c"], s["p_d"]
        with nc.Block(no_gpsimd_drain=True) as block:
            @block.tensor
            def _(pe):
                with pe.Fori(0, G // 2) as i:
                    for u in range(2):
                        g = 2 * i + u
                        tok = bass.ds(g * GT, GT)
                        for r in range(10):
                            j, c = r // 2, r % 2
                            pe.wait_ge(*mixed.at(g * 10 + r - 3))
                            pe.matmul(k.ps[:, (u * 10 + r) % 4, 0:GT], wx2[:, j, c * KP:(c + 1) * KP],
                                      (z0 if j < 4 else z1)[:, tok], start=True, stop=True).then_inc(mus.sem, 1)
                    for u in range(2):
                        g = 2 * i + u

                        def product(q, rows, w, j):
                            pe.wait_ge(*done.at(g * 8 + q - 3))
                            pe.wait_ge(*mixed.at(g * 10 + 2 * j + 2))
                            for c in range(2):
                                last = pe.matmul(k.ps[0:rows, 4 + q % 4, 0:GT], w[:, c, :], inp[:, u, j, c, :],
                                                 start=(c == 0), stop=(c == 1))
                            last.then_inc(prod.sem, 1)

                        product(0, KP, wr, R_)
                        product(1, 64, wa, W_)
                        product(2, KP, wk, K_)
                        pe.wait_ge(*done.at(g * 8 + 2))
                        pe.matmul(k.ps[:, 7, 0:GT], p("wb"), ta[:, u, :], start=True, stop=True).then_inc(
                            prod.sem, 1)
                        for q, (w, j) in enumerate([(wv, V_), (wv, V_), (wg, G_), (wg, G_)]):
                            pe.wait_ge(*done.at(g * 8 + 4 + q - 3))
                            pe.wait_ge(*mixed.at(g * 10 + 2 * j + 2))
                            for b in range(2):
                                at = (2 * (q % 2) + b) * T
                                for c in range(2):
                                    last = pe.matmul(k.ps[0:T, 4 + q, b * D:(b + 1) * D], inp[:, u, j, c, at:at + T],
                                                     w[:, c, :], start=(c == 0), stop=(c == 1))
                            last.then_inc(prod.sem, 1)

            @block.vector
            def _(v):
                ch = Chain(v, s["vec_step"])
                with v.Fori(0, G // 2) as i:
                    ch.turn(i, 20)
                    for u in range(2):
                        g = 2 * i + u
                        tok = bass.ds(g * GT, GT)
                        for r in range(10):
                            j, c = r // 2, r % 2
                            v.wait_ge(*mus.at(g * 10 + r + 1))
                            ch.link(v.scalar_tensor_tensor(tmp[:, r % 2, :], k.ps[:, (u * 10 + r) % 4, 0:GT],
                                                           p("x_bias")[:, r:r + 1], dT[:, c, tok], ALU.add,
                                                           ALU.mult))
                            if r == 0:
                                v.wait_ge(*prod.at((g - 1) * 8))
                            v.tensor_tensor(inp[:, u, j, c, :], tmp[:, r % 2, :], k.XT[:, c, tok],
                                            ALU.add).then_inc(mixed.sem, 1)
                    ch.end(G // 2)
                ch.close()

            @block.scalar
            def _(act):
                k.table(act, ACT.Tanh)
                with act.Fori(0, G // 2) as i:
                    for u in range(2):
                        g = 2 * i + u
                        tok = bass.ds(g * GT, GT)
                        for q, (dst, rows, fn) in enumerate([(R[:, tok], KP, ACT.Copy), (ta[:, u, :], 64, ACT.Tanh),
                                                             (K[:, tok], KP, ACT.Copy)]):
                            act.wait_ge(*prod.at(g * 8 + q + 1))
                            act.activation(dst, k.ps[0:rows, 4 + q, 0:GT], fn).then_inc(done.sem, 1)
                        act.wait_ge(*prod.at(g * 8 + 4))
                        act.activation(E[:, tok], k.ps[:, 7, 0:GT], ACT.Exp, bias=p("b_w")).then_inc(done.sem, 1)
                        for q in range(4):
                            dst = V if q < 2 else GV
                            act.wait_ge(*prod.at(g * 8 + 5 + q))
                            act.activation(dst[:, bass.ds((g * GB + 2 * (q % 2)) * D, 2 * D)],
                                           k.ps[0:T, 4 + q, 0:2 * D], ACT.Copy).then_inc(done.sem, 1)
        k.advance(p_a=10 * G, p_b=10 * G, p_c=8 * G, p_d=8 * G)

    O = outer("O", [T, B * D])
    rwkv_matrix(k, name, p, R, K, E, V, O)

    with ExitStack() as mid:
        sb = lambda n, sh: k.tile(mid, name + "_" + n, sh, F32)
        BH, HV = B * 4, D // 4
        gw, sq = sb("gw", [T, B * D]), sb("sq", [T, B * D])
        mean, var, rstd, half = (sb(n, [T, BH]) for n in ("mean", "var", "rstd", "half"))
        heads = lambda t: t[:, :].rearrange("p (h v) -> p h v", v=HV)
        batches = lambda t: t[:, :].rearrange("p (b d) -> p b d", b=B)
        wide = lambda t: t[:, :].unsqueeze(2).broadcast_to([T, BH, HV])
        row = lambda f: p(f)[0:T, :].unsqueeze(1).broadcast_to([T, B, D])
        with nc.Block(no_gpsimd_drain=True) as block:
            @block.vector
            def _(v):
                ch = Chain(v, s["vec_step"])
                v.memset(half[:, :], -0.5)
                ch.link(v.tensor_reduce(mean[:, :], heads(O), AX.X, ALU.add))
                ch.link(v.tensor_scalar(mean[:, :], mean[:, :], 1.0 / HV, None, ALU.mult))
                v.tensor_tensor(heads(O), heads(O), wide(mean), ALU.subtract).then_inc(s["p_a"].sem, 1)
                v.wait_ge(*s["p_b"].at(1))
                ch.link(v.tensor_reduce(var[:, :], heads(sq), AX.X, ALU.add))
                v.tensor_scalar(var[:, :], var[:, :], 1.0 / HV, LN_EPS, ALU.mult, ALU.add).then_inc(s["p_a"].sem, 1)
                v.wait_ge(*s["p_b"].at(2))
                v.tensor_tensor(batches(gw), batches(GV), row("gn_w"), ALU.mult)
                ch.link(v.tensor_tensor(batches(GV), batches(GV), row("gn_b"), ALU.mult))
                v.wait_ge(*s["p_c"].at(1))
                ch.link(v.tensor_tensor(heads(O), heads(O), wide(rstd), ALU.mult))
                ch.link(v.tensor_tensor(O[:, :], O[:, :], gw[:, :], ALU.mult))
                ch.close()

            @block.scalar
            def _(act):
                act.wait_ge(*s["p_a"].at(1))
                act.activation(sq[:, :], O[:, :], ACT.Square).then_inc(s["p_b"].sem, 1)
                act.activation(GV[:, :], GV[:, :], ACT.Silu).then_inc(s["p_b"].sem, 1)

            @block.gpsimd
            def _(g):
                g.wait_ge(*s["p_a"].at(2))
                g.tensor_tensor(rstd[:, :], var[:, :], half[:, :], ALU.pow).then_inc(s["p_c"].sem, 1)
        k.advance(p_a=2, p_b=2, p_c=1)

    def gated(v, ch, b, dst):
        return v.tensor_tensor(dst, O[:, bass.ds(b * D, D)], GV[:, bass.ds(b * D, D)], ALU.add)

    project_out(k, gated, chunks(p("wo"), 2))


def rwkv_matrix(k, name, p, R, K, E, V, O):
    nc, s = k.nc, k.signals
    with ExitStack() as ctx:
        sb = lambda n, sh: k.tile(ctx, name + "_" + n, sh, F32)
        ci, cx, eq, ek, qd, kd = (sb(n, [KP, GT]) for n in ("ci", "cx", "eq", "ek", "qd", "kd"))
        gd = sb("gd", [KP, GCH])
        PW = CH * (CH - 1) // 2
        dd = sb("dd", [KP, PW, GCH])
        PP = sb("P", [KP, CH, GT])
        KA = sb("KA", [KP, NCH, GB, T])
        QB = sb("QB", [KP, GB, 4, T])
        ad = sb("ad", [T, GB, CH, 4])
        tm = sb("tm", [T, 4, NCH, CH])
        A = sb("A", [T, GB, 4, T])
        by_chunk = lambda t: t.rearrange("p (n s) -> p s n", s=CH)


        def pairs(d):
            return bass.AP(tensor=PP[:, :, :].tensor, offset=d * GT,
                           ap=[[CH * GT, KP], [GT + 1, CH - d], [CH, GCH]])

        offs = [0]
        for d in range(1, CH):
            offs.append(offs[-1] + CH - d)
        sums, exps, made, part, whole, outs, copied = (s[n] for n in ("p_a", "p_b", "p_c", "p_d", "p_e",
                                                                      "p_f", "p_g"))
        with nc.Block(no_gpsimd_drain=True) as block:
            @block.vector
            def _(v):
                v.memset(PP[:, :, :], 0.0)

            @block.gpsimd
            def _(g):
                g.memset(KA[:, :, :, :], 0.0)
                g.drain()

        with nc.Block(no_gpsimd_drain=True) as block:
            @block.vector
            def _(v):
                ch = Chain(v, s["vec_step"])
                with v.Fori(0, G) as g:
                    tok = bass.ds(g * GT, GT)
                    ch.turn(g, 23)
                    r, kk, e = by_chunk(R[:, tok]), by_chunk(K[:, tok]), E[:, tok]
                    ch.link(v.tensor_tensor_scan(ci[:, :], p("reset"), e, 0.0, ALU.mult, ALU.add))
                    ch.link(v.tensor_tensor(cx[:, :], ci[:, :], e, ALU.subtract))
                    c3, x3 = by_chunk(ci[:, :]), by_chunk(cx[:, :])
                    ends = c3[:, CH - 1:CH, :].broadcast_to([KP, CH, GCH])
                    v.tensor_tensor(by_chunk(ek[:, :]), c3, ends, ALU.subtract)
                    for d in range(1, CH):
                        last = v.tensor_tensor(dd[:, offs[d - 1]:offs[d], :], c3[:, 0:CH - d, :], x3[:, d:CH, :],
                                               ALU.subtract)
                    last.then_inc(sums.sem, 1)
                    v.wait_ge(*exps.at(g + 1))
                    v.wait_ge(*part.at(g))
                    ch.link(v.tensor_tensor(qd[:, :], R[:, tok], eq[:, :], ALU.mult))
                    v.tensor_tensor(QB[:, :, :, :],
                                    qd[:, :].rearrange("p (b t) -> p b t", b=GB).unsqueeze(2)
                                    .broadcast_to([KP, GB, 4, T]),
                                    p("hmask").unsqueeze(1).unsqueeze(3).broadcast_to([KP, GB, 4, T]), ALU.mult)
                    ch.link(v.tensor_tensor(kd[:, :], K[:, tok], ek[:, :], ALU.mult))
                    flat = KA[:, :, :, :].rearrange("p i b (c s) -> p (i b c) s", s=CH)
                    for b in range(GB):
                        first = GCH + b * NCH
                        last = v.tensor_copy(flat[:, first:first + (GCH + 1) * (NCH - 2) + 1:GCH + 1, :],
                                             kd[:, b * T:(b + 1) * T - CH].rearrange("p (c s) -> p c s", s=CH))
                    ch.link(last)
                    g4 = gd[:, :].rearrange("p (b n) -> p b n", b=GB)
                    for i in range(2, NCH):
                        ch.link(v.tensor_tensor(KA[:, i, :, 0:CH * (i - 1)], KA[:, i - 1, :, 0:CH * (i - 1)],
                                                g4[:, :, i - 1:i].broadcast_to([KP, GB, CH * (i - 1)]), ALU.mult))
                    for d in range(1, CH):
                        at = dd[:, offs[d - 1]:offs[d], :]
                        last = v.tensor_tensor(at, at, kk[:, 0:CH - d, :], ALU.mult)
                    ch.link(last)
                    for d in range(1, CH):
                        last = v.tensor_tensor(pairs(d), dd[:, offs[d - 1]:offs[d], :], r[:, d:CH, :], ALU.mult)
                    v.scalar_tensor_tensor(pairs(0), r, p("bonus"), kk, ALU.mult,
                                           ALU.mult).then_inc(made.sem, 1)
                    v.wait_ge(*part.at(g + 1))
                    ch.link(v.tensor_copy(ad[:, :, :, :], k.ps[0:T, 4, 0:GB * CH * 4].rearrange(
                        "p (b j h) -> p b j h", b=GB, j=CH)))
                    v.wait_ge(*outs.at(g * GB))
                    for b in range(GB):
                        v.wait_ge(*whole.at(g * GB + b))
                        ch.link(v.tensor_tensor(
                            tm[:, :, :, :],
                            ad[:, b, :, :].rearrange("p j h -> p h j").unsqueeze(2).broadcast_to([T, 4, NCH, CH]),
                            p("same")[0:T, :].rearrange("p (n j) -> p n j", j=CH).unsqueeze(1)
                            .broadcast_to([T, 4, NCH, CH]), ALU.mult))
                        v.tensor_tensor(A[:, b, :, :], tm[:, :, :, :].rearrange("p h n j -> p h (n j)"),
                                        chunks(k.ps[0:T, b, 0:GT], 4), ALU.add).then_inc(whole.sem, 1)
                    ch.end(G)
                ch.close()

            @block.scalar
            def _(act):
                k.table(act, ACT.Exp)
                with act.Fori(0, G) as g:
                    act.wait_ge(*sums.at(g + 1))
                    act.activation(eq[:, :], cx[:, :], ACT.Exp, scale=-1.0)
                    act.activation(ek[:, :], ek[:, :], ACT.Exp)
                    act.activation(gd[:, :], by_chunk(ci[:, :])[:, CH - 1, :], ACT.Exp, scale=-1.0)
                    act.activation(dd[:, :, :], dd[:, :, :], ACT.Exp).then_inc(exps.sem, 1)
                    for b in range(GB):
                        act.wait_ge(*outs.at(g * GB + b + 1))
                        act.activation(O[:, bass.ds((g * GB + b) * D, D)], k.ps[0:T, 5 + b % 2, 0:D],
                                       ACT.Copy).then_inc(copied.sem, 1)

            @block.tensor
            def _(pe):
                with pe.Fori(0, G) as g:
                    pe.wait_ge(*made.at(g + 1))
                    pe.wait_ge(*whole.at(g * GB))
                    for b in range(GB):
                        for j in range(CH):
                            at = (b * CH + j) * 4
                            last = pe.matmul(k.ps[0:T, 4, at:at + 4],
                                             PP[:, j, b * T:(b + 1) * T], p("hmask"), start=True, stop=True)
                    for b in range(GB):
                        out = chunks(k.ps[0:T, b, 0:GT], 4)
                        for i in range(NCH):
                            last = pe.matmul(out[:, :, i * CH:(i + 1) * CH], KA[:, i, b, :],
                                             QB[:, b, :, i * CH:(i + 1) * CH], start=True, stop=True)
                    last.then_inc(part.sem, 1)
                    for b in range(GB):
                        pe.wait_ge(*whole.at(g * GB + b + 1))
                        pe.wait_ge(*copied.at(g * GB + b - 1))
                        for h in range(4):
                            last = pe.matmul(k.ps[0:T, 5 + b % 2, h * 64:(h + 1) * 64], A[:, b, h, :],
                                             V[:, bass.ds((g * GB + b) * D + h * 64, 64)], start=True, stop=True)
                        last.then_inc(outs.sem, 1)
        k.advance(p_a=G, p_b=G, p_c=G, p_d=G, p_e=B, p_f=B, p_g=B)


def host_l0_attn(name, a):
    w = {key[len(name) + 1:]: v for key, v in a.items() if key.startswith(name + "_")}
    wx2 = np.zeros((KP, 5, D), np.float32)
    per_mix = w["W_x2"].reshape(D, 5, 32)
    for j in range(4):
        wx2[32 * j:32 * j + 32, j] = per_mix[:, j].T
    wx2[0:32, 4] = per_mix[:, 4].T
    wx1 = np.zeros((D, 2 * KP), np.float32)
    wx1[:, :160] = w["W_x1"].T
    reset = np.ones((1, GT), np.float32)
    reset[:, ::CH] = 0.0
    f = dict(mu_x=columns(w["mu_x"]), wx1=by_rows(wx1), wx2=wx2.reshape(KP, -1),
             x_bias=w["x_bias"].reshape(5, 2, KP).transpose(2, 0, 1).reshape(KP, 10),
             wr=by_rows(w["W_r"].T), wk=by_rows(w["W_k"].T), wv=by_rows(w["W_v"].T), wg=by_rows(w["W_g"].T),
             wa=by_rows(w["A_w"].T), wb=w["B_w"].T, b_w=w["b_w"][:, None], bonus=w["bonus"].reshape(KP, 1),
             gn_w=on_rows(w["gn_weight"]), gn_b=on_rows(w["gn_bias"]), wo=by_rows(w["W_o"].T),
             hmask=head_rows(32), reset=on_rows(reset),
             same=np.repeat(np.repeat(np.eye(NCH, dtype=np.float32), CH, axis=0), CH, axis=1))
    return {name: packed(f)}



def project_features(k, w, C, dst, bias=None, fn=ACT.Identity):
    s = k.signals
    with k.nc.Block(no_gpsimd_drain=True) as block:
        @block.tensor
        def _(pe):
            with pe.Fori(0, G) as g:
                for c in range(C):
                    pe.wait_ge(*s["lin_act"].at(g * C + c - C + 1))
                    for kc in range(2):
                        last = pe.matmul(k.ps[:, c, 0:GT], w[:, kc, c * KP:(c + 1) * KP],
                                         k.XT[:, kc, bass.ds(g * GT, GT)], start=(kc == 0), stop=(kc == 1))
                    last.then_inc(s["lin_mm"].sem, 1)

        @block.scalar
        def _(act):
            k.table(act, fn)
            with act.Fori(0, G) as g:
                for c in range(C):
                    act.wait_ge(*s["lin_mm"].at(g * C + c + 1))
                    act.activation(dst[:, c, bass.ds(g * GT, GT)], k.ps[:, c, 0:GT], fn,
                                   bias=bias[:, c:c + 1] if bias is not None else 0.0).then_inc(
                                       s["lin_act"].sem, 1)
    k.advance(lin_mm=G * C, lin_act=G * C)


def backwards(ap):
    step, n = ap.ap[-1]
    return bass.AP(tensor=ap.tensor, offset=ap.offset + (n - 1) * step, ap=[*ap.ap[:-1], [-step, n]])


TQ = 64
NQ = D // TQ


def sub_l1_attn(k, ctx, name, packs):
    nc, s = k.nc, k.signals
    lay, dram = packs[name]
    tile, p = pack_tile(k, ctx, name + "_pack", lay)
    outer = lambda n, sh: k.tile(ctx, name + "_" + n, sh, F32)
    U = outer("u", [T, B * D])
    layer_norm(k, pack=(tile, dram, lay["_total"]), keep=U, rms_w=p("pre_w"))
    YR = outer("yr", [T, B * D])
    rows_dram = nc.dram_tensor(name + "_h", [2 * T - 1, D], F32).ap()
    with ExitStack() as mid:
        sb = lambda n, sh: k.tile(mid, name + "_" + n, sh, F32)
        XV, X2 = sb("xv", [T, B, D]), sb("x2", [T, B, D])
        poles = 16
        with ExitStack() as inner:
            ib = lambda n, sh: k.tile(inner, name + "_" + n, sh, F32)
            h, ex = ib("filter", [KP, 2, T]), ib("ex", [KP, 4, T])
            hT, zero = ib("hT", [T, D]), ib("zero", [T, D])
            with nc.Block(no_gpsimd_drain=True) as block:
                @block.vector
                def _(v):
                    ch = Chain(v, s["vec_step"])
                    v.memset(zero[:, :], 0.0).then_inc(s["p_d"].sem, 1)
                    ch.link(v.memset(h[:, :, :], 0.0))
                    with v.Fori(0, poles // 2) as i:
                        for r in range(4):
                            c, at = r % 2, r // 2 + 2 * i
                            v.wait_ge(*s["p_a"].at(4 * i + r + 1))
                            v.scalar_tensor_tensor(h[:, c, :], ex[:, r, :],
                                                   p("residues")[:, bass.ds(c * poles + at, 1)],
                                                   h[:, c, :], ALU.mult, ALU.add).then_inc(s["p_f"].sem, 1)
                            v.wait_ge(*s["p_f"].at(4 * i + r + 1))
                    v.tensor_tensor(h[:, :, T - 1:T], h[:, :, T - 1:T], p("skip").unsqueeze(2), ALU.add).then_inc(
                        s["p_b"].sem, 1)
                    ch.close()

                @block.scalar
                def _(act):
                    k.table(act, ACT.Exp)
                    with act.Fori(0, poles // 2) as i:
                        for r in range(4):
                            c, at = r % 2, r // 2 + 2 * i
                            act.wait_ge(*s["p_f"].at(4 * i + r - 3))
                            act.activation(ex[:, r, :], p("times"), ACT.Exp,
                                           scale=p("poles")[:, bass.ds(c * poles + at, 1)]).then_inc(
                                               s["p_a"].sem, 1)
                    act.wait_ge(*s["p_c"].at(1))
                    act.activation(hT[:, :], k.ps[0:T, 0, 0:D], ACT.Copy).then_inc(s["p_d"].sem, 1)

                @block.tensor
                def _(pe):
                    pe.wait_ge(*s["p_b"].at(1))
                    for c in range(2):
                        last = pe.transpose(k.ps[0:T, 0, c * KP:(c + 1) * KP], h[:, c, :], k.ident[:, :])
                    last.then_inc(s["p_c"].sem, 1)

                @block.sync
                def _(sp):
                    sp.wait_ge(*s["p_d"].at(2))
                    sp.dma_start(rows_dram[T:2 * T - 1, :], zero[0:T - 1, :]).then_inc(s["p_e"].sem, 16)
                    sp.dma_start(rows_dram[0:T, :], hT[:, :]).then_inc(s["p_e"].sem, 16)
                    sp.wait_ge(*s["p_e"].at(32))
            k.advance(p_a=2 * poles, p_b=1, p_c=1, p_d=2, p_e=32, p_f=2 * poles)

        with ExitStack() as inner:
            ib = lambda n, sh: k.tile(inner, name + "_" + n, sh, F32)
            z = ib("z", [KP, 2, 6, GT])
            xv = ib("xvT", [KP, 2, 2, GT])
            w = chunks(p("in_proj"), 2)
            sw = p("short_w").rearrange("p (m j) -> p m j", j=3)
            prod, based, conv, ready, turned, moved = (s[n] for n in ("p_a", "p_b", "p_c", "p_d", "p_e", "p_f"))
            with nc.Block(no_gpsimd_drain=True) as block:
                @block.tensor
                def _(pe):
                    with pe.Fori(0, G // 2) as i:
                        for u in range(2):
                            g = 2 * i + u
                            for m in range(6):
                                pe.wait_ge(*conv.at(g * 6 + m - 5))
                                for kc in range(2):
                                    last = pe.matmul(k.ps[:, m, 0:GT], w[:, kc, m * KP:(m + 1) * KP],
                                                     k.XT[:, kc, bass.ds(g * GT, GT)], start=(kc == 0),
                                                     stop=(kc == 1))
                                last.then_inc(prod.sem, 1)
                        for u in range(2):
                            g = 2 * i + u
                            pe.wait_ge(*ready.at(g + 1))
                            for b in range(GB):
                                pe.wait_ge(*moved.at(2 * (g * GB + b - 1)))
                                for c in range(2):
                                    pe.transpose(k.ps[0:T, 6 + b % 2, c * KP:(c + 1) * KP],
                                                 xv[:, u, c, b * T:(b + 1) * T], k.ident[:, :])
                                for c in range(2):
                                    last = pe.transpose(k.ps[0:T, 6 + b % 2, D + c * KP:D + (c + 1) * KP],
                                                        z[:, u, c, b * T:(b + 1) * T], k.ident[:, :])
                                last.then_inc(turned.sem, 1)

                @block.scalar
                def _(act):
                    k.table(act, ACT.Identity)
                    with act.Fori(0, G // 2) as i:
                        for u in range(2):
                            g = 2 * i + u
                            act.wait_ge(*turned.at((g - 1) * GB))
                            for m in range(6):
                                act.wait_ge(*prod.at(g * 6 + m + 1))
                                act.activation(z[:, u, m, :], k.ps[:, m, 0:GT], ACT.Identity,
                                               scale=sw[:, m, 2:3], bias=p("short_b")[:, m:m + 1]).then_inc(
                                                   based.sem, 1)
                        for u in range(2):
                            g = 2 * i + u
                            for b in range(GB):
                                act.wait_ge(*turned.at(g * GB + b + 1))
                                act.activation(XV[:, bass.ds(g * GB + b, 1), :],
                                               k.ps[0:T, 6 + b % 2, 0:D].unsqueeze(1), ACT.Copy)
                                act.activation(X2[:, bass.ds(g * GB + b, 1), :],
                                               k.ps[0:T, 6 + b % 2, D:2 * D].unsqueeze(1), ACT.Copy).then_inc(
                                                   moved.sem, 2)

                @block.vector
                def _(v):
                    ch = Chain(v, s["vec_step"])
                    with v.Fori(0, G // 2) as i:
                        ch.turn(i, 14)
                        for u in range(2):
                            g = 2 * i + u
                            for m in range(6):
                                v.wait_ge(*based.at(g * 6 + m + 1))
                                z3 = z[:, u, m, :].rearrange("p (b t) -> p b t", b=GB)
                                p3 = chunks(k.ps[:, m, 0:GT], GB)
                                ch.link(v.scalar_tensor_tensor(z3[:, :, 1:T], p3[:, :, 0:T - 1], sw[:, m, 1:2],
                                                               z3[:, :, 1:T], ALU.mult, ALU.add))
                                v.scalar_tensor_tensor(z3[:, :, 2:T], p3[:, :, 0:T - 2], sw[:, m, 0:1],
                                                       z3[:, :, 2:T], ALU.mult, ALU.add).then_inc(conv.sem, 1)
                            v.wait_ge(*conv.at(g * 6 + 6))
                            v.wait_ge(*turned.at((g - 1) * GB))
                            ch.link(v.tensor_tensor(xv[:, u, :, :], z[:, u, 2:4, :], z[:, u, 4:6, :], ALU.mult))
                            v.sem_inc(ready.sem, 1)
                        ch.end(G // 2)
                    ch.close()
            k.advance(p_a=6 * G, p_b=6 * G, p_c=6 * G, p_d=G, p_e=B, p_f=2 * B)

        with ExitStack() as inner:
            ib = lambda n, sh: k.tile(inner, name + "_" + n, sh, F32)
            TP = ib("toeplitz", [T, 2, T, TQ])
            xq = ib("xq", [T, 2, 32, TQ])
            ys = ib("ys", [KP, 2, GT])
            cut, prod, out, turned, done = (s[n] for n in ("p_a", "p_b", "p_c", "p_d", "p_e"))
            t_in = [s["toep_in0"], s["toep_in1"]]
            per = TQ // 16
            with nc.Block(no_gpsimd_drain=True) as block:
                @block.vector
                def _(v):
                    v.memset(xq[:, :, :, :], 0.0)

            with nc.Block(no_gpsimd_drain=True) as block:
                @block.sync
                def _(sp):
                    for q in range(NQ):
                        if q >= 2:
                            sp.wait_ge(*prod.at((q - 1) * per))
                        sp.dma_start(TP[:, q % 2, :, :],
                                     bass.AP(tensor=rows_dram.tensor, offset=q * TQ, ap=[[D, T], [D, T], [1, TQ]])).then_inc(t_in[q % 2].sem, 16)

                @block.tensor
                def _(pe):
                    def back(q, r):
                        n = q * per + r
                        pe.wait_ge(*out.at(n + 1))
                        pe.wait_ge(*done.at(n - 1))
                        for f in range(4):
                            last = pe.transpose(k.ps[0:T, 4 + r % 2, f * KP:(f + 1) * KP],
                                                ys[:, r % 2, f * T:(f + 1) * T], k.ident[:, :])
                        last.then_inc(turned.sem, 1)

                    with pe.Fori(0, NQ // 2) as i:
                        for u in range(2):
                            q = 2 * i + u
                            pe.wait_ge(*cut.at(q + 1))
                            pe.wait_ge(*t_in[u].at((i + 1) * 16))
                            for r in range(per):
                                pe.wait_ge(*out.at(q * per + r - 3))
                                for f in range(4):
                                    for j in range(4):
                                        d = r * 16 + f * 4 + j
                                        last = pe.matmul(k.ps[32 * j:32 * j + 32, r % 4, f * T:(f + 1) * T],
                                                         xq[:, u, :, d], TP[:, u, :, d], start=True, stop=True)
                                last.then_inc(prod.sem, 1)
                                if r >= 1:
                                    back(q, r - 1)
                            back(q, per - 1)

                @block.scalar
                def _(act):
                    k.table(act, ACT.Copy)
                    with act.Fori(0, NQ // 2) as i:
                        for r in range(2 * per):
                            n = i * 2 * per + r
                            act.wait_ge(*prod.at(n + 1))
                            act.wait_ge(*turned.at(n - 1))
                            act.activation(ys[:, r % 2, :].rearrange("p (f t) -> p f t", f=4),
                                           backwards(chunks(k.ps[:, r % 4, 0:GT], 4)), ACT.Copy).then_inc(
                                               out.sem, 1)

                @block.vector
                def _(v):
                    with v.Fori(0, NQ // 2) as i:
                        for u in range(2):
                            q = 2 * i + u
                            v.wait_ge(*prod.at((q - 1) * per))
                            v.tensor_copy(xq[:, u, 0:B, :], XV[:, :, bass.ds(q * TQ, TQ)]).then_inc(cut.sem, 1)
                            for r in range(per):
                                n = q * per + r
                                v.wait_ge(*turned.at(n + 1))
                                y = X2[:, :, bass.ds(q * TQ + r * 16, 16)].rearrange("p b d -> p d b")
                                v.tensor_tensor(y, k.ps[0:T, 4 + r % 2, 0:512].rearrange("p (d b) -> p d b", b=32)
                                                [:, :, 0:B], y, ALU.mult).then_inc(done.sem, 1)
            nb = NQ * per
            k.advance(p_a=NQ, p_b=nb, p_c=nb, p_d=nb, p_e=nb, toep_in0=32, toep_in1=32)

        def gated(v, ch, b, dst):
            return v.tensor_copy(dst, X2[:, bass.ds(b, 1), :].rearrange("p b d -> p (b d)"))

        project_out(k, gated, chunks(p("out_proj"), 2), residual=U, out=YR)
    layer_norm(k, rms_w=p("post_w"), source=YR, plain=False)
    with nc.Block(no_gpsimd_drain=True) as block:
        @block.vector
        def _(v):
            v.tensor_tensor(k.X[:, :], k.X[:, :], YR[:, :], ALU.add)
    lay2, dram2 = packs[name + "_mlp"]
    feed_forward(k, name + "_mlp", dram2, lay2, 1, T, 6, True, ACT.Gelu_apprx_tanh)


def host_l1_attn(name, a):
    w = {key[len(name) + 1:]: v for key, v in a.items() if key.startswith(name + "_")}
    by_channel = lambda v: v.reshape(2, KP, -1).transpose(1, 0, 2).reshape(KP, -1)
    f = dict(pre_w=columns(w["pre_norm_w"]), post_w=columns(w["post_norm_w"]), in_proj=by_rows(w["in_proj_w"].T),
             short_w=w["short_w"].reshape(6, KP, 3).transpose(1, 0, 2).reshape(KP, 18),
             short_b=columns(w["short_b"]), poles=by_channel(w["log_poles"]), residues=by_channel(w["residues"]),
             skip=columns(w["D_skip"]), out_proj=by_rows(w["out_proj_w"].T),
             times=on_rows(np.arange(T, dtype=np.float32)[::-1]))
    both = np.concatenate([w["l1_w"], w["l2_w"]], axis=0).T
    done, lay = packed(dict(w1=by_rows(both), w2=by_rows(w["l3_w"].T, T)))
    return {name: packed(f), name + "_mlp": (done[None], lay)}


def sub_l2_attn(k, ctx, name, packs):
    nc, s = k.nc, k.signals
    lay, dram = packs[name]
    tile, p = pack_tile(k, ctx, name + "_pack", lay)
    sb = lambda n, sh: k.tile(ctx, name + "_" + n, sh, F32)
    U = sb("u", [T, B * D])
    layer_norm(k, pack=(tile, dram, lay["_total"]), keep=U)
    QT = sb("qT", [KP, 2, N])
    project_features(k, chunks(p("wq"), 2), 2, QT, bias=p("bq"))
    AT = sb("aT", [KP, 2, N])
    hd, HV = 16, 32
    xs = sb("xs", [KP, 2, 2, T])
    kv, sq, kn = (sb(n, [T, 2, 2 * D]) for n in ("kv", "sq", "kn"))
    mean, var, rstd = (sb(n, [T, 2, HV]) for n in ("mean", "var", "rstd"))
    km = sb("km", [KP, 2, 2, KP])
    wkv = chunks(p("wkv"), 2)
    copied, prod, cent, sqd, vard, roots, normed, mats, mixed, atts, added = (
        s[n] for n in ("p_a", "p_b", "p_c", "p_d", "p_e", "p_f", "p_g", "p_h", "p_i", "p_j", "p_k"))
    heads = lambda t: t.rearrange("p (h d) -> p h d", d=hd)
    with nc.Block(no_gpsimd_drain=True) as block:
        @block.gpsimd
        def _(g):
            x3 = k.X[:, :].rearrange("p (b d) -> p b d", b=B)
            g.tensor_tensor(k.X[:, :], k.X[:, :], U[:, :], ALU.add).then_inc(s["pool_step"].sem, 1)
            g.wait_ge(*s["pool_step"].at(1))
            g.tensor_tensor(x3, x3, p("p2_b")[0:T, :].unsqueeze(1).broadcast_to([T, B, D]), ALU.add)
            g.drain()

        @block.tensor
        def _(pe):
            with pe.Fori(0, B // 2) as i:
                for u in range(2):
                    b = 2 * i + u
                    pe.wait_ge(*copied.at(b + 1))
                    pe.wait_ge(*cent.at(b - 1))
                    for c in range(2):
                        last = pe.matmul(k.ps[0:T, u, 0:2 * D], xs[:, u, c, :], wkv[:, c, :], start=(c == 0),
                                         stop=(c == 1))
                    last.then_inc(prod.sem, 1)
                for u in range(2):
                    b = 2 * i + u
                    pe.wait_ge(*normed.at(b + 1))
                    pe.wait_ge(*mixed.at(b - 1))
                    for c in range(2):
                        last = pe.matmul(k.ps[:, 2 + u, c * KP:(c + 1) * KP], kn[:, u, c * KP:(c + 1) * KP],
                                         kn[:, u, D + c * KP:D + (c + 1) * KP], start=True, stop=True)
                    last.then_inc(mats.sem, 1)
                for u in range(2):
                    b = 2 * i + u
                    pe.wait_ge(*mixed.at(b + 1))
                    pe.wait_ge(*added.at(b - 1))
                    for c in range(2):
                        last = pe.matmul(k.ps[:, 4 + u, c * T:(c + 1) * T], km[:, u, c, :],
                                         QT[:, c, bass.ds(b * T, T)], start=True, stop=True)
                    last.then_inc(atts.sem, 1)

        @block.scalar
        def _(act):
            k.table(act, ACT.Square)
            with act.Fori(0, B // 2) as i:
                for u in range(2):
                    b = 2 * i + u
                    act.wait_ge(*cent.at(b + 1))
                    act.activation(sq[:, u, :], kv[:, u, :], ACT.Square).then_inc(sqd.sem, 1)
                for u in range(2):
                    b = 2 * i + u
                    act.wait_ge(*vard.at(b + 1))
                    act.activation(rstd[:, u, :], var[:, u, :], ACT.Sqrt).then_inc(roots.sem, 1)

        @block.vector
        def _(v):
            ch = Chain(v, s["vec_step"])
            with v.Fori(0, B // 2) as i:
                ch.turn(i, 18)
                for u in range(2):
                    b = 2 * i + u
                    v.wait_ge(*prod.at(b - 1))
                    v.tensor_copy(xs[:, u, :, :], k.XT[:, :, bass.ds(b * T, T)]).then_inc(copied.sem, 1)
                for u in range(2):
                    b = 2 * i + u
                    v.wait_ge(*prod.at(b + 1))
                    ch.link(v.tensor_tensor(kv[:, u, :], k.ps[0:T, u, 0:2 * D], p("bkv")[0:T, :], ALU.add))
                    ch.link(v.tensor_reduce(mean[:, u, :], heads(kv[:, u, :]), AX.X, ALU.add))
                    ch.link(v.tensor_scalar(mean[:, u, :], mean[:, u, :], 1.0 / hd, None, ALU.mult))
                    v.tensor_tensor(heads(kv[:, u, :]), heads(kv[:, u, :]),
                                    mean[:, u, :].unsqueeze(2).broadcast_to([T, HV, hd]),
                                    ALU.subtract).then_inc(cent.sem, 1)
                for u in range(2):
                    b = 2 * i + u
                    v.wait_ge(*sqd.at(b + 1))
                    ch.link(v.tensor_reduce(var[:, u, :], heads(sq[:, u, :]), AX.X, ALU.add))
                    v.tensor_scalar(var[:, u, :], var[:, u, :], 1.0 / hd, LN_EPS, ALU.mult, ALU.add).then_inc(
                        vard.sem, 1)
                for u in range(2):
                    b = 2 * i + u
                    v.wait_ge(*roots.at(b + 1))
                    ch.link(v.reciprocal(rstd[:, u, :], rstd[:, u, :]))
                    v.wait_ge(*mats.at(b - 1))
                    ch.link(v.tensor_tensor(heads(kv[:, u, :]), heads(kv[:, u, :]),
                                            rstd[:, u, :].unsqueeze(2).broadcast_to([T, HV, hd]), ALU.mult))
                    ch.link(v.tensor_tensor(kv[:, u, :], kv[:, u, :], p("gamma")[0:T, :], ALU.mult))
                    v.tensor_tensor(kn[:, u, :], kv[:, u, :], p("beta")[0:T, :], ALU.add).then_inc(normed.sem, 1)
                for u in range(2):
                    b = 2 * i + u
                    v.wait_ge(*mats.at(b + 1))
                    v.wait_ge(*atts.at(b - 1))
                    ch.link(v.scalar_tensor_tensor(km[:, u, :, :], chunks(k.ps[:, 2 + u, 0:2 * KP], 2), 1.0 / T,
                                                   chunks(p("temp"), 2), ALU.mult, ALU.mult))
                    v.tensor_tensor(km[:, u, :, :], km[:, u, :, :], chunks(p("bias"), 2), ALU.add).then_inc(
                        mixed.sem, 1)
                for u in range(2):
                    b = 2 * i + u
                    v.wait_ge(*atts.at(b + 1))
                    ch.link(v.tensor_tensor(AT[:, :, bass.ds(b * T, T)], chunks(k.ps[:, 4 + u, 0:2 * T], 2),
                                            k.XT[:, :, bass.ds(b * T, T)], ALU.add))
                    v.sem_inc(added.sem, 1)
                ch.end(B // 2)
            ch.close()
    k.advance(pool_step=1, p_a=B, p_b=B, p_c=B, p_d=B, p_e=B, p_f=B, p_g=B, p_h=B, p_i=B, p_j=B, p_k=B)
    lay2, dram2 = packs[name + "_mlp"]
    feed_forward(k, name + "_mlp", dram2, lay2, 1, KP, 2, False, ACT.Gelu, src=AT)


def on_diagonal(blocks, rows=16):
    out = np.zeros((KP, 2, KP), np.float32)
    for h in range(16):
        c, at = h // 8, (h % 8) * rows
        out[at:at + rows, c, at:at + rows] = blocks[h]
    return out.reshape(KP, -1)


def host_l2_attn(name, a):
    w = {key[len(name) + 1:]: v for key, v in a.items() if key.startswith(name + "_")}
    wt = w["qkv_w"].T
    each = lambda kk, vv: on_rows(np.concatenate([np.tile(kk, 16), np.tile(vv, 16)]))
    f = dict(wq=by_rows(wt[:, :D]), wkv=by_rows(wt[:, D:]), bq=columns(w["qkv_b"][:D]),
             bkv=on_rows(w["qkv_b"][D:]), gamma=each(w["kn_g"], w["vn_g"]), beta=each(w["kn_b"], w["vn_b"]),
             temp=on_diagonal(np.broadcast_to(w["temperature"], (16, 16, 16))), bias=on_diagonal(w["attn_bias"]),
             p2_b=on_rows(w["p2_b"]))
    done, lay = packed(dict(w1=by_rows(w["p1_w"].T), w2=by_rows(w["p2_w"].T), b1=columns(w["p1_b"])))
    return {name: packed(f), name + "_mlp": (done[None], lay)}



def build_program(nc, aps, layouts, layers):
    with ExitStack() as ctx:
        k = Core(nc, ctx)
        packs = {name: (lay, aps["in_" + name]) for name, lay in layouts.items()}
        k.aps = aps
        with nc.Block(no_gpsimd_drain=True) as block:
            names = list(SIGNALS)

            @block.gpsimd
            def _(g):
                g.memset(k.spark[:, :], 0.0)

            def raise_all(eng, part):
                for name in names[part::4]:
                    eng.sem_inc(k[name].sem, HEAD)

            @block.vector
            def _(v):
                raise_all(v, 0)

            @block.scalar
            def _(act):
                raise_all(act, 1)

            @block.tensor
            def _(pe):
                raise_all(pe, 2)

            @block.sync
            def _(sp):
                raise_all(sp, 3)

        tiles = token_tiles(8) + 2
        k.rows_in = nc.dram_tensor("rows_in", [tiles * KT, D], F32).ap()
        k.rows_out = nc.dram_tensor("rows_out", [(tiles - 2) * KT, D], F32).ap()
        routed_zeros = k.tile(ctx, "zeros", [KT, D])
        with nc.Block(no_gpsimd_drain=True) as block:
            @block.vector
            def _(v):
                v.memset(routed_zeros[:, :], 0.0).then_inc(k["vec_step"].sem, 1)
                v.wait_ge(*k["vec_step"].at(1))

            @block.scalar
            def _(act):
                act.wait_ge(*k["vec_step"].at(1))
                act.dma_start(k.rows_in.rearrange("(n p) d -> p n d", p=KT),
                              routed_zeros[:, :].unsqueeze(1).broadcast_to([KT, tiles, D])).then_inc(
                                  k["rows_zeroed"].sem, 16)

            @block.sync
            def _(sp):
                sp.dma_start(k.X[:, :].rearrange("t (b d) -> t b d", b=B),
                             aps["in_x"].rearrange("b t d -> t b d")).then_inc(k["x_in"].sem, 16)
                sp.wait_ge(*k["x_in"].at(16))

            @block.gpsimd
            def _(g):
                g.memset(k.ident[:, :], 0.0).then_inc(k["pool_step"].sem, 1)
                g.wait_ge(*k["pool_step"].at(1))
                g.affine_select(out=k.ident[:, :], in_=k.ident[:, :], compare_op=ALU.not_equal, fill=1.0, base=0,
                                pattern=[[-1, KP]], channel_multiplier=1).then_inc(k["pool_step"].sem, 1)
                g.wait_ge(*k["pool_step"].at(2))
        k.advance(pool_step=2, x_in=16, vec_step=1)

        for name in layers:
            with ExitStack() as layer:
                if name in FFN and FFN[name]["experts"] == 8:
                    sub_routed_ffn(k, layer, name, packs, FFN[name])
                elif name in FFN:
                    sub_ffn(k, layer, name, packs, FFN[name])
                elif name in ATTENTION:
                    sub_attention(k, layer, name, packs, ATTENTION[name])
                else:
                    SUB[name](k, layer, name, packs)

        with nc.Block(no_gpsimd_drain=True) as block:
            @block.sync
            def _(sp):
                sp.dma_start(aps["out"].rearrange("b t d -> t b d"),
                             k.X[:, :].rearrange("t (b d) -> t b d", b=B)).then_inc(k["x_out"].sem, 16)
                sp.wait_ge(*k["x_out"].at(16))
                sp.wait_ge(*k["rows_zeroed"].at(16))



def by_rows(w, rows=KP):
    return w.reshape(-1, rows, w.shape[1]).transpose(1, 0, 2).reshape(rows, -1)


def columns(v, rows=KP):
    return v.reshape(-1, rows).T


def on_rows(v, parts=KP):
    return np.broadcast_to(v.reshape(1, -1), (parts, v.size))


def packed(fields):
    total = sum(a.shape[1] for a in fields.values())
    out, lay, off = np.zeros((KP, total), np.float32), {}, 0
    for name, a in fields.items():
        out[:a.shape[0], off:off + a.shape[1]] = a
        lay[name] = (off, a.shape[0], a.shape[1])
        off += a.shape[1]
    lay["_total"] = total
    return out, lay


def host_ffn(name, a):
    w = {key[len(name) + 1:]: v for key, v in a.items() if key.startswith(name + "_")}
    if name == "L0_ffn":
        small = dict(router=by_rows(w["router_w"]), b2=w["b2"][None])
        experts = [dict(w1=by_rows(w["w1"]), w2=by_rows(w["w2"]), b1=columns(w["b1"]))]
    elif name == "L1_ffn":
        small = dict(router=by_rows(w["Wr"]), router_b=w["br"][:, None], b2=w["b2"])
        experts = [dict(w1=by_rows(w["W1"][e]), w2=by_rows(w["W2"][e]), b1=columns(w["b1"][e])) for e in range(8)]
    elif name == "L2_ffn":
        small = dict(router=by_rows(w["w_gate"].T), b2=w["b2"])
        experts = [dict(w1=by_rows(w["W1"][e]), w2=by_rows(w["W2"][e]), b1=columns(w["b1"][e])) for e in range(8)]
    else:
        small = dict(b2=w["b2"][:4])
        experts = [dict(w1=by_rows(w["W1"][e]), w2=by_rows(w["W2"][e]), b1=columns(w["b1"][e])) for e in range(4)]
    done = [packed(e) for e in experts]
    return {name: packed(small), name + "_experts": (np.stack([d[0] for d in done]), done[0][1])}


def lay_out(inputs, layers):
    a = {n: np.asarray(v) for n, v in inputs.items()}
    out = {}
    for name in layers:
        host = host_ffn if name in FFN else host_attention if name in ATTENTION else HOST[name]
        out.update(host(name, a))
    return out


def kernel(**inputs):
    import concourse.bacc as bacc
    from concourse.bass_utils import run_bass_kernel_spmd

    laid = lay_out(inputs, LAYERS)
    arrays = {"in_" + n: np.ascontiguousarray(v[0]) for n, v in laid.items()}
    arrays["in_x"] = np.ascontiguousarray(inputs["x"])
    if "ctx_768" in inputs:
        arrays.update(host_context(inputs))
    nc = bacc.Bacc("TRN2", target_bir_lowering=False, num_devices=1)
    aps = {n: nc.dram_tensor(n, v.shape, mybir.dt.from_np(v.dtype), kind="ExternalInput").ap()
           for n, v in arrays.items()}
    aps["out"] = nc.dram_tensor("out", (B, T, D), F32, kind="ExternalOutput").ap()
    build_program(nc, aps, {n: v[1] for n, v in laid.items()}, LAYERS)
    r = run_bass_kernel_spmd(nc, [arrays], core_ids=[0])
    return r.results[0]["out"]


def host_context(inputs):
    c = np.asarray(inputs["ctx_768"]).transpose(0, 2, 1).reshape(B, 2, CR, S2).transpose(0, 2, 1, 3)
    m = np.asarray(inputs["mask_BxS2_bf1"]).view(np.uint8)
    return {"in_ctx": np.ascontiguousarray(c), "in_mask": np.ascontiguousarray(m)}

SUB = {"L3_xattn": sub_l3_xattn, "L0_attn": sub_l0_attn, "L1_attn": sub_l1_attn, "L2_attn": sub_l2_attn}
HOST = {"L3_xattn": host_l3_xattn, "L0_attn": host_l0_attn, "L1_attn": host_l1_attn, "L2_attn": host_l2_attn}
LAYERS = ["L0_attn", "L0_xattn", "L0_ffn", "L1_attn", "L1_xattn", "L1_ffn", "L2_attn", "L2_xattn", "L2_ffn",
          "L3_attn", "L3_xattn", "L3_ffn"]
```

```python
from contextlib import ExitStack

import numpy as np
import concourse.bass as bass
from concourse import mybir

F32 = mybir.dt.float32
U8 = mybir.dt.uint8
ACT = mybir.ActivationFunctionType
ALU = mybir.AluOpType
AX = mybir.AxisListType

T, B, D = 112, 16, 256
N = T * B
S2, CD = 375, 192
GB = 4
G = B // GB
GT = GB * T
KP = 128
KW, KN = 125, 3
CR = CD // 2
LN_EPS = 1e-5
RMS_EPS = 1e-6
HEAD = 64
CLAMP = 10000.0
FMAX = float(np.finfo(np.float32).max)


class Signal:

    def __init__(self, sem, base=HEAD):
        self.sem, self.base = sem, base

    def at(self, n):
        return self.sem, self.base + n

    def advance(self, n):
        self.base += n


class Chain:

    def __init__(self, eng, signal):
        self.eng, self.counter, self.n, self.start = eng, signal, 0, 0

    def link(self, ins):
        ins.then_inc(self.counter.sem, 1)
        self.n += 1
        self.eng.wait_ge(*self.counter.at(self.start + self.n))

    def mark(self, ins):
        ins.then_inc(self.counter.sem, 1)
        self.n += 1

    def turn(self, i, per):
        self.per, self.done = per, self.start + self.n
        self.start = self.done + i * per
        self.n = 0

    def end(self, trips):
        assert self.n == self.per, f"links a turn: {self.n}, stated: {self.per}"
        self.start, self.n = self.done + trips * self.per, 0

    def close(self):
        self.counter.advance(self.start + self.n)


class Core:

    def __init__(self, nc, ctx):
        self.nc, self.signals, self.tiles = nc, {}, 0
        self.X = ctx.enter_context(nc.sbuf_tensor("X", [T, B * D], F32))
        self.XT = ctx.enter_context(nc.sbuf_tensor("XT", [KP, 2, N], F32))
        self.ident = ctx.enter_context(nc.sbuf_tensor("ident", [KP, KP], F32))
        self.ps = ctx.enter_context(nc.psum_tensor("ps", [KP, 8, 512], F32))
        self.spark, self.sparks = ctx.enter_context(nc.sbuf_tensor("spark", [1, 64], F32)), 0
        for name in SIGNALS:
            self.signals[name] = Signal(ctx.enter_context(nc.semaphore(name)))
        for name in FROM_ZERO:
            self.signals[name] = Signal(ctx.enter_context(nc.semaphore(name)), 0)

    def tile(self, ctx, name, shape, dtype=F32):
        self.tiles += 1
        return ctx.enter_context(self.nc.sbuf_tensor(f"{name}_{self.tiles}", shape, dtype))

    def __getitem__(self, name):
        return self.signals[name]

    def advance(self, **events):
        for name, n in events.items():
            self.signals[name].advance(n)

    def table(self, act, fn):
        self.sparks += 1
        act.activation(self.spark[0:1, self.sparks:self.sparks + 1], self.spark[0:1, 0:1], fn)

    def x(self, b):
        return self.X[:, bass.ds(b * D, D)]


SIGNALS = ["vec_step", "act_step", "pool_step",
           "pack_in", "const_in", "ctx_in0", "ctx_in1", "exp_in0", "exp_in1", "toep_in0", "toep_in1",
           "x_in", "x_out", "stats_done", "rstd_done", "norm_done", "norm_tr", "norm_ev",
           "up_mm", "up_act", "up_used", "down_mm", "down_added",
           "lin_mm", "lin_act", "lin_vec",
           "rt_mm", "rt_ev", "rt_tr", "rt_lg", "gate_v", "gate_a", "gs_copied", "gt_tr", "gt_ev", "gb_mm", "gb_added",
           "rows_zeroed", "rg_const", "rg_chosen", "rg_counted", "rg_placed", "rg_in0", "rg_in1", "rg_out0",
           "rg_out1", "rg_turned", "rg_xT", "rg_up", "rg_hs", "rg_ut", "rg_first", "rg_hT", "rg_down", "rg_y",
           "rg_added",
           "v_padded", "ones_row", "kt_mm", "kt_ev", "v_mm", "v_ev", "qm_done", "ctx_used", "xs_copied",
           "sc_mm", "sc_read", "max_done", "exp_done", "prob_done", "pt_mm", "pt_ev_a",
           "pv_mm", "ot_ev", "wo_mm", "res_done", "mask_done",
           "p_a", "p_b", "p_c", "p_d", "p_e", "p_f", "p_g", "p_h", "p_i", "p_j", "p_k", "p_l"]


FROM_ZERO = ["rg_put", "rg_got0", "rg_got1", "rg_got2", "rg_got3"]


def pack_tile(k, ctx, name, layout):
    total = layout["_total"]
    tile = k.tile(ctx, name, [KP, total], F32)

    def view(field, parts=None):
        off, p, cols = layout[field]
        return tile[0:(parts or p), off:off + cols]

    return tile, view


def chunks(ap, n):
    return ap.rearrange("p (k n) -> p k n", k=n)


def layer_norm(k, pack=None, keep=None, rms_w=None, source=None, plain=True, ahead=None,
               meanwhile=None):
    nc = k.nc
    src = source if source is not None else k.X
    with ExitStack() as ctx:
        sb = lambda n, s: k.tile(ctx, n, s, F32)
        st = sb("ln_st", [T, B * 6])
        mv = sb("ln_mv", [T, B * 2])
        rstd = sb("ln_rstd", [T, B])
        both = sb("ln_both", [T, B])
        tmp = sb("ln_tmp", [T, B])
        half = sb("ln_half", [T, B])
        xn = sb("ln_xn", [T, 4, D])
        mv3 = mv[:, :].rearrange("p (b s) -> p b s", s=2)
        two_pows = plain and rms_w is not None
        HB = B // 2
        stats, rdone, ndone, ntr, nev = (k[s] for s in ("stats_done", "rstd_done", "norm_done", "norm_tr",
                                                        "norm_ev"))
        with nc.Block(no_gpsimd_drain=True) as block:
            @block.sync
            def _(sp):
                if pack is not None:
                    tile, dram, total = pack
                    h = total // 2
                    sp.dma_start(tile[:, 0:h], dram[:, 0:h]).then_inc(k["pack_in"].sem, 16)
                    sp.dma_start(tile[:, h:total], dram[:, h:total]).then_inc(k["pack_in"].sem, 16)
                    if ahead is not None:
                        ahead(sp)
                    sp.wait_ge(*k["pack_in"].at(32))

            @block.vector
            def _(v):
                ch = Chain(v, k["vec_step"])
                ch.link(v.memset(half[:, :], -0.5))

                def moments(h):
                    cols = slice(h * HB, (h + 1) * HB)
                    for b in range(h * HB, (h + 1) * HB):
                        last = v.bn_stats(st[:, 6 * b:6 * b + 6], src[:, b * D:(b + 1) * D])
                    ch.link(last)
                    for b in range(h * HB, (h + 1) * HB):
                        last = v.bn_aggr(mv[:, 2 * b:2 * b + 2], st[:, 6 * b:6 * b + 6])
                    ch.link(last)
                    if plain:
                        v.tensor_scalar(tmp[:, cols], mv3[:, cols, 1], LN_EPS, None, ALU.add).then_inc(
                            stats.sem, 1)
                    else:
                        ch.link(v.tensor_tensor(both[:, cols], mv3[:, cols, 0], mv3[:, cols, 0], ALU.mult))
                        ch.link(v.tensor_tensor(both[:, cols], both[:, cols], mv3[:, cols, 1], ALU.add))
                        v.tensor_scalar(tmp[:, cols], both[:, cols], RMS_EPS, None, ALU.add).then_inc(stats.sem, 1)

                def second(h):
                    cols = slice(h * HB, (h + 1) * HB)
                    v.wait_ge(*rdone.at(h + 1))
                    ch.link(v.tensor_tensor(both[:, cols], rstd[:, cols], rstd[:, cols], ALU.mult))
                    ch.link(v.tensor_tensor(both[:, cols], both[:, cols], mv3[:, cols, 1], ALU.mult))
                    v.tensor_scalar(tmp[:, cols], both[:, cols], RMS_EPS, None, ALU.add).then_inc(stats.sem, 1)

                scale = both if two_pows else rstd

                def normalise(h):
                    v.wait_ge(*rdone.at(h + 1 + (2 if two_pows else 0)))
                    if two_pows:
                        cols = slice(h * HB, (h + 1) * HB)
                        ch.link(v.tensor_tensor(both[:, cols], both[:, cols], rstd[:, cols], ALU.mult))
                    for b in range(h * HB, (h + 1) * HB):
                        u = b % 4
                        v.wait_ge(*ntr.at(b - 3))
                        xin = src[:, b * D:(b + 1) * D]
                        if plain:
                            v.tensor_scalar(xn[:, u, :], xin, mv[:, 2 * b:2 * b + 1], scale[:, b:b + 1],
                                            ALU.subtract, ALU.mult).then_inc(ndone.sem, 1)
                            if keep is not None:
                                v.tensor_scalar(keep[:, b * D:(b + 1) * D], xin, mv[:, 2 * b:2 * b + 1],
                                                rstd[:, b:b + 1], ALU.subtract, ALU.mult)
                        else:
                            v.tensor_scalar(xn[:, u, :], xin, scale[:, b:b + 1], None,
                                            ALU.mult).then_inc(ndone.sem, 1)

                for step in (moments, second, normalise) if two_pows else (moments, normalise):
                    for h in range(2):
                        step(h)
                ch.close()

            @block.gpsimd
            def _(g):
                for n in range(4 if two_pows else 2):
                    cols = slice(n % 2 * HB, (n % 2 + 1) * HB)
                    out = rstd if n < 2 else both
                    g.wait_ge(*stats.at(n + 1))
                    g.tensor_tensor(out[:, cols], tmp[:, cols], half[:, cols], ALU.pow).then_inc(rdone.sem, 1)
                if meanwhile is not None:
                    meanwhile(g)

            @block.tensor
            def _(pe):
                with pe.Fori(0, B // 4) as i:
                    for u in range(4):
                        pe.wait_ge(*ndone.at(4 * i + u + 1))
                        pe.wait_ge(*nev.at(4 * i + u - 3))
                        for c in range(2):
                            last = pe.transpose(k.ps[0:KP, u, c * T:(c + 1) * T], xn[:, u, c * KP:(c + 1) * KP],
                                                k.ident[0:T, 0:T])
                        last.then_inc(ntr.sem, 1)

            @block.scalar
            def _(act):
                if rms_w is not None and pack is not None:
                    act.wait_ge(*k["pack_in"].at(32))
                k.table(act, ACT.Copy)
                with act.Fori(0, B // 4) as i:
                    for u in range(4):
                        act.wait_ge(*ntr.at(4 * i + u + 1))
                        if rms_w is None:
                            last = act.activation(k.XT[:, :, bass.ds((4 * i + u) * T, T)],
                                                  chunks(k.ps[0:KP, u, 0:2 * T], 2), ACT.Copy)
                        else:
                            for c in range(2):
                                last = act.activation(k.XT[:, c, bass.ds((4 * i + u) * T, T)],
                                                      k.ps[0:KP, u, c * T:(c + 1) * T], ACT.Copy,
                                                      scale=rms_w[:, c:c + 1])
                        last.then_inc(nev.sem, 1)
        k.advance(pack_in=32 if pack is not None else 0, stats_done=4 if two_pows else 2,
                  rstd_done=4 if two_pows else 2, norm_done=B, norm_tr=B, norm_ev=B)


def feed_forward(k, name, dram, layout, experts, rows, hidden, gated, act_fn, gates=None, src=None):
    nc = k.nc
    src = k.XT if src is None else src
    ring = min(hidden, 4)
    up, used, down, added = k["up_mm"], k["up_used"], k["down_mm"], k["down_added"]
    acted = k["up_act"]
    w_in = [k["exp_in0"], k["exp_in1"]]
    pairs = max(experts // 2, 1)
    per_pair = min(experts, 2)
    with ExitStack() as ctx:
        total = layout["_total"]
        slots = [k.tile(ctx, f"{name}_w{e}", [KP, total], F32) for e in range(per_pair)]
        hT = k.tile(ctx, f"{name}_h", [rows, 2, hidden, GT], F32)
        if gated:
            first = k.tile(ctx, f"{name}_a", [rows, 2, GT], F32)

        def part(slot, field):
            off, p, cols = layout[field]
            return slots[slot][0:p, off:off + cols]

        w1 = [chunks(part(s, "w1"), 2) for s in range(per_pair)]
        w2 = [chunks(part(s, "w2"), hidden) for s in range(per_pair)]
        b1 = [part(s, "b1") for s in range(per_pair)] if "b1" in layout else None

        def steps(eng):
            if pairs == 1:
                for ep in range(per_pair):
                    with eng.Fori(0, G // 2) as g0:
                        for gu in range(2):
                            yield 2 * g0 + gu + ep * G, ep, gu, ep, 2 * g0 + gu
            else:
                with eng.Fori(0, pairs) as ei:
                    for ep in range(per_pair):
                        with eng.Fori(0, G // 2) as g0:
                            for gu in range(2):
                                yield (ei * 2 + ep) * G + 2 * g0 + gu, ep, gu, ei * 2 + ep, 2 * g0 + gu

        with nc.Block(no_gpsimd_drain=True) as block:
            @block.sync
            def _(sp):
                if pairs == 1:
                    for ep in range(per_pair):
                        sp.dma_start(slots[ep][:, :], dram[ep, :, :]).then_inc(w_in[ep].sem, 16)
                else:
                    with sp.Fori(0, pairs) as ei:
                        for ep in range(2):
                            sp.wait_ge(*down.at((ei * 2 + ep - 1) * G))
                            sp.dma_start(slots[ep][:, :], dram[bass.ds(ei * 2 + ep, 1), :, :].rearrange(
                                "e p n -> (e p) n")).then_inc(w_in[ep].sem, 16)

            @block.tensor
            def _(pe):
                for t, s, h, e, g in steps(pe):
                    turn = e // 2 if isinstance(e, int) else None
                    pe.wait_ge(*w_in[s].at(16 * (e // 2 + 1) if turn is not None else 8 * (e - s) + 16))
                    for m in range(hidden):
                        if gated:
                            pe.wait_ge(*used.at(t * hidden + m - 1))
                        else:
                            pe.wait_ge(*acted.at(t * hidden + m - ring + 1))
                        for half in range(2 if gated else 1):
                            bank = 2 * (m % 2) + half if gated else m % ring
                            col = (half * hidden + m) * rows
                            for c in range(2):
                                last = pe.matmul(k.ps[0:rows, bank, 0:GT], w1[s][:, c, col:col + rows],
                                                 src[:, c, bass.ds(g * GT, GT)], start=(c == 0), stop=(c == 1))
                        last.then_inc(up.sem, 1)
                    for m in range(hidden):
                        if gated:
                            pe.wait_ge(*used.at(t * hidden + m + 1))
                        else:
                            pe.wait_ge(*acted.at(t * hidden + m + 1))
                        for j in range(GB):
                            if m == 0:
                                pe.wait_ge(*added.at((t - 1) * GB + j + 1))
                            last = pe.matmul(k.ps[0:T, 4 + j, 0:D], hT[:, h, m, j * T:(j + 1) * T], w2[s][:, m, :],
                                             start=(m == 0), stop=(m == hidden - 1))
                    last.then_inc(down.sem, 1)

            @block.scalar
            def _(act):
                for t, s, h, e, g in steps(act):
                    if gated:
                        for m in range(hidden):
                            act.wait_ge(*up.at(t * hidden + m + 1))
                            act.wait_ge(*used.at(t * hidden + m - 1))
                            act.activation(first[:, m % 2, :], k.ps[0:rows, 2 * (m % 2), 0:GT], act_fn,
                                           bias=b1[s][:, m:m + 1] if b1 else 0.0).then_inc(acted.sem, 1)
                    else:
                        act.wait_ge(*down.at(t - 1))
                        for m in range(hidden):
                            act.wait_ge(*up.at(t * hidden + m + 1))
                            act.activation(hT[:, h, m, :], k.ps[0:rows, m % ring, 0:GT], act_fn,
                                           bias=b1[s][:, m:m + 1] if b1 else 0.0).then_inc(acted.sem, 1)

            @block.vector
            def _(v):
                for t, s, h, e, g in steps(v):
                    if gated:
                        v.wait_ge(*down.at(t - 1))
                        for m in range(hidden):
                            v.wait_ge(*acted.at(t * hidden + m + 1))
                            second = k.ps[0:rows, 2 * (m % 2) + 1, 0:GT]
                            if b1:
                                v.scalar_tensor_tensor(hT[:, h, m, :], second, b1[s][:, hidden + m:hidden + m + 1],
                                                       first[:, m % 2, :], ALU.add, ALU.mult).then_inc(used.sem, 1)
                            else:
                                v.tensor_tensor(hT[:, h, m, :], second, first[:, m % 2, :],
                                                ALU.mult).then_inc(used.sem, 1)
                    v.wait_ge(*down.at(t + 1))
                    for j in range(GB):
                        b = g * GB + j
                        if gates is None:
                            v.tensor_tensor(k.x(b), k.ps[0:T, 4 + j, 0:D], k.x(b), ALU.add).then_inc(added.sem, 1)
                        else:
                            v.scalar_tensor_tensor(k.x(b), k.ps[0:T, 4 + j, 0:D],
                                                   gates[:, bass.ds(e * B + b, 1)], k.x(b), ALU.mult,
                                                   ALU.add).then_inc(added.sem, 1)
        n = experts * G
        k.advance(up_mm=n * hidden, up_act=n * hidden, up_used=n * hidden if gated else 0, down_mm=n,
                  down_added=n * GB, exp_in0=16 * ((experts + 1) // 2), exp_in1=16 * (experts // 2))


def router(k, E, w, bias, gates, mode):
    nc = k.nc
    with ExitStack() as ctx:
        sb = lambda n, s: k.tile(ctx, n, s, F32)
        lt = sb("rt_lt", [E, 2, GT])
        lg = sb("rt_lg_t", [T, B, E])
        ahead = sb("rt_ahead", [T, B, E])
        cmp = sb("rt_cmp", [T, B, E])
        ex = sb("rt_ex", [T, B, E])
        one = sb("rt_one", [T, B])
        inv = sb("rt_inv", [T, B])
        mm, ev, tr, lgd = k["rt_mm"], k["rt_ev"], k["rt_tr"], k["rt_lg"]
        gv, ga = k["gate_v"], k["gate_a"]
        n_g = 1 if mode == "topk_sum" else E
        g3 = gates[:, :].rearrange("p (e b) -> p b e", b=B)
        with nc.Block(no_gpsimd_drain=True) as block:
            @block.tensor
            def _(pe):
                def logits(g):
                    pe.wait_ge(*ev.at(g - 1))
                    for c in range(2):
                        last = pe.matmul(k.ps[0:E, g % 2, 0:GT], w[:, c, :], k.XT[:, c, g * GT:(g + 1) * GT],
                                         start=(c == 0), stop=(c == 1))
                    last.then_inc(mm.sem, 1)

                logits(0)
                for g in range(G):
                    u = g % 2
                    if g + 1 < G:
                        logits(g + 1)
                    pe.wait_ge(*ev.at(g + 1))
                    pe.wait_ge(*lgd.at(g - 1))
                    for j in range(GB):
                        last = pe.transpose(k.ps[0:T, 2 + u, j * E:(j + 1) * E], lt[:, u, j * T:(j + 1) * T],
                                            k.ident[0:E, 0:E])
                    last.then_inc(tr.sem, 1)

            @block.scalar
            def _(act):
                k.table(act, ACT.Identity)
                with act.Fori(0, G // 2) as i:
                    for u in range(2):
                        act.wait_ge(*mm.at(2 * i + u + 1))
                        act.wait_ge(*tr.at(2 * i + u - 1))
                        act.activation(lt[:, u, :], k.ps[0:E, u, 0:GT], ACT.Identity,
                                       bias=bias if bias is not None else 0.0).then_inc(ev.sem, 1)
                act.wait_ge(*gv.at(1))
                act.activation(ex[:, :, :], ex[:, :, :], ACT.Exp).then_inc(ga.sem, 1)

            @block.vector
            def _(v):
                ch = Chain(v, k["vec_step"])
                with v.Fori(0, G // 2) as i:
                    for u in range(2):
                        v.wait_ge(*tr.at(2 * i + u + 1))
                        v.tensor_copy(lg[:, bass.ds((2 * i + u) * GB, GB), :],
                                      chunks(k.ps[0:T, 2 + u, 0:GB * E], GB)).then_inc(lgd.sem, 1)
                v.wait_ge(*lgd.at(G))
                ch.link(v.memset(ahead[:, :, :], 0.0))
                for e in range(E):
                    other = lg[:, :, e:e + 1]
                    if e + 1 < E:
                        v.tensor_tensor(cmp[:, :, e + 1:E], other.broadcast_to([T, B, E - e - 1]),
                                        lg[:, :, e + 1:E], ALU.is_ge)
                    ch.link(v.tensor_tensor(cmp[:, :, 0:e + 1], other.broadcast_to([T, B, e + 1]),
                                            lg[:, :, 0:e + 1], ALU.is_gt))
                    ch.link(v.tensor_tensor(ahead[:, :, :], ahead[:, :, :], cmp[:, :, :], ALU.add))
                ch.link(v.tensor_scalar(ahead[:, :, :], ahead[:, :, :], 2.0, None, ALU.is_lt))
                ch.link(v.tensor_reduce(one[:, :], lg[:, :, :], AX.X, ALU.max))
                v.tensor_tensor(ex[:, :, :], lg[:, :, :], one[:, :].unsqueeze(2).broadcast_to([T, B, E]),
                                ALU.subtract).then_inc(gv.sem, 1)
                v.wait_ge(*ga.at(1))
                if mode in ("topk_sum", "topk_softmax"):
                    ch.link(v.tensor_reduce(one[:, :], ex[:, :, :], AX.X, ALU.add))
                    ch.link(v.reciprocal(inv[:, :], one[:, :]))
                    ch.link(v.tensor_tensor(ex[:, :, :], ex[:, :, :],
                                            inv[:, :].unsqueeze(2).broadcast_to([T, B, E]), ALU.mult))
                if mode == "topk_softmax":
                    ch.link(v.tensor_tensor(g3, ex[:, :, :], ahead[:, :, :], ALU.mult))
                else:
                    ch.link(v.tensor_tensor(ex[:, :, :], ex[:, :, :], ahead[:, :, :], ALU.mult))
                    ch.link(v.tensor_reduce(one[:, :], ex[:, :, :], AX.X, ALU.add))
                    ch.link(v.reciprocal(inv[:, :], one[:, :]))
                    if mode == "softmax_topk":
                        ch.link(v.tensor_tensor(g3, ex[:, :, :], inv[:, :].unsqueeze(2).broadcast_to([T, B, E]),
                                                ALU.mult))
                    else:
                        ch.link(v.tensor_tensor(ex[:, :, :], ex[:, :, :],
                                                inv[:, :].unsqueeze(2).broadcast_to([T, B, E]), ALU.mult))
                        ch.link(v.tensor_reduce(gates[:, :], ex[:, :, :], AX.X, ALU.add))
                ch.close()
        k.advance(rt_mm=G, rt_ev=G, rt_tr=G, rt_lg=G, gate_v=1, gate_a=1)


def add_second_biases(k, gates, n_g, b2, meanwhile=None):
    g3 = gates[:, :].rearrange("p (e b) -> p b e", b=B)
    with ExitStack() as ctx:
        gs = k.tile(ctx, "gates_in_order", [T, B, n_g], F32)
        gT = k.tile(ctx, "gates_turned", [n_g, B, T], F32)
        with k.nc.Block(no_gpsimd_drain=True) as block:
            if meanwhile is not None:
                block.gpsimd(meanwhile)

            @block.tensor
            def _(pe):
                pe.wait_ge(*k["gs_copied"].at(1))
                for q in range(B // 4):
                    for j in range(4):
                        last = pe.transpose(k.ps[0:n_g, q, j * T:(j + 1) * T], gs[:, 4 * q + j, :],
                                            k.ident[0:T, 0:T])
                    last.then_inc(k["gt_tr"].sem, 1)
                for b in range(0, B, 2):
                    pe.wait_ge(*k["gt_ev"].at(b // 4 + 1))
                    pe.wait_ge(*k["gb_added"].at(b // 2 - 1))
                    for j in range(2):
                        last = pe.matmul(k.ps[0:T, 4 + b // 2 % 2, j * D:(j + 1) * D], gT[:, b + j, :], b2,
                                         start=True, stop=True)
                    last.then_inc(k["gb_mm"].sem, 1)

            @block.scalar
            def _(act):
                for q in range(B // 4):
                    act.wait_ge(*k["gt_tr"].at(q + 1))
                    act.activation(gT[:, 4 * q:4 * q + 4, :], chunks(k.ps[0:n_g, q, 0:4 * T], 4),
                                   ACT.Copy).then_inc(k["gt_ev"].sem, 1)

            @block.vector
            def _(v):
                v.tensor_copy(gs[:, :, :], g3).then_inc(k["gs_copied"].sem, 1)
                for b in range(0, B, 2):
                    v.wait_ge(*k["gb_mm"].at(b // 2 + 1))
                    v.tensor_tensor(k.X[:, b * D:(b + 2) * D], k.ps[0:T, 4 + b // 2 % 2, 0:2 * D],
                                    k.X[:, b * D:(b + 2) * D], ALU.add).then_inc(k["gb_added"].sem, 1)
        k.advance(gs_copied=1, gt_tr=B // 4, gt_ev=B // 4, gb_mm=B // 2, gb_added=B // 2)




def sub_ffn(k, ctx, name, packs, spec):
    lay, dram = packs[name]
    tile, p = pack_tile(k, ctx, name + "_pack", lay)
    gates = k.tile(ctx, name + "_gates", [T, spec["experts"] * B], F32)
    layer_norm(k, pack=(tile, dram, lay["_total"]))
    if spec["mode"] == "fixed":
        fixed_gates(k, gates, p("b2"))
    else:
        E = lay["router"][2] // 2
        gates_n = 1 if spec["mode"] == "topk_sum" else E
        router(k, E, chunks(p("router"), 2), p("router_b") if "router_b" in lay else None, gates, spec["mode"])
        add_second_biases(k, gates, gates_n, p("b2"))
    elay, edram = packs[name + "_experts"]
    feed_forward(k, name, edram, elay, spec["experts"], KP, spec["hidden"], spec["gated"], spec["act"], gates)


def fixed_gates(k, gates, b2):
    nc = k.nc
    logits = [0.0, 100.0, 0.0, 0.0]
    E = len(logits)
    with ExitStack() as ctx:
        sb = lambda n, s: k.tile(ctx, n, s, F32)
        ex = sb("fg_ex", [T, E])
        sm = sb("fg_sum", [T, 1])
        gT = sb("fg_gT", [E, T])
        br = sb("fg_b", [T, D])
        with nc.Block(no_gpsimd_drain=True) as block:
            @block.vector
            def _(v):
                ch = Chain(v, k["vec_step"])
                for e, x in enumerate(logits):
                    last = v.memset(ex[:, e:e + 1], x - max(logits))
                last.then_inc(k["gate_v"].sem, 1)
                v.wait_ge(*k["gate_a"].at(1))
                ch.link(v.tensor_reduce(sm[:, :], ex[:, :], AX.X, ALU.add))
                ch.link(v.reciprocal(sm[:, :], sm[:, :]))
                ch.link(v.tensor_scalar(ex[:, :], ex[:, :], sm[:, :], None, ALU.mult))
                for e in range(E):
                    last = v.tensor_copy(gates[:, e * B:(e + 1) * B], ex[:, e:e + 1].broadcast_to([T, B]))
                last.then_inc(k["gate_v"].sem, 1)
                v.wait_ge(*k["gb_mm"].at(1))
                ch.link(v.tensor_copy(br[:, :], k.ps[0:T, 6, 0:D]))
                v.tensor_tensor(k.X[:, :].rearrange("p (b d) -> p b d", b=B),
                                k.X[:, :].rearrange("p (b d) -> p b d", b=B),
                                br[:, :].unsqueeze(1).broadcast_to([T, B, D]), ALU.add)
                ch.close()

            @block.scalar
            def _(act):
                act.wait_ge(*k["gate_v"].at(1))
                act.activation(ex[:, :], ex[:, :], ACT.Exp).then_inc(k["gate_a"].sem, 1)
                act.wait_ge(*k["gt_tr"].at(1))
                act.activation(gT[:, :], k.ps[0:E, 4, 0:T], ACT.Copy).then_inc(k["gt_ev"].sem, 1)

            @block.tensor
            def _(pe):
                pe.wait_ge(*k["gate_v"].at(2))
                pe.transpose(k.ps[0:E, 4, 0:T], ex[:, :], k.ident[0:T, 0:T]).then_inc(k["gt_tr"].sem, 1)
                pe.wait_ge(*k["gt_ev"].at(1))
                pe.matmul(k.ps[0:T, 6, 0:D], gT[:, :], b2, start=True, stop=True).then_inc(k["gb_mm"].sem, 1)
        k.advance(gate_v=2, gate_a=1, gt_tr=1, gt_ev=1, gb_mm=1)


FFN = {
    "L0_ffn": dict(mode="topk_sum", experts=1, hidden=8, gated=False, act=ACT.Gelu_apprx_tanh),
    "L1_ffn": dict(mode="softmax_topk", experts=8, hidden=4, gated=True, act=ACT.Silu),
    "L2_ffn": dict(mode="topk_softmax", experts=8, hidden=8, gated=False, act=ACT.Gelu),
    "L3_ffn": dict(mode="fixed", experts=4, hidden=4, gated=False, act=ACT.Relu),
}




KT = 128
PICKS = 2


def token_tiles(E):
    return (PICKS * N + E * (KT - 1)) // KT


class Routing:

    def __init__(self, k, ctx, E):
        self.tiles = token_tiles(E)
        self.slot = k.tile(ctx, "slot", [T, PICKS, B], mybir.dt.int32)
        self.weight = k.tile(ctx, "weight", [T, PICKS, B], F32)
        self.expert = k.tile(ctx, "expert", [1, self.tiles], mybir.dt.int32)


def place_tokens(k, route, gates, E, steps, turns):
    nc, s = k.nc, k.signals
    most = N // KT
    none = float((route.tiles + 1) * KT)
    with ExitStack() as ctx:
        sb = lambda n, sh: k.tile(ctx, n, sh, F32)
        earlier, ones = sb("earlier", [T, T]), sb("ones", [T, T])
        chosen, slot, hit = sb("chosen", [T, E, B]), sb("slot_f", [T, E, B]), sb("hit", [T, E, B])
        total, sums = sb("total", [T, E, B]), sb("sums", [T, 2, E, B])
        over, used = sb("over", [T, E, most]), sb("used", [T, E])
        ends, start = sb("ends", [T, 2, E]), sb("start", [T, E])
        passed, owner = sb("passed", [1, route.tiles, E]), sb("owner", [1, route.tiles])
        pick = sb("pick", [T, PICKS, B])
        two = sb("two", [T, B])
        flat = lambda ap: ap[:, :, :].rearrange("p e b -> p (e b)")
        by_token = lambda ap: ap[:, :, :].rearrange("p e b -> p b e")
        g3 = gates[:, :].rearrange("p (e b) -> p e b", e=E)
        with nc.Block(no_gpsimd_drain=True) as block:
            @block.gpsimd
            def _(g):
                g.memset(ones[:, :], 1.0).then_inc(s["rg_const"].sem, 1)
                g.wait_ge(*s["rg_const"].at(1))
                g.affine_select(out=earlier[:, :], in_=ones[:, :], compare_op=ALU.is_gt, fill=0.0, base=0,
                                pattern=[[1, T]], channel_multiplier=-1).then_inc(s["rg_const"].sem, 1)

            @block.tensor
            def _(pe):
                pe.wait_ge(*s["rg_const"].at(2))
                pe.wait_ge(*s["rg_chosen"].at(1))
                pe.matmul(k.ps[0:T, 0, 0:E * B], earlier[:, :], flat(chosen), start=True, stop=True)
                pe.matmul(k.ps[0:T, 1, 0:E * B], ones[:, :], flat(chosen), start=True, stop=True).then_inc(
                    s["rg_counted"].sem, 1)

            @block.vector
            def _(v):
                ch = Chain(v, s["vec_step"])
                v.tensor_scalar(flat(chosen), gates[:, :], 0.0, None, ALU.is_gt).then_inc(s["rg_chosen"].sem, 1)
                v.wait_ge(*s["rg_chosen"].at(1))
                v.wait_ge(*s["rg_counted"].at(1))
                v.tensor_copy(flat(total), k.ps[0:T, 1, 0:E * B])
                ch.link(v.tensor_copy(sums[:, 0, :, :].rearrange("p e b -> p (e b)"), k.ps[0:T, 1, 0:E * B]))
                at = 0
                reach = 1
                while reach < B:
                    v.tensor_copy(sums[:, 1 - at, :, 0:reach], sums[:, at, :, 0:reach])
                    ch.link(v.tensor_tensor(sums[:, 1 - at, :, reach:B], sums[:, at, :, reach:B],
                                            sums[:, at, :, 0:B - reach], ALU.add))
                    at, reach = 1 - at, 2 * reach
                count = sums[:, at, :, B - 1:B]
                ch.link(v.tensor_tensor(over[:, :, :], count.broadcast_to([T, E, most]), steps[0:T, :, :],
                                        ALU.is_gt))
                ch.link(v.tensor_reduce(used[:, :], over[:, :, :], AX.X, ALU.add))
                ch.link(v.tensor_copy(ends[:, 0, :], used[:, :]))
                ea, reach = 0, 1
                while reach < E:
                    v.tensor_copy(ends[:, 1 - ea, 0:reach], ends[:, ea, 0:reach])
                    ch.link(v.tensor_tensor(ends[:, 1 - ea, reach:E], ends[:, ea, reach:E],
                                            ends[:, ea, 0:E - reach], ALU.add))
                    ea, reach = 1 - ea, 2 * reach
                ch.link(v.tensor_tensor(start[:, :], ends[:, ea, :], used[:, :], ALU.subtract))
                ch.link(v.tensor_scalar(start[:, :], start[:, :], float(KT), None, ALU.mult))
                ch.link(v.tensor_tensor(slot[:, :, :], sums[:, at, :, :], total[:, :, :], ALU.subtract))
                ch.link(v.tensor_tensor(flat(slot), flat(slot), k.ps[0:T, 0, 0:E * B], ALU.add))
                ch.link(v.tensor_tensor(slot[:, :, :], slot[:, :, :],
                                        start[:, :].unsqueeze(2).broadcast_to([T, E, B]), ALU.add))
                ch.link(v.scalar_tensor_tensor(hit[:, :, :], slot[:, :, :], none, chosen[:, :, :], ALU.subtract,
                                               ALU.mult))
                ch.link(v.tensor_reduce(pick[:, 0, :], by_token(hit), AX.X, ALU.min))
                ch.link(v.tensor_scalar(pick[:, 0, :], pick[:, 0, :], none, None, ALU.add))
                ch.link(v.scalar_tensor_tensor(hit[:, :, :], slot[:, :, :], 1.0, chosen[:, :, :], ALU.add,
                                               ALU.mult))
                ch.link(v.tensor_reduce(pick[:, 1, :], by_token(hit), AX.X, ALU.max))
                ch.link(v.tensor_scalar(pick[:, 1, :], pick[:, 1, :], 1.0, None, ALU.subtract))
                ch.link(v.tensor_tensor(pick[:, 1, :], pick[:, 1, :], pick[:, 0, :], ALU.max))
                v.tensor_copy(route.slot[:, :, :], pick[:, :, :]).then_inc(s["rg_placed"].sem, 1)
                for n in range(PICKS):
                    ch.link(v.tensor_tensor(hit[:, :, :], slot[:, :, :],
                                            pick[:, n:n + 1, :].broadcast_to([T, E, B]), ALU.is_equal))
                    ch.link(v.tensor_tensor(hit[:, :, :], hit[:, :, :], g3, ALU.mult))
                    ch.link(v.tensor_reduce(route.weight[:, n, :], by_token(hit), AX.X, ALU.add))
                ch.link(v.tensor_tensor(two[:, :], pick[:, 1, :], pick[:, 0, :], ALU.is_gt))
                v.tensor_tensor(route.weight[:, 1, :], route.weight[:, 1, :], two[:, :], ALU.mult)
                ch.link(v.tensor_tensor(passed[:, :, :], turns[:, :, :],
                                        ends[0:1, ea:ea + 1, :].broadcast_to([1, route.tiles, E]), ALU.is_ge))
                ch.link(v.tensor_reduce(owner[:, :], passed[:, :, :], AX.X, ALU.add))
                ch.link(v.tensor_scalar(owner[:, :], owner[:, :], float(E - 1), None, ALU.min))
                v.tensor_copy(route.expert[:, :], owner[:, :])
                ch.close()
        k.advance(rg_const=2, rg_chosen=1, rg_counted=1, rg_placed=1)


def scatter_tokens(k, route, xn, rows):
    s = k.signals

    def scatter(g):
        g.wait_ge(*s["rows_zeroed"].at(16))
        for b in range(B):
            for n in range(PICKS):
                g.indirect_dma_start(rows[:, :],
                                     bass.IndirectOffsetOnAxis(ap=route.slot[:, n, b:b + 1], axis=0),
                                     xn[:, b * D:(b + 1) * D], None).then_inc(s["rg_put"].sem, 16)
        g.wait_ge(*s["rg_put"].at(16 * PICKS * B))
    return scatter


def expert_tiles(k, route, name, weights, layout, rows_in, rows_out, hidden, gated, act_fn):
    nc, s = k.nc, k.signals
    NT, total = route.tiles, layout["_total"]
    o1, o2, ob = (layout[f][0] for f in ("w1", "w2", "b1"))
    turned = (2 if gated else 1) * hidden
    wide = turned * KP
    halves = wide // 512
    assert halves == 2 and NT % 2 == 1
    with ExitStack() as ctx:
        sb = lambda n, sh: k.tile(ctx, name + "_" + n, sh, F32)
        xs, xT = sb("xs", [KT, 2, D]), sb("xsT", [KP, 2, 2, KT])
        hs = sb("hs", [KT, wide])
        hT = sb("hT", [KP, 2, hidden, KT])
        if gated:
            first = sb("first", [KP, hidden, KT])
        y = sb("y", [KT, 2, D])
        x_in, y_out = [s["rg_in0"], s["rg_in1"]], [s["rg_out0"], s["rg_out1"]]

        def expert(eng, t):
            return nc.values_load(route.expert[0:1, bass.ds(t, 1)], engines=[eng], min_val=0,
                                  max_val=layout["_experts"] - 1,
                                  skip_runtime_bounds_check_because="place_tokens clamps it to the experts")

        def in_turn(eng, step):
            step(0, 0)
            with eng.Fori(0, NT // 2) as i:
                for u in range(2):
                    step(2 * i + u + 1, 1 - u)

        with nc.Block(no_gpsimd_drain=True) as block:
            @block.sync
            def _(sp):
                def load(t, u):
                    sp.dma_start(xs[:, u, :], rows_in[bass.ds(t * KT, KT), :]).then_inc(x_in[u].sem, 16)

                def store(t, u):
                    sp.wait_ge(*s["rg_y"].at(t + 1))
                    sp.dma_start(rows_out[bass.ds(t * KT, KT), :], y[:, u, :]).then_inc(y_out[u].sem, 16)

                load(0, 0)
                load(1, 1)
                sp.wait_ge(*s["rg_turned"].at(1))
                load(2, 0)
                with sp.Fori(0, NT // 2) as i:
                    for u in range(2):
                        t = 2 * i + u + 1
                        sp.wait_ge(*s["rg_turned"].at(t + 1))
                        load(t + 2, 1 - u)
                        store(t - 1, u)
                store(NT - 1, 0)
                sp.wait_ge(*x_in[0].at(16 * ((NT + 3) // 2)))
                sp.wait_ge(*x_in[1].at(16 * ((NT + 2) // 2)))
                sp.wait_ge(*y_out[0].at(16 * ((NT + 1) // 2)))
                sp.wait_ge(*y_out[1].at(16 * (NT // 2)))

            @block.tensor
            def _(pe):
                def turn_tokens(t, u):
                    pe.wait_ge(*x_in[u].at(8 * (t - u) + 16))
                    pe.wait_ge(*s["rg_xT"].at(t - 1))
                    for c in range(2):
                        last = pe.transpose(k.ps[:, 4 + u, c * KT:(c + 1) * KT], xs[:, u, c * KP:(c + 1) * KP],
                                            k.ident[:, :])
                    last.then_inc(s["rg_turned"].sem, 1)

                def first_product(t, u):
                    e = expert(mybir.EngineType.PE, t)
                    pe.wait_ge(*s["rg_xT"].at(t + 1))
                    for half in range(2):
                        pe.wait_ge(*s["rg_hs"].at(2 * t + half - 1))
                        for c in range(2):
                            last = pe.matmul(k.ps[:, half, 0:512], xT[:, u, c, :],
                                             weights[:, bass.ds(e * total + (o1 + c * wide + half * 512), 512)],
                                             start=(c == 0), stop=(c == 1))
                        last.then_inc(s["rg_up"].sem, 1)

                def second_product(t, u):
                    e = expert(mybir.EngineType.PE, t)
                    pe.wait_ge(*s["rg_hT"].at(t + 1))
                    pe.wait_ge(*s["rg_y"].at(t - 1))
                    for m in range(hidden):
                        last = pe.matmul(k.ps[:, 6 + u, 0:D], hT[:, u, m, :],
                                         weights[:, bass.ds(e * total + (o2 + m * D), D)],
                                         start=(m == 0), stop=(m == hidden - 1))
                    last.then_inc(s["rg_down"].sem, 1)

                def turn_hidden(t, u):
                    for half in range(2):
                        pe.wait_ge(*s["rg_hs"].at(2 * t + half + 1))
                        pe.wait_ge(*s["rg_first" if gated and half == 0 else "rg_hT"].at(t))
                        for j in range(4):
                            last = pe.transpose(k.ps[:, 2 + half, j * KT:(j + 1) * KT],
                                                hs[:, (half * 4 + j) * KP:(half * 4 + j + 1) * KP], k.ident[:, :])
                        last.then_inc(s["rg_ut"].sem, 1)

                turn_tokens(0, 0)
                first_product(0, 0)
                turn_tokens(1, 1)
                turn_hidden(0, 0)
                with pe.Fori(0, NT // 2) as i:
                    for u in range(2):
                        t = 2 * i + u + 1
                        first_product(t, 1 - u)
                        turn_tokens(t + 1, u)
                        second_product(t - 1, u)
                        turn_hidden(t, 1 - u)
                second_product(NT - 1, 0)

            @block.scalar
            def _(act):
                def copy_tokens(t, u):
                    act.wait_ge(*s["rg_turned"].at(t + 1))
                    act.wait_ge(*s["rg_up"].at(2 * (t - 1)))
                    act.activation(xT[:, u, :, :], chunks(k.ps[:, 4 + u, 0:2 * KT], 2), ACT.Copy).then_inc(
                        s["rg_xT"].sem, 1)

                def step(t, u):
                    copy_tokens(t + 1, 1 - u)
                    e = expert(mybir.EngineType.Activation, t)
                    act.wait_ge(*s["rg_ut"].at(2 * t + 1))
                    if gated:
                        act.wait_ge(*s["rg_hT"].at(t))
                    else:
                        act.wait_ge(*s["rg_down"].at(t - 1))
                    for m in range(hidden):
                        if m == 4:
                            act.wait_ge(*s["rg_ut"].at(2 * t + 2))
                        last = act.activation(first[:, m, :] if gated else hT[:, u, m, :],
                                              k.ps[:, 2 + m // 4, (m % 4) * KT:(m % 4 + 1) * KT], act_fn,
                                              bias=weights[:, bass.ds(e * total + (ob + m), 1)])
                    last.then_inc(s["rg_first" if gated else "rg_hT"].sem, 1)

                copy_tokens(0, 0)
                in_turn(act, step)

            @block.vector
            def _(v):
                def copy_y(t, u):
                    v.wait_ge(*s["rg_down"].at(t + 1))
                    v.wait_ge(*y_out[u].at(8 * (t - u)))
                    v.tensor_copy(y[:, u, :], k.ps[:, 6 + u, 0:D]).then_inc(s["rg_y"].sem, 1)

                def step(t, u):
                    v.wait_ge(*s["rg_ut"].at(2 * t))
                    for half in range(2):
                        v.wait_ge(*s["rg_up"].at(2 * t + half + 1))
                        v.tensor_copy(hs[:, half * 512:(half + 1) * 512], k.ps[:, half, 0:512]).then_inc(
                            s["rg_hs"].sem, 1)
                    if not (isinstance(t, int) and t == 0):
                        copy_y(t - 1, 1 - u)
                    if gated:
                        e = expert(mybir.EngineType.DVE, t)
                        v.wait_ge(*s["rg_first"].at(t + 1))
                        v.wait_ge(*s["rg_ut"].at(2 * t + 2))
                        v.wait_ge(*s["rg_down"].at(t - 1))
                        for m in range(hidden):
                            last = v.scalar_tensor_tensor(hT[:, u, m, :], k.ps[:, 3, m * KT:(m + 1) * KT],
                                                          weights[:, bass.ds(e * total + (ob + 4 + m), 1)],
                                                          first[:, m, :], ALU.add, ALU.mult)
                        last.then_inc(s["rg_hT"].sem, 1)

                in_turn(v, step)
                copy_y(NT - 1, 0)
        k.advance(rg_in0=16 * ((NT + 3) // 2), rg_in1=16 * ((NT + 2) // 2), rg_out0=16 * ((NT + 1) // 2),
                  rg_out1=16 * (NT // 2), rg_turned=NT + 1, rg_xT=NT + 1, rg_up=2 * NT, rg_hs=2 * NT,
                  rg_ut=2 * NT, rg_hT=NT, rg_first=NT if gated else 0, rg_down=NT, rg_y=NT)


def gather_results(k, route, name, rows):
    s = k.signals
    ring = 4
    with ExitStack() as ctx:
        got = k.tile(ctx, name + "_got", [T, ring, PICKS * D], F32)
        into = [s[f"rg_got{r}"] for r in range(ring)]
        with k.nc.Block(no_gpsimd_drain=True) as block:
            @block.gpsimd
            def _(g):
                for b in range(B):
                    if b >= ring:
                        g.wait_ge(*s["rg_added"].at(b - ring + 1))
                    for n in range(PICKS):
                        g.indirect_dma_start(got[:, b % ring, n * D:(n + 1) * D], None, rows[:, :],
                                             bass.IndirectOffsetOnAxis(ap=route.slot[:, n, b:b + 1], axis=0)
                                             ).then_inc(into[b % ring].sem, 16)

            @block.vector
            def _(v):
                ch = Chain(v, s["vec_step"])
                for b in range(B):
                    v.wait_ge(*into[b % ring].at(16 * PICKS * (b // ring + 1)))
                    ch.link(v.scalar_tensor_tensor(k.x(b), got[:, b % ring, 0:D], route.weight[:, 0, b:b + 1],
                                                   k.x(b), ALU.mult, ALU.add))
                    v.scalar_tensor_tensor(k.x(b), got[:, b % ring, D:2 * D], route.weight[:, 1, b:b + 1],
                                           k.x(b), ALU.mult, ALU.add).then_inc(s["rg_added"].sem, 1)
                ch.close()
        k.advance(rg_added=B, **{f"rg_got{r}": 16 * PICKS * (B // ring) for r in range(ring)})


def sub_routed_ffn(k, ctx, name, packs, spec):
    E = spec["experts"]
    lay, dram = packs[name]
    tile, p = pack_tile(k, ctx, name + "_pack", lay)
    elay, edram = packs[name + "_experts"]
    elay = dict(elay, _experts=E)
    total = elay["_total"]
    weights = k.tile(ctx, name + "_weights", [KP, E * total])
    gates = k.tile(ctx, name + "_gates", [T, E * B])
    xn = k.tile(ctx, name + "_xn", [T, B * D])
    route = Routing(k, ctx, E)

    def load_experts(sp):
        for e in range(E):
            sp.dma_start(weights[:, e * total:(e + 1) * total], edram[e, :, :]).then_inc(k["exp_in0"].sem, 16)

    layer_norm(k, pack=(tile, dram, lay["_total"]), keep=xn, ahead=load_experts)
    router(k, E, chunks(p("router"), 2), p("router_b") if "router_b" in lay else None, gates, spec["mode"])
    place_tokens(k, route, gates, E, p("steps").rearrange("p (e j) -> p e j", e=E),
                 p("turns").rearrange("p (t e) -> p t e", e=E))
    add_second_biases(k, gates, E, p("b2"), meanwhile=scatter_tokens(k, route, xn, k.rows_in))
    k.advance(rg_put=16 * PICKS * B)
    with k.nc.Block(no_gpsimd_drain=True) as block:
        @block.tensor
        def _(pe):
            pe.wait_ge(*k["exp_in0"].at(16 * E))
    k.advance(exp_in0=16 * E)
    expert_tiles(k, route, name, weights, elay, k.rows_in, k.rows_out, spec["hidden"], spec["gated"], spec["act"])
    gather_results(k, route, name, k.rows_out)



def attention(k, name, pack, H, dh, self_attn=False, mask=False, clamp=False, head_mask=False):
    nc = k.nc
    HD = H * dh
    C = HD // KP
    HC = KP // dh
    OW = max(dh, 32)
    OH = KP // OW
    OC = H // OH
    kn, kw = (1, T) if self_attn else (KN, KW)
    keys = kn * kw
    kr = KP if self_attn else CR
    scale = float(dh) ** -0.5
    W = 4 if self_attn else 2
    UB = H // W
    U = 2 * UB
    TURNS = B // 2
    first_pass = mask or clamp
    wq, wk, wv, wo = (pack[n] for n in ("wq", "wk", "wv", "wo"))
    with ExitStack() as ctx:
        sb = lambda n, s, d=F32: k.tile(ctx, name + "_" + n, s, d)
        QT = sb("qT", [KP, C, N])
        src = sb("src", [KP, 2, 2, keys])
        KT = sb("kT", [KP, 2, C, keys])
        V = sb("v", [kw, 2, kn, H, OW])
        qm = sb("qm", [KP, 2, H, T])
        sa = sb("sa", [T, 2, 2, keys]) if first_pass else None
        P = sb("p", [T, 4, W, keys])
        PT = sb("pT", [kw, 2, kn, W, T])
        oT = sb("oT", [KP, 2, OC, T])
        mx = sb("mx", [T, 4, W])
        ng = sb("ng", [T, 4, W])
        rs = sb("rs", [T, 4, W])
        ri = sb("ri", [T, 4, W])
        mu8 = sb("mu8", [T, B * S2], U8) if mask else None
        mb = sb("mb", [T, 2, S2]) if mask else None
        s = k.signals
        ctx_in = [s["ctx_in0"], s["ctx_in1"]]
        sc_read = s["sc_read"] if first_pass else s["exp_done"]

        def project_queries(pe):
            with pe.Fori(0, G) as g:
                for c in range(C):
                    pe.wait_ge(*s["lin_act"].at(g * C + c - C + 1))
                    for kc in range(2):
                        last = pe.matmul(k.ps[:, c, 0:GT], wq[:, kc, c * KP:(c + 1) * KP],
                                         k.XT[:, kc, bass.ds(g * GT, GT)], start=(kc == 0), stop=(kc == 1))
                    last.then_inc(s["lin_mm"].sem, 1)

        def store_queries(act):
            k.table(act, ACT.Identity)
            with act.Fori(0, G) as g:
                for c in range(C):
                    act.wait_ge(*s["lin_mm"].at(g * C + c + 1))
                    act.activation(QT[:, c, bass.ds(g * GT, GT)], k.ps[:, c, 0:GT], ACT.Identity,
                                   bias=pack["bq"][:, c:c + 1] if "bq" in pack else 0.0).then_inc(
                                       s["lin_act"].sem, 1)

        if UB == 8:
            places = {(c, "early"): ("K", c) for c in range(C)}
            places[4, "late"] = ("O", 0)
            places.update({(5 + j, "early"): ("V", j) for j in range(kn)})
        elif self_attn:
            assert UB == 4 and C == 2 and kn == 1
            places = {(0, "early"): ("K", 0), (1, "early"): ("K", 1), (2, "late"): ("V", 0), (3, "late"): ("O", 0)}
        else:
            assert UB == 4 and C == 4 and kn == 3
            places = {(0, "early"): ("K", 0), (0, "late"): ("K", 1), (1, "early"): ("K", 2),
                      (1, "late"): ("K", 3), (2, "early"): ("V", 0), (2, "late"): ("V", 1),
                      (3, "early"): ("O", 0), (3, "late"): ("V", 2)}
        order = list(places.values())
        SHARE, TURN, OUT = (2, 3, 4) if UB == 8 else (1, 2, 3)
        END = OUT + 1

        def stream(eng, step, before_loop=lambda i: None, after_loop=lambda: None):
            for n in range(U):
                step(0, n, True, False)
            with eng.Fori(1, TURNS - 1) as i:
                before_loop(i)
                for n in range(U):
                    step(i, n, False, False)
                after_loop()
            for n in range(U + END):
                step(TURNS - 1, n, False, True)

        RING = 4 if W * keys <= 512 else 2

        def scores(n):
            if RING == 4:
                return k.ps[0:T, n % 4, 0:512].rearrange("p (j n) -> p j n", j=W)[:, :, 0:keys]
            return k.ps[0:T, 2 * (n % 2):2 * (n % 2) + 2, 0:keys]

        def all_turned():
            if kn == 1:
                return k.ps[0:kw, 4:5, 0:W * T]
            return k.ps[0:kw, 4:6, :].rearrange("p b (c n) -> p (b c) n", c=2)[:, 0:kn, 0:W * T]

        def turned(kc):
            return all_turned()[:, kc, :]

        def batch_of(i, n):
            return 2 * i + n // UB, (n // UB) % 2, n % UB

        with nc.Block(no_gpsimd_drain=True) as block:
            @block.sync
            def _(sp):
                if mask:
                    sp.dma_start(mu8[:, :], k.aps["in_mask"].rearrange("(a b) n -> a (b n)", a=1)
                                 .broadcast_to([T, B * S2])).then_inc(s["x_in"].sem, 16)
                if not self_attn:
                    with sp.Fori(0, TURNS) as i:
                        for u in range(2):
                            sp.wait_ge(*s["v_mm"].at((i * 2 + u - 1) * kn))
                            sp.dma_start(src[0:CR, u, :, :], k.aps["in_ctx"][bass.ds(i * 2 + u, 1), :, :, :]
                                         .rearrange("b p c n -> (b p) c n")).then_inc(ctx_in[u].sem, 16)

            @block.gpsimd
            def _(g):
                def own_rows(b, u):
                    g.wait_ge(*s["sc_mm"].at((b - 1) * UB))
                    for c in range(C):
                        last = g.tensor_tensor(
                            qm[:, u, c * HC:(c + 1) * HC, :],
                            QT[:, c, bass.ds(b * T, T)].unsqueeze(1).broadcast_to([KP, HC, T]),
                            pack["hmask"][:, 0:HC].unsqueeze(2).broadcast_to([KP, HC, T]), ALU.mult)
                    last.then_inc(s["qm_done"].sem, 1)

                if OW > dh:
                    g.memset(V[:, :, :, :, dh:OW], 0.0).then_inc(s["v_padded"].sem, 1)
                g.wait_ge(*s["lin_act"].at(C))
                own_rows(0, 0)
                own_rows(1, 1)
                g.wait_ge(*s["lin_act"].at(G * C))
                with g.Fori(1, TURNS) as i:
                    for u in range(2):
                        own_rows(2 * i + u, u)

            @block.tensor
            def _(pe):
                def bank_free(b, what, first):
                    j = order.index(what)
                    kind, c = order[j - 1]
                    at = b if j == 0 else b + 1
                    if kind == "O" and j == 0:
                        pe.wait_ge(*s["v_ev"].at((b + 1) * kn))
                        pe.wait_ge(*s["res_done"].at(b - 1))
                        return
                    if kind == "O":
                        if not first:
                            pe.wait_ge(*s["res_done"].at(b))
                            return
                        kind, c = order[j - 2]
                    if kind == "K":
                        pe.wait_ge(*s["kt_ev"].at(at * C + c + 1))
                    else:
                        pe.wait_ge(*s["v_ev"].at(at * kn + c + 1))

                def project(b, u, kind, c):
                    if kind == "K":
                        if c == 0 and self_attn:
                            pe.wait_ge(*s["xs_copied"].at(b + 1))
                        elif c == 0:
                            pe.wait_ge(*ctx_in[u].at(8 * (b - u) + 16))
                        for kc in range(2):
                            last = pe.matmul(k.ps[:, 6, 0:keys], wk[0:kr, kc, c * KP:(c + 1) * KP],
                                             src[0:kr, u, kc, :], start=(kc == 0), stop=(kc == 1))
                        last.then_inc(s["kt_mm"].sem, 1)
                    else:
                        for kc in range(2):
                            rows = kr if kc == 0 or self_attn else kr + 1
                            last = pe.matmul(k.ps[0:kw, 6, 0:HD], src[0:rows, u, kc, c * kw:(c + 1) * kw],
                                             wv[0:rows, kc, :], start=(kc == 0), stop=(kc == 1))
                        last.then_inc(s["v_mm"].sem, 1)

                def in_bank6(i, n, place, first, last_turn):
                    b, u, p = batch_of(i, n)
                    kind, c = places.get((p, place), (None, 0))
                    opening = first and n < UB
                    closing = last_turn and n >= UB
                    if kind == "O" and not opening:
                        if closing:
                            pe.wait_ge(*s["v_ev"].at(B * kn))
                            pe.wait_ge(*s["res_done"].at(b - 1))
                        else:
                            bank_free(b, (kind, c), opening)
                        pe.wait_ge(*s["ot_ev"].at(b))
                        for c in range(OC):
                            last = pe.matmul(k.ps[0:T, 6, 0:D], oT[:, 1 - u, c, :], wo[:, c, :],
                                             start=(c == 0), stop=(c == OC - 1))
                        last.then_inc(s["wo_mm"].sem, 1)
                    elif kind in ("K", "V") and not closing:
                        bank_free(b, (kind, c), opening)
                        project(b + 1, 1 - u, kind, c)

                def step(i, n, first, last_turn):
                    if n < U:
                        b, u, p = batch_of(i, n)
                        if p == 0:
                            pe.wait_ge(*s["kt_ev"].at((b + 1) * C))
                            pe.wait_ge(*s["qm_done"].at(b + 1))
                        pe.wait_ge(*sc_read.at(i * U + n - RING + 1))
                        for j in range(W):
                            h = W * p + j
                            last = pe.matmul(scores(n)[:, j, :], qm[:, u, h, :],
                                             KT[:, u, h // HC, :], start=True, stop=True)
                        last.then_inc(s["sc_mm"].sem, 1)
                    in_bank6(i, n, "early", first, last_turn)
                    m = n - TURN
                    if m < U and not (first and m < 0):
                        pe.wait_ge(*s["prob_done"].at(i * U + m + 1))
                        pe.wait_ge(*s["pt_ev_a"].at(i * U + m))
                        for kc in range(kn):
                            for j in range(W):
                                last = pe.transpose(turned(kc)[:, j * T:(j + 1) * T],
                                                    P[:, m % 4, j, kc * kw:(kc + 1) * kw], k.ident[0:T, 0:T])
                        last.then_inc(s["pt_mm"].sem, 1)
                    m = n - OUT
                    if m < U and not (first and m < 0):
                        b, u, p = batch_of(i, m)
                        pe.wait_ge(*s["pt_ev_a"].at(i * U + m + 1))
                        if p == 0:
                            pe.wait_ge(*s["v_ev"].at((b + 1) * kn))
                            pe.wait_ge(*s["ot_ev"].at(b))
                        for kc in range(kn):
                            for j in range(W):
                                h = W * p + j
                                row = (h % OH) * OW
                                last = pe.matmul(k.ps[row:row + OW, 7, (h // OH) * T:(h // OH + 1) * T],
                                                 V[:, u, kc, h, :], PT[:, m % 2, kc, j, :],
                                                 start=(kc == 0), stop=(kc == kn - 1))
                        last.then_inc(s["pv_mm"].sem, 1)
                    in_bank6(i, n, "late", first, last_turn)

                project_queries(pe)
                if not self_attn:
                    pe.wait_ge(*s["ones_row"].at(1))
                for kind, c in [what for what in order if what[0] != "O"]:
                    if kind == "K":
                        pe.wait_ge(*s["kt_ev"].at(c))
                    else:
                        pe.wait_ge(*s["kt_ev"].at(C))
                        pe.wait_ge(*s["v_ev"].at(c))
                    project(0, 0, kind, c)
                pe.wait_ge(*s["lin_act"].at(G * C))
                if OW > dh:
                    pe.wait_ge(*s["v_padded"].at(1))
                stream(pe, step)

            @block.scalar
            def _(act):
                def evacuate(b, u, c):
                    act.wait_ge(*s["kt_mm"].at(b * C + c + 1))
                    if c == 0:
                        act.wait_ge(*s["sc_mm"].at((b - 1) * UB))
                    act.activation(KT[:, u, c, :], k.ps[:, 6, 0:keys], ACT.Identity,
                                   bias=pack["bk"][:, c:c + 1] if "bk" in pack else 0.0).then_inc(
                                       s["kt_ev"].sem, 1)

                def in_bank6(i, n, place, last_turn):
                    b, u, p = batch_of(i, n)
                    kind, c = places.get((p, place), (None, 0))
                    if kind == "K" and not (last_turn and n >= UB):
                        evacuate(b + 1, 1 - u, c)

                def step(i, n, first, last_turn):
                    if n > 0 or not first:
                        in_bank6(i, n - 1, "late", last_turn)
                    in_bank6(i, n, "early", last_turn)
                    if n < U:
                        act.wait_ge(*s["max_done"].at(i * U + n + 1))
                        act.wait_ge(*s["pt_mm"].at(i * U + n - 3))
                        for j in range(W):
                            at = sa[:, n % 2, j, :] if first_pass else scores(n)[:, j, :]
                            last = act.activation(P[:, n % 4, j, :], at, ACT.Exp, bias=ng[:, n % 4, j:j + 1],
                                                  scale=1.0 if mask else scale,
                                                  accum_out=rs[:, n % 4, j:j + 1])
                        last.then_inc(s["exp_done"].sem, 1)
                    m = n - TURN
                    if m < U and not (first and m < 0):
                        act.wait_ge(*s["pt_mm"].at(i * U + m + 1))
                        act.wait_ge(*s["pv_mm"].at(i * U + m - 1))
                        act.activation(PT[:, m % 2, :, :, :].rearrange("p c h t -> p c (h t)"), all_turned(),
                                       ACT.Copy).then_inc(s["pt_ev_a"].sem, 1)
                    b, u, p = batch_of(i, n)
                    if p == OUT - 1 and not (first and n < UB):
                        act.wait_ge(*s["pv_mm"].at(b * UB))
                        act.wait_ge(*s["wo_mm"].at(b - 2))
                        act.activation(oT[:, 1 - u, :, :], chunks(k.ps[:, 7, 0:OC * T], OC), ACT.Copy).then_inc(
                            s["ot_ev"].sem, 1)

                store_queries(act)
                for c in range(C):
                    evacuate(0, 0, c)
                stream(act, step)

            @block.vector
            def _(v):
                ch = Chain(v, s["vec_step"])
                per = U * (2 + head_mask) + (2 if "bo" in pack else 0)

                def copy_tokens(b, u):
                    v.wait_ge(*s["v_mm"].at((b - 1) * kn))
                    v.tensor_copy(src[:, u, :, :], k.XT[:, :, bass.ds(b * T, T)]).then_inc(
                        s["xs_copied"].sem, 1)

                def spread_mask(b, u):
                    v.tensor_scalar(mb[:, u, :], mu8[:, bass.ds(b * S2, S2)], -1.0, FMAX, ALU.add,
                                    ALU.mult).then_inc(s["mask_done"].sem, 1)

                def store_v(b, u, j):
                    v.wait_ge(*s["v_mm"].at(b * kn + j + 1))
                    if j == 0:
                        v.wait_ge(*s["pv_mm"].at((b - 1) * UB))
                    at = k.ps[0:kw, 6, 0:HD].rearrange("p (h d) -> p h d", h=H)
                    if self_attn:
                        v.tensor_tensor(V[:, u, j, :, 0:dh], at,
                                        pack["bv"][0:kw, :].rearrange("p (h d) -> p h d", h=H),
                                        ALU.add).then_inc(s["v_ev"].sem, 1)
                    else:
                        v.tensor_copy(V[:, u, j, :, 0:dh], at).then_inc(s["v_ev"].sem, 1)

                def in_bank6(i, n, place, first, last_turn):
                    b, u, p = batch_of(i, n)
                    kind, c = places.get((p, place), (None, 0))
                    if kind == "V" and not (last_turn and n >= UB):
                        store_v(b + 1, 1 - u, c)
                    if kind == "O" and not (first and n < UB):
                        v.wait_ge(*s["wo_mm"].at(b))
                        v.tensor_tensor(k.x(b - 1), k.ps[0:T, 6, 0:D], k.x(b - 1), ALU.add).then_inc(
                            s["res_done"].sem, 1)
                        if "bo" in pack:
                            v.wait_ge(*s["res_done"].at(b))
                            ch.link(v.tensor_tensor(k.x(b - 1), pack["bo"][0:T, :], k.x(b - 1), ALU.add))

                def step(i, n, first, last_turn):
                    if n > 0 or not first:
                        in_bank6(i, n - 1, "late", first, last_turn)
                    b, u, p = batch_of(i, n)
                    more = not (last_turn and n >= UB)
                    if n < U:
                        v.wait_ge(*s["sc_mm"].at(i * U + n + 1))
                        at = scores(n)
                        r = n % 4
                        if first_pass:
                            v.wait_ge(*s["exp_done"].at(i * U + n - 1))
                            if clamp:
                                v.tensor_scalar(sa[:, n % 2, :, :], at, CLAMP / scale, -CLAMP / scale, ALU.min,
                                                ALU.max).then_inc(s["sc_read"].sem, 1)
                            else:
                                if p == 0:
                                    v.wait_ge(*s["mask_done"].at(b + 1))
                                v.scalar_tensor_tensor(
                                    sa[:, n % 2, :, :], at, scale,
                                    mb[:, u, :].unsqueeze(1).broadcast_to([T, 2, keys]), ALU.mult,
                                    ALU.add).then_inc(s["sc_read"].sem, 1)
                            v.wait_ge(*s["sc_read"].at(i * U + n + 1))
                            at = sa[:, n % 2, :, :]
                        ch.link(v.tensor_reduce(mx[:, r, :], at, AX.X, ALU.max))
                        v.tensor_scalar(ng[:, r, :], mx[:, r, :], -1.0 if mask else -scale, None,
                                        ALU.mult).then_inc(s["max_done"].sem, 1)
                    m = n - SHARE
                    if m < U and not (first and m < 0):
                        v.wait_ge(*s["exp_done"].at(i * U + m + 1))
                        ch.link(v.reciprocal(ri[:, m % 4, :], rs[:, m % 4, :]))
                        if head_mask:
                            h = W * (m % UB)
                            ch.link(v.tensor_tensor(ri[:, m % 4, :], ri[:, m % 4, :], pack["hm"][0:T, h:h + W],
                                                    ALU.mult))
                        if self_attn:
                            last = v.tensor_tensor(P[:, m % 4, :, :], P[:, m % 4, :, :],
                                                   ri[:, m % 4, :].unsqueeze(2).broadcast_to([T, W, keys]),
                                                   ALU.mult)
                        else:
                            for j in range(W):
                                last = v.tensor_scalar(P[:, m % 4, j, :], P[:, m % 4, j, :], ri[:, m % 4, j:j + 1],
                                                       None, ALU.mult)
                        last.then_inc(s["prob_done"].sem, 1)
                    in_bank6(i, n, "early", first, last_turn)
                    if more and n < U:
                        if self_attn and p == UB - 2:
                            if not (last_turn and n >= 0 and n // UB == 0):
                                copy_tokens(b + 2, u)
                        if mask and p == UB // 2:
                            spread_mask(b + 1, 1 - u)

                if self_attn:
                    copy_tokens(0, 0)
                    copy_tokens(1, 1)
                else:
                    v.memset(src[CR:CR + 1, :, :, :], 1.0).then_inc(s["ones_row"].sem, 1)
                if mask:
                    v.wait_ge(*s["x_in"].at(16))
                    spread_mask(0, 0)
                for j in range(kn):
                    store_v(0, 0, j)
                stream(v, step, lambda i: ch.turn(i - 1, per), lambda: ch.end(TURNS - 2))
                in_bank6(TURNS - 1, U + END - 1, "late", False, True)
                ch.close()

        units = TURNS * U
        k.advance(lin_mm=G * C, lin_act=G * C, x_in=16 if mask else 0, v_padded=1 if OW > dh else 0,
                  ones_row=0 if self_attn else 1)
        k.advance(xs_copied=B if self_attn else 0, kt_mm=B * C, kt_ev=B * C, v_mm=B * kn, v_ev=B * kn, qm_done=B,
                  sc_mm=units, sc_read=units if first_pass else 0, max_done=units, exp_done=units, prob_done=units,
                  pt_mm=units, pt_ev_a=units, pv_mm=units, ot_ev=B, wo_mm=B,
                  res_done=B, mask_done=B if mask else 0)
        if not self_attn:
            k.advance(ctx_in0=TURNS * 16, ctx_in1=TURNS * 16)


def sub_attention(k, ctx, name, packs, spec):
    lay, dram = packs[name]
    tile, p = pack_tile(k, ctx, name + "_pack", lay)
    pack = {f: p(f) for f in lay if f != "_total"}
    for f in ("wq", "wk", "wv"):
        pack[f] = chunks(pack[f], 2)
    heads_out = KP // max(spec["dh"], 32)
    pack["wo"] = chunks(pack["wo"], spec["H"] // heads_out)
    layer_norm(k, pack=(tile, dram, lay["_total"]))
    attention(k, name, pack, **spec)


ATTENTION = {
    "L0_xattn": dict(H=16, dh=16, clamp=True),
    "L1_xattn": dict(H=8, dh=64),
    "L2_xattn": dict(H=16, dh=16, mask=True),
    "L3_attn": dict(H=16, dh=16, self_attn=True, head_mask=True),
}


def head_rows(dh):
    return np.repeat(np.eye(KP // dh, dtype=np.float32), dh, axis=0)


def spread_heads(wo, H, dh):
    wide = np.zeros((H, max(dh, 32), wo.shape[1]), np.float32)
    wide[:, :dh] = wo.reshape(H, dh, -1)
    return wide.reshape(-1, wo.shape[1])


def with_bias_row(w, bias):
    out = np.zeros((CR + 1, 2, w.shape[1]), np.float32)
    out[:CR] = w.reshape(2, CR, -1).transpose(1, 0, 2)
    if bias is not None:
        out[CR, 1] = bias
    return out.reshape(CR + 1, -1)


def host_attention(name, a):
    w = {key[len(name) + 1:]: v for key, v in a.items() if key.startswith(name + "_")}
    spec = ATTENTION[name]
    H, dh = spec["H"], spec["dh"]
    turned = spec.get("self_attn")
    m = {n: (w[n].T if turned else w[n]) for n in ("Wq", "Wk", "Wv", "Wo")}
    f = dict(wq=by_rows(m["Wq"]), wo=by_rows(spread_heads(m["Wo"], H, dh)), hmask=head_rows(dh))
    if turned:
        f.update(wk=by_rows(m["Wk"]), wv=by_rows(m["Wv"]), bv=on_rows(w["bv"]), hm=on_rows(w["head_mask"]))
    else:
        f.update(wk=by_rows(m["Wk"], CR), wv=with_bias_row(m["Wv"], w.get("bv")))
    for n in ("bq", "bk"):
        if n in w:
            f[n] = columns(w[n])
    if "bo" in w:
        f["bo"] = on_rows(w["bo"])
    return {name: packed(f)}



def sub_l3_xattn(k, ctx, name, packs):
    nc = k.nc
    lay, dram = packs[name]
    tile, p = pack_tile(k, ctx, name + "_pack", lay)
    wq, wk, wv = (chunks(p(n), 2) for n in ("wq", "wk", "wv"))
    scale = float(D) ** -0.5
    s = k.signals
    sb = lambda n, sh: k.tile(ctx, name + "_" + n, sh, F32)
    src = sb("src", [CR + 1, 2, 2, S2])

    def bias_row(g):
        g.wait_ge(*s["rstd_done"].at(2))
        g.memset(src[CR:CR + 1, :, :, :], 1.0).then_inc(s["pool_step"].sem, 1)
        g.wait_ge(*s["pool_step"].at(1))

    layer_norm(k, pack=(tile, dram, lay["_total"]), meanwhile=bias_row)
    k.advance(pool_step=1)
    qT = sb("qT", [KP, 2, 2, T])
    KT = sb("kT", [KP, 2, 2, S2])
    V = sb("v", [KW, 2, KN, D])
    P = sb("p", [T, 2, S2])
    PT = sb("pT", [KW, 2, KN, T])
    mx, ng, rs, ri = (sb(n, [T, 2]) for n in ("mx", "ng", "rs", "ri"))
    ctx_in = [s["ctx_in0"], s["ctx_in1"]]
    TURNS = B // 2
    with nc.Block(no_gpsimd_drain=True) as block:
        @block.sync
        def _(sp):
            with sp.Fori(0, TURNS) as i:
                for u in range(2):
                    sp.wait_ge(*s["v_mm"].at((i * 2 + u - 1) * KN))
                    sp.dma_start(src[0:CR, u, :, :], k.aps["in_ctx"][bass.ds(i * 2 + u, 1), :, :, :]
                                 .rearrange("b p c n -> (b p) c n")).then_inc(ctx_in[u].sem, 16)

        @block.tensor
        def _(pe):
            with pe.Fori(0, TURNS) as i:
                for u in range(2):
                    b = i * 2 + u
                    pe.wait_ge(*ctx_in[u].at((i + 1) * 16))
                    pe.wait_ge(*s["qm_done"].at(b))
                    for c in range(2):
                        for kc in range(2):
                            last = pe.matmul(k.ps[:, 0, c * T:(c + 1) * T], wq[:, kc, c * KP:(c + 1) * KP],
                                             k.XT[:, kc, bass.ds(b * T, T)], start=(kc == 0), stop=(kc == 1))
                    last.then_inc(s["lin_mm"].sem, 1)
                    for c in range(2):
                        pe.wait_ge(*s["kt_ev"].at(b * 2 + c - 1))
                        for kc in range(2):
                            rows = CR + kc
                            last = pe.matmul(k.ps[:, 1 + c, 0:S2], wk[0:rows, kc, c * KP:(c + 1) * KP],
                                             src[0:rows, u, kc, :], start=(kc == 0), stop=(kc == 1))
                        last.then_inc(s["kt_mm"].sem, 1)
                    for j in range(KN):
                        pe.wait_ge(*s["v_ev"].at(b * KN + j - 1))
                        bank = 3 + (u * KN + j) % 2
                        for kc in range(2):
                            rows = CR + kc
                            last = pe.matmul(k.ps[0:KW, bank, 0:D], src[0:rows, u, kc, j * KW:(j + 1) * KW],
                                             wv[0:rows, kc, :], start=(kc == 0), stop=(kc == 1))
                        last.then_inc(s["v_mm"].sem, 1)
                for u in range(2):
                    b = i * 2 + u
                    pe.wait_ge(*s["qm_done"].at(b + 1))
                    pe.wait_ge(*s["kt_ev"].at((b + 1) * 2))
                    pe.wait_ge(*s["exp_done"].at(b - 1))
                    for c in range(2):
                        last = pe.matmul(k.ps[0:T, 5 + u, 0:S2], qT[:, u, c, :], KT[:, u, c, :], start=(c == 0),
                                         stop=(c == 1))
                    last.then_inc(s["sc_mm"].sem, 1)
                for u in range(2):
                    b = i * 2 + u
                    pe.wait_ge(*s["exp_done"].at(b + 1))
                    pe.wait_ge(*s["res_done"].at(b))
                    pe.wait_ge(*s["pt_ev_a"].at(b))
                    for kc in range(KN):
                        last = pe.transpose(k.ps[0:KW, 7, kc * T:(kc + 1) * T], P[:, u, kc * KW:(kc + 1) * KW],
                                            k.ident[0:T, 0:T])
                    last.then_inc(s["pt_mm"].sem, 1)
                    pe.wait_ge(*s["pt_ev_a"].at(b + 1))
                    pe.wait_ge(*s["v_ev"].at((b + 1) * KN))
                    for kc in range(KN):
                        last = pe.matmul(k.ps[0:T, 7, 0:D], PT[:, u, kc, :], V[:, u, kc, :], start=(kc == 0),
                                         stop=(kc == KN - 1))
                    last.then_inc(s["pv_mm"].sem, 1)

        @block.scalar
        def _(act):
            k.table(act, ACT.Exp)
            with act.Fori(0, TURNS) as i:
                for u in range(2):
                    b = i * 2 + u
                    act.wait_ge(*s["lin_mm"].at(b + 1))
                    act.wait_ge(*s["sc_mm"].at(b - 1))
                    for c in range(2):
                        last = act.activation(qT[:, u, c, :], k.ps[:, 0, c * T:(c + 1) * T], ACT.Identity,
                                              bias=p("bq")[:, c:c + 1])
                    last.then_inc(s["qm_done"].sem, 1)
                    for c in range(2):
                        act.wait_ge(*s["kt_mm"].at(b * 2 + c + 1))
                        act.activation(KT[:, u, c, :], k.ps[:, 1 + c, 0:S2], ACT.Copy).then_inc(s["kt_ev"].sem, 1)
                for u in range(2):
                    b = i * 2 + u
                    act.wait_ge(*s["max_done"].at(b + 1))
                    act.wait_ge(*s["pt_mm"].at(b - 1))
                    act.activation(P[:, u, :], k.ps[0:T, 5 + u, 0:S2], ACT.Exp, bias=ng[:, u:u + 1], scale=scale,
                                   accum_out=rs[:, u:u + 1]).then_inc(s["exp_done"].sem, 1)
                for u in range(2):
                    b = i * 2 + u
                    act.wait_ge(*s["pt_mm"].at(b + 1))
                    act.wait_ge(*s["pv_mm"].at(b - 1))
                    act.activation(PT[:, u, :, :], chunks(k.ps[0:KW, 7, 0:KN * T], KN), ACT.Copy).then_inc(
                        s["pt_ev_a"].sem, 1)

        @block.vector
        def _(v):
            ch = Chain(v, s["vec_step"])
            with v.Fori(0, TURNS) as i:
                ch.turn(i, 4)
                for u in range(2):
                    b = i * 2 + u
                    v.wait_ge(*s["pv_mm"].at(b - 1))
                    for j in range(KN):
                        v.wait_ge(*s["v_mm"].at(b * KN + j + 1))
                        v.tensor_copy(V[:, u, j, :], k.ps[0:KW, 3 + (u * KN + j) % 2, 0:D]).then_inc(
                            s["v_ev"].sem, 1)
                for u in range(2):
                    b = i * 2 + u
                    v.wait_ge(*s["sc_mm"].at(b + 1))
                    ch.link(v.tensor_reduce(mx[:, u:u + 1], k.ps[0:T, 5 + u, 0:S2], AX.X, ALU.max))
                    v.tensor_scalar(ng[:, u:u + 1], mx[:, u:u + 1], -scale, None, ALU.mult).then_inc(
                        s["max_done"].sem, 1)
                for u in range(2):
                    b = i * 2 + u
                    v.wait_ge(*s["exp_done"].at(b + 1))
                    ch.link(v.reciprocal(ri[:, u:u + 1], rs[:, u:u + 1]))
                    v.wait_ge(*s["pv_mm"].at(b + 1))
                    v.scalar_tensor_tensor(k.x(b), k.ps[0:T, 7, 0:D], ri[:, u:u + 1], k.x(b), ALU.mult,
                                           ALU.add).then_inc(s["res_done"].sem, 1)
                ch.end(TURNS)
            ch.close()
    k.advance(lin_mm=B, qm_done=B, kt_mm=2 * B, kt_ev=2 * B, v_mm=B * KN, v_ev=B * KN, sc_mm=B, max_done=B,
              exp_done=B, pt_mm=B, pt_ev_a=B, pv_mm=B, res_done=B, ctx_in0=TURNS * 16, ctx_in1=TURNS * 16)


def host_l3_xattn(name, a):
    w = {key[len(name) + 1:]: v for key, v in a.items() if key.startswith(name + "_")}
    return {name: packed(dict(wq=by_rows(w["Wq"].T), wk=with_bias_row(w["Wk"].T, w["bk"]),
                              wv=with_bias_row(w["Wv"].T, w["bv"]), bq=columns(w["bq"])))}



CH = 8
NCH = T // CH
GCH = GB * NCH


def project_out(k, make, wo, residual="X", out=None):
    nc = k.nc
    s = k.signals
    with ExitStack() as ctx:
        sb = lambda n, sh: k.tile(ctx, "po_" + n, sh, F32)
        xo = sb("x", [T, 2, D])
        oT = sb("oT", [KP, 2, 2, T])

        def two_by_two(eng, begin, finish):
            begin(0)
            with eng.Fori(0, B // 2 - 1) as i:
                begin(i + 1)
                finish(i)
            finish(B // 2 - 1)

        with nc.Block(no_gpsimd_drain=True) as block:
            @block.vector
            def _(v):
                def begin(i):
                    for u in range(2):
                        b = 2 * i + u
                        v.wait_ge(*s["norm_tr"].at(b - 1))
                        make(v, b, xo[:, u, :]).then_inc(s["norm_done"].sem, 1)

                def finish(i):
                    for u in range(2):
                        b = 2 * i + u
                        v.wait_ge(*s["wo_mm"].at(b + 1))
                        if out is None:
                            v.tensor_tensor(k.x(b), k.ps[0:T, 2 + u, 0:D], k.x(b), ALU.add).then_inc(
                                s["res_done"].sem, 1)
                        else:
                            v.tensor_tensor(out[:, bass.ds(b * D, D)], k.ps[0:T, 2 + u, 0:D],
                                            residual[:, bass.ds(b * D, D)], ALU.add).then_inc(s["res_done"].sem, 1)

                two_by_two(v, begin, finish)

            @block.tensor
            def _(pe):
                def begin(i):
                    for u in range(2):
                        b = 2 * i + u
                        pe.wait_ge(*s["norm_done"].at(b + 1))
                        pe.wait_ge(*s["norm_ev"].at(b - 1))
                        for c in range(2):
                            last = pe.transpose(k.ps[:, u, c * T:(c + 1) * T], xo[:, u, c * KP:(c + 1) * KP],
                                                k.ident[0:T, 0:T])
                        last.then_inc(s["norm_tr"].sem, 1)

                def finish(i):
                    for u in range(2):
                        b = 2 * i + u
                        pe.wait_ge(*s["norm_ev"].at(b + 1))
                        pe.wait_ge(*s["res_done"].at(b - 1))
                        for c in range(2):
                            last = pe.matmul(k.ps[0:T, 2 + u, 0:D], oT[:, u, c, :], wo[:, c, :], start=(c == 0),
                                             stop=(c == 1))
                        last.then_inc(s["wo_mm"].sem, 1)

                two_by_two(pe, begin, finish)

            @block.scalar
            def _(act):
                k.table(act, ACT.Copy)
                with act.Fori(0, B // 2) as i:
                    for u in range(2):
                        b = 2 * i + u
                        act.wait_ge(*s["norm_tr"].at(b + 1))
                        act.wait_ge(*s["wo_mm"].at(b - 1))
                        act.activation(oT[:, u, :, :], chunks(k.ps[:, u, 0:2 * T], 2), ACT.Copy).then_inc(
                            s["norm_ev"].sem, 1)
        k.advance(norm_done=B, norm_tr=B, norm_ev=B, wo_mm=B, res_done=B)


def sub_l0_attn(k, ctx, name, packs):
    nc = k.nc
    lay, dram = packs[name]
    tile, p = pack_tile(k, ctx, name + "_pack", lay)
    layer_norm(k, pack=(tile, dram, lay["_total"]))
    s = k.signals
    outer = lambda n, sh: k.tile(ctx, name + "_" + n, sh, F32)
    V = outer("V", [T, B * D])
    GV = outer("G", [T, B * D])
    R, K, E = (outer(n, [KP, N]) for n in ("R", "K", "E"))

    with ExitStack() as mid:
        sb = lambda n, sh: k.tile(mid, name + "_" + n, sh, F32)
        dT = sb("dT", [KP, 2, N])
        z0 = sb("z0", [KP, N])
        z1 = sb("z1", [KP, N])
        wx1, wx2 = chunks(p("wx1"), 2), p("wx2").rearrange("p (i n) -> p i n", i=5)
        with ExitStack() as inner:
            xm = k.tile(inner, name + "_xm", [KP, 2, N], F32)
            with nc.Block(no_gpsimd_drain=True) as block:
                @block.vector
                def _(v):
                    for c in range(2):
                        x3 = k.XT[:, c, :].rearrange("p (b t) -> p b t", b=B)
                        d3 = dT[:, c, :].rearrange("p (b t) -> p b t", b=B)
                        v.tensor_tensor(d3[:, :, 1:T], x3[:, :, 0:T - 1], x3[:, :, 1:T], ALU.subtract)
                        v.tensor_scalar(d3[:, :, 0:1], x3[:, :, 0:1], -1.0, None, ALU.mult).then_inc(
                            s["p_a"].sem, 1)
                        v.wait_ge(*s["p_a"].at(c + 1))
                        v.scalar_tensor_tensor(xm[:, c, :], dT[:, c, :], p("mu_x")[:, c:c + 1], k.XT[:, c, :],
                                               ALU.mult, ALU.add).then_inc(s["p_b"].sem, 1)

                @block.tensor
                def _(pe):
                    pe.wait_ge(*s["p_b"].at(2))
                    with pe.Fori(0, G) as g:
                        for m in range(2):
                            pe.wait_ge(*s["lin_act"].at(2 * g + m - 1))
                            for c in range(2):
                                last = pe.matmul(k.ps[:, m, 0:GT], wx1[:, c, m * KP:(m + 1) * KP],
                                                 xm[:, c, bass.ds(g * GT, GT)], start=(c == 0), stop=(c == 1))
                            last.then_inc(s["lin_mm"].sem, 1)

                @block.scalar
                def _(act):
                    k.table(act, ACT.Tanh)
                    with act.Fori(0, G) as g:
                        for m in range(2):
                            z = (z0, z1)[m]
                            act.wait_ge(*s["lin_mm"].at(2 * g + m + 1))
                            act.activation(z[:, bass.ds(g * GT, GT)], k.ps[:, m, 0:GT], ACT.Tanh).then_inc(
                                s["lin_act"].sem, 1)
            k.advance(p_a=2, p_b=2, lin_mm=2 * G, lin_act=2 * G)

        inp = sb("inp", [KP, 2, 5, 2, GT])
        tmp = sb("tmp", [KP, 2, GT])
        ta = sb("ta", [64, 2, GT])
        wr, wk, wa, wv, wg = (chunks(p(n), 2) for n in ("wr", "wk", "wa", "wv", "wg"))
        R_, W_, K_, V_, G_ = range(5)
        mixed, mus, prod, done = s["p_a"], s["p_b"], s["p_c"], s["p_d"]
        with nc.Block(no_gpsimd_drain=True) as block:
            @block.tensor
            def _(pe):
                def mix(g, r):
                    n = g * 10 + r
                    pe.wait_ge(*mixed.at(n - 3))
                    pe.matmul(k.ps[:, n % 4, 0:GT], wx2[:, r // 2, (r % 2) * KP:(r % 2 + 1) * KP],
                              (z0 if r < 8 else z1)[:, g * GT:(g + 1) * GT], start=True, stop=True).then_inc(
                                  mus.sem, 1)

                def wide(g, q, rows, w, j):
                    for c in range(2):
                        last = pe.matmul(k.ps[0:rows, 4 + q, 0:GT], w[:, c, :], inp[:, g % 2, j, c, :],
                                         start=(c == 0), stop=(c == 1))
                    return last

                def tall(g, q, w, j):
                    for b in range(2):
                        at = (2 * (q % 2) + b) * T
                        for c in range(2):
                            last = pe.matmul(k.ps[0:T, q, b * D:(b + 1) * D], inp[:, g % 2, j, c, at:at + T],
                                             w[:, c, :], start=(c == 0), stop=(c == 1))
                    return last

                def product(g, q):
                    pe.wait_ge(*done.at(g * 8 + q - 3))
                    if q == 3:
                        pe.wait_ge(*done.at(g * 8 + 2))
                        last = pe.matmul(k.ps[:, 7, 0:GT], p("wb"), ta[:, g % 2, :], start=True, stop=True)
                    else:
                        j = (R_, W_, K_, None, V_, V_, G_, G_)[q]
                        pe.wait_ge(*mixed.at(g * 10 + 2 * j + 2))
                        if q < 3:
                            last = wide(g, q, *((KP, wr), (64, wa), (KP, wk))[q], j)
                        else:
                            last = tall(g, q, wv if q < 6 else wg, j)
                    last.then_inc(prod.sem, 1)

                for r in range(10):
                    mix(0, r)
                for g in range(G):
                    for q in range(8):
                        if g + 1 < G:
                            for r in ((0, 1), (2,), (3,), (4,), (5, 6), (7,), (8,), (9,))[q]:
                                mix(g + 1, r)
                        product(g, q)

            @block.vector
            def _(v):
                ch = Chain(v, s["vec_step"])
                for g in range(G):
                    u, tok = g % 2, slice(g * GT, (g + 1) * GT)
                    for r in range(10):
                        j, c = r // 2, r % 2
                        v.wait_ge(*mus.at(g * 10 + r + 1))
                        ch.link(v.scalar_tensor_tensor(tmp[:, r % 2, :], k.ps[:, (g * 10 + r) % 4, 0:GT],
                                                       p("x_bias")[:, r:r + 1], dT[:, c, tok], ALU.add,
                                                       ALU.mult))
                        if r == 0:
                            v.wait_ge(*prod.at((g - 1) * 8))
                        v.tensor_tensor(inp[:, u, j, c, :], tmp[:, r % 2, :], k.XT[:, c, tok],
                                        ALU.add).then_inc(mixed.sem, 1)
                ch.close()

            @block.scalar
            def _(act):
                for g in range(G):
                    tok = slice(g * GT, (g + 1) * GT)
                    for q, (dst, rows, fn) in enumerate([(R[:, tok], KP, ACT.Copy), (ta[:, g % 2, :], 64, ACT.Tanh),
                                                         (K[:, tok], KP, ACT.Copy)]):
                        act.wait_ge(*prod.at(g * 8 + q + 1))
                        act.activation(dst, k.ps[0:rows, 4 + q, 0:GT], fn).then_inc(done.sem, 1)
                    act.wait_ge(*prod.at(g * 8 + 4))
                    act.activation(E[:, tok], k.ps[:, 7, 0:GT], ACT.Exp, bias=p("b_w")).then_inc(done.sem, 1)
                    for q in range(4):
                        dst, at = V if q < 2 else GV, (g * GB + 2 * (q % 2)) * D
                        act.wait_ge(*prod.at(g * 8 + 5 + q))
                        act.activation(dst[:, at:at + 2 * D], k.ps[0:T, 4 + q, 0:2 * D], ACT.Copy).then_inc(
                            done.sem, 1)
        k.advance(p_a=10 * G, p_b=10 * G, p_c=8 * G, p_d=8 * G)

    O = V
    rwkv_matrix(k, name, p, R, K, E, V, O)

    with ExitStack() as mid:
        sb = lambda n, sh: k.tile(mid, name + "_" + n, sh, F32)
        BH, HV = B * 4, D // 4
        gw, sq = sb("gw", [T, B * D]), sb("sq", [T, B * D])
        mean, var, rstd, half = (sb(n, [T, BH]) for n in ("mean", "var", "rstd", "half"))
        heads = lambda t: t[:, :].rearrange("p (h v) -> p h v", v=HV)
        batches = lambda t: t[:, :].rearrange("p (b d) -> p b d", b=B)
        wide = lambda t: t[:, :].unsqueeze(2).broadcast_to([T, BH, HV])
        row = lambda f: p(f)[0:T, :].unsqueeze(1).broadcast_to([T, B, D])
        with nc.Block(no_gpsimd_drain=True) as block:
            @block.vector
            def _(v):
                ch = Chain(v, s["vec_step"])
                v.memset(half[:, :], -0.5)
                ch.link(v.tensor_reduce(mean[:, :], heads(O), AX.X, ALU.add))
                ch.link(v.tensor_scalar(mean[:, :], mean[:, :], 1.0 / HV, None, ALU.mult))
                v.tensor_tensor(heads(O), heads(O), wide(mean), ALU.subtract).then_inc(s["p_a"].sem, 1)
                v.wait_ge(*s["p_b"].at(1))
                ch.link(v.tensor_reduce(var[:, :], heads(sq), AX.X, ALU.add))
                v.tensor_scalar(var[:, :], var[:, :], 1.0 / HV, LN_EPS, ALU.mult, ALU.add).then_inc(s["p_a"].sem, 1)
                v.wait_ge(*s["p_b"].at(2))
                v.tensor_tensor(batches(gw), batches(GV), row("gn_w"), ALU.mult)
                ch.link(v.tensor_tensor(batches(GV), batches(GV), row("gn_b"), ALU.mult))
                v.wait_ge(*s["p_c"].at(1))
                ch.link(v.tensor_tensor(heads(O), heads(O), wide(rstd), ALU.mult))
                ch.link(v.tensor_tensor(O[:, :], O[:, :], gw[:, :], ALU.mult))
                ch.close()

            @block.scalar
            def _(act):
                act.wait_ge(*s["p_a"].at(1))
                act.activation(sq[:, :], O[:, :], ACT.Square).then_inc(s["p_b"].sem, 1)
                act.activation(GV[:, :], GV[:, :], ACT.Silu).then_inc(s["p_b"].sem, 1)

            @block.gpsimd
            def _(g):
                g.wait_ge(*s["p_a"].at(2))
                g.tensor_tensor(rstd[:, :], var[:, :], half[:, :], ALU.pow).then_inc(s["p_c"].sem, 1)
        k.advance(p_a=2, p_b=2, p_c=1)

    def gated(v, b, dst):
        return v.tensor_tensor(dst, O[:, bass.ds(b * D, D)], GV[:, bass.ds(b * D, D)], ALU.add)

    project_out(k, gated, chunks(p("wo"), 2))


def rwkv_matrix(k, name, p, R, K, E, V, O):
    nc, s = k.nc, k.signals
    with ExitStack() as ctx:
        sb = lambda n, sh: k.tile(ctx, name + "_" + n, sh, F32)
        ci, cx, eq, ek = (sb(n, [KP, GT]) for n in ("ci", "cx", "eq", "ek"))
        gd = sb("gd", [KP, GCH])
        PW = CH * (CH - 1) // 2
        dd = sb("dd", [KP, PW, GCH])
        PP = sb("P", [KP, 2, CH, GT])
        KA = sb("KA", [KP, 2, NCH, GB, T])
        QB = k.XT[:, :, :].rearrange("p u (b h t) -> p u b h t", b=GB, h=4)
        ad = sb("ad", [T, GB, CH, 4])
        tm = sb("tm", [T, 4, NCH, CH])
        A = sb("A", [T, GB, 4, T])
        by_chunk = lambda t: t.rearrange("p (n s) -> p s n", s=CH)

        def pairs(u, d):
            return bass.AP(tensor=PP[:, :, :, :].tensor, offset=(u * CH + d) * GT,
                           ap=[[2 * CH * GT, KP], [GT + 1, CH - d], [CH, GCH]])

        offs = [0]
        for d in range(1, CH):
            offs.append(offs[-1] + CH - d)
        sums, exps, made, part, whole, outs, copied = (s[n] for n in ("p_a", "p_b", "p_c", "p_d", "p_e",
                                                                      "p_f", "p_g"))
        with nc.Block(no_gpsimd_drain=True) as block:
            @block.gpsimd
            def _(g):
                g.memset(KA[:, 1, :, :, :], 0.0)
                g.memset(PP[:, 1, :, :], 0.0).then_inc(s["p_h"].sem, 1)

            @block.vector
            def _(v):
                ch = Chain(v, s["vec_step"])

                def factors(g):
                    u, tok = g % 2, slice(g * GT, (g + 1) * GT)
                    r, kk, e = by_chunk(R[:, tok]), by_chunk(K[:, tok]), E[:, tok]
                    ch.link(v.tensor_tensor_scan(ci[:, :], p("reset"), e, 0.0, ALU.mult, ALU.add))
                    ch.link(v.tensor_tensor(cx[:, :], ci[:, :], e, ALU.subtract))
                    c3, x3 = by_chunk(ci[:, :]), by_chunk(cx[:, :])
                    ends = c3[:, CH - 1:CH, :].broadcast_to([KP, CH, GCH])
                    v.tensor_tensor(by_chunk(ek[:, :]), c3, ends, ALU.subtract)
                    for d in range(1, CH):
                        last = v.tensor_tensor(dd[:, offs[d - 1]:offs[d], :], c3[:, 0:CH - d, :], x3[:, d:CH, :],
                                               ALU.subtract)
                    last.then_inc(sums.sem, 1)
                    v.wait_ge(*exps.at(g + 1))
                    if g == 1:
                        v.wait_ge(*s["p_h"].at(1))
                    v.wait_ge(*part.at(g - 1))
                    ch.link(v.tensor_tensor(eq[:, :], R[:, tok], eq[:, :], ALU.mult))
                    v.tensor_tensor(QB[:, u, :, :, :],
                                    eq[:, :].rearrange("p (b t) -> p b t", b=GB).unsqueeze(2)
                                    .broadcast_to([KP, GB, 4, T]),
                                    p("hmask").unsqueeze(1).unsqueeze(3).broadcast_to([KP, GB, 4, T]), ALU.mult)
                    ch.link(v.tensor_tensor(ek[:, :], K[:, tok], ek[:, :], ALU.mult))
                    flat = KA[:, u, :, :, :].rearrange("p i b (c s) -> p (i b c) s", s=CH)
                    for b in range(GB):
                        first = GCH + b * NCH
                        last = v.tensor_copy(flat[:, first:first + (GCH + 1) * (NCH - 2) + 1:GCH + 1, :],
                                             ek[:, b * T:(b + 1) * T - CH].rearrange("p (c s) -> p c s", s=CH))
                    ch.link(last)
                    g4 = gd[:, :].rearrange("p (b n) -> p b n", b=GB)
                    for i in range(2, NCH):
                        ch.link(v.tensor_tensor(KA[:, u, i, :, 0:CH * (i - 1)], KA[:, u, i - 1, :, 0:CH * (i - 1)],
                                                g4[:, :, i - 1:i].broadcast_to([KP, GB, CH * (i - 1)]), ALU.mult))
                    for d in range(1, CH):
                        at = dd[:, offs[d - 1]:offs[d], :]
                        last = v.tensor_tensor(at, at, kk[:, 0:CH - d, :], ALU.mult)
                    ch.link(last)
                    for d in range(1, CH):
                        last = v.tensor_tensor(pairs(u, d), dd[:, offs[d - 1]:offs[d], :], r[:, d:CH, :], ALU.mult)
                    last = v.scalar_tensor_tensor(pairs(u, 0), r, p("bonus"), kk, ALU.mult, ALU.mult)
                    last.then_inc(made.sem, 1)

                def matrix(g):
                    v.wait_ge(*part.at(g + 1))
                    ch.link(v.tensor_copy(ad[:, :, :, :], k.ps[0:T, 4, 0:GB * CH * 4].rearrange(
                        "p (b j h) -> p b j h", b=GB, j=CH)))
                    v.wait_ge(*outs.at(g * GB))
                    for b in range(GB):
                        v.wait_ge(*whole.at(g * GB + b))
                        ch.link(v.tensor_tensor(
                            tm[:, :, :, :],
                            ad[:, b, :, :].rearrange("p j h -> p h j").unsqueeze(2).broadcast_to([T, 4, NCH, CH]),
                            p("same")[0:T, :].rearrange("p (n j) -> p n j", j=CH).unsqueeze(1)
                            .broadcast_to([T, 4, NCH, CH]), ALU.mult))
                        v.tensor_tensor(A[:, b, :, :], tm[:, :, :, :].rearrange("p h n j -> p h (n j)"),
                                        chunks(k.ps[0:T, b, 0:GT], 4), ALU.add).then_inc(whole.sem, 1)

                v.memset(PP[:, 0, :, :], 0.0)
                ch.link(v.memset(KA[:, 0, :, :, :], 0.0))
                factors(0)
                for g in range(G):
                    if g + 1 < G:
                        factors(g + 1)
                    matrix(g)
                ch.close()

            @block.scalar
            def _(act):
                def exponentials(g):
                    act.wait_ge(*sums.at(g + 1))
                    act.activation(eq[:, :], cx[:, :], ACT.Exp, scale=-1.0)
                    act.activation(ek[:, :], ek[:, :], ACT.Exp)
                    act.activation(gd[:, :], by_chunk(ci[:, :])[:, CH - 1, :], ACT.Exp, scale=-1.0)
                    act.activation(dd[:, :, :], dd[:, :, :], ACT.Exp).then_inc(exps.sem, 1)

                exponentials(0)
                exponentials(1)
                for g in range(G):
                    if g + 2 < G:
                        exponentials(g + 2)
                    for b in range(GB):
                        act.wait_ge(*outs.at(g * GB + b + 1))
                        act.activation(O[:, (g * GB + b) * D:(g * GB + b + 1) * D], k.ps[0:T, 5 + b % 2, 0:D],
                                       ACT.Copy).then_inc(copied.sem, 1)

            @block.tensor
            def _(pe):
                def products(g):
                    u = g % 2
                    pe.wait_ge(*made.at(g + 1))
                    pe.wait_ge(*whole.at(g * GB))
                    for b in range(GB):
                        for j in range(CH):
                            at = (b * CH + j) * 4
                            last = pe.matmul(k.ps[0:T, 4, at:at + 4],
                                             PP[:, u, j, b * T:(b + 1) * T], p("hmask"), start=True, stop=True)
                    for b in range(GB):
                        out = chunks(k.ps[0:T, b, 0:GT], 4)
                        for i in range(NCH):
                            last = pe.matmul(out[:, :, i * CH:(i + 1) * CH], KA[:, u, i, b, :],
                                             QB[:, u, b, :, i * CH:(i + 1) * CH], start=True, stop=True)
                    last.then_inc(part.sem, 1)

                def outputs(g):
                    for b in range(GB):
                        pe.wait_ge(*whole.at(g * GB + b + 1))
                        pe.wait_ge(*copied.at(g * GB + b - 1))
                        for h in range(4):
                            at = (g * GB + b) * D + h * 64
                            last = pe.matmul(k.ps[0:T, 5 + b % 2, h * 64:(h + 1) * 64], A[:, b, h, :],
                                             V[:, at:at + 64], start=True, stop=True)
                        last.then_inc(outs.sem, 1)

                products(0)
                for g in range(G):
                    if g + 1 < G:
                        products(g + 1)
                    outputs(g)
        k.advance(p_a=G, p_b=G, p_c=G, p_d=G, p_e=B, p_f=B, p_g=B, p_h=1)


def host_l0_attn(name, a):
    w = {key[len(name) + 1:]: v for key, v in a.items() if key.startswith(name + "_")}
    wx2 = np.zeros((KP, 5, D), np.float32)
    per_mix = w["W_x2"].reshape(D, 5, 32)
    for j in range(4):
        wx2[32 * j:32 * j + 32, j] = per_mix[:, j].T
    wx2[0:32, 4] = per_mix[:, 4].T
    wx1 = np.zeros((D, 2 * KP), np.float32)
    wx1[:, :160] = w["W_x1"].T
    reset = np.ones((1, GT), np.float32)
    reset[:, ::CH] = 0.0
    f = dict(mu_x=columns(w["mu_x"]), wx1=by_rows(wx1), wx2=wx2.reshape(KP, -1),
             x_bias=w["x_bias"].reshape(5, 2, KP).transpose(2, 0, 1).reshape(KP, 10),
             wr=by_rows(w["W_r"].T), wk=by_rows(w["W_k"].T), wv=by_rows(w["W_v"].T), wg=by_rows(w["W_g"].T),
             wa=by_rows(w["A_w"].T), wb=w["B_w"].T, b_w=w["b_w"][:, None], bonus=w["bonus"].reshape(KP, 1),
             gn_w=on_rows(w["gn_weight"]), gn_b=on_rows(w["gn_bias"]), wo=by_rows(w["W_o"].T),
             hmask=head_rows(32), reset=on_rows(reset),
             same=np.repeat(np.repeat(np.eye(NCH, dtype=np.float32), CH, axis=0), CH, axis=1))
    return {name: packed(f)}



def project_features(k, w, C, dst, bias=None, fn=ACT.Identity):
    s = k.signals
    with k.nc.Block(no_gpsimd_drain=True) as block:
        @block.tensor
        def _(pe):
            with pe.Fori(0, G) as g:
                for c in range(C):
                    pe.wait_ge(*s["lin_act"].at(g * C + c - C + 1))
                    for kc in range(2):
                        last = pe.matmul(k.ps[:, c, 0:GT], w[:, kc, c * KP:(c + 1) * KP],
                                         k.XT[:, kc, bass.ds(g * GT, GT)], start=(kc == 0), stop=(kc == 1))
                    last.then_inc(s["lin_mm"].sem, 1)

        @block.scalar
        def _(act):
            k.table(act, fn)
            with act.Fori(0, G) as g:
                for c in range(C):
                    act.wait_ge(*s["lin_mm"].at(g * C + c + 1))
                    act.activation(dst[:, c, bass.ds(g * GT, GT)], k.ps[:, c, 0:GT], fn,
                                   bias=bias[:, c:c + 1] if bias is not None else 0.0).then_inc(
                                       s["lin_act"].sem, 1)
    k.advance(lin_mm=G * C, lin_act=G * C)


def backwards(ap):
    step, n = ap.ap[-1]
    return bass.AP(tensor=ap.tensor, offset=ap.offset + (n - 1) * step, ap=[*ap.ap[:-1], [-step, n]])


TQ = 64
NQ = D // TQ


def sub_l1_attn(k, ctx, name, packs):
    nc, s = k.nc, k.signals
    lay, dram = packs[name]
    tile, p = pack_tile(k, ctx, name + "_pack", lay)
    outer = lambda n, sh: k.tile(ctx, name + "_" + n, sh, F32)
    U = outer("u", [T, B * D])
    layer_norm(k, pack=(tile, dram, lay["_total"]), keep=U, rms_w=p("pre_w"))
    YR = outer("yr", [T, B * D])
    rows_dram = nc.dram_tensor(name + "_h", [2 * T - 1, D], F32).ap()
    with ExitStack() as mid:
        sb = lambda n, sh: k.tile(mid, name + "_" + n, sh, F32)
        XV, X2 = sb("xv", [T, B, D]), sb("x2", [T, B, D])
        poles = 16
        TP = sb("toeplitz", [T, 2, T, TQ])
        t_in = [s["toep_in0"], s["toep_in1"]]

        def load_toeplitz(sp, q):
            sp.dma_start(TP[:, q % 2, :, :],
                         bass.AP(tensor=rows_dram.tensor, offset=q * TQ, ap=[[D, T], [D, T], [1, TQ]])).then_inc(
                             t_in[q % 2].sem, 16)

        with ExitStack() as inner:
            ib = lambda n, sh: k.tile(inner, name + "_" + n, sh, F32)
            z = ib("z", [KP, 2, 6, GT])
            xv = ib("xvT", [KP, 2, 2, GT])
            h, ex = ib("filter", [KP, 2, T]), ib("ex", [KP, 8, T])
            hT, zero = ib("hT", [T, D]), ib("zero", [T, D])
            grown, added, summed, filter_turned, rows_ready, rows_out = (
                s[n] for n in ("p_g", "p_h", "p_i", "p_j", "p_k", "p_l"))
            w = chunks(p("in_proj"), 2)
            sw = p("short_w").rearrange("p (m j) -> p m j", j=3)
            prod, based, conv, ready, turned, moved = (s[n] for n in ("p_a", "p_b", "p_c", "p_d", "p_e", "p_f"))
            with nc.Block(no_gpsimd_drain=True) as block:
                @block.sync
                def _(sp):
                    sp.wait_ge(*rows_ready.at(2))
                    sp.dma_start(rows_dram[T:2 * T - 1, :], zero[0:T - 1, :]).then_inc(rows_out.sem, 16)
                    sp.dma_start(rows_dram[0:T, :], hT[:, :]).then_inc(rows_out.sem, 16)
                    sp.wait_ge(*rows_out.at(32))
                    load_toeplitz(sp, 0)
                    load_toeplitz(sp, 1)

                @block.tensor
                def _(pe):
                    def project(g):
                        for m in range(6):
                            pe.wait_ge(*conv.at(g * 6 + m - 5))
                            for kc in range(2):
                                last = pe.matmul(k.ps[:, m, 0:GT], w[:, kc, m * KP:(m + 1) * KP],
                                                 k.XT[:, kc, bass.ds(g * GT, GT)], start=(kc == 0),
                                                 stop=(kc == 1))
                            last.then_inc(prod.sem, 1)

                    def turn(g, u):
                        pe.wait_ge(*ready.at(g + 1))
                        for b in range(GB):
                            pe.wait_ge(*moved.at(2 * (g * GB + b - 1)))
                            for c in range(2):
                                pe.transpose(k.ps[0:T, 6 + b % 2, c * KP:(c + 1) * KP],
                                             xv[:, u, c, b * T:(b + 1) * T], k.ident[:, :])
                            for c in range(2):
                                last = pe.transpose(k.ps[0:T, 6 + b % 2, D + c * KP:D + (c + 1) * KP],
                                                    z[:, u, c, b * T:(b + 1) * T], k.ident[:, :])
                            last.then_inc(turned.sem, 1)

                    project(0)
                    pe.wait_ge(*summed.at(1))
                    for c in range(2):
                        last = pe.transpose(k.ps[0:T, 7, c * KP:(c + 1) * KP], h[:, c, :], k.ident[:, :])
                    last.then_inc(filter_turned.sem, 1)
                    project(1)
                    turn(0, 0)
                    turn(1, 1)
                    with pe.Fori(1, G // 2) as i:
                        for u in range(2):
                            project(2 * i + u)
                        for u in range(2):
                            turn(2 * i + u, u)

                @block.scalar
                def _(act):
                    k.table(act, ACT.Exp)
                    with act.Fori(0, poles // 4) as i:
                        for r in range(8):
                            c, at = r % 2, r // 2 + 4 * i
                            act.wait_ge(*added.at(8 * i + r - 7))
                            act.activation(ex[:, r, :], p("times"), ACT.Exp,
                                           scale=p("poles")[:, bass.ds(c * poles + at, 1)]).then_inc(grown.sem, 1)
                    act.wait_ge(*filter_turned.at(1))
                    act.activation(hT[:, :], k.ps[0:T, 7, 0:D], ACT.Copy).then_inc(rows_ready.sem, 1)
                    k.table(act, ACT.Identity)
                    with act.Fori(0, G // 2) as i:
                        for u in range(2):
                            g = 2 * i + u
                            act.wait_ge(*turned.at((g - 1) * GB))
                            for m in range(6):
                                act.wait_ge(*prod.at(g * 6 + m + 1))
                                act.activation(z[:, u, m, :], k.ps[:, m, 0:GT], ACT.Identity,
                                               scale=sw[:, m, 2:3], bias=p("short_b")[:, m:m + 1]).then_inc(
                                                   based.sem, 1)
                        for u in range(2):
                            g = 2 * i + u
                            for b in range(GB):
                                act.wait_ge(*turned.at(g * GB + b + 1))
                                act.activation(XV[:, bass.ds(g * GB + b, 1), :],
                                               k.ps[0:T, 6 + b % 2, 0:D].unsqueeze(1), ACT.Copy)
                                act.activation(X2[:, bass.ds(g * GB + b, 1), :],
                                               k.ps[0:T, 6 + b % 2, D:2 * D].unsqueeze(1), ACT.Copy).then_inc(
                                                   moved.sem, 2)

                @block.vector
                def _(v):
                    ch = Chain(v, s["vec_step"])
                    v.memset(zero[:, :], 0.0).then_inc(rows_ready.sem, 1)
                    ch.link(v.memset(h[:, :, :], 0.0))
                    with v.Fori(0, poles // 4) as i:
                        for r in range(8):
                            c, at = r % 2, r // 2 + 4 * i
                            v.wait_ge(*grown.at(8 * i + r + 1))
                            v.wait_ge(*added.at(8 * i + r - 1))
                            v.scalar_tensor_tensor(h[:, c, :], ex[:, r, :],
                                                   p("residues")[:, bass.ds(c * poles + at, 1)],
                                                   h[:, c, :], ALU.mult, ALU.add).then_inc(added.sem, 1)
                    v.wait_ge(*added.at(2 * poles))
                    v.tensor_tensor(h[:, :, T - 1:T], h[:, :, T - 1:T], p("skip").unsqueeze(2), ALU.add).then_inc(
                        summed.sem, 1)
                    with v.Fori(0, G // 2) as i:
                        ch.turn(i, 14)
                        for u in range(2):
                            g = 2 * i + u
                            for m in range(6):
                                v.wait_ge(*based.at(g * 6 + m + 1))
                                z3 = z[:, u, m, :].rearrange("p (b t) -> p b t", b=GB)
                                p3 = chunks(k.ps[:, m, 0:GT], GB)
                                ch.link(v.scalar_tensor_tensor(z3[:, :, 1:T], p3[:, :, 0:T - 1], sw[:, m, 1:2],
                                                               z3[:, :, 1:T], ALU.mult, ALU.add))
                                v.scalar_tensor_tensor(z3[:, :, 2:T], p3[:, :, 0:T - 2], sw[:, m, 0:1],
                                                       z3[:, :, 2:T], ALU.mult, ALU.add).then_inc(conv.sem, 1)
                            v.wait_ge(*conv.at(g * 6 + 6))
                            v.wait_ge(*turned.at((g - 1) * GB))
                            ch.link(v.tensor_tensor(xv[:, u, :, :], z[:, u, 2:4, :], z[:, u, 4:6, :], ALU.mult))
                            v.sem_inc(ready.sem, 1)
                        ch.end(G // 2)
                    ch.close()
            k.advance(p_a=6 * G, p_b=6 * G, p_c=6 * G, p_d=G, p_e=B, p_f=2 * B,
                      p_g=2 * poles, p_h=2 * poles, p_i=1, p_j=1, p_k=2, p_l=32)

        with ExitStack() as inner:
            ib = lambda n, sh: k.tile(inner, name + "_" + n, sh, F32)
            xq = ib("xq", [T, 2, 32, TQ])
            ys = ib("ys", [KP, 2, GT])
            cut, prod, out, turned, done = (s[n] for n in ("p_a", "p_b", "p_c", "p_d", "p_e"))
            per = TQ // 16
            with nc.Block(no_gpsimd_drain=True) as block:
                @block.sync
                def _(sp):
                    for q in range(2, NQ):
                        sp.wait_ge(*prod.at((q - 1) * per))
                        load_toeplitz(sp, q)

                @block.tensor
                def _(pe):
                    def back(q, r):
                        n = q * per + r
                        pe.wait_ge(*out.at(n + 1))
                        pe.wait_ge(*done.at(n - 1))
                        for f in range(4):
                            last = pe.transpose(k.ps[0:T, 4 + r % 2, f * KP:(f + 1) * KP],
                                                ys[:, r % 2, f * T:(f + 1) * T], k.ident[:, :])
                        last.then_inc(turned.sem, 1)

                    with pe.Fori(0, NQ // 2) as i:
                        for u in range(2):
                            q = 2 * i + u
                            pe.wait_ge(*cut.at(q + 1))
                            pe.wait_ge(*t_in[u].at((i + 1) * 16))
                            for r in range(per):
                                pe.wait_ge(*out.at(q * per + r - 3))
                                for f in range(4):
                                    for j in range(4):
                                        d = r * 16 + f * 4 + j
                                        last = pe.matmul(k.ps[32 * j:32 * j + 32, r % 4, f * T:(f + 1) * T],
                                                         xq[:, u, :, d], TP[:, u, :, d], start=True, stop=True)
                                last.then_inc(prod.sem, 1)
                                if r >= 1:
                                    back(q, r - 1)
                            back(q, per - 1)

                @block.scalar
                def _(act):
                    k.table(act, ACT.Copy)
                    with act.Fori(0, NQ // 2) as i:
                        for r in range(2 * per):
                            n = i * 2 * per + r
                            act.wait_ge(*prod.at(n + 1))
                            act.wait_ge(*turned.at(n - 1))
                            act.activation(ys[:, r % 2, :].rearrange("p (f t) -> p f t", f=4),
                                           backwards(chunks(k.ps[:, r % 4, 0:GT], 4)), ACT.Copy).then_inc(
                                               out.sem, 1)

                @block.vector
                def _(v):
                    v.memset(xq[:, :, :, :], 0.0).then_inc(s["vec_step"].sem, 1)
                    v.wait_ge(*s["vec_step"].at(1))
                    with v.Fori(0, NQ // 2) as i:
                        for u in range(2):
                            q = 2 * i + u
                            v.wait_ge(*prod.at((q - 1) * per))
                            v.tensor_copy(xq[:, u, 0:B, :], XV[:, :, bass.ds(q * TQ, TQ)]).then_inc(cut.sem, 1)
                            for r in range(per):
                                n = q * per + r
                                v.wait_ge(*turned.at(n + 1))
                                y = X2[:, :, bass.ds(q * TQ + r * 16, 16)].rearrange("p b d -> p d b")
                                v.tensor_tensor(y, k.ps[0:T, 4 + r % 2, 0:512].rearrange("p (d b) -> p d b", b=32)
                                                [:, :, 0:B], y, ALU.mult).then_inc(done.sem, 1)
            nb = NQ * per
            k.advance(p_a=NQ, p_b=nb, p_c=nb, p_d=nb, p_e=nb, toep_in0=32, toep_in1=32,
                      vec_step=1)

        def gated(v, b, dst):
            return v.tensor_copy(dst, X2[:, bass.ds(b, 1), :].rearrange("p b d -> p (b d)"))

        project_out(k, gated, chunks(p("out_proj"), 2), residual=U, out=YR)

    def add_to_stream(g):
        g.tensor_tensor(k.X[:, :], k.X[:, :], YR[:, :], ALU.add).then_inc(s["pool_step"].sem, 1)
        g.wait_ge(*s["pool_step"].at(1))

    layer_norm(k, rms_w=p("post_w"), source=YR, plain=False, meanwhile=add_to_stream)
    k.advance(pool_step=1)
    lay2, dram2 = packs[name + "_mlp"]
    feed_forward(k, name + "_mlp", dram2, lay2, 1, T, 6, True, ACT.Gelu_apprx_tanh)


def host_l1_attn(name, a):
    w = {key[len(name) + 1:]: v for key, v in a.items() if key.startswith(name + "_")}
    by_channel = lambda v: v.reshape(2, KP, -1).transpose(1, 0, 2).reshape(KP, -1)
    f = dict(pre_w=columns(w["pre_norm_w"]), post_w=columns(w["post_norm_w"]), in_proj=by_rows(w["in_proj_w"].T),
             short_w=w["short_w"].reshape(6, KP, 3).transpose(1, 0, 2).reshape(KP, 18),
             short_b=columns(w["short_b"]), poles=by_channel(w["log_poles"]), residues=by_channel(w["residues"]),
             skip=columns(w["D_skip"]), out_proj=by_rows(w["out_proj_w"].T),
             times=on_rows(np.arange(T, dtype=np.float32)[::-1]))
    both = np.concatenate([w["l1_w"], w["l2_w"]], axis=0).T
    done, lay = packed(dict(w1=by_rows(both), w2=by_rows(w["l3_w"].T, T)))
    return {name: packed(f), name + "_mlp": (done[None], lay)}


def sub_l2_attn(k, ctx, name, packs):
    nc, s = k.nc, k.signals
    lay, dram = packs[name]
    tile, p = pack_tile(k, ctx, name + "_pack", lay)
    sb = lambda n, sh: k.tile(ctx, name + "_" + n, sh, F32)
    U = sb("u", [T, B * D])
    layer_norm(k, pack=(tile, dram, lay["_total"]), keep=U)
    QT = sb("qT", [KP, 2, N])
    project_features(k, chunks(p("wq"), 2), 2, QT, bias=p("bq"))
    AT = sb("aT", [KP, 2, N])
    hd, HV = 16, 32
    xs = sb("xs", [KP, 2, 2, T])
    kv, sq, kn = sb("kv", [T, 4, 2 * D]), sb("sq", [T, 2, 2 * D]), sb("kn", [T, 2, 2 * D])
    mean, var, rstd = (sb(n, [T, 4, HV]) for n in ("mean", "var", "rstd"))
    km = sb("km", [KP, 2, 2, KP])
    wkv = chunks(p("wkv"), 2)
    copied, prod, cent, sqd, vard, roots, normed, mats, mixed, atts, added = (
        s[n] for n in ("p_a", "p_b", "p_c", "p_d", "p_e", "p_f", "p_g", "p_h", "p_i", "p_j", "p_k"))
    heads = lambda t: t.rearrange("p (h d) -> p h d", d=hd)

    def skewed(eng, parts, before_turn=lambda i: None, after_loop=lambda: None):
        def step(i, n):
            for lag, part in parts:
                m = n - lag
                if isinstance(i, int) and not 0 <= 4 * i + m < B:
                    continue
                part(4 * i + m, m % 4)

        for n in range(4):
            step(0, n)
        with eng.Fori(1, B // 4 - 1) as i:
            before_turn(i)
            for n in range(4):
                step(i, n)
        after_loop()
        for n in range(4 + 4):
            step(B // 4 - 1, n)

    with nc.Block(no_gpsimd_drain=True) as block:
        @block.gpsimd
        def _(g):
            x3 = k.X[:, :].rearrange("p (b d) -> p b d", b=B)
            g.tensor_tensor(k.X[:, :], k.X[:, :], U[:, :], ALU.add).then_inc(s["pool_step"].sem, 1)
            g.wait_ge(*s["pool_step"].at(1))
            g.tensor_tensor(x3, x3, p("p2_b")[0:T, :].unsqueeze(1).broadcast_to([T, B, D]), ALU.add)
            g.drain()

        @block.tensor
        def _(pe):
            def product(b, u):
                pe.wait_ge(*copied.at(b + 1))
                pe.wait_ge(*cent.at(b - 1))
                for c in range(2):
                    last = pe.matmul(k.ps[0:T, u % 2, 0:2 * D], xs[:, u % 2, c, :], wkv[:, c, :], start=(c == 0),
                                     stop=(c == 1))
                last.then_inc(prod.sem, 1)

            def matrices(b, u):
                pe.wait_ge(*normed.at(b + 1))
                pe.wait_ge(*mixed.at(b - 1))
                for c in range(2):
                    last = pe.matmul(k.ps[:, 2 + u % 2, c * KP:(c + 1) * KP], kn[:, u % 2, c * KP:(c + 1) * KP],
                                     kn[:, u % 2, D + c * KP:D + (c + 1) * KP], start=True, stop=True)
                last.then_inc(mats.sem, 1)

            def attend(b, u):
                pe.wait_ge(*mixed.at(b + 1))
                pe.wait_ge(*added.at(b - 1))
                for c in range(2):
                    last = pe.matmul(k.ps[:, 4 + u % 2, c * T:(c + 1) * T], km[:, u % 2, c, :],
                                     QT[:, c, bass.ds(b * T, T)], start=True, stop=True)
                last.then_inc(atts.sem, 1)

            product(0, 0)
            skewed(pe, [(-1, product), (2, matrices), (3, attend)])

        @block.scalar
        def _(act):
            def square(b, u):
                act.wait_ge(*cent.at(b + 1))
                act.wait_ge(*vard.at(b - 1))
                act.activation(sq[:, u % 2, :], kv[:, u, :], ACT.Square).then_inc(sqd.sem, 1)

            def root(b, u):
                act.wait_ge(*vard.at(b + 1))
                act.activation(rstd[:, u, :], var[:, u, :], ACT.Sqrt).then_inc(roots.sem, 1)

            k.table(act, ACT.Sqrt)
            skewed(act, [(0, square), (1, root)])

        @block.vector
        def _(v):
            ch = Chain(v, s["vec_step"])

            def copy_tokens(b, u):
                v.wait_ge(*prod.at(b - 1))
                v.tensor_copy(xs[:, u % 2, :, :], k.XT[:, :, bass.ds(b * T, T)]).then_inc(copied.sem, 1)

            def centre(b, u):
                v.wait_ge(*prod.at(b + 1))
                ch.link(v.tensor_tensor(kv[:, u, :], k.ps[0:T, u % 2, 0:2 * D], p("bkv")[0:T, :], ALU.add))
                ch.link(v.tensor_reduce(mean[:, u, :], heads(kv[:, u, :]), AX.X, ALU.add))
                ch.link(v.tensor_scalar(mean[:, u, :], mean[:, u, :], 1.0 / hd, None, ALU.mult))
                v.tensor_tensor(heads(kv[:, u, :]), heads(kv[:, u, :]),
                                mean[:, u, :].unsqueeze(2).broadcast_to([T, HV, hd]),
                                ALU.subtract).then_inc(cent.sem, 1)

            def variance(b, u):
                v.wait_ge(*sqd.at(b + 1))
                ch.link(v.tensor_reduce(var[:, u, :], heads(sq[:, u % 2, :]), AX.X, ALU.add))
                v.tensor_scalar(var[:, u, :], var[:, u, :], 1.0 / hd, LN_EPS, ALU.mult, ALU.add).then_inc(
                    vard.sem, 1)

            def normalise(b, u):
                v.wait_ge(*roots.at(b + 1))
                ch.link(v.reciprocal(rstd[:, u, :], rstd[:, u, :]))
                v.wait_ge(*mats.at(b - 1))
                ch.link(v.tensor_tensor(heads(kv[:, u, :]), heads(kv[:, u, :]),
                                        rstd[:, u, :].unsqueeze(2).broadcast_to([T, HV, hd]), ALU.mult))
                ch.link(v.tensor_tensor(kv[:, u, :], kv[:, u, :], p("gamma")[0:T, :], ALU.mult))
                v.tensor_tensor(kn[:, u % 2, :], kv[:, u, :], p("beta")[0:T, :], ALU.add).then_inc(
                    normed.sem, 1)

            def mix(b, u):
                v.wait_ge(*mats.at(b + 1))
                v.wait_ge(*atts.at(b - 1))
                ch.link(v.scalar_tensor_tensor(km[:, u % 2, :, :], chunks(k.ps[:, 2 + u % 2, 0:2 * KP], 2),
                                               1.0 / T, chunks(p("temp"), 2), ALU.mult, ALU.mult))
                v.tensor_tensor(km[:, u % 2, :, :], km[:, u % 2, :, :], chunks(p("bias"), 2), ALU.add).then_inc(
                    mixed.sem, 1)

            def add_input(b, u):
                v.wait_ge(*atts.at(b + 1))
                v.tensor_tensor(AT[:, :, bass.ds(b * T, T)], chunks(k.ps[:, 4 + u % 2, 0:2 * T], 2),
                                k.XT[:, :, bass.ds(b * T, T)], ALU.add).then_inc(added.sem, 1)

            copy_tokens(0, 0)
            copy_tokens(1, 1)
            skewed(v, [(-2, copy_tokens), (0, centre), (1, variance), (2, normalise), (3, mix), (4, add_input)],
                   lambda i: ch.turn(i - 1, 4 * 8), lambda: ch.end(B // 4 - 2))
            v.wait_ge(*added.at(B))
            ch.close()
    k.advance(pool_step=1, p_a=B, p_b=B, p_c=B, p_d=B, p_e=B, p_f=B, p_g=B, p_h=B, p_i=B, p_j=B, p_k=B)
    lay2, dram2 = packs[name + "_mlp"]
    feed_forward(k, name + "_mlp", dram2, lay2, 1, KP, 2, False, ACT.Gelu, src=AT)


def on_diagonal(blocks, rows=16):
    out = np.zeros((KP, 2, KP), np.float32)
    for h in range(16):
        c, at = h // 8, (h % 8) * rows
        out[at:at + rows, c, at:at + rows] = blocks[h]
    return out.reshape(KP, -1)


def host_l2_attn(name, a):
    w = {key[len(name) + 1:]: v for key, v in a.items() if key.startswith(name + "_")}
    wt = w["qkv_w"].T
    each = lambda kk, vv: on_rows(np.concatenate([np.tile(kk, 16), np.tile(vv, 16)]))
    f = dict(wq=by_rows(wt[:, :D]), wkv=by_rows(wt[:, D:]), bq=columns(w["qkv_b"][:D]),
             bkv=on_rows(w["qkv_b"][D:]), gamma=each(w["kn_g"], w["vn_g"]), beta=each(w["kn_b"], w["vn_b"]),
             temp=on_diagonal(np.broadcast_to(w["temperature"], (16, 16, 16))), bias=on_diagonal(w["attn_bias"]),
             p2_b=on_rows(w["p2_b"]))
    done, lay = packed(dict(w1=by_rows(w["p1_w"].T), w2=by_rows(w["p2_w"].T), b1=columns(w["p1_b"])))
    return {name: packed(f), name + "_mlp": (done[None], lay)}



def build_program(nc, aps, layouts, layers):
    with ExitStack() as ctx:
        k = Core(nc, ctx)
        packs = {name: (lay, aps["in_" + name]) for name, lay in layouts.items()}
        k.aps = aps
        with nc.Block(no_gpsimd_drain=True) as block:
            names = list(SIGNALS)

            @block.gpsimd
            def _(g):
                g.memset(k.spark[:, :], 0.0)

            def raise_all(eng, part):
                for name in names[part::4]:
                    eng.sem_inc(k[name].sem, HEAD)

            @block.vector
            def _(v):
                raise_all(v, 0)

            @block.scalar
            def _(act):
                raise_all(act, 1)

            @block.tensor
            def _(pe):
                raise_all(pe, 2)

            @block.sync
            def _(sp):
                raise_all(sp, 3)

        tiles = token_tiles(8) + 2
        k.rows_in = nc.dram_tensor("rows_in", [tiles * KT, D], F32).ap()
        k.rows_out = nc.dram_tensor("rows_out", [(tiles - 2) * KT, D], F32).ap()
        routed_zeros = k.tile(ctx, "zeros", [KT, D])
        with nc.Block(no_gpsimd_drain=True) as block:
            @block.vector
            def _(v):
                v.memset(routed_zeros[:, :], 0.0).then_inc(k["vec_step"].sem, 1)
                v.wait_ge(*k["vec_step"].at(1))

            @block.scalar
            def _(act):
                act.wait_ge(*k["vec_step"].at(1))
                act.dma_start(k.rows_in.rearrange("(n p) d -> p n d", p=KT),
                              routed_zeros[:, :].unsqueeze(1).broadcast_to([KT, tiles, D])).then_inc(
                                  k["rows_zeroed"].sem, 16)

            @block.sync
            def _(sp):
                sp.dma_start(k.X[:, :].rearrange("t (b d) -> t b d", b=B),
                             aps["in_x"].rearrange("b t d -> t b d")).then_inc(k["x_in"].sem, 16)
                sp.wait_ge(*k["x_in"].at(16))

            @block.gpsimd
            def _(g):
                g.memset(k.ident[:, :], 0.0).then_inc(k["pool_step"].sem, 1)
                g.wait_ge(*k["pool_step"].at(1))
                g.affine_select(out=k.ident[:, :], in_=k.ident[:, :], compare_op=ALU.not_equal, fill=1.0, base=0,
                                pattern=[[-1, KP]], channel_multiplier=1).then_inc(k["pool_step"].sem, 1)
                g.wait_ge(*k["pool_step"].at(2))
        k.advance(pool_step=2, x_in=16, vec_step=1)

        for name in layers:
            with ExitStack() as layer:
                if name in FFN and FFN[name]["experts"] == 8:
                    sub_routed_ffn(k, layer, name, packs, FFN[name])
                elif name in FFN:
                    sub_ffn(k, layer, name, packs, FFN[name])
                elif name in ATTENTION:
                    sub_attention(k, layer, name, packs, ATTENTION[name])
                else:
                    SUB[name](k, layer, name, packs)

        with nc.Block(no_gpsimd_drain=True) as block:
            @block.sync
            def _(sp):
                sp.dma_start(aps["out"].rearrange("b t d -> t b d"),
                             k.X[:, :].rearrange("t (b d) -> t b d", b=B)).then_inc(k["x_out"].sem, 16)
                sp.wait_ge(*k["x_out"].at(16))
                sp.wait_ge(*k["rows_zeroed"].at(16))



def by_rows(w, rows=KP):
    return w.reshape(-1, rows, w.shape[1]).transpose(1, 0, 2).reshape(rows, -1)


def columns(v, rows=KP):
    return v.reshape(-1, rows).T


def on_rows(v, parts=KP):
    return np.broadcast_to(v.reshape(1, -1), (parts, v.size))


def packed(fields):
    total = sum(a.shape[1] for a in fields.values())
    out, lay, off = np.zeros((KP, total), np.float32), {}, 0
    for name, a in fields.items():
        out[:a.shape[0], off:off + a.shape[1]] = a
        lay[name] = (off, a.shape[0], a.shape[1])
        off += a.shape[1]
    lay["_total"] = total
    return out, lay


def host_ffn(name, a):
    w = {key[len(name) + 1:]: v for key, v in a.items() if key.startswith(name + "_")}
    if name == "L0_ffn":
        small = dict(router=by_rows(w["router_w"]), b2=w["b2"][None])
        experts = [dict(w1=by_rows(w["w1"]), w2=by_rows(w["w2"]), b1=columns(w["b1"]))]
    elif name == "L1_ffn":
        small = dict(router=by_rows(w["Wr"]), router_b=w["br"][:, None], b2=w["b2"])
        experts = [dict(w1=by_rows(w["W1"][e]), w2=by_rows(w["W2"][e]), b1=columns(w["b1"][e])) for e in range(8)]
    elif name == "L2_ffn":
        small = dict(router=by_rows(w["w_gate"].T), b2=w["b2"])
        experts = [dict(w1=by_rows(w["W1"][e]), w2=by_rows(w["W2"][e]), b1=columns(w["b1"][e])) for e in range(8)]
    else:
        small = dict(b2=w["b2"][:4])
        experts = [dict(w1=by_rows(w["W1"][e]), w2=by_rows(w["W2"][e]), b1=columns(w["b1"][e])) for e in range(4)]
    if FFN[name]["experts"] == 8:
        small["steps"] = on_rows(np.tile(np.arange(N // KT, dtype=np.float32) * KT, 8))
        small["turns"] = on_rows(np.repeat(np.arange(token_tiles(8), dtype=np.float32), 8), 1)
    done = [packed(e) for e in experts]
    return {name: packed(small), name + "_experts": (np.stack([d[0] for d in done]), done[0][1])}


def lay_out(inputs, layers):
    a = {n: np.asarray(v) for n, v in inputs.items()}
    out = {}
    for name in layers:
        host = host_ffn if name in FFN else host_attention if name in ATTENTION else HOST[name]
        out.update(host(name, a))
    return out


def kernel(**inputs):
    import concourse.bacc as bacc
    from concourse.bass_utils import run_bass_kernel_spmd

    laid = lay_out(inputs, LAYERS)
    arrays = {"in_" + n: np.ascontiguousarray(v[0]) for n, v in laid.items()}
    arrays["in_x"] = np.ascontiguousarray(inputs["x"])
    if "ctx_768" in inputs:
        arrays.update(host_context(inputs))
    nc = bacc.Bacc("TRN2", target_bir_lowering=False, num_devices=1)
    aps = {n: nc.dram_tensor(n, v.shape, mybir.dt.from_np(v.dtype), kind="ExternalInput").ap()
           for n, v in arrays.items()}
    aps["out"] = nc.dram_tensor("out", (B, T, D), F32, kind="ExternalOutput").ap()
    build_program(nc, aps, {n: v[1] for n, v in laid.items()}, LAYERS)
    r = run_bass_kernel_spmd(nc, [arrays], core_ids=[0])
    return r.results[0]["out"]


def host_context(inputs):
    c = np.asarray(inputs["ctx_768"]).transpose(0, 2, 1).reshape(B, 2, CR, S2).transpose(0, 2, 1, 3)
    m = np.asarray(inputs["mask_BxS2_bf1"]).view(np.uint8)
    return {"in_ctx": np.ascontiguousarray(c), "in_mask": np.ascontiguousarray(m)}

SUB = {"L3_xattn": sub_l3_xattn, "L0_attn": sub_l0_attn, "L1_attn": sub_l1_attn, "L2_attn": sub_l2_attn}
HOST = {"L3_xattn": host_l3_xattn, "L0_attn": host_l0_attn, "L1_attn": host_l1_attn, "L2_attn": host_l2_attn}
LAYERS = ["L0_attn", "L0_xattn", "L0_ffn", "L1_attn", "L1_xattn", "L1_ffn", "L2_attn", "L2_xattn", "L2_ffn",
          "L3_attn", "L3_xattn", "L3_ffn"]
```
